# Optimizing a Trainium2 kernel written in Bass

```python
import numpy as np
import jax
import jax.numpy as jnp

def _softmax(x, axis=-1):
    return jax.nn.softmax(x, axis=axis)

def _gelu(x):
    return jax.nn.gelu(x, approximate=True)

def _silu(x):
    return jax.nn.silu(x)

def _sigmoid(x):
    return jax.nn.sigmoid(x)

def _layernorm(x, axis=-1, eps=1e-05):
    m = jnp.mean(x, axis=axis, keepdims=True)
    v = jnp.var(x, axis=axis, keepdims=True)
    return (x - m) / jnp.sqrt(v + eps)

def _scatter_add(tgt, idx, src, axis=0):
    return tgt.at[idx].add(src)

def _segment_sum(src, seg, n):
    return jax.ops.segment_sum(src, seg, n)
kernel_name = 'mk_seq_preln_d4_jaxref_r8_f0166e'

def setup_inputs(seed: int=0):
    np.random.seed(seed)
    _w = jnp.asarray

    def _L0_attn_setup():
        import jax, jax.numpy as jnp
        import numpy as np
        D_MODEL = 128
        NUM_HEADS = 16
        D_K = 128
        D_V = 128
        D_IN = 128
        THETA = 10000.0
        B, S = (2, 256)

        def _rope(t, theta):
            hd = t.shape[-1]
            inv_freq = 1.0 / theta ** (jnp.arange(0, hd, 2, dtype=jnp.float32) / hd)
            pos = jnp.arange(t.shape[-2], dtype=jnp.float32)
            ang = pos[:, None] * inv_freq[None, :]
            cos, sin = (jnp.cos(ang), jnp.sin(ang))
            tp = t.reshape(t.shape[:-1] + (hd // 2, 2))
            t0, t1 = (tp[..., 0], tp[..., 1])
            out = jnp.stack([t0 * cos - t1 * sin, t0 * sin + t1 * cos], axis=-1)
            return out.reshape(t.shape)
        key = jax.random.key(seed)
        k1, k2, k3, k4, k5 = jax.random.split(key, 5)
        std_qkv = (2.0 / (D_IN + D_K)) ** 0.5
        std_o = (2.0 / (D_V + D_MODEL)) ** 0.5
        x = jax.random.normal(k1, (B, S, D_IN), jnp.float32)
        wq = jax.random.normal(k2, (D_IN, D_K), jnp.float32) * std_qkv
        wk = jax.random.normal(k3, (D_IN, D_K), jnp.float32) * std_qkv
        wv = jax.random.normal(k4, (D_IN, D_V), jnp.float32) * std_qkv
        wo = jax.random.normal(k5, (D_V, D_MODEL), jnp.float32) * std_o
        return {'x': x, 'wq': wq, 'wk': wk, 'wv': wv, 'wo': wo}
    _L0_attn_in = _L0_attn_setup()

    def _L0_ffn_setup():
        import jax, jax.numpy as jnp
        import numpy as np
        DIM = 128
        DEPTH = 2
        HEADS = 8
        DIM_HEAD = 64
        WINDOW = 64
        INNER = HEADS * DIM_HEAD
        HID = int(DIM * 4 * 2 / 3)
        B, N = (2, 1024)
        QK_SCALE = 8.0

        def shift_token(t):
            t1, t2 = jnp.split(t, 2, axis=-1)
            t2 = jnp.pad(t2, ((0, 0), (1, 0), (0, 0)))[:, :-1]
            return jnp.concatenate([t1, t2], axis=-1)

        def l2norm(t):
            return t / jnp.clip(jnp.linalg.norm(t, axis=-1, keepdims=True), 1e-12)

        def rotate_half(x):
            x1, x2 = jnp.split(x, 2, axis=-1)
            return jnp.concatenate([-x2, x1], axis=-1)

        def rotary_xpos(q, k):
            n = q.shape[-2]
            half_idx = jnp.arange(0, DIM_HEAD, 2, dtype=jnp.float32)
            inv_freq = 1.0 / 10000.0 ** (half_idx / DIM_HEAD)
            t = jnp.arange(n, dtype=jnp.float32)
            freqs = t[:, None] * inv_freq[None, :]
            freqs = jnp.concatenate([freqs, freqs], axis=-1)
            base = (half_idx + 0.4 * DIM_HEAD) / (1.4 * DIM_HEAD)
            power = (t - n // 2) / float(WINDOW // 2)
            scale = base[None, :] ** power[:, None]
            scale = jnp.concatenate([scale, scale], axis=-1)
            cos, sin = (jnp.cos(freqs), jnp.sin(freqs))
            q = q * cos * scale + rotate_half(q) * sin * scale
            k = k * cos / scale + rotate_half(k) * sin / scale
            return (q, k)

        def local_attention(q, k, v):
            b, h, n, d = q.shape
            w = n // WINDOW
            bq = q.reshape(b, h, w, WINDOW, d) * QK_SCALE
            bk = k.reshape(b, h, w, WINDOW, d)
            bv = v.reshape(b, h, w, WINDOW, d)

            def look_around(t):
                p = jnp.pad(t, ((0, 0), (0, 0), (1, 0), (0, 0), (0, 0)))
                return jnp.concatenate([p[:, :, :w], p[:, :, 1:]], axis=3)
            bk, bv = (look_around(bk), look_around(bv))
            bt = jnp.arange(n).reshape(w, WINDOW)
            btp = jnp.pad(bt, ((1, 0), (0, 0)), constant_values=-1)
            btk = jnp.concatenate([btp[:w], btp[1:]], axis=1)
            sim = jnp.einsum('bhwid,bhwjd->bhwij', bq, bk)
            i = bt[:, :, None]
            j = btk[:, None, :]
            mask = (i < j) | (i > j + WINDOW) | (j == -1)
            sim = jnp.where(mask, -jnp.finfo(sim.dtype).max, sim)
            attn = jax.nn.softmax(sim, axis=-1)
            out = jnp.einsum('bhwij,bhwjd->bhwid', attn, bv)
            return out.reshape(b, h, n, d)

        def _layer(x, wqkv, qs, ksc, wo, lg, lb, w1, b1, w2, b2):
            b, n, _ = x.shape
            h = shift_token(x)
            qkv = h @ wqkv
            q, k, v = jnp.split(qkv, 3, axis=-1)
            to_heads = lambda t: t.reshape(b, n, HEADS, DIM_HEAD).transpose(0, 2, 1, 3)
            q, k, v = (to_heads(q), to_heads(k), to_heads(v))
            q = l2norm(q) * qs
            k = l2norm(k) * ksc
            q, k = rotary_xpos(q, k)
            o = local_attention(q, k, v)
            o = o.transpose(0, 2, 1, 3).reshape(b, n, INNER)
            x = x + o @ wo
            h = shift_token(x)
            mu = h.mean(-1, keepdims=True)
            var = h.var(-1, keepdims=True)
            h = (h - mu) / jnp.sqrt(var + 1e-05) * lg + lb
            h = h @ w1 + b1
            a, g = jnp.split(h, 2, axis=-1)
            h = a * jax.nn.gelu(g, approximate=False)
            x = x + h @ w2 + b2
            return x
        key = jax.random.key(seed)
        ks = jax.random.split(key, 6)
        return {'x': jax.random.normal(ks[0], (B, N, DIM), jnp.float32), 'wqkv': jax.random.normal(ks[1], (DEPTH, DIM, 3 * INNER), jnp.float32) * 0.02, 'q_scale': jnp.ones((DEPTH, DIM_HEAD), jnp.float32), 'k_scale': jnp.ones((DEPTH, DIM_HEAD), jnp.float32), 'wo': jax.random.normal(ks[2], (DEPTH, INNER, DIM), jnp.float32) * 0.02, 'ln_g': jnp.ones((DEPTH, DIM), jnp.float32), 'ln_b': jnp.zeros((DEPTH, DIM), jnp.float32), 'w1': jax.random.normal(ks[3], (DEPTH, DIM, 2 * HID), jnp.float32) * 0.02, 'b1': jnp.zeros((DEPTH, 2 * HID), jnp.float32), 'w2': jax.random.normal(ks[4], (DEPTH, HID, DIM), jnp.float32) * 0.02, 'b2': jnp.zeros((DEPTH, DIM), jnp.float32)}
    _L0_ffn_in = _L0_ffn_setup()

    def _L1_attn_setup():
        import jax, jax.numpy as jnp
        import numpy as np
        HEADS = 8
        DIM_HEAD = 128
        BLOCK_N = 128

        def castle_attention(q, k, v, qu, ku, vu, scale):
            b, h, s, d = q.shape
            q = q * scale
            qu = qu * scale
            qk = jnp.einsum('bhid,bhjd->bhij', q, k)
            quku = jnp.einsum('bhid,bhjd->bhij', qu, ku)
            i = jnp.arange(s)[:, None]
            j = jnp.arange(s)[None, :]
            causal = i >= j
            qk = jnp.where(causal, qk, -jnp.inf)
            la = jnp.where(causal, 0.0, jax.nn.sigmoid(quku))
            nb = s // BLOCK_N
            la_b = la.reshape(b, h, s, nb, BLOCK_N)
            vu_b = vu.reshape(b, h, nb, BLOCK_N, d)
            su = jnp.einsum('bhmtc,bhtcd->bhmtd', la_b, vu_b)
            scores = qk.reshape(b, h, s, nb, BLOCK_N) - jax.nn.silu(su)
            scores = scores.reshape(b, h, s, s)
            p = jax.nn.softmax(scores, axis=-1)
            return jnp.einsum('bhij,bhjd->bhid', p, v)
        key = jax.random.key(seed)
        k1, k2, k3 = jax.random.split(key, 3)
        B, S, D = (1, 256, 128)
        dim_inner = HEADS * DIM_HEAD
        x = jax.random.normal(k1, (B, S, D), dtype=jnp.float32)
        w_qkv = jax.random.normal(k2, (D, 6 * dim_inner), dtype=jnp.float32) * 0.02
        w_out = jax.random.normal(k3, (dim_inner, D), dtype=jnp.float32) * 0.02
        return {'x': x, 'w_qkv': w_qkv, 'w_out': w_out}
    _L1_attn_in = _L1_attn_setup()

    def _L1_ffn_setup():
        import jax, jax.numpy as jnp
        import numpy as np
        D_MODEL = 128
        D_FF = 512
        NUM_EXPERTS = 8
        TOP_K = 2
        BATCH = 4
        SEQ = 256
        key = jax.random.key(seed)
        ks = jax.random.split(key, 8)
        s = 0.02
        x = jax.random.normal(ks[0], (BATCH, SEQ, D_MODEL), dtype=jnp.float32)
        router_w = jax.random.normal(ks[1], (D_MODEL, NUM_EXPERTS), dtype=jnp.float32) * s
        router_b = jnp.zeros((NUM_EXPERTS,), dtype=jnp.float32)
        W1 = jax.random.normal(ks[2], (NUM_EXPERTS, D_MODEL, D_FF), dtype=jnp.float32) * s
        b1 = jnp.zeros((NUM_EXPERTS, D_FF), dtype=jnp.float32)
        W2 = jax.random.normal(ks[3], (NUM_EXPERTS, D_FF, D_MODEL), dtype=jnp.float32) * s
        b2 = jnp.zeros((NUM_EXPERTS, D_MODEL), dtype=jnp.float32)
        return {'x': x, 'router_w': router_w, 'router_b': router_b, 'W1': W1, 'b1': b1, 'W2': W2, 'b2': b2}
    _L1_ffn_in = _L1_ffn_setup()

    def _L2_attn_setup():
        import jax, jax.numpy as jnp
        import numpy as np
        B, S, D = (4, 256, 128)

        def _wkv(k, v, time_decay, u):
            w = -jnp.exp(time_decay)
            b, s, d = k.shape
            aa = jnp.zeros((b, d), k.dtype)
            bb = jnp.zeros((b, d), k.dtype)
            pp = jnp.full((b, d), -1e+30, k.dtype)

            def step(carry, kv):
                aa, bb, pp = carry
                kk, vv = kv
                ww = u + kk
                p = jnp.maximum(pp, ww)
                e1 = jnp.exp(pp - p)
                e2 = jnp.exp(ww - p)
                out = (e1 * aa + e2 * vv) / (e1 * bb + e2)
                ww2 = w + pp
                p2 = jnp.maximum(ww2, kk)
                e1b = jnp.exp(ww2 - p2)
                e2b = jnp.exp(kk - p2)
                return ((e1b * aa + e2b * vv, e1b * bb + e2b, p2), out)
            _, outs = jax.lax.scan(step, (aa, bb, pp), (k.transpose(1, 0, 2), v.transpose(1, 0, 2)))
            return outs.transpose(1, 0, 2)
        key = jax.random.key(seed)
        ks = jax.random.split(key, 10)
        s = 0.02
        return {'x': jax.random.normal(ks[0], (B, S, D), jnp.float32), 'time_mix_k': jax.random.uniform(ks[1], (1, 1, D), jnp.float32), 'time_mix_v': jax.random.uniform(ks[2], (1, 1, D), jnp.float32), 'time_mix_r': jax.random.uniform(ks[3], (1, 1, D), jnp.float32), 'time_decay': jax.random.normal(ks[4], (D,), jnp.float32) * 0.1, 'time_first': jax.random.normal(ks[5], (D,), jnp.float32) * 0.1, 'Wk': jax.random.normal(ks[6], (D, D), jnp.float32) * s, 'Wv': jax.random.normal(ks[7], (D, D), jnp.float32) * s, 'Wr': jax.random.normal(ks[8], (D, D), jnp.float32) * s, 'Wo': jax.random.normal(ks[9], (D, D), jnp.float32) * s}
    _L2_attn_in = _L2_attn_setup()

    def _L2_ffn_setup():
        import math
        import jax, jax.numpy as jnp
        import numpy as np
        E = 8
        H = 128
        HP = 128
        SPARSITY = 8
        N_ROTATE = 64
        ROPE_BASE = 10000.0

        def _rope(x, pos):
            half = N_ROTATE // 2
            inv_freq = 1.0 / ROPE_BASE ** (jnp.arange(half, dtype=jnp.float32) * 2.0 / N_ROTATE)
            ang = pos.astype(jnp.float32)[..., None] * inv_freq
            sin, cos = (jnp.sin(ang), jnp.cos(ang))
            x1, x2 = (x[..., :half], x[..., half:])
            return jnp.concatenate([x1 * cos - x2 * sin, x2 * cos + x1 * sin], axis=-1)
        key = jax.random.key(seed)
        k1, k2, k3, k4 = jax.random.split(key, 4)
        B, T = (4, 1024)
        X = jax.random.normal(k1, (B, T, H), dtype=jnp.float32)
        Wr = jax.random.uniform(k2, (E, H), minval=-1 / math.sqrt(H), maxval=1 / math.sqrt(H), dtype=jnp.float32)
        bq = 1 / math.sqrt(3 * HP)
        Wqkv = jax.random.uniform(k3, (E, H, 3 * HP), minval=-bq, maxval=bq, dtype=jnp.float32)
        bo = 1 / math.sqrt(H * E)
        Wo = jax.random.uniform(k4, (E, HP, H), minval=-bo, maxval=bo, dtype=jnp.float32)
        return {'X': X, 'Wr': Wr, 'Wqkv': Wqkv, 'Wo': Wo}
    _L2_ffn_in = _L2_ffn_setup()

    def _L3_attn_setup():
        import jax, jax.numpy as jnp
        import numpy as np
        D_MODEL, D_STATE, D_INNER = (128, 16, 256)
        B, S = (2, 512)
        EPS = 1e-05
        key = jax.random.key(seed)
        ks = jax.random.split(key, 8)
        return {'x': jax.random.normal(ks[0], (B, S, D_MODEL), dtype=jnp.float32), 'norm_w': jnp.ones((D_MODEL,), jnp.float32), 'norm_b': jnp.zeros((D_MODEL,), jnp.float32), 'W_in': jax.random.normal(ks[1], (D_INNER, D_MODEL), jnp.float32) * (1.0 / np.sqrt(D_MODEL)), 'b_in': jnp.zeros((D_INNER,), jnp.float32), 'A': jax.random.normal(ks[2], (D_INNER, D_STATE), jnp.float32), 'B_ssm': jax.random.normal(ks[3], (D_INNER, D_STATE), jnp.float32), 'C_ssm': jax.random.normal(ks[4], (D_INNER, D_STATE), jnp.float32), 'W_out': jax.random.normal(ks[5], (D_MODEL, D_INNER), jnp.float32) * (1.0 / np.sqrt(D_INNER)), 'b_out': jnp.zeros((D_MODEL,), jnp.float32)}
    _L3_attn_in = _L3_attn_setup()

    def _L3_ffn_setup():
        import jax, jax.numpy as jnp
        import numpy as np
        NUM_EXPERTS = 64
        TOP_K = 8
        HIDDEN = 128
        INTER = 96
        BATCH, SEQ = (1, 128)
        CAPACITY = 32

        def _moe_forward(hidden_states, gate_w, w_gate, w_up, w_down):
            B, S, H = hidden_states.shape
            x = hidden_states.reshape(-1, H)
            T = x.shape[0]
            logits = (x @ gate_w.T).astype(jnp.float32)
            probs = jax.nn.softmax(logits, axis=-1)
            topk_p, topk_i = jax.lax.top_k(probs, TOP_K)
            topk_p = topk_p / jnp.sum(topk_p, axis=-1, keepdims=True)
            flat_e = topk_i.reshape(-1)
            onehot = jax.nn.one_hot(flat_e, NUM_EXPERTS, dtype=jnp.int32)
            pos_all = jnp.cumsum(onehot, axis=0) - 1
            pos = jnp.take_along_axis(pos_all, flat_e[:, None], axis=1)[:, 0]
            x_rep = jnp.repeat(x, TOP_K, axis=0)
            dispatch = jnp.zeros((NUM_EXPERTS, CAPACITY, H), x.dtype)
            dispatch = dispatch.at[flat_e, pos].set(x_rep, mode='drop')
            g = jax.nn.silu(jnp.einsum('ech,eih->eci', dispatch, w_gate))
            u = jnp.einsum('ech,eih->eci', dispatch, w_up)
            y = jnp.einsum('eci,ehi->ech', g * u, w_down)
            valid = pos < CAPACITY
            y_tok = y[flat_e, jnp.minimum(pos, CAPACITY - 1)]
            w = (topk_p.reshape(-1) * valid.astype(topk_p.dtype)).astype(x.dtype)
            out = (y_tok * w[:, None]).reshape(T, TOP_K, H).sum(axis=1)
            return out.reshape(B, S, H)
        key = jax.random.key(seed)
        k1, k2, k3, k4, k5 = jax.random.split(key, 5)
        scale = 0.02
        return {'hidden_states': jax.random.normal(k1, (BATCH, SEQ, HIDDEN), dtype=jnp.float32), 'gate_w': jax.random.normal(k2, (NUM_EXPERTS, HIDDEN), dtype=jnp.float32) * scale, 'w_gate': jax.random.normal(k3, (NUM_EXPERTS, INTER, HIDDEN), dtype=jnp.float32) * scale, 'w_up': jax.random.normal(k4, (NUM_EXPERTS, INTER, HIDDEN), dtype=jnp.float32) * scale, 'w_down': jax.random.normal(k5, (NUM_EXPERTS, HIDDEN, INTER), dtype=jnp.float32) * scale}
    _L3_ffn_in = _L3_ffn_setup()
    _d = {'L0_attn_x': _L0_attn_in['x'], 'L0_attn_wq': _L0_attn_in['wq'], 'L0_attn_wk': _L0_attn_in['wk'], 'L0_attn_wv': _L0_attn_in['wv'], 'L0_attn_wo': _L0_attn_in['wo'], 'L0_ffn_wqkv': _L0_ffn_in['wqkv'], 'L0_ffn_q_scale': _L0_ffn_in['q_scale'], 'L0_ffn_k_scale': _L0_ffn_in['k_scale'], 'L0_ffn_wo': _L0_ffn_in['wo'], 'L0_ffn_ln_g': _L0_ffn_in['ln_g'], 'L0_ffn_ln_b': _L0_ffn_in['ln_b'], 'L0_ffn_w1': _L0_ffn_in['w1'], 'L0_ffn_b1': _L0_ffn_in['b1'], 'L0_ffn_w2': _L0_ffn_in['w2'], 'L0_ffn_b2': _L0_ffn_in['b2'], 'L1_attn_w_qkv': _L1_attn_in['w_qkv'], 'L1_attn_w_out': _L1_attn_in['w_out'], 'L1_ffn_router_w': _L1_ffn_in['router_w'], 'L1_ffn_router_b': _L1_ffn_in['router_b'], 'L1_ffn_W1': _L1_ffn_in['W1'], 'L1_ffn_b1': _L1_ffn_in['b1'], 'L1_ffn_W2': _L1_ffn_in['W2'], 'L1_ffn_b2': _L1_ffn_in['b2'], 'L2_attn_time_mix_k': _L2_attn_in['time_mix_k'], 'L2_attn_time_mix_v': _L2_attn_in['time_mix_v'], 'L2_attn_time_mix_r': _L2_attn_in['time_mix_r'], 'L2_attn_time_decay': _L2_attn_in['time_decay'], 'L2_attn_time_first': _L2_attn_in['time_first'], 'L2_attn_Wk': _L2_attn_in['Wk'], 'L2_attn_Wv': _L2_attn_in['Wv'], 'L2_attn_Wr': _L2_attn_in['Wr'], 'L2_attn_Wo': _L2_attn_in['Wo'], 'L2_ffn_Wr': _L2_ffn_in['Wr'], 'L2_ffn_Wqkv': _L2_ffn_in['Wqkv'], 'L2_ffn_Wo': _L2_ffn_in['Wo'], 'L3_attn_norm_w': _L3_attn_in['norm_w'], 'L3_attn_norm_b': _L3_attn_in['norm_b'], 'L3_attn_W_in': _L3_attn_in['W_in'], 'L3_attn_b_in': _L3_attn_in['b_in'], 'L3_attn_A': _L3_attn_in['A'], 'L3_attn_B_ssm': _L3_attn_in['B_ssm'], 'L3_attn_C_ssm': _L3_attn_in['C_ssm'], 'L3_attn_W_out': _L3_attn_in['W_out'], 'L3_attn_b_out': _L3_attn_in['b_out'], 'L3_ffn_gate_w': _L3_ffn_in['gate_w'], 'L3_ffn_w_gate': _L3_ffn_in['w_gate'], 'L3_ffn_w_up': _L3_ffn_in['w_up'], 'L3_ffn_w_down': _L3_ffn_in['w_down']}
    _x0 = _d['L0_attn_x']
    _d['L0_attn_x'] = jax.random.normal(jax.random.fold_in(jax.random.key(seed), 1), (4, 512, 128), dtype=_x0.dtype)
    del _x0
    return _d

def reference(L0_attn_x, L0_attn_wq, L0_attn_wk, L0_attn_wv, L0_attn_wo, L0_ffn_wqkv, L0_ffn_q_scale, L0_ffn_k_scale, L0_ffn_wo, L0_ffn_ln_g, L0_ffn_ln_b, L0_ffn_w1, L0_ffn_b1, L0_ffn_w2, L0_ffn_b2, L1_attn_w_qkv, L1_attn_w_out, L1_ffn_router_w, L1_ffn_router_b, L1_ffn_W1, L1_ffn_b1, L1_ffn_W2, L1_ffn_b2, L2_attn_time_mix_k, L2_attn_time_mix_v, L2_attn_time_mix_r, L2_attn_time_decay, L2_attn_time_first, L2_attn_Wk, L2_attn_Wv, L2_attn_Wr, L2_attn_Wo, L2_ffn_Wr, L2_ffn_Wqkv, L2_ffn_Wo, L3_attn_norm_w, L3_attn_norm_b, L3_attn_W_in, L3_attn_b_in, L3_attn_A, L3_attn_B_ssm, L3_attn_C_ssm, L3_attn_W_out, L3_attn_b_out, L3_ffn_gate_w, L3_ffn_w_gate, L3_ffn_w_up, L3_ffn_w_down):

    def _L0_attn_ref(x, wq, wk, wv, wo):
        import jax, jax.numpy as jnp
        import numpy as np
        D_MODEL = 128
        NUM_HEADS = 16
        D_K = 128
        D_V = 128
        D_IN = 128
        THETA = 10000.0
        B, S = (2, 256)

        def _rope(t, theta):
            hd = t.shape[-1]
            inv_freq = 1.0 / theta ** (jnp.arange(0, hd, 2, dtype=jnp.float32) / hd)
            pos = jnp.arange(t.shape[-2], dtype=jnp.float32)
            ang = pos[:, None] * inv_freq[None, :]
            cos, sin = (jnp.cos(ang), jnp.sin(ang))
            tp = t.reshape(t.shape[:-1] + (hd // 2, 2))
            t0, t1 = (tp[..., 0], tp[..., 1])
            out = jnp.stack([t0 * cos - t1 * sin, t0 * sin + t1 * cos], axis=-1)
            return out.reshape(t.shape)
        b, s, _ = x.shape
        hd = D_K // NUM_HEADS
        hdv = D_V // NUM_HEADS
        q = jnp.einsum('bsd,de->bse', x, wq).reshape(b, s, NUM_HEADS, hd).transpose(2, 0, 1, 3)
        k = jnp.einsum('bsd,de->bse', x, wk).reshape(b, s, NUM_HEADS, hd).transpose(2, 0, 1, 3)
        v = jnp.einsum('bsd,de->bse', x, wv).reshape(b, s, NUM_HEADS, hdv).transpose(2, 0, 1, 3)
        q = _rope(q, THETA)
        k = _rope(k, THETA)
        scale = 1.0 / jnp.sqrt(jnp.asarray(hd, jnp.float32))
        scores = jnp.einsum('hbqd,hbkd->hbqk', q, k) * scale
        causal = jnp.tril(jnp.ones((s, s), dtype=bool))
        scores = jnp.where(causal, scores, -jnp.inf)
        attn = jax.nn.softmax(scores, axis=-1)
        o = jnp.einsum('hbqk,hbkd->hbqd', attn, v)
        o = o.transpose(1, 2, 0, 3).reshape(b, s, D_V)
        return jnp.einsum('bsd,de->bse', o, wo)

    def _L0_ffn_ref(x, wqkv, q_scale, k_scale, wo, ln_g, ln_b, w1, b1, w2, b2):
        import jax, jax.numpy as jnp
        import numpy as np
        DIM = 128
        DEPTH = 2
        HEADS = 8
        DIM_HEAD = 64
        WINDOW = 64
        INNER = HEADS * DIM_HEAD
        HID = int(DIM * 4 * 2 / 3)
        B, N = (2, 1024)
        QK_SCALE = 8.0

        def shift_token(t):
            t1, t2 = jnp.split(t, 2, axis=-1)
            t2 = jnp.pad(t2, ((0, 0), (1, 0), (0, 0)))[:, :-1]
            return jnp.concatenate([t1, t2], axis=-1)

        def l2norm(t):
            return t / jnp.clip(jnp.linalg.norm(t, axis=-1, keepdims=True), 1e-12)

        def rotate_half(x):
            x1, x2 = jnp.split(x, 2, axis=-1)
            return jnp.concatenate([-x2, x1], axis=-1)

        def rotary_xpos(q, k):
            n = q.shape[-2]
            half_idx = jnp.arange(0, DIM_HEAD, 2, dtype=jnp.float32)
            inv_freq = 1.0 / 10000.0 ** (half_idx / DIM_HEAD)
            t = jnp.arange(n, dtype=jnp.float32)
            freqs = t[:, None] * inv_freq[None, :]
            freqs = jnp.concatenate([freqs, freqs], axis=-1)
            base = (half_idx + 0.4 * DIM_HEAD) / (1.4 * DIM_HEAD)
            power = (t - n // 2) / float(WINDOW // 2)
            scale = base[None, :] ** power[:, None]
            scale = jnp.concatenate([scale, scale], axis=-1)
            cos, sin = (jnp.cos(freqs), jnp.sin(freqs))
            q = q * cos * scale + rotate_half(q) * sin * scale
            k = k * cos / scale + rotate_half(k) * sin / scale
            return (q, k)

        def local_attention(q, k, v):
            b, h, n, d = q.shape
            w = n // WINDOW
            bq = q.reshape(b, h, w, WINDOW, d) * QK_SCALE
            bk = k.reshape(b, h, w, WINDOW, d)
            bv = v.reshape(b, h, w, WINDOW, d)

            def look_around(t):
                p = jnp.pad(t, ((0, 0), (0, 0), (1, 0), (0, 0), (0, 0)))
                return jnp.concatenate([p[:, :, :w], p[:, :, 1:]], axis=3)
            bk, bv = (look_around(bk), look_around(bv))
            bt = jnp.arange(n).reshape(w, WINDOW)
            btp = jnp.pad(bt, ((1, 0), (0, 0)), constant_values=-1)
            btk = jnp.concatenate([btp[:w], btp[1:]], axis=1)
            sim = jnp.einsum('bhwid,bhwjd->bhwij', bq, bk)
            i = bt[:, :, None]
            j = btk[:, None, :]
            mask = (i < j) | (i > j + WINDOW) | (j == -1)
            sim = jnp.where(mask, -jnp.finfo(sim.dtype).max, sim)
            attn = jax.nn.softmax(sim, axis=-1)
            out = jnp.einsum('bhwij,bhwjd->bhwid', attn, bv)
            return out.reshape(b, h, n, d)

        def _layer(x, wqkv, qs, ksc, wo, lg, lb, w1, b1, w2, b2):
            b, n, _ = x.shape
            h = shift_token(x)
            qkv = h @ wqkv
            q, k, v = jnp.split(qkv, 3, axis=-1)
            to_heads = lambda t: t.reshape(b, n, HEADS, DIM_HEAD).transpose(0, 2, 1, 3)
            q, k, v = (to_heads(q), to_heads(k), to_heads(v))
            q = l2norm(q) * qs
            k = l2norm(k) * ksc
            q, k = rotary_xpos(q, k)
            o = local_attention(q, k, v)
            o = o.transpose(0, 2, 1, 3).reshape(b, n, INNER)
            x = x + o @ wo
            h = shift_token(x)
            mu = h.mean(-1, keepdims=True)
            var = h.var(-1, keepdims=True)
            h = (h - mu) / jnp.sqrt(var + 1e-05) * lg + lb
            h = h @ w1 + b1
            a, g = jnp.split(h, 2, axis=-1)
            h = a * jax.nn.gelu(g, approximate=False)
            x = x + h @ w2 + b2
            return x
        for l in range(DEPTH):
            x = _layer(x, wqkv[l], q_scale[l], k_scale[l], wo[l], ln_g[l], ln_b[l], w1[l], b1[l], w2[l], b2[l])
        return x

    def _L1_attn_ref(x, w_qkv, w_out):
        import jax, jax.numpy as jnp
        import numpy as np
        HEADS = 8
        DIM_HEAD = 128
        BLOCK_N = 128

        def castle_attention(q, k, v, qu, ku, vu, scale):
            b, h, s, d = q.shape
            q = q * scale
            qu = qu * scale
            qk = jnp.einsum('bhid,bhjd->bhij', q, k)
            quku = jnp.einsum('bhid,bhjd->bhij', qu, ku)
            i = jnp.arange(s)[:, None]
            j = jnp.arange(s)[None, :]
            causal = i >= j
            qk = jnp.where(causal, qk, -jnp.inf)
            la = jnp.where(causal, 0.0, jax.nn.sigmoid(quku))
            nb = s // BLOCK_N
            la_b = la.reshape(b, h, s, nb, BLOCK_N)
            vu_b = vu.reshape(b, h, nb, BLOCK_N, d)
            su = jnp.einsum('bhmtc,bhtcd->bhmtd', la_b, vu_b)
            scores = qk.reshape(b, h, s, nb, BLOCK_N) - jax.nn.silu(su)
            scores = scores.reshape(b, h, s, s)
            p = jax.nn.softmax(scores, axis=-1)
            return jnp.einsum('bhij,bhjd->bhid', p, v)
        B, S, D = x.shape
        scale = DIM_HEAD ** (-0.5)
        qkvs = (x @ w_qkv).reshape(B, S, 6, HEADS, DIM_HEAD)
        qkvs = jnp.transpose(qkvs, (2, 0, 3, 1, 4))
        qu, ku, vu, qc, kc, vc = (qkvs[t] for t in range(6))
        o = castle_attention(qc, kc, vc, qu, ku, vu, scale)
        o = jnp.transpose(o, (0, 2, 1, 3)).reshape(B, S, HEADS * DIM_HEAD)
        return o @ w_out

    def _L1_ffn_ref(x, router_w, router_b, W1, b1, W2, b2):
        import jax, jax.numpy as jnp
        import numpy as np
        D_MODEL = 128
        D_FF = 512
        NUM_EXPERTS = 8
        TOP_K = 2
        BATCH = 4
        SEQ = 256
        logits = jnp.einsum('bsd,de->bse', x, router_w) + router_b
        topk_scores, topk_idx = jax.lax.top_k(logits, TOP_K)
        topk_gates = jax.nn.softmax(topk_scores, axis=-1)
        onehot = jax.nn.one_hot(topk_idx, NUM_EXPERTS, dtype=x.dtype)
        combine = jnp.einsum('bsk,bske->bse', topk_gates, onehot)
        combine_e = jnp.moveaxis(combine, -1, 0)

        def expert_step(acc, params):
            w1, bb1, w2, bb2, c = params
            h = jax.nn.relu(jnp.einsum('bsd,df->bsf', x, w1) + bb1)
            y = jnp.einsum('bsf,fd->bsd', h, w2) + bb2
            return (acc + y * c[..., None], None)
        out, _ = jax.lax.scan(expert_step, jnp.zeros_like(x), (W1, b1, W2, b2, combine_e))
        return out

    def _L2_attn_ref(x, time_mix_k, time_mix_v, time_mix_r, time_decay, time_first, Wk, Wv, Wr, Wo):
        import jax, jax.numpy as jnp
        import numpy as np
        B, S, D = (4, 256, 128)

        def _wkv(k, v, time_decay, u):
            w = -jnp.exp(time_decay)
            b, s, d = k.shape
            aa = jnp.zeros((b, d), k.dtype)
            bb = jnp.zeros((b, d), k.dtype)
            pp = jnp.full((b, d), -1e+30, k.dtype)

            def step(carry, kv):
                aa, bb, pp = carry
                kk, vv = kv
                ww = u + kk
                p = jnp.maximum(pp, ww)
                e1 = jnp.exp(pp - p)
                e2 = jnp.exp(ww - p)
                out = (e1 * aa + e2 * vv) / (e1 * bb + e2)
                ww2 = w + pp
                p2 = jnp.maximum(ww2, kk)
                e1b = jnp.exp(ww2 - p2)
                e2b = jnp.exp(kk - p2)
                return ((e1b * aa + e2b * vv, e1b * bb + e2b, p2), out)
            _, outs = jax.lax.scan(step, (aa, bb, pp), (k.transpose(1, 0, 2), v.transpose(1, 0, 2)))
            return outs.transpose(1, 0, 2)
        shifted = jnp.concatenate([jnp.zeros_like(x[:, :1, :]), x[:, :-1, :]], axis=1)
        xk = x * time_mix_k + shifted * (1.0 - time_mix_k)
        xv = x * time_mix_v + shifted * (1.0 - time_mix_v)
        xr = x * time_mix_r + shifted * (1.0 - time_mix_r)
        k = jnp.einsum('bsd,ed->bse', xk, Wk)
        v = jnp.einsum('bsd,ed->bse', xv, Wv)
        r = jax.nn.sigmoid(jnp.einsum('bsd,ed->bse', xr, Wr))
        wkv = _wkv(k, v, time_decay, time_first)
        out = jnp.einsum('bsd,ed->bse', r * wkv, Wo)
        return out

    def _L2_ffn_ref(X, Wr, Wqkv, Wo):
        import math
        import jax, jax.numpy as jnp
        import numpy as np
        E = 8
        H = 128
        HP = 128
        SPARSITY = 8
        N_ROTATE = 64
        ROPE_BASE = 10000.0

        def _rope(x, pos):
            half = N_ROTATE // 2
            inv_freq = 1.0 / ROPE_BASE ** (jnp.arange(half, dtype=jnp.float32) * 2.0 / N_ROTATE)
            ang = pos.astype(jnp.float32)[..., None] * inv_freq
            sin, cos = (jnp.sin(ang), jnp.cos(ang))
            x1, x2 = (x[..., :half], x[..., half:])
            return jnp.concatenate([x1 * cos - x2 * sin, x2 * cos + x1 * sin], axis=-1)
        B, T, _ = X.shape
        k = min(max(T // SPARSITY, 2), T)
        logits = jax.nn.sigmoid(jnp.einsum('bth,eh->bte', X, Wr))
        topk_vals, topk_I = jax.lax.top_k(logits.transpose(0, 2, 1), k)
        idx_flat = topk_I.reshape(B, E * k)
        Xg = jnp.take_along_axis(X, idx_flat[:, :, None], axis=1).reshape(B, E, k, H)
        QKV = jnp.einsum('beki,eij->bekj', Xg, Wqkv)
        Q, K, V = jnp.split(QKV, 3, axis=-1)
        Q = jnp.concatenate([_rope(Q[..., :N_ROTATE], topk_I), Q[..., N_ROTATE:]], axis=-1)
        K = jnp.concatenate([_rope(K[..., :N_ROTATE], topk_I), K[..., N_ROTATE:]], axis=-1)
        M = topk_I[..., :, None] >= topk_I[..., None, :]
        scores = jnp.einsum('bekd,bemd->bekm', Q, K) / math.sqrt(HP)
        scores = jnp.where(M, scores, -jnp.inf)
        A = jax.nn.softmax(scores, axis=-1)
        AV = jnp.einsum('bekm,bemd->bekd', A, V)
        AV = AV * topk_vals[..., None]
        Xpre = jnp.einsum('bekj,eji->beki', AV, Wo)
        out = jnp.zeros((B, T, H), dtype=X.dtype)
        out = out.at[jnp.arange(B)[:, None], idx_flat].add(Xpre.reshape(B, E * k, H))
        return out

    def _L3_attn_ref(x, norm_w, norm_b, W_in, b_in, A, B_ssm, C_ssm, W_out, b_out):
        import jax, jax.numpy as jnp
        import numpy as np
        D_MODEL, D_STATE, D_INNER = (128, 16, 256)
        B, S = (2, 512)
        EPS = 1e-05
        residual = x
        mu = jnp.mean(x, axis=-1, keepdims=True)
        var = jnp.mean(jnp.square(x - mu), axis=-1, keepdims=True)
        xn = (x - mu) * jax.lax.rsqrt(var + EPS) * norm_w + norm_b
        h = jnp.einsum('bsd,ed->bse', xn, W_in) + b_in
        a = jax.nn.sigmoid(jnp.einsum('bse,en->bsn', h, A))
        u = jnp.einsum('bse,en->bsn', h, B_ssm)

        def step(s, inp):
            a_t, u_t = inp
            s = s * a_t + u_t
            return (s, s)
        s0 = jnp.zeros((x.shape[0], D_STATE), x.dtype)
        _, states = jax.lax.scan(step, s0, (jnp.swapaxes(a, 0, 1), jnp.swapaxes(u, 0, 1)))
        y = jnp.einsum('sbn,en->bse', states, C_ssm)
        out = jnp.einsum('bse,de->bsd', y, W_out) + b_out
        return out + residual

    def _L3_ffn_ref(hidden_states, gate_w, w_gate, w_up, w_down):
        import jax, jax.numpy as jnp
        import numpy as np
        NUM_EXPERTS = 64
        TOP_K = 8
        HIDDEN = 128
        INTER = 96
        BATCH, SEQ = (1, 128)
        CAPACITY = 32

        def _moe_forward(hidden_states, gate_w, w_gate, w_up, w_down):
            B, S, H = hidden_states.shape
            x = hidden_states.reshape(-1, H)
            T = x.shape[0]
            logits = (x @ gate_w.T).astype(jnp.float32)
            probs = jax.nn.softmax(logits, axis=-1)
            topk_p, topk_i = jax.lax.top_k(probs, TOP_K)
            topk_p = topk_p / jnp.sum(topk_p, axis=-1, keepdims=True)
            flat_e = topk_i.reshape(-1)
            onehot = jax.nn.one_hot(flat_e, NUM_EXPERTS, dtype=jnp.int32)
            pos_all = jnp.cumsum(onehot, axis=0) - 1
            pos = jnp.take_along_axis(pos_all, flat_e[:, None], axis=1)[:, 0]
            x_rep = jnp.repeat(x, TOP_K, axis=0)
            dispatch = jnp.zeros((NUM_EXPERTS, CAPACITY, H), x.dtype)
            dispatch = dispatch.at[flat_e, pos].set(x_rep, mode='drop')
            g = jax.nn.silu(jnp.einsum('ech,eih->eci', dispatch, w_gate))
            u = jnp.einsum('ech,eih->eci', dispatch, w_up)
            y = jnp.einsum('eci,ehi->ech', g * u, w_down)
            valid = pos < CAPACITY
            y_tok = y[flat_e, jnp.minimum(pos, CAPACITY - 1)]
            w = (topk_p.reshape(-1) * valid.astype(topk_p.dtype)).astype(x.dtype)
            out = (y_tok * w[:, None]).reshape(T, TOP_K, H).sum(axis=1)
            return out.reshape(B, S, H)
        return _moe_forward(hidden_states, gate_w, w_gate, w_up, w_down)
    x = L0_attn_x
    x = x + _L0_attn_ref(_layernorm(x, axis=-1), L0_attn_wq, L0_attn_wk, L0_attn_wv, L0_attn_wo)
    x = x + _L0_ffn_ref(_layernorm(x, axis=-1), L0_ffn_wqkv, L0_ffn_q_scale, L0_ffn_k_scale, L0_ffn_wo, L0_ffn_ln_g, L0_ffn_ln_b, L0_ffn_w1, L0_ffn_b1, L0_ffn_w2, L0_ffn_b2)
    x = x + _L1_attn_ref(_layernorm(x, axis=-1), L1_attn_w_qkv, L1_attn_w_out)
    x = x + _L1_ffn_ref(_layernorm(x, axis=-1), L1_ffn_router_w, L1_ffn_router_b, L1_ffn_W1, L1_ffn_b1, L1_ffn_W2, L1_ffn_b2)
    x = x + _L2_attn_ref(_layernorm(x, axis=-1), L2_attn_time_mix_k, L2_attn_time_mix_v, L2_attn_time_mix_r, L2_attn_time_decay, L2_attn_time_first, L2_attn_Wk, L2_attn_Wv, L2_attn_Wr, L2_attn_Wo)
    x = x + _L2_ffn_ref(_layernorm(x, axis=-1), L2_ffn_Wr, L2_ffn_Wqkv, L2_ffn_Wo)
    x = x + _L3_attn_ref(_layernorm(x, axis=-1), L3_attn_norm_w, L3_attn_norm_b, L3_attn_W_in, L3_attn_b_in, L3_attn_A, L3_attn_B_ssm, L3_attn_C_ssm, L3_attn_W_out, L3_attn_b_out)
    x = x + _L3_ffn_ref(_layernorm(x, axis=-1), L3_ffn_gate_w, L3_ffn_w_gate, L3_ffn_w_up, L3_ffn_w_down)
    return x

_drawn_inputs = setup_inputs


def setup_inputs(seed=0):
    import zlib

    import numpy as np

    out = dict(_drawn_inputs(seed))
    spreads = {'L0_ffn_q_scale': (1.0, 0.6),
     'L0_ffn_k_scale': (1.0, 0.6),
     'L0_ffn_ln_g': (1.0, 0.6),
     'L0_ffn_ln_b': (0.0, 0.8),
     'L0_ffn_b1': (0.0, 0.73),
     'L0_ffn_b2': (0.0, 0.1),
     'L1_ffn_router_b': (0.0, 0.1),
     'L1_ffn_b1': (0.0, 0.401),
     'L1_ffn_b2': (0.0, 0.1),
     'L3_attn_norm_w': (1.0, 0.2),
     'L3_attn_norm_b': (0.0, 0.1),
     'L3_attn_b_in': (0.0, 0.1),
     'L3_attn_b_out': (0.0, 2.0)}
    factors = {'L0_ffn_w1': 3.138,
     'L0_ffn_w2': 3.267,
     'L2_attn_time_mix_k': 8.0,
     'L2_attn_time_mix_v': 8.0,
     'L2_attn_time_mix_r': 8.0,
     'L2_attn_time_decay': 8.0,
     'L2_attn_time_first': 8.0,
     'L2_attn_Wk': 8.0,
     'L2_attn_Wv': 4.152,
     'L2_attn_Wr': 8.0,
     'L2_attn_Wo': 4.254,
     'L2_ffn_Wr': 4.227,
     'L2_ffn_Wqkv': 4.195,
     'L2_ffn_Wo': 4.046,
     'L3_ffn_gate_w': 64.0,
     'L3_ffn_w_gate': 64.0,
     'L3_ffn_w_up': 64.0,
     'L3_ffn_w_down': 64.0}
    for name, (base, spread) in spreads.items():
        noise = np.random.default_rng([zlib.crc32(name.encode()), seed]).standard_normal(out[name].shape)
        drawn = base * np.exp(spread * noise) if base else spread * noise
        out[name] = jnp.asarray(drawn.astype(out[name].dtype))
    for name, factor in factors.items():
        out[name] = (out[name] * factor).astype(out[name].dtype)
    return out
```

```python
from contextlib import ExitStack

import concourse.bass as bass
from concourse import mybir
from concourse.alu_op_type import AluOpType as ALU

ACT = mybir.ActivationFunctionType
AX = mybir.AxisListType.X
F32 = mybir.dt.float32
BF16 = mybir.dt.bfloat16
U32 = mybir.dt.uint32

P = 128
B, S, D = 4, 512, 128
TB = S // P
NT = B * TB
EPS = 1e-5
NEG = -1e30


class Chain:

    def __init__(self, eng, sem, base=0):
        self.eng, self.sem, self.base, self.n = eng, sem, base, 0

    def __call__(self, ins):
        self.n += 1
        return ins.then_inc(self.sem, 1)

    def wait(self, back=0):
        self.eng.wait_ge(self.sem, self.base + self.n - back)


class LayerNorm:
    STEPS = 2 * TB + 4

    def __init__(self, nc, ctx, name, core):
        sb = nc.sbuf_tensor
        self.eps = core.eps
        self.stats = ctx.enter_context(sb(name + "_stats", [P, TB, 6], F32))
        self.mv = ctx.enter_context(sb(name + "_meanvar", [P, TB, 2], F32))
        self.lnv = ctx.enter_context(sb(name + "_lnvar", [P, TB], F32))
        self.guess = ctx.enter_context(sb(name + "_guess", [P, TB], F32))
        self.corr = ctx.enter_context(sb(name + "_corr", [P, TB], F32))
        self.rstd = ctx.enter_context(sb(name + "_rstd", [P, TB], F32))
        self.step = core.semaphore(ctx, name + "_step")
        self.guessed = core.semaphore(ctx, name + "_guessed")
        self.ready = core.semaphore(ctx, name + "_ready")

    def vector(self, dve, n, src, dst):
        step = Chain(dve, self.step, n * self.STEPS)
        for t in range(TB):
            step(dve.bn_stats(self.stats[:, t, :], src(t)))
        step.wait()
        dve.memset(self.corr[:, 0:1], 0.0)
        for t in range(TB):
            step(dve.bn_aggr(self.mv[:, t, :], self.stats[:, t, :]))
        dve.wait_ge(self.guessed, n * 2 + 2)
        step(dve.tensor_tensor(self.corr[:, :], self.guess[:, :], self.guess[:, :], ALU.mult))
        step.wait()
        step(dve.scalar_tensor_tensor(out=self.corr[:, :], in0=self.mv[:, :, 1], scalar=EPS, in1=self.corr[:, :],
                                      op0=ALU.add, op1=ALU.mult))
        step.wait()
        step(dve.tensor_scalar(self.corr[:, :], self.corr[:, :], -0.5, 1.5, ALU.mult, ALU.add))
        step.wait()
        step(dve.tensor_tensor(self.rstd[:, :], self.corr[:, :], self.guess[:, :], ALU.mult))
        step.wait()
        assert step.n == self.STEPS
        for t in range(TB):
            dve.tensor_scalar(dst(t), src(t), self.mv[:, t, 0:1], self.rstd[:, t:t + 1],
                              ALU.subtract, ALU.mult).then_inc(self.ready, 1)

    def scalar(self, act, n):
        act.wait_ge(self.step, n * self.STEPS + 2 * TB)
        act.activation(self.lnv[:, :], self.mv[:, :, 1], ACT.Ln, bias=self.eps).then_inc(self.guessed, 1)
        act.wait_ge(self.guessed, n * 2 + 1)
        act.activation(self.guess[:, :], self.lnv[:, :], ACT.Exp, scale=-0.5).then_inc(self.guessed, 1)


class Core:

    def __init__(self, nc, ctx, dram):
        self.nc, self.dram, self.w = nc, dram, {}

        def sb(name, shape, dt=F32):
            return ctx.enter_context(nc.sbuf_tensor(name, shape, dt))

        self.sb = sb
        self.X = sb("X", [P, NT, D])
        self.cf = sb("const_f32", [P, CONST_COLS])
        self.ident = self.cf[:, C_IDENT:C_IDENT + P]
        self.eps = self.cf[:, C_EPS:C_EPS + 1]
        self.ones_row = self.cf[0:1, C_ONES:C_ONES + P]
        self.identb = sb("ident_bf16", [P, P], BF16)
        self.causal = sb("causal_bf16", [P, P], BF16)
        self.band = sb("band_bf16", [P, 64 + P], BF16)
        self.pair_mask = sb("pair_mask_bf16", [P, P], BF16)
        self.arena = sb("arena", [P, ARENA])
        self.x_loaded = ctx.enter_context(nc.semaphore("x_loaded"))
        self.const_loaded = ctx.enter_context(nc.semaphore("const_loaded"))
        self.stored = ctx.enter_context(nc.semaphore("stored"))
        self.n_loads = {}
        self.of_layer = []
        self.loaded = {}
        self.ctx = ctx

    def semaphore(self, ctx, name):
        sem = ctx.enter_context(self.nc.semaphore(name))
        self.of_layer.append(sem)
        return sem

    def retire(self):
        sems, self.of_layer = self.of_layer, []
        with self.nc.Block() as block:
            @block.gpsimd
            def _(pool):
                for sem in sems:
                    pool.sem_clear(sem)

    def load(self, eng, stage, dst, src):
        if stage not in self.loaded:
            self.loaded[stage] = self.ctx.enter_context(self.nc.semaphore(f"{stage}_weights"))
            self.n_loads[stage] = 0
        self.n_loads[stage] += 16
        eng.dma_start(dst, src).then_inc(self.loaded[stage], 16)

    def wait_weights(self, eng, stage):
        eng.wait_ge(self.loaded[stage], self.n_loads[stage])


def turn(pe, core, ln, n, xn, ps, turned):
    for t in range(TB):
        pe.wait_ge(ln.ready, n * TB + t + 1)
        last = pe.transpose(ps[:, t * P:(t + 1) * P], xn[:, t, :], core.ident)
    last.then_inc(turned, 1)


def add_to_stream(dve, core, b, ps, done):
    x = core.X[:, bass.ds(b * TB, TB), :]
    dve.tensor_tensor(x, x, ps.rearrange("p (t d) -> p t d", t=TB), ALU.add).then_inc(done, 1)


def layer2_attn(nc, core):
    with ExitStack() as ctx:
        def sb(name, shape, dt=F32):
            return ctx.enter_context(nc.sbuf_tensor("L2a_" + name, shape, dt))

        def sem(name):
            return core.semaphore(ctx, "L2a_" + name)

        ln = LayerNorm(nc, ctx, "L2a_ln", core)
        w = core.w["L2a"]
        xn = sb("xn", [P, TB, D])
        xT = sb("xT", [P, S + 1])
        mixed = sb("mixed", [P, 3, S])
        one_less_mix = sb("one_less_mix", [P, 3])
        neg_decay = sb("neg_decay", [P, 1])
        decay_row = sb("decay_row", [P, S])
        top = sb("top", [P, S + 1])
        num = sb("num", [P, S + 1])
        den = sb("den", [P, S + 1])
        ww = sb("ww", [P, S])
        peak = sb("peak", [P, S])
        diff = sb("diff", [P, 4, S])
        gate = sb("gate", [P, S])
        tmp = sb("tmp", [P, S])
        out_num = sb("out_num", [P, S])
        out_den = sb("out_den", [P, S])
        res = sb("res", [P, S])
        psT = ctx.enter_context(nc.psum_tensor("L2a_psT", [P, S], F32))
        psY = ctx.enter_context(nc.psum_tensor("L2a_psY", [P, S], F32))
        psK, psV, psR = (ctx.enter_context(nc.psum_tensor("L2a_ps" + c, [P, S], F32)) for c in "KVR")
        setup, exp_decay = sem("setup"), sem("exp_decay")
        turned, xt_ready, mixed_ready, projected = sem("turned"), sem("xt_ready"), sem("mixed_ready"), sem("projected")
        vec, diffs_ready, exps_ready, res_ready, y_ready, added = (
            sem("vec"), sem("diffs_ready"), sem("exps_ready"), sem("res_ready"), sem("y_ready"), sem("added"))
        VEC = 19
        SETUP = 7
        mix, first = w["mix"], w["cols"][:, 1:2]
        with nc.Block() as block:
            @block.sync
            def _(sp):
                load_late_weights(core, sp)

            @block.scalar
            def _(act):
                core.wait_weights(act, "L2a")
                act.activation(neg_decay[:, :], w["cols"][:, 0:1], ACT.Exp).then_inc(exp_decay, 1)
                with act.Fori(0, B) as b:
                    ln.scalar(act, b)
                    act.wait_ge(turned, b + 1)
                    act.activation(xT[:, 1:S + 1], psT[:, :], ACT.Copy).then_inc(xt_ready, 1)
                    act.wait_ge(projected, b + 1)
                    act.activation(gate[:, :], psR[:, :], ACT.Exp, scale=-1.0).then_inc(exps_ready, 1)
                    for j in range(4):
                        act.wait_ge(diffs_ready, b * 4 + j + 1)
                        act.activation(diff[:, j, :], diff[:, j, :], ACT.Exp).then_inc(exps_ready, 1)

            @block.tensor
            def _(pe):
                core.wait_weights(pe, "L2a")
                with pe.Fori(0, B) as b:
                    turn(pe, core, ln, b, xn, psT, turned)
                    pe.wait_ge(mixed_ready, b + 1)
                    for j, ps in enumerate((psK, psV, psR)):
                        last = pe.matmul(ps[:, :], w["kvr"][:, j, :], mixed[:, j, :], start=True, stop=True)
                    last.then_inc(projected, 1)
                    pe.wait_ge(res_ready, b + 1)
                    for t in range(TB):
                        last = pe.matmul(psY[:, t * P:(t + 1) * P], res[:, t * P:(t + 1) * P], w["out"][:, :],
                                         start=True, stop=True)
                    last.then_inc(y_ready, 1)

            @block.vector
            def _(dve):
                core.wait_weights(dve, "L2a")
                c = Chain(dve, setup)
                c(dve.memset(xT[:, 0:1], 0.0))
                c(dve.memset(top[:, 0:1], -1e30))
                c(dve.memset(num[:, 0:1], 0.0))
                c(dve.memset(den[:, 0:1], 0.0))
                c(dve.memset(decay_row[:, :], 0.0))
                c(dve.tensor_scalar(one_less_mix[:, :], mix, -1.0, 1.0, ALU.mult, ALU.add))
                dve.wait_ge(exp_decay, 1)
                c.wait()
                c(dve.tensor_scalar(decay_row[:, :], decay_row[:, :], neg_decay[:, 0:1], None, ALU.subtract))
                c.wait()
                assert c.n == SETUP
                with dve.Fori(0, B) as b:
                    ln.vector(dve, b, lambda t: core.X[:, b * TB + t, :], lambda t: xn[:, t, :])
                    c = Chain(dve, vec, b * VEC)
                    dve.wait_ge(xt_ready, b + 1)
                    for j in range(3):
                        c(dve.tensor_scalar(mixed[:, j, :], xT[:, 0:S], one_less_mix[:, j:j + 1], None, ALU.mult))
                    for j in range(3):
                        c.wait(2)
                        last = dve.scalar_tensor_tensor(out=mixed[:, j, :], in0=xT[:, 1:S + 1], scalar=mix[:, j:j + 1],
                                                        in1=mixed[:, j, :], op0=ALU.mult, op1=ALU.add)
                        c(last) if j < 2 else last.then_inc(mixed_ready, 1)
                    dve.wait_ge(projected, b + 1)
                    c(dve.tensor_tensor_scan(top[:, 1:S + 1], decay_row[:, :], psK[:, :], -1e30, ALU.add, ALU.max))
                    c.wait()
                    dve.tensor_tensor(diff[:, 0, :], psK[:, :], top[:, 1:S + 1], ALU.subtract).then_inc(diffs_ready, 1)
                    c(dve.tensor_tensor(tmp[:, :], top[:, 0:S], decay_row[:, :], ALU.add))
                    c.wait()
                    dve.tensor_tensor(diff[:, 1, :], tmp[:, :], top[:, 1:S + 1], ALU.subtract).then_inc(diffs_ready, 1)
                    c(dve.tensor_scalar(ww[:, :], psK[:, :], first, None, ALU.add))
                    c.wait()
                    c(dve.tensor_tensor(peak[:, :], ww[:, :], top[:, 0:S], ALU.max))
                    c.wait()
                    dve.tensor_tensor(diff[:, 2, :], top[:, 0:S], peak[:, :], ALU.subtract).then_inc(diffs_ready, 1)
                    dve.tensor_tensor(diff[:, 3, :], ww[:, :], peak[:, :], ALU.subtract).then_inc(diffs_ready, 1)
                    dve.wait_ge(exps_ready, b * 5 + 2)
                    c(dve.tensor_tensor(tmp[:, :], diff[:, 0, :], psV[:, :], ALU.mult))
                    dve.wait_ge(exps_ready, b * 5 + 3)
                    c.wait()
                    c(dve.tensor_tensor_scan(num[:, 1:S + 1], diff[:, 1, :], tmp[:, :], 0.0, ALU.mult, ALU.add))
                    c(dve.tensor_tensor_scan(den[:, 1:S + 1], diff[:, 1, :], diff[:, 0, :], 0.0, ALU.mult, ALU.add))
                    dve.wait_ge(exps_ready, b * 5 + 5)
                    c(dve.tensor_tensor(out_num[:, :], diff[:, 3, :], psV[:, :], ALU.mult))
                    c.wait(1)
                    c(dve.tensor_tensor(tmp[:, :], diff[:, 2, :], num[:, 0:S], ALU.mult))
                    c(dve.tensor_tensor(out_den[:, :], diff[:, 2, :], den[:, 0:S], ALU.mult))
                    c.wait()
                    c(dve.tensor_tensor(out_num[:, :], out_num[:, :], tmp[:, :], ALU.add))
                    c(dve.tensor_tensor(out_den[:, :], out_den[:, :], diff[:, 3, :], ALU.add))
                    c.wait()
                    c(dve.scalar_tensor_tensor(out=out_den[:, :], in0=gate[:, :], scalar=1.0, in1=out_den[:, :],
                                               op0=ALU.add, op1=ALU.mult))
                    c.wait()
                    c(dve.reciprocal(out_den[:, :], out_den[:, :]))
                    c.wait()
                    dve.tensor_tensor(res[:, :], out_num[:, :], out_den[:, :], ALU.mult).then_inc(res_ready, 1)
                    dve.wait_ge(y_ready, b + 1)
                    add_to_stream(dve, core, b, psY[:, :], added)
                    dve.wait_ge(added, b + 1)
                    assert c.n == VEC, c.n


def layer3_attn(nc, core):
    NS, CH = 16, 2
    with ExitStack() as ctx:
        def sb(name, shape, dt=F32):
            return ctx.enter_context(nc.sbuf_tensor("L3a_" + name, shape, dt))

        def sem(name):
            return core.semaphore(ctx, "L3a_" + name)

        ln = LayerNorm(nc, ctx, "L3a_ln", core)
        w = core.w["L3a"]
        xo = sb("xo", [P, TB, D])
        xn = sb("xn", [P, TB, D])
        xT = sb("xT", [P, S])
        hT = sb("hT", [P, CH, S])
        decay = sb("decay", [NS, S])
        drive = sb("drive", [NS, S])
        states = sb("states", [NS, S])
        yT = sb("yT", [P, CH, S])
        psT, psA, psU, psY = (ctx.enter_context(nc.psum_tensor("L3a_ps" + c, [P, S], F32)) for c in "TAUY")
        psH = ctx.enter_context(nc.psum_tensor("L3a_psH", [P, CH, S], F32))
        turned, xt_ready, h_done, h_ready, au_done, exp_ready = (
            sem(n) for n in ("turned", "xt_ready", "h_done", "h_ready", "au_done", "exp_ready"))
        vec, states_ready, yt_done, yt_ready, out_done, added = (
            sem(n) for n in ("vec", "states_ready", "yt_done", "yt_ready", "out_done", "added"))
        VEC = 3
        nw, nb = w["cols"][:, 0:1], w["cols"][:, 1:2]
        with nc.Block() as block:
            @block.scalar
            def _(act):
                core.wait_weights(act, "L3a")
                with act.Fori(0, B) as b:
                    ln.scalar(act, b * 2)
                    ln.scalar(act, b * 2 + 1)
                    act.wait_ge(turned, b + 1)
                    act.activation(xT[:, :], psT[:, :], ACT.Identity, bias=nb, scale=nw).then_inc(xt_ready, 1)
                    for c in range(CH):
                        act.wait_ge(h_done, b * CH + c + 1)
                        act.activation(hT[:, c, :], psH[:, c, :], ACT.Identity,
                                       bias=w["cols"][:, 2 + c:3 + c]).then_inc(h_ready, 1)
                    act.wait_ge(au_done, b + 1)
                    act.activation(decay[:, :], psA[0:NS, :], ACT.Exp, scale=-1.0).then_inc(exp_ready, 1)
                    act.activation(drive[:, :], psU[0:NS, :], ACT.Copy).then_inc(exp_ready, 1)
                    for c in range(CH):
                        act.wait_ge(yt_done, b * CH + c + 1)
                        act.activation(yT[:, c, :], psH[:, c, :], ACT.Copy).then_inc(yt_ready, 1)

            @block.tensor
            def _(pe):
                core.wait_weights(pe, "L3a")
                with pe.Fori(0, B) as b:
                    for t in range(TB):
                        pe.wait_ge(ln.ready, b * 2 * TB + TB + t + 1)
                        last = pe.transpose(psT[:, t * P:(t + 1) * P], xn[:, t, :], core.ident)
                    last.then_inc(turned, 1)
                    pe.wait_ge(xt_ready, b + 1)
                    for c in range(CH):
                        pe.matmul(psH[:, c, :], w["in"][:, c * P:(c + 1) * P], xT[:, :],
                                  start=True, stop=True).then_inc(h_done, 1)
                    for c in range(CH):
                        pe.wait_ge(h_ready, b * CH + c + 1)
                        pe.matmul(psA[0:NS, :], w["A"][:, c, :], hT[:, c, :], start=c == 0, stop=c == CH - 1)
                        last = pe.matmul(psU[0:NS, :], w["B"][:, c, :], hT[:, c, :], start=c == 0, stop=c == CH - 1)
                    last.then_inc(au_done, 1)
                    pe.wait_ge(states_ready, b + 1)
                    for c in range(CH):
                        pe.matmul(psH[:, c, :], w["C"][:, c * P:(c + 1) * P], states[:, :],
                                  start=True, stop=True).then_inc(yt_done, 1)
                    pe.wait_ge(yt_ready, (b + 1) * CH)
                    for t in range(TB):
                        o = psY[:, t * P:(t + 1) * P]
                        for c in range(CH):
                            pe.matmul(o, yT[:, c, t * P:(t + 1) * P], w["out"][:, c, :], start=c == 0, stop=False)
                        last = pe.matmul(o, core.ones_row, w["b_out"][0:1, :], start=False, stop=True)
                    last.then_inc(out_done, 1)

            @block.vector
            def _(dve):
                with dve.Fori(0, B) as b:
                    ln.vector(dve, b * 2, lambda t: core.X[:, b * TB + t, :], lambda t: xo[:, t, :])
                    dve.wait_ge(ln.ready, b * 2 * TB + TB)
                    ln.vector(dve, b * 2 + 1, lambda t: xo[:, t, :], lambda t: xn[:, t, :])
                    c = Chain(dve, vec, b * VEC)
                    x = core.X[:, bass.ds(b * TB, TB), :]
                    c(dve.tensor_tensor(x, x, xo[:, :, :], ALU.add))
                    dve.wait_ge(exp_ready, b * 2 + 2)
                    c(dve.tensor_scalar(decay[:, :], decay[:, :], 1.0, None, ALU.add))
                    c.wait()
                    c(dve.reciprocal(decay[:, :], decay[:, :]))
                    c.wait()
                    dve.tensor_tensor_scan(states[:, :], decay[:, :], drive[:, :], 0.0,
                                           ALU.mult, ALU.add).then_inc(states_ready, 1)
                    dve.wait_ge(out_done, b + 1)
                    add_to_stream(dve, core, b, psY[:, :], added)
                    dve.wait_ge(added, b + 1)
                    assert c.n == VEC


def layer1_ffn(nc, core):
    E, FC = 8, 4
    with ExitStack() as ctx:
        def sb(name, shape, dt=F32):
            return ctx.enter_context(nc.sbuf_tensor("L1f_" + name, shape, dt))

        def sem(name):
            return core.semaphore(ctx, "L1f_" + name)

        ln = LayerNorm(nc, ctx, "L1f_ln", core)
        w = core.w["L1f"]
        xn = sb("xn", [P, TB, D])
        xT = sb("xT", [P, S])
        hT = sb("hT", [P, 2, FC, S])
        logits = sb("logits", [P, TB, E])
        hit = sb("hit", [P, TB, E])
        first = sb("first", [P, TB, E])
        second = sb("second", [P, TB, E])
        gates = sb("gates", [P, TB, E])
        best = sb("best", [P, 3, TB])
        place = sb("place", [P, TB])
        e21 = sb("e21", [P, TB])
        g1 = sb("g1", [P, TB])
        g2 = sb("g2", [P, TB])
        gatesT = sb("gatesT", [E, S])
        psT, psL = (ctx.enter_context(nc.psum_tensor("L1f_ps" + c, [P, S], F32)) for c in "TL")
        psH = ctx.enter_context(nc.psum_tensor("L1f_psH", [P, FC, S], F32))
        psY = ctx.enter_context(nc.psum_tensor("L1f_psY", [P, 2, S], F32))
        names = ("turned xt_ready logits_done vec margin_ready exp_ready gates_ready gates_turned gatesT_ready "
                 "bias_done bias_added h_done h_ready y_done y_used").split()
        (turned, xt_ready, logits_done, vec, margin_ready, exp_ready, gates_ready, gates_turned, gatesT_ready,
         bias_done, bias_added, h_done, h_ready, y_done, y_used) = (sem(n) for n in names)
        VEC = 17
        order = core.cf[:, C_ORDER8:C_ORDER8 + E].unsqueeze(1).to_broadcast([P, TB, E])
        with nc.Block() as block:
            @block.scalar
            def _(act):
                core.wait_weights(act, "L1f")
                with act.Fori(0, B) as b:
                    ln.scalar(act, b)
                    act.wait_ge(turned, b + 1)
                    act.activation(xT[:, :], psT[:, :], ACT.Copy).then_inc(xt_ready, 1)
                    for e in range(E):
                        for f in range(FC):
                            act.wait_ge(h_done, b * (E * FC) + e * FC + f + 1)
                            if e >= 2:
                                act.wait_ge(y_done, b * E + e - 1)
                            act.activation(hT[:, e % 2, f, :], psH[:, f, :], ACT.Relu,
                                           bias=w["b1"][:, e * FC + f:e * FC + f + 1]).then_inc(h_ready, 1)
                        if e == 0:
                            act.wait_ge(margin_ready, b + 1)
                            act.activation(e21[:, :], e21[:, :], ACT.Exp).then_inc(exp_ready, 1)

            @block.tensor
            def _(pe):
                core.wait_weights(pe, "L1f")

                def expand(b, e):
                    for f in range(FC):
                        if e >= 1:
                            pe.wait_ge(h_ready, b * (E * FC) + (e - 1) * FC + f + 1)
                        pe.matmul(psH[:, f, :], w["W1"][:, e, f * P:(f + 1) * P], xT[:, :],
                                  start=True, stop=True).then_inc(h_done, 1)

                def contract(b, e):
                    if e >= 2:
                        pe.wait_ge(y_used, b * E + e - 1)
                    pe.wait_ge(h_ready, b * (E * FC) + e * FC + FC)
                    for t in range(TB):
                        for f in range(FC):
                            last = pe.matmul(psY[:, e % 2, t * P:(t + 1) * P], hT[:, e % 2, f, t * P:(t + 1) * P],
                                             w["W2"][:, e, f, :], start=f == 0, stop=f == FC - 1)
                    last.then_inc(y_done, 1)

                with pe.Fori(0, B) as b:
                    turn(pe, core, ln, b, xn, psT, turned)
                    pe.wait_ge(xt_ready, b + 1)
                    for t in range(TB):
                        o = psL[:, t * E:(t + 1) * E]
                        pe.matmul(o, xT[:, t * P:(t + 1) * P], w["router"][:, :], start=True, stop=False)
                        last = pe.matmul(o, core.ones_row, w["router_b"][0:1, :], start=False, stop=True)
                    last.then_inc(logits_done, 1)
                    expand(b, 0)
                    for e in range(E):
                        if e + 1 < E:
                            expand(b, e + 1)
                        if e == 0:
                            pe.wait_ge(gates_ready, b + 1)
                            for t in range(TB):
                                last = pe.transpose(psT[0:E, t * P:(t + 1) * P], gates[:, t, :], core.ident)
                            last.then_inc(gates_turned, 1)
                        contract(b, e)
                        if e == 0:
                            pe.wait_ge(gatesT_ready, b + 1)
                            for t in range(TB):
                                last = pe.matmul(psL[:, t * P:(t + 1) * P], gatesT[:, t * P:(t + 1) * P],
                                                 w["b2"][0:E, :], start=True, stop=True)
                            last.then_inc(bias_done, 1)

            @block.vector
            def _(dve):
                with dve.Fori(0, B) as b:
                    ln.vector(dve, b, lambda t: core.X[:, b * TB + t, :], lambda t: xn[:, t, :])
                    c = Chain(dve, vec, b * VEC)
                    dve.wait_ge(logits_done, b + 1)
                    c(dve.tensor_copy(logits[:, :, :], psL[:, 0:TB * E].rearrange("p (t e) -> p t e", t=TB)))
                    for k, chosen in enumerate((first, second)):
                        c.wait()
                        c(dve.tensor_reduce(best[:, k, :], logits[:, :, :], AX, ALU.max))
                        c.wait()
                        c(dve.tensor_tensor(hit[:, :, :], logits[:, :, :],
                                            best[:, k, :].unsqueeze(2).to_broadcast([P, TB, E]), ALU.is_equal))
                        c.wait()
                        c(dve.tensor_tensor(hit[:, :, :], hit[:, :, :], order, ALU.mult))
                        c.wait()
                        c(dve.tensor_reduce(place[:, :], hit[:, :, :], AX, ALU.max))
                        c.wait()
                        c(dve.tensor_tensor(chosen[:, :, :], order,
                                            place[:, :].unsqueeze(2).to_broadcast([P, TB, E]), ALU.is_equal))
                        c.wait()
                        if k == 0:
                            c(dve.scalar_tensor_tensor(out=logits[:, :, :], in0=chosen[:, :, :], scalar=-3e38,
                                                       in1=logits[:, :, :], op0=ALU.mult, op1=ALU.add))
                    dve.tensor_tensor(e21[:, :], best[:, 1, :], best[:, 0, :], ALU.subtract).then_inc(margin_ready, 1)
                    dve.wait_ge(exp_ready, b + 1)
                    c(dve.tensor_scalar(g2[:, :], e21[:, :], 1.0, None, ALU.add))
                    c.wait()
                    c(dve.reciprocal(g1[:, :], g2[:, :]))
                    c.wait()
                    c(dve.tensor_tensor(g2[:, :], g1[:, :], e21[:, :], ALU.mult))
                    c(dve.tensor_tensor(first[:, :, :], first[:, :, :],
                                        g1[:, :].unsqueeze(2).to_broadcast([P, TB, E]), ALU.mult))
                    c.wait(1)
                    c(dve.tensor_tensor(second[:, :, :], second[:, :, :],
                                        g2[:, :].unsqueeze(2).to_broadcast([P, TB, E]), ALU.mult))
                    c.wait()
                    dve.tensor_tensor(gates[:, :, :], first[:, :, :], second[:, :, :], ALU.add).then_inc(gates_ready, 1)
                    dve.wait_ge(gates_turned, b + 1)
                    dve.tensor_copy(gatesT[:, :], psT[0:E, :]).then_inc(gatesT_ready, 1)
                    dve.wait_ge(gates_ready, b + 1)
                    for e in range(E):
                        dve.wait_ge(y_done, b * E + e + 1)
                        if e >= 1:
                            dve.wait_ge(y_used, b * E + e)
                        for t in range(TB):
                            x = core.X[:, b * TB + t, :]
                            last = dve.scalar_tensor_tensor(out=x, in0=psY[:, e % 2, t * P:(t + 1) * P],
                                                            scalar=gates[:, t, e:e + 1], in1=x,
                                                            op0=ALU.mult, op1=ALU.add)
                        last.then_inc(y_used, 1)
                    dve.wait_ge(y_used, (b + 1) * E)
                    dve.wait_ge(bias_done, b + 1)
                    add_to_stream(dve, core, b, psL[:, :], bias_added)
                    dve.wait_ge(bias_added, b + 1)
                    assert c.n == VEC, c.n


UNITS = (((3, 0),), ((2, 0), (0, 384)), ((1, 0),))


def unit_width(u):
    return sum((i + 1) * P for i, _ in UNITS[u])


UNITS_T = (((0, 0),), ((1, 0), (3, 384)), ((2, 0),))


def unit_width_t(u):
    return sum((TB - k) * P for k, _ in UNITS_T[u])


def layer0_attn(nc, core):
    H, DH, PER = 16, 8, 4
    NU = len(UNITS)
    PARTS = 3
    ROWS = 32 * PARTS
    KEEP = 4
    PSLOTS = 6
    LAG = 3
    assert PSLOTS * sum(unit_width_t(u) for u in range(NU)) == PROBS_COLS
    G = H // PER
    with ExitStack() as ctx:
        def sb(name, shape, dt=F32):
            return ctx.enter_context(nc.sbuf_tensor("L0a_" + name, shape, dt))

        def sem(name):
            return core.semaphore(ctx, "L0a_" + name)

        ln = LayerNorm(nc, ctx, "L0a_ln", core)
        w = core.w["L0a"]
        xn = sb("xn", [P, TB, D])
        xT = sb("xT", [P, S])
        scratch = sb("scratch", [P, G, S])
        rot, part, o_heads = scratch[:, 0:2, :], scratch[:, 2:4, :], scratch
        parts = sb("parts", [P, 2, PARTS, S], BF16)
        q_stack = sb("q_stack", [P, KEEP, S], BF16)
        k_stack = sb("k_stack", [P, KEEP, S], BF16)
        pick_q = sb("pick_q", [P, H, 32], BF16)
        pick_k = sb("pick_k", [P, H, 112], BF16)
        causal_t = sb("causal_t", [P, P], BF16)
        v = sb("v", [P, TB, H, 32])
        neg_max = sb("neg_max", [P, 2, TB])
        rest = sb("rest", [P, TB])
        zero = sb("zero", [P, TB])
        max_parts = sb("max_parts", [P, 3, TB, PARTS], BF16)
        probs = core.arena[:, 0:PROBS_COLS].rearrange("p (n c) -> p n c", n=PSLOTS)
        inv = sb("inv", [P, TB, H])
        o = sb("o", [P, TB, D])
        oT = sb("oT", [P, S])
        psM = ctx.enter_context(nc.psum_tensor("L0a_psM", [P, S], F32))
        psO = ctx.enter_context(nc.psum_tensor("L0a_psO", [P, S], F32))
        psR = ctx.enter_context(nc.psum_tensor("L0a_psR", [P, 2, S], F32))
        psA = ctx.enter_context(nc.psum_tensor("L0a_psA", [P, 2, S], F32))
        psB = ctx.enter_context(nc.psum_tensor("L0a_psB", [P, 2, S], F32))
        (setup, turned, xt_ready, qk_done, v_done, v_ready, vec, rot_ready, first_parts, second_parts, parts_ready,
         q_picked, k_picked, q_ready, k_ready, scores_done, max_ready, max_split, max_turned, max_rows, keyed_done,
         probs_ready, av_done, heads_ready, heads_turned, inv_ready, o_ready, o_turned, ot_ready, y_done, added) = (
            sem(n) for n in (
                "setup turned xt_ready qk_done v_done v_ready vec rot_ready first_parts second_parts parts_ready "
                "q_picked k_picked q_ready k_ready scores_done max_ready max_split max_turned max_rows keyed_done "
                "probs_ready av_done heads_ready heads_turned inv_ready o_ready o_turned ot_ready y_done added"
            ).split())
        VEC = 4
        SETUP = 6
        SPLIT = 4
        unit_at = [sum(unit_width_t(j) for j in range(u)) for u in range(NU)]
        key_at = {k: (unit_at[u] + at, (TB - k) * P) for u in range(NU) for k, at in UNITS_T[u]}

        def bank(m):
            return psB[:, m % 2, :]

        def tile_bank(t):
            return (psA if t < 2 else psB)[:, t % 2, :]

        with nc.Block() as block:
            @block.scalar
            def _(act):
                core.wait_weights(act, "L0a")
                act.activation(pick_k[:, :, :], w["pick_k"], ACT.Copy).then_inc(setup, 1)
                with act.Fori(0, B) as b:
                    ln.scalar(act, b)
                    act.wait_ge(turned, b + 1)
                    act.activation(xT[:, :], psM[:, :], ACT.Copy).then_inc(xt_ready, 1)
                    act.wait_ge(v_done, b + 1)
                    act.activation(v[:, :, :, 0:DH], psM[:, :].rearrange("p (t h d) -> p t h d", t=TB, h=H),
                                   ACT.Copy).then_inc(v_ready, 1)
                    for j in range(2):
                        act.wait_ge(rot_ready, b * 2 + j + 1)
                        act.activation(parts[:, j, 0, :], rot[:, j, :], ACT.Copy).then_inc(first_parts, 1)
                        act.wait_ge(second_parts, b * 2 + j + 1)
                        act.activation(parts[:, j, 1, :], part[:, j, :], ACT.Copy).then_inc(first_parts, 1)
                    for n in range(H + LAG):
                        m = n - LAG
                        if m >= 0:
                            act.wait_ge(max_turned, b * H + m + 1)
                            act.activation(q_stack[ROWS:ROWS + PARTS, m % KEEP, :], psM[ROWS:ROWS + PARTS, :],
                                           ACT.Copy).then_inc(max_rows, 1)
                        if n < H:
                            act.wait_ge(q_picked, b * H + n + 1)
                            act.activation(q_stack[0:ROWS, n % KEEP, :], psR[0:ROWS, 0, :],
                                           ACT.Copy).then_inc(q_ready, 1)
                        if m >= 0:
                            if m >= PSLOTS:
                                act.wait_ge(av_done, b * G + (m - PSLOTS) // PER + 1)
                            for u in range(NU):
                                act.wait_ge(keyed_done, b * (H * NU) + m * NU + u + 1)
                                act.activation(probs[:, m % PSLOTS, unit_at[u]:unit_at[u] + unit_width_t(u)],
                                               bank(m * NU + u)[:, 0:unit_width_t(u)],
                                               ACT.Exp).then_inc(probs_ready, 1)
                        if n >= 2 * PER and n % PER == 0:
                            g = n // PER - 2
                            act.wait_ge(av_done, b * G + g + 1)
                            act.activation(o_heads[:, g, :], psO[:, :], ACT.Copy).then_inc(heads_ready, 1)
                    act.wait_ge(av_done, b * G + G)
                    act.activation(o_heads[:, G - 1, :], psO[:, :], ACT.Copy).then_inc(heads_ready, 1)
                    act.wait_ge(o_turned, b + 1)
                    act.activation(oT[:, :], psM[:, :], ACT.Copy).then_inc(ot_ready, 1)

            @block.tensor
            def _(pe):
                core.wait_weights(pe, "L0a")
                pe.wait_ge(setup, SETUP + 1)

                def pick_queries(b, n):
                    if n >= 1:
                        pe.wait_ge(q_ready, b * H + n)
                    for i in range(PARTS):
                        last = pe.matmul(psR[32 * i:32 * (i + 1), 0, :], pick_q[:, n, :], parts[:, 0, i, :],
                                         start=True, stop=True)
                    last.then_inc(q_picked, 1)

                def pick_keys(b, n):
                    if n >= 1:
                        pe.wait_ge(k_ready, b * H + n)
                    for j in range(PARTS):
                        at = DH * (PARTS - 1 - j)
                        last = pe.matmul(psR[0:ROWS, 1, :], pick_k[:, n, at:at + ROWS], parts[:, 1, j, :],
                                         start=j == 0, stop=j == PARTS - 1)
                    last.then_inc(k_picked, 1)

                def scores(b, n, u):
                    m = n * NU + u
                    if u == 0:
                        pe.wait_ge(q_ready, b * H + n + 1)
                        pe.wait_ge(k_ready, b * H + n + 1)
                    if m >= 2:
                        pe.wait_ge(max_ready, b * (H * NU) + m - 1)
                    for i, at in UNITS[u]:
                        pe.matmul(psA[:, m % 2, at:at + (i + 1) * P], q_stack[0:ROWS, n % KEEP, i * P:(i + 1) * P],
                                  k_stack[0:ROWS, n % KEEP, 0:(i + 1) * P], start=True, stop=False)
                        last = pe.matmul(psA[:, m % 2, at + i * P:at + (i + 1) * P], core.identb[:, :],
                                         core.causal[:, :], start=False, stop=True)
                    last.then_inc(scores_done, 1)

                def turn_maxima(b, n):
                    pe.wait_ge(max_split, (b * H + n) * SPLIT + SPLIT)
                    if n >= 1:
                        pe.wait_ge(max_rows, b * H + n)
                    for t in range(TB):
                        last = pe.matmul(psM[ROWS:ROWS + PARTS, t * P:(t + 1) * P], max_parts[:, n % 3, t, :],
                                         core.identb[:, :], start=True, stop=True)
                    last.then_inc(max_turned, 1)

                def keyed_scores(b, n, u):
                    m = n * NU + u
                    if u == 0:
                        pe.wait_ge(max_rows, b * H + n + 1)
                    if m >= 2:
                        pe.wait_ge(probs_ready, b * (H * NU) + m - 1)
                    for k, at in UNITS_T[u]:
                        pe.matmul(bank(m)[:, at:at + (TB - k) * P],
                                  k_stack[0:ROWS + PARTS, n % KEEP, k * P:(k + 1) * P],
                                  q_stack[0:ROWS + PARTS, n % KEEP, k * P:S], start=True, stop=False)
                        last = pe.matmul(bank(m)[:, at:at + P], core.identb[:, :], causal_t[:, :],
                                         start=False, stop=True)
                    last.then_inc(keyed_done, 1)

                def weigh_values(b, g):
                    pe.wait_ge(probs_ready, b * (H * NU) + (g + 1) * PER * NU)
                    if g >= 1:
                        pe.wait_ge(heads_ready, b * G + g)
                    for k in range(TB):
                        at, width = key_at[k]
                        for j in range(PER):
                            n = g * PER + j
                            last = pe.matmul(psO[32 * j:32 * (j + 1), k * P:S], v[:, k, n, :],
                                             probs[:, n % PSLOTS, at:at + width], start=k == 0, stop=k == TB - 1)
                    last.then_inc(av_done, 1)

                with pe.Fori(0, B) as b:
                    turn(pe, core, ln, b, xn, psM, turned)
                    pe.wait_ge(xt_ready, b + 1)
                    for j in range(4):
                        last = pe.matmul((psR if j < 2 else psA)[:, j % 2, :], w["qk"][:, j, :], xT[:, :],
                                         start=True, stop=True)
                        if j % 2:
                            last.then_inc(qk_done, 1)
                    for t in range(TB):
                        last = pe.matmul(psM[:, t * P:(t + 1) * P], xT[:, t * P:(t + 1) * P], w["v"][:, :],
                                         start=True, stop=True)
                    last.then_inc(v_done, 1)
                    pe.wait_ge(parts_ready, b * 2 + 2)
                    pe.wait_ge(v_ready, b + 1)
                    for n in range(H + LAG):
                        if n >= LAG:
                            turn_maxima(b, n - LAG)
                        if n < H:
                            pick_queries(b, n)
                        if 1 <= n <= H:
                            scores(b, n - 1, 0)
                            scores(b, n - 1, 1)
                        if n >= LAG:
                            keyed_scores(b, n - LAG, 0)
                        if n < H:
                            pick_keys(b, n)
                        if 1 <= n <= H:
                            scores(b, n - 1, 2)
                        if n >= LAG:
                            keyed_scores(b, n - LAG, 1)
                            keyed_scores(b, n - LAG, 2)
                        if n >= PER + LAG and (n - LAG) % PER == 0:
                            weigh_values(b, (n - LAG) // PER - 1)
                    weigh_values(b, G - 1)
                    pe.wait_ge(heads_ready, b * G + G)
                    for t in range(TB):
                        for g in range(G):
                            last = pe.transpose(tile_bank(t)[:, g * P:(g + 1) * P],
                                                o_heads[:, g, t * P:(t + 1) * P], core.ident)
                        last.then_inc(heads_turned, 1)
                    for t in range(TB):
                        pe.wait_ge(o_ready, b * TB + t + 1)
                        last = pe.transpose(psM[:, t * P:(t + 1) * P], o[:, t, :], core.ident)
                    last.then_inc(o_turned, 1)
                    pe.wait_ge(ot_ready, b + 1)
                    for t in range(TB):
                        last = pe.matmul(psO[:, t * P:(t + 1) * P], oT[:, t * P:(t + 1) * P], w["o"][:, :],
                                         start=True, stop=True)
                    last.then_inc(y_done, 1)

            @block.gpsimd
            def _(pool):
                pool.wait_ge(setup, SETUP + 1)
                with pool.Fori(0, B) as b:
                    for n in range(H):
                        c = Chain(pool, max_split, (b * H + n) * SPLIT)
                        pool.wait_ge(max_ready, b * (H * NU) + (n + 1) * NU)
                        if n >= 3:
                            pool.wait_ge(max_turned, b * H + n - 2)
                        c(pool.tensor_tensor(max_parts[:, n % 3, :, 0], neg_max[:, n % 2, :], zero[:, :], ALU.add))
                        c.wait()
                        c(pool.tensor_tensor(rest[:, :], neg_max[:, n % 2, :], max_parts[:, n % 3, :, 0],
                                             ALU.subtract))
                        c.wait()
                        c(pool.tensor_tensor(max_parts[:, n % 3, :, 1], rest[:, :], zero[:, :], ALU.add))
                        c.wait()
                        c(pool.tensor_tensor(max_parts[:, n % 3, :, 2], rest[:, :], max_parts[:, n % 3, :, 1],
                                             ALU.subtract))
                        c.wait()

            @block.vector
            def _(dve):
                core.wait_weights(dve, "L0a")
                c = Chain(dve, setup)
                c(dve.tensor_copy(pick_q[:, :, :], w["pick_q"]))
                c(dve.tensor_copy(causal_t[:, :], w["causal_t"]))
                c(dve.memset(v[:, :, :, :], 0.0))
                c(dve.memset(k_stack[ROWS:P, :, :], 1.0))
                c(dve.memset(zero[:, :], 0.0))
                dve.wait_ge(setup, SETUP)
                c(dve.memset(v[:, :, :, DH], 1.0))
                dve.wait_ge(setup, SETUP + 1)
                with dve.Fori(0, B) as b:
                    ln.vector(dve, b, lambda t: core.X[:, b * TB + t, :], lambda t: xn[:, t, :])
                    c = Chain(dve, vec, b * VEC)
                    for j in range(2):
                        ps = psA if j else psR
                        dve.wait_ge(qk_done, b * 2 + j + 1)
                        c(dve.tensor_tensor(rot[:, j, :], ps[:, 0, :], w["cos"][:, j, :], ALU.mult))
                        c(dve.tensor_tensor(part[:, j, :], ps[:, 1, :], w["sin"][:, j, :], ALU.mult))
                        c.wait()
                        dve.tensor_tensor(rot[:, j, :], rot[:, j, :], part[:, j, :], ALU.add).then_inc(rot_ready, 1)
                    for j in range(2):
                        dve.wait_ge(first_parts, b * 4 + 2 * j + 1)
                        dve.tensor_tensor(part[:, j, :], rot[:, j, :], parts[:, j, 0, :],
                                          ALU.subtract).then_inc(second_parts, 1)
                        dve.wait_ge(first_parts, b * 4 + 2 * j + 2)
                        dve.tensor_tensor(parts[:, j, 2, :], part[:, j, :], parts[:, j, 1, :],
                                          ALU.subtract).then_inc(parts_ready, 1)
                    for n in range(H + 1):
                        if n >= 3:
                            dve.wait_ge(max_split, (b * H + n - 2) * SPLIT)
                        for u in range(NU):
                            if u == NU - 1 and n < H:
                                dve.wait_ge(k_picked, b * H + n + 1)
                                dve.tensor_copy(k_stack[0:ROWS, n % KEEP, :], psR[0:ROWS, 1, :]).then_inc(k_ready, 1)
                            if 1 <= n <= H:
                                m = (n - 1) * NU + u
                                dve.wait_ge(scores_done, b * (H * NU) + m + 1)
                                for i, at in UNITS[u]:
                                    last = dve.tensor_reduce(neg_max[:, (n - 1) % 2, i:i + 1],
                                                             psA[:, m % 2, at:at + (i + 1) * P],
                                                             AX, ALU.max, negate=True)
                                last.then_inc(max_ready, 1)
                    for t in range(TB):
                        heads = tile_bank(t).rearrange("p (h c) -> p h c", c=32)
                        dve.wait_ge(heads_turned, b * TB + t + 1)
                        dve.reciprocal(inv[:, t, :], heads[:, :, DH]).then_inc(inv_ready, 1)
                        dve.wait_ge(inv_ready, b * TB + t + 1)
                        dve.tensor_tensor(o[:, t, :].rearrange("p (h d) -> p h d", h=H), heads[:, :, 0:DH],
                                          inv[:, t, :].unsqueeze(2).to_broadcast([P, H, DH]),
                                          ALU.mult).then_inc(o_ready, 1)
                    dve.wait_ge(y_done, b + 1)
                    add_to_stream(dve, core, b, psO[:, :], added)
                    dve.wait_ge(added, b + 1)
                    assert c.n == VEC, c.n


def layer1_attn(nc, core):
    H = 8
    SCALE = float(D) ** -0.5
    KINDS = 6
    QU, KU, VU, QC, KC, VC = range(KINDS)
    NU = len(UNITS)
    with ExitStack() as ctx:
        def sb(name, shape, dt=F32):
            return ctx.enter_context(nc.sbuf_tensor("L1a_" + name, shape, dt))

        def sem(name):
            return core.semaphore(ctx, "L1a_" + name)

        ln = LayerNorm(nc, ctx, "L1a_ln", core)
        w = core.w["L1a"]
        xn = sb("xn", [P, TB, D])
        xT = sb("xT", [P, S])
        proj = sb("proj", [P, 2, KINDS, S])
        th_look = sb("th_look", [P, S])
        look = sb("look", [P, S])
        th_sum = sb("th_sum", [P, S])
        lower = sb("lower", [P, S])
        neg_max = sb("neg_max", [P, TB])
        sums = sb("sums", [P, TB])
        inv = sb("inv", [P, TB])
        probs = sb("probs", [P, NU, S])
        probsT = sb("probsT", [P, TB, S])
        oT = sb("oT", [P, H, S])
        psJ = ctx.enter_context(nc.psum_tensor("L1a_psJ", [P, 2, S], F32))
        psD = ctx.enter_context(nc.psum_tensor("L1a_psD", [P, S], F32))
        psS = ctx.enter_context(nc.psum_tensor("L1a_psS", [P, NU, S], F32))
        psP = ctx.enter_context(nc.psum_tensor("L1a_psP", [P, S], F32))
        psO = ctx.enter_context(nc.psum_tensor("L1a_psO", [P, S], F32))
        (turned, xt_ready, proj_done, proj_ready, look_done, look_tanh, look_ready, sum_done, sum_tanh, lower_ready,
         scores_done, vec, max_ready, probs_ready, normed, probs_turned, pt_ready, av_done, o_ready, y_done, added) = (
            sem(n) for n in (
                "turned xt_ready proj_done proj_ready look_done look_tanh look_ready sum_done sum_tanh lower_ready "
                "scores_done vec max_ready probs_ready normed probs_turned pt_ready av_done o_ready y_done added"
            ).split())
        VEC = 8
        after = core.cf[:, C_AFTER:C_AFTER + P].unsqueeze(1).to_broadcast([P, TB, P])

        with nc.Block() as block:
            @block.scalar
            def _(act):
                def evacuate(b, n):
                    h, kind = n // KINDS, n % KINDS
                    act.wait_ge(proj_done, b * (H * KINDS) + n + 1)
                    act.activation(proj[:, h % 2, kind, :], psJ[:, n % 2, :], ACT.Copy,
                                   scale=SCALE if kind == QC else 1.0).then_inc(proj_ready, 1)

                def exponential(b, h, u):
                    act.wait_ge(max_ready, b * (H * NU) + h * NU + u + 1)
                    for i, at in UNITS[u]:
                        last = act.activation(probs[:, u, at:at + (i + 1) * P], psS[:, u, at:at + (i + 1) * P],
                                              ACT.Exp, bias=neg_max[:, i:i + 1], accum_out=sums[:, i:i + 1])
                    last.then_inc(probs_ready, 1)

                with act.Fori(0, B) as b:
                    ln.scalar(act, b)
                    act.wait_ge(turned, b + 1)
                    act.activation(xT[:, :], psJ[:, 0, :], ACT.Copy).then_inc(xt_ready, 1)
                    for n in range(KINDS):
                        evacuate(b, n)
                    for h in range(H):
                        nxt = (h + 1) * KINDS
                        more = h + 1 < H
                        act.wait_ge(look_done, b * H + h + 1)
                        act.activation(th_look[:, :], psD[:, :], ACT.Tanh, scale=0.5 * SCALE).then_inc(look_tanh, 1)
                        if more:
                            evacuate(b, nxt)
                            evacuate(b, nxt + 1)
                        act.wait_ge(sum_done, b * H + h + 1)
                        act.activation(th_sum[:, :], psD[:, :], ACT.Tanh, scale=0.5).then_inc(sum_tanh, 1)
                        for u in range(NU):
                            exponential(b, h, u)
                            if more:
                                evacuate(b, nxt + 2 + u)
                        if more:
                            evacuate(b, nxt + 5)
                        for u in range(NU):
                            act.wait_ge(probs_turned, b * (H * NU) + h * NU + u + 1)
                            for i, at in UNITS[u]:
                                last = act.activation(
                                    probsT[:, 0:i + 1, i * P:(i + 1) * P],
                                    psP[:, at:at + (i + 1) * P].rearrange("p (k q) -> p k q", q=P), ACT.Copy)
                            last.then_inc(pt_ready, 1)
                        act.wait_ge(av_done, b * H + h + 1)
                        act.activation(oT[:, h, :], psO[:, :], ACT.Copy).then_inc(o_ready, 1)

            @block.tensor
            def _(pe):
                core.wait_weights(pe, "L1a")

                def project(b, n):
                    h, kind = n // KINDS, n % KINDS
                    if n >= 2:
                        pe.wait_ge(proj_ready, b * (H * KINDS) + n - 1)
                    if kind in (VU, VC):
                        for t in range(TB):
                            last = pe.matmul(psJ[:, n % 2, t * P:(t + 1) * P], xT[:, t * P:(t + 1) * P],
                                             w["qkv"][:, h, kind, :], start=True, stop=True)
                    else:
                        last = pe.matmul(psJ[:, n % 2, :], w["qkv"][:, h, kind, :], xT[:, :], start=True, stop=True)
                    last.then_inc(proj_done, 1)

                with pe.Fori(0, B) as b:
                    turn(pe, core, ln, b, xn, psJ[:, 0, :], turned)
                    pe.wait_ge(xt_ready, b + 1)
                    for n in range(KINDS):
                        project(b, n)
                    for h in range(H):
                        nxt = (h + 1) * KINDS
                        more = h + 1 < H
                        of = proj[:, h % 2, :, :]
                        pe.wait_ge(proj_ready, b * (H * KINDS) + h * KINDS + KINDS)
                        if h >= 1:
                            pe.wait_ge(lower_ready, b * H + h)
                        for t in range(TB):
                            blk = slice(t * P, (t + 1) * P)
                            last = pe.matmul(psD[:, blk], of[:, KU, blk], of[:, QU, blk], start=True, stop=True)
                        last.then_inc(look_done, 1)
                        if more:
                            project(b, nxt)
                            project(b, nxt + 1)
                        pe.wait_ge(look_ready, b * H + h + 1)
                        for t in range(TB):
                            blk = slice(t * P, (t + 1) * P)
                            last = pe.matmul(psD[:, blk], look[:, blk], of[:, VU, blk], start=True, stop=True)
                        last.then_inc(sum_done, 1)
                        for u in range(NU):
                            for i, at in UNITS[u]:
                                pe.matmul(psS[:, u, at:at + (i + 1) * P], of[:, QC, i * P:(i + 1) * P],
                                          of[:, KC, 0:(i + 1) * P], start=True, stop=False)
                                last = pe.matmul(psS[:, u, at + i * P:at + (i + 1) * P], core.identb[:, :],
                                                 core.causal[:, :], start=False, stop=True)
                            last.then_inc(scores_done, 1)
                        if more:
                            for n in range(nxt + 2, nxt + KINDS):
                                project(b, n)
                        for u in range(NU):
                            pe.wait_ge(normed, b * (H * NU) + h * NU + u + 1)
                            if u >= 1:
                                pe.wait_ge(pt_ready, b * (H * NU) + h * NU + u)
                            for c in range(unit_width(u) // P):
                                last = pe.transpose(psP[:, c * P:(c + 1) * P], probs[:, u, c * P:(c + 1) * P],
                                                    core.ident)
                            last.then_inc(probs_turned, 1)
                        pe.wait_ge(pt_ready, b * (H * NU) + h * NU + NU)
                        if h >= 1:
                            pe.wait_ge(o_ready, b * H + h)
                        for k in range(TB):
                            last = pe.matmul(psO[:, k * P:S], of[:, VC, k * P:(k + 1) * P], probsT[:, k, k * P:S],
                                             start=k == 0, stop=k == TB - 1)
                        last.then_inc(av_done, 1)
                    pe.wait_ge(o_ready, b * H + H)
                    for t in range(TB):
                        for h in range(H):
                            last = pe.matmul(psO[:, t * P:(t + 1) * P], oT[:, h, t * P:(t + 1) * P], w["out"][:, h, :],
                                             start=h == 0, stop=h == H - 1)
                    last.then_inc(y_done, 1)

            @block.vector
            def _(dve):
                with dve.Fori(0, B) as b:
                    ln.vector(dve, b, lambda t: core.X[:, b * TB + t, :], lambda t: xn[:, t, :])
                    for h in range(H):
                        c = Chain(dve, vec, b * (H * VEC) + h * VEC)
                        dve.wait_ge(look_tanh, b * H + h + 1)
                        dve.scalar_tensor_tensor(out=look[:, :].rearrange("p (t i) -> p t i", t=TB),
                                                 in0=th_look[:, :].rearrange("p (t i) -> p t i", t=TB), scalar=1.0,
                                                 in1=after, op0=ALU.add, op1=ALU.mult).then_inc(look_ready, 1)
                        dve.wait_ge(sum_tanh, b * H + h + 1)
                        dve.scalar_tensor_tensor(out=lower[:, :], in0=th_sum[:, :], scalar=1.0, in1=psD[:, :],
                                                 op0=ALU.add, op1=ALU.mult).then_inc(lower_ready, 1)
                        dve.wait_ge(lower_ready, b * H + h + 1)
                        for u in range(NU + 1):
                            if u < NU:
                                dve.wait_ge(scores_done, b * (H * NU) + h * NU + u + 1)
                                for i, at in UNITS[u]:
                                    diag = psS[:, u, at + i * P:at + (i + 1) * P]
                                    c(dve.scalar_tensor_tensor(out=diag, in0=lower[:, i * P:(i + 1) * P], scalar=-0.5,
                                                               in1=diag, op0=ALU.mult, op1=ALU.add))
                                c.wait()
                                for i, at in UNITS[u]:
                                    last = dve.tensor_reduce(neg_max[:, i:i + 1], psS[:, u, at:at + (i + 1) * P],
                                                             AX, ALU.max, negate=True)
                                last.then_inc(max_ready, 1)
                            if u >= 1:
                                dve.wait_ge(probs_ready, b * (H * NU) + h * NU + u)
                                for i, at in UNITS[u - 1]:
                                    c(dve.reciprocal(inv[:, i:i + 1], sums[:, i:i + 1]))
                                c.wait()
                                for i, at in UNITS[u - 1]:
                                    row = probs[:, u - 1, at:at + (i + 1) * P]
                                    last = dve.tensor_scalar(row, row, inv[:, i:i + 1], None, ALU.mult)
                                last.then_inc(normed, 1)
                        assert c.n == VEC, c.n
                    dve.wait_ge(y_done, b + 1)
                    add_to_stream(dve, core, b, psO[:, :], added)
                    dve.wait_ge(added, b + 1)


def layer0_ffn(nc, core):
    DEPTH, H, DH, WIN = 2, 8, 64, 64
    HALF = D // 2
    HID = 341
    CH = (HID + P - 1) // P
    last_rows = HID - (CH - 1) * P
    K = WIN + P
    QK_SCALE = 8.0
    NU = TB * 2
    HU = H // 2
    with ExitStack() as ctx:
        def sb(name, shape, dt=F32):
            return ctx.enter_context(nc.sbuf_tensor("L0f_" + name, shape, dt))

        def sem(name):
            return core.semaphore(ctx, "L0f_" + name)

        ln = LayerNorm(nc, ctx, "L0f_ln", core)
        w = core.w["L0f"]
        x = sb("x", [P, TB, D])
        h = sb("h", [P, TB, D])
        hn = sb("hn", [P, TB, D])
        hT = sb("hT", [P, S])
        table = sb("table", [P, DEPTH, 2, 2, TB * DH])
        scratch = sb("scratch", [P, 2 * HU * K])
        squares = scratch[:, 0:2 * S].rearrange("p (j n) -> p j n", j=2)
        norms = sb("norms", [P, TB, 2, H])
        qk = sb("qk", [P, 2, TB, S])
        part = sb("part", [P, 2, S])
        qkT = sb("qkT", [P, 2, HU, S])
        v = sb("v", [P, TB, S])
        v_before = sb("v_before", [WIN, TB, S])
        neg_max = sb("neg_max", [P, TB, H])
        bias = sb("bias", [P, TB, H])
        sums = sb("sums", [P, TB, H])
        inv = sb("inv", [P, TB, H])
        probs = scratch[:, :].rearrange("p (j g k) -> p j g k", j=2, g=HU)
        own_T = qk[:, 1, 0:2, :]
        before_T = qk[0:WIN, 1, 2:4, :]
        o = part[:, 0, :]
        oT = part[:, 1, :]
        gelu = qk[:, 0, 0:CH, :]
        gated = qk[:, 1, 0:CH, :]
        psS = ctx.enter_context(nc.psum_tensor("L0f_psS", [P, 4, S], F32))
        psP = ctx.enter_context(nc.psum_tensor("L0f_psP", [P, 2, S], F32))
        psO = ctx.enter_context(nc.psum_tensor("L0f_psO", [P, S], F32))
        psX = ctx.enter_context(nc.psum_tensor("L0f_psX", [P, S], F32))
        (tables, shifted, half_ready, h_ready, turned, ht_ready, qk_done, squared, vec, v_done, v_ready, squares_used,
         roots, qk_ready, qk_turned, qkt_ready, scores_done, bias_ready, probs_ready, own_turned, before_turned,
         own_ready, before_ready, av_done, o_ready, o_turned, ot_ready, y_done, x_ready, a_done, g_done, gelu_ready,
         gated_ready, out_done, added) = (sem(n) for n in (
             "tables shifted half_ready h_ready turned ht_ready qk_done squared vec v_done v_ready squares_used "
             "roots qk_ready qk_turned qkt_ready scores_done bias_ready probs_ready own_turned before_turned "
             "own_ready before_ready av_done o_ready o_turned ot_ready y_done x_ready a_done g_done gelu_ready "
             "gated_ready out_done added").split())
        VEC = 78
        shift_in = core.cf[:, C_SHIFT:C_SHIFT + P]
        shift_over = core.cf[:, C_OVER:C_OVER + P]

        def rows(c):
            return P if c < CH - 1 else last_rows

        def halves(ap):
            return ap.rearrange("p (h a d) -> p h a d", h=H, a=2)

        def first_key(t):
            return WIN if t == 0 else 0

        def scores_of(n):
            return psS[:, 2 * (n % 2):2 * (n % 2) + 2, 0:2 * K].rearrange("p b (g k) -> p b g k", g=2)

        with nc.Block() as block:
            @block.sync
            def _(sp):
                load_layer1_weights(core, sp)

            @block.scalar
            def _(act):
                core.wait_weights(act, "L0f")

                def shift_and_turn(b, s):
                    act.wait_ge(shifted, b * 4 + s + 1)
                    act.activation(h[:, :, HALF:D], psX[:, 0:TB * HALF].rearrange("p (t d) -> p t d", t=TB),
                                   ACT.Copy).then_inc(half_ready, 1)

                with act.Fori(0, B) as b:
                    ln.scalar(act, b * 3)
                    for l in range(DEPTH):
                        bl = b * DEPTH + l
                        shift_and_turn(b, 2 * l)
                        act.wait_ge(turned, bl * 2 + 1)
                        act.activation(hT[:, :], psX[:, :], ACT.Copy).then_inc(ht_ready, 1)
                        for t in range(TB):
                            for j in range(2):
                                act.wait_ge(qk_done, bl * 8 + 2 * t + j + 1)
                                if 2 * t + j >= 2:
                                    act.wait_ge(squares_used, bl * 8 + 2 * t + j - 1)
                                act.activation(squares[:, j, :], psS[:, 2 * (t % 2) + j, :],
                                               ACT.Square).then_inc(squared, 1)
                            act.wait_ge(v_done, bl * 4 + t + 1)
                            if t >= 1:
                                act.activation(v_before[:, t, :], psP[0:WIN, 1, :], ACT.Copy)
                            act.activation(v[:, t, :], psP[:, 0, :], ACT.Copy).then_inc(v_ready, 1)
                        act.wait_ge(squares_used, bl * 8 + 8)
                        act.activation(norms[:, :, :, :], norms[:, :, :, :], ACT.Sqrt).then_inc(roots, 1)
                        for j in range(2):
                            for t in range(TB):
                                act.wait_ge(qk_turned, bl * 8 + j * TB + t + 1)
                                act.activation(qkT[:, j, :, t * P:(t + 1) * P],
                                               psP[:, t % 2, :].rearrange("p (g k) -> p g k", g=HU),
                                               ACT.Copy).then_inc(qkt_ready, 1)
                        for n in range(NU + 3):
                            if n < NU:
                                t, half = n // 2, n % 2
                                act.wait_ge(bias_ready, bl * NU + n + 1)
                                if n >= 2:
                                    act.wait_ge(before_turned, bl * NU + n - 1)
                                for g in range(HU):
                                    hd, k0 = half * HU + g, first_key(t)
                                    last = act.activation(probs[:, n % 2, g, k0:K], scores_of(n)[:, g % 2, g // 2, k0:K],
                                                          ACT.Exp, bias=bias[:, t, hd:hd + 1],
                                                          scale=norms[:, t, 0, hd:hd + 1],
                                                          accum_out=sums[:, t, hd:hd + 1])
                                last.then_inc(probs_ready, 1)
                            m = n - 1
                            if 0 <= m < NU:
                                act.wait_ge(before_turned, bl * NU + m + 1)
                                if m >= 2:
                                    act.wait_ge(av_done, bl * NU + m - 1)
                                if m < 2:
                                    act.wait_ge(own_turned, bl * NU + m + 1)
                                    act.activation(before_T[:, m % 2, 0:1], before_T[:, m % 2, 0:1],
                                                   ACT.Copy).then_inc(before_ready, 1)
                                else:
                                    act.activation(before_T[:, m % 2, :], psP[0:WIN, 1, :],
                                                   ACT.Copy).then_inc(before_ready, 1)
                            m = n - 3
                            if m >= 0 and m % 2:
                                act.wait_ge(o_turned, bl * TB + m // 2 + 1)
                                act.activation(oT, psX[:, :], ACT.Copy).then_inc(ot_ready, 1)
                        shift_and_turn(b, 2 * l + 1)
                        ln.scalar(act, b * 3 + 1 + l)
                        act.wait_ge(turned, bl * 2 + 2)
                        act.activation(hT[:, :], psX[:, :], ACT.Identity, bias=w["ln"][:, 2 * l + 1:2 * l + 2],
                                       scale=w["ln"][:, 2 * l:2 * l + 1]).then_inc(ht_ready, 1)
                        for c in range(CH):
                            act.wait_ge(g_done, bl * CH + c + 1)
                            col = w["b1"][0:rows(c), (l * 2 + 1) * CH + c:(l * 2 + 1) * CH + c + 1]
                            ps = psS[:, 3, :] if c == 0 else psP[:, c - 1, :]
                            act.activation(gelu[0:rows(c), c, :], ps[0:rows(c), :], ACT.Gelu,
                                           bias=col).then_inc(gelu_ready, 1)

            @block.tensor
            def _(pe):
                core.wait_weights(pe, "L0f")

                def shift(n_x, b):
                    pe.matmul(psX[:, 0:TB * HALF], shift_in, x[:, :, HALF:D], start=True, stop=False)
                    pe.matmul(psX[:, HALF:TB * HALF], shift_over, x[:, 0:TB - 1, HALF:D],
                              start=False, stop=True).then_inc(shifted, 1)

                def scores(bl, n):
                    t, half = n // 2, n % 2
                    k0 = first_key(t)
                    if n >= 2:
                        pe.wait_ge(probs_ready, bl * NU + n - 1)
                    for g in range(HU):
                        hd = half * HU + g
                        r = slice(DH * (hd % 2), DH * (hd % 2) + DH)
                        out = scores_of(n)[:, g % 2, g // 2, k0:K]
                        pe.matmul(out, qkT[r, 0, hd // 2, t * P:(t + 1) * P],
                                  qkT[r, 1, hd // 2, t * P - WIN + k0:(t + 1) * P], start=True, stop=False)
                        last = pe.matmul(out, core.identb[:, :], core.band[:, k0:K], start=False, stop=True)
                    last.then_inc(scores_done, 1)

                def turn_probs(bl, n):
                    t = n // 2
                    pe.wait_ge(probs_ready, bl * NU + n + 1)
                    if n >= 1:
                        pe.wait_ge(own_ready, bl * NU + n)
                        pe.wait_ge(before_ready, bl * NU + n)
                    for g in range(HU):
                        last = pe.transpose(psP[:, 0, g * P:(g + 1) * P], probs[:, n % 2, g, WIN:K], core.ident)
                    last.then_inc(own_turned, 1)
                    for g in range(HU):
                        if t == 0:
                            last = pe.transpose(psP[:, 1, g * P:(g + 1) * P], probs[:, n % 2, g, WIN:K], core.ident)
                        else:
                            last = pe.transpose(psP[0:WIN, 1, g * P:(g + 1) * P], probs[:, n % 2, g, 0:WIN],
                                                core.ident)
                    last.then_inc(before_turned, 1)

                def weigh_values(bl, n):
                    t, half = n // 2, n % 2
                    pe.wait_ge(own_ready, bl * NU + n + 1)
                    pe.wait_ge(before_ready, bl * NU + n + 1)
                    if half == 0 and t >= 1:
                        pe.wait_ge(o_ready, bl * TB + t)
                    for g in range(HU):
                        hd = half * HU + g
                        out = psO[:, hd * DH:(hd + 1) * DH]
                        if t >= 1:
                            pe.matmul(out, before_T[:, n % 2, g * P:(g + 1) * P],
                                      v_before[:, t, hd * DH:(hd + 1) * DH], start=True, stop=False)
                        last = pe.matmul(out, own_T[:, n % 2, g * P:(g + 1) * P], v[:, t, hd * DH:(hd + 1) * DH],
                                         start=t == 0, stop=True)
                    last.then_inc(av_done, 1)

                def turn_out(bl, t):
                    pe.wait_ge(o_ready, bl * TB + t + 1)
                    if t >= 1:
                        pe.wait_ge(x_ready, bl * (TB + 1) + t)
                    for g in range(HU):
                        last = pe.transpose(psX[:, g * P:(g + 1) * P], o[:, g * P:(g + 1) * P], core.ident)
                    last.then_inc(o_turned, 1)

                def project_out(bl, l, t):
                    pe.wait_ge(ot_ready, bl * TB + t + 1)
                    for g in range(HU):
                        last = pe.matmul(psX[:, 0:D], oT[:, g * P:(g + 1) * P], w["wo"][:, l, g, :],
                                         start=g == 0, stop=g == HU - 1)
                    last.then_inc(y_done, 1)

                with pe.Fori(0, B) as b:
                    for l in range(DEPTH):
                        bl = b * DEPTH + l
                        if l == 0:
                            pe.wait_ge(ln.ready, b * (3 * TB) + TB)
                        else:
                            pe.wait_ge(x_ready, b * (2 * TB + 2) + TB + 1)
                        shift(0, b)
                        pe.wait_ge(h_ready, bl * 2 + 1)
                        pe.wait_ge(half_ready, bl * 2 + 1)
                        for t in range(TB):
                            last = pe.transpose(psX[:, t * P:(t + 1) * P], h[:, t, :], core.ident)
                        last.then_inc(turned, 1)
                        pe.wait_ge(ht_ready, bl * 2 + 1)
                        for t in range(TB):
                            if t >= 2:
                                pe.wait_ge(qk_ready, bl * (3 * TB) + 2 * t - 2)
                                pe.wait_ge(squared, bl * 8 + 2 * t - 2)
                            for j in range(2):
                                pe.matmul(psS[:, 2 * (t % 2) + j, :], hT[:, t * P:(t + 1) * P], w["wqkv"][:, l, j, :],
                                          start=True, stop=True).then_inc(qk_done, 1)
                            if t >= 1:
                                pe.wait_ge(v_ready, bl * TB + t)
                                pe.matmul(psP[0:WIN, 1, :], hT[:, t * P - WIN:t * P], w["wqkv"][:, l, 2, :],
                                          start=True, stop=True)
                            pe.matmul(psP[:, 0, :], hT[:, t * P:(t + 1) * P], w["wqkv"][:, l, 2, :],
                                      start=True, stop=True).then_inc(v_done, 1)
                        pe.wait_ge(v_ready, bl * TB + TB)
                        for j in range(2):
                            for t in range(TB):
                                if j == 0:
                                    pe.wait_ge(qk_ready, bl * (3 * TB) + 2 * TB)
                                else:
                                    pe.wait_ge(qk_ready, bl * (3 * TB) + 2 * TB + t + 1)
                                if j * TB + t >= 2:
                                    pe.wait_ge(qkt_ready, bl * 8 + j * TB + t - 1)
                                for g in range(HU):
                                    last = pe.transpose(psP[:, t % 2, g * P:(g + 1) * P], qk[:, j, t, g * P:(g + 1) * P],
                                                        core.ident)
                                last.then_inc(qk_turned, 1)
                        pe.wait_ge(qkt_ready, bl * 8 + 8)
                        for n in range(NU + 4):
                            if n < NU:
                                scores(bl, n)
                            if 0 <= n - 1 < NU:
                                turn_probs(bl, n - 1)
                            if 0 <= n - 2 < NU:
                                weigh_values(bl, n - 2)
                            if n - 3 >= 0 and (n - 3) % 2 and n - 3 < NU:
                                turn_out(bl, (n - 3) // 2)
                            if n - 4 >= 0 and (n - 4) % 2:
                                project_out(bl, l, (n - 4) // 2)
                        pe.wait_ge(x_ready, bl * (TB + 1) + TB)
                        shift(0, b)
                        for t in range(TB):
                            pe.wait_ge(ln.ready, b * (3 * TB) + (l + 1) * TB + t + 1)
                            last = pe.transpose(psX[:, t * P:(t + 1) * P], hn[:, t, :], core.ident)
                        last.then_inc(turned, 1)
                        pe.wait_ge(ht_ready, bl * 2 + 2)
                        for c in range(CH):
                            ps = psS[:, 3, :] if c == 0 else psP[:, c - 1, :]
                            pe.matmul(ps[0:rows(c), :], w["w1"][:, l, HID + c * P:HID + c * P + rows(c)], hT[:, :],
                                      start=True, stop=True).then_inc(g_done, 1)
                            pe.matmul(psS[0:rows(c), c, :], w["w1"][:, l, c * P:c * P + rows(c)], hT[:, :],
                                      start=True, stop=True).then_inc(a_done, 1)
                        pe.wait_ge(gated_ready, bl * CH + CH)
                        for t in range(TB):
                            out = psO[:, t * P:(t + 1) * P]
                            for c in range(CH):
                                pe.matmul(out, gated[0:rows(c), c, t * P:(t + 1) * P], w["w2"][0:rows(c), l, c, :],
                                          start=c == 0, stop=False)
                            last = pe.matmul(out, core.ones_row, w["b2"][0:1, l, :], start=False, stop=True)
                        last.then_inc(out_done, 1)

            @block.vector
            def _(dve):
                core.wait_weights(dve, "L0f")
                for l in range(DEPTH):
                    for j in range(2):
                        for f in range(2):
                            last = dve.tensor_tensor(
                                table[:, l, j, f, :].rearrange("p (t d) -> p t d", t=TB),
                                w["pos"][:, j, f, :].rearrange("p (t d) -> p t d", t=TB),
                                w["scales"][:, l * 4 + j * 2 + f, :].unsqueeze(1).to_broadcast([P, TB, DH]), ALU.mult)
                last.then_inc(tables, 1)
                dve.wait_ge(tables, 1)
                with dve.Fori(0, B) as b:
                    ln.vector(dve, b * 3, lambda t: core.X[:, b * TB + t, :], lambda t: x[:, t, :])
                    c = Chain(dve, vec, b * VEC)
                    for l in range(DEPTH):
                        bl = b * DEPTH + l
                        if l == 0:
                            dve.wait_ge(ln.ready, b * (3 * TB) + TB)
                        dve.tensor_copy(h[:, :, 0:HALF], x[:, :, 0:HALF]).then_inc(h_ready, 1)
                        for t in range(TB):
                            for j in range(2):
                                ps = psS[:, 2 * (t % 2) + j, :]
                                cos = table[:, l, j, 0, t * DH:(t + 1) * DH].unsqueeze(1).to_broadcast([P, H, DH])
                                sin = table[:, l, j, 1, t * DH:(t + 1) * DH].rearrange(
                                    "p (a d) -> p a d", a=2)
                                dve.wait_ge(squared, bl * 8 + 2 * t + j + 1)
                                dve.tensor_reduce(norms[:, t, j, :], squares[:, j, :].rearrange("p (h d) -> p h d", h=H),
                                                  AX, ALU.add).then_inc(squares_used, 1)
                                c(dve.tensor_tensor(qk[:, j, t, :].rearrange("p (h d) -> p h d", h=H),
                                                    ps.rearrange("p (h d) -> p h d", h=H), cos, ALU.mult))
                                if 2 * t + j >= 2:
                                    dve.wait_ge(qk_ready, bl * (3 * TB) + 2 * t + j - 1)
                                for a in range(2):
                                    c(dve.tensor_tensor(halves(part[:, j, :])[:, :, a, :], halves(ps)[:, :, 1 - a, :],
                                                        sin[:, a, :].unsqueeze(1).to_broadcast([P, H, DH // 2]),
                                                        ALU.mult))
                                c.wait()
                                dve.tensor_tensor(qk[:, j, t, :], qk[:, j, t, :], part[:, j, :],
                                                  ALU.add).then_inc(qk_ready, 1)
                        dve.wait_ge(roots, bl + 1)
                        c(dve.tensor_scalar(norms[:, :, :, :], norms[:, :, :, :], 1e-12, None, ALU.max))
                        c.wait()
                        c(dve.reciprocal(norms[:, :, :, :], norms[:, :, :, :]))
                        c.wait()
                        c(dve.tensor_scalar(norms[:, :, 0, :], norms[:, :, 0, :], QK_SCALE, None, ALU.mult))
                        dve.wait_ge(qk_ready, bl * (3 * TB) + 2 * TB)
                        for t in range(TB):
                            k = qk[:, 1, t, :].rearrange("p (h d) -> p h d", h=H)
                            dve.tensor_tensor(k, k, norms[:, t, 1, :].unsqueeze(2).to_broadcast([P, H, DH]),
                                              ALU.mult).then_inc(qk_ready, 1)
                        for n in range(NU + 4):
                            if n < NU:
                                t, half = n // 2, n % 2
                                hs = slice(half * HU, half * HU + HU)
                                dve.wait_ge(scores_done, bl * NU + n + 1)
                                c(dve.tensor_reduce(neg_max[:, t, hs].rearrange("p (g b) -> p b g", b=2),
                                                    scores_of(n)[:, :, :, first_key(t):K], AX, ALU.max, negate=True))
                                c.wait()
                                dve.tensor_tensor(bias[:, t, hs], neg_max[:, t, hs], norms[:, t, 0, hs],
                                                  ALU.mult).then_inc(bias_ready, 1)
                            m = n - 1
                            if 0 <= m < NU:
                                dve.wait_ge(own_turned, bl * NU + m + 1)
                                if m >= 2:
                                    dve.wait_ge(av_done, bl * NU + m - 1)
                                dve.tensor_copy(own_T[:, m % 2, :], psP[:, 0, :]).then_inc(own_ready, 1)
                            m = n - 2
                            if m >= 0 and m % 2 and m < NU:
                                t = m // 2
                                dve.wait_ge(av_done, bl * NU + m + 1)
                                dve.wait_ge(probs_ready, bl * NU + m + 1)
                                if t >= 1:
                                    dve.wait_ge(o_turned, bl * TB + t)
                                c(dve.reciprocal(inv[:, t, :], sums[:, t, :]))
                                c.wait()
                                dve.tensor_tensor(o.rearrange("p (h d) -> p h d", h=H),
                                                  psO[:, :].rearrange("p (h d) -> p h d", h=H),
                                                  inv[:, t, :].unsqueeze(2).to_broadcast([P, H, DH]),
                                                  ALU.mult).then_inc(o_ready, 1)
                            m = n - 4
                            if m >= 0 and m % 2:
                                t = m // 2
                                dve.wait_ge(y_done, bl * TB + t + 1)
                                dve.tensor_tensor(x[:, t, :], x[:, t, :], psX[:, 0:D], ALU.add).then_inc(x_ready, 1)
                        dve.wait_ge(x_ready, bl * (TB + 1) + TB)
                        dve.tensor_copy(h[:, :, 0:HALF], x[:, :, 0:HALF]).then_inc(h_ready, 1)
                        dve.wait_ge(h_ready, bl * 2 + 2)
                        dve.wait_ge(half_ready, bl * 2 + 2)
                        ln.vector(dve, b * 3 + 1 + l, lambda t: h[:, t, :], lambda t: hn[:, t, :])
                        for k in range(CH):
                            r = rows(k)
                            dve.wait_ge(gelu_ready, bl * CH + k + 1)
                            dve.wait_ge(a_done, bl * CH + k + 1)
                            dve.scalar_tensor_tensor(out=gated[0:r, k, :], in0=psS[0:r, k, :],
                                                     scalar=w["b1"][0:r, l * 2 * CH + k:l * 2 * CH + k + 1],
                                                     in1=gelu[0:r, k, :], op0=ALU.add,
                                                     op1=ALU.mult).then_inc(gated_ready, 1)
                        dve.wait_ge(out_done, bl + 1)
                        dve.tensor_tensor(x[:, :, :], x[:, :, :], psO[:, :].rearrange("p (t d) -> p t d", t=TB),
                                          ALU.add).then_inc(x_ready, 1)
                        dve.wait_ge(x_ready, bl * (TB + 1) + TB + 1)
                    xb = core.X[:, bass.ds(b * TB, TB), :]
                    dve.tensor_tensor(xb, xb, x[:, :, :], ALU.add).then_inc(added, 1)
                    dve.wait_ge(added, b + 1)
                    assert c.n == VEC, c.n


def layer2_ffn(nc, core):
    E, TOPK = 8, 64
    PAIRS = E // 2
    ROT = 32
    SCALE = float(D) ** -0.5
    G = D + 2 * ROT
    BP = P // B
    TOP = 23
    with ExitStack() as ctx:
        def sb(name, shape, dt=F32):
            return ctx.enter_context(nc.sbuf_tensor("L2f_" + name, shape, dt))

        def sem(name):
            return core.semaphore(ctx, "L2f_" + name)

        ln = LayerNorm(nc, ctx, "L2f_ln", core)
        w = core.w["L2f"]
        xg = sb("xg", [P, NT, G])
        xT = sb("xT", [P, S])
        score = sb("score", [P, S])
        work = sb("work", [P, S])
        top8 = sb("top8", [P, 8])
        chosen = sb("chosen", [P, S])
        rank = sb("rank", [P, S])
        rankT = sb("rankT", [P, TB, P])
        scoreT = sb("scoreT", [P, TB, P])
        (turned, xt_ready, logits_done, exp_ready, top, angles, rank_turned, rank_ready) = (
            sem(n) for n in "turned xt_ready logits_done exp_ready top angles rank_turned rank_ready".split())
        with ExitStack() as first:
            psT = first.enter_context(nc.psum_tensor("L2f_psT", [P, S], F32))
            psL = first.enter_context(nc.psum_tensor("L2f_psL", [P, S], F32))
            psK = first.enter_context(nc.psum_tensor("L2f_psK", [P, 2, S], F32))
            with nc.Block() as block:
                @block.gpsimd
                def _(pool):
                    core.wait_weights(pool, "L2f")
                    for b in range(B):
                        last = pool.tensor_copy(xg[:, b * TB:(b + 1) * TB, D:G], w["angles"])
                    last.then_inc(angles, 1)

                @block.scalar
                def _(act):
                    core.wait_weights(act, "L2f")
                    for b in range(B):
                        ln.scalar(act, b)
                        act.wait_ge(turned, b + 1)
                        act.activation(xT[:, :], psT[:, :], ACT.Copy).then_inc(xt_ready, 1)
                        act.wait_ge(logits_done, b + 1)
                        if b == 0:
                            act.wait_ge(top, 1)
                        act.activation(score[b * BP:b * BP + E, :], psL[b * BP:b * BP + E, :], ACT.Exp,
                                       scale=-1.0).then_inc(exp_ready, 1)
                    for j, dst in enumerate((rankT, scoreT)):
                        act.wait_ge(rank_turned, j + 1)
                        act.activation(dst[:, :, :], psK[:, j, :].rearrange("p (t r) -> p t r", t=TB),
                                       ACT.Copy).then_inc(rank_ready, 1)

                @block.tensor
                def _(pe):
                    core.wait_weights(pe, "L2f")
                    for b in range(B):
                        for t in range(TB):
                            pe.wait_ge(ln.ready, b * TB + t + 1)
                            last = pe.transpose(psT[:, t * P:(t + 1) * P], xg[:, b * TB + t, 0:D], core.ident)
                        last.then_inc(turned, 1)
                        pe.wait_ge(xt_ready, b + 1)
                        pe.matmul(psL[b * BP:b * BP + E, :], w["router"], xT[:, :],
                                  start=True, stop=True).then_inc(logits_done, 1)
                    for j, src in enumerate((rank, score)):
                        if j == 0:
                            pe.wait_ge(top, TOP)
                        for t in range(TB):
                            last = pe.transpose(psK[:, j, t * P:(t + 1) * P], src[:, t * P:(t + 1) * P], core.ident)
                        last.then_inc(rank_turned, 1)

                @block.vector
                def _(dve):
                    c = Chain(dve, top)
                    c(dve.memset(score[:, :], 0.0))
                    for b in range(B):
                        ln.vector(dve, b, lambda t: core.X[:, b * TB + t, :], lambda t: xg[:, b * TB + t, 0:D])
                    dve.wait_ge(exp_ready, B)
                    c(dve.tensor_scalar(score[:, :], score[:, :], 1.0, None, ALU.add))
                    c.wait()
                    c(dve.reciprocal(score[:, :], score[:, :]))
                    c.wait()
                    c(dve.tensor_copy(work[:, :], score[:, :]))
                    for _ in range(TOPK // 8):
                        c.wait()
                        c(dve.max(top8[:, :], work[:, :]))
                        c.wait()
                        c(dve.match_replace(work[:, :], top8[:, :], work[:, :], -1.0))
                    c.wait()
                    c(dve.tensor_scalar(chosen[:, :], work[:, :], -1.0, None, ALU.is_equal))
                    c.wait()
                    c(dve.tensor_tensor_scan(rank[:, :], chosen[:, :], chosen[:, :], 0.0, ALU.add, ALU.max))
                    c.wait()
                    c(dve.tensor_tensor(rank[:, :], rank[:, :], chosen[:, :], ALU.mult))
                    assert c.n == TOP, c.n
        onehot = sb("onehot", [P, TB, E * TOPK])
        weighted = sb("weighted", [P, TB, E * TOPK])
        weightedT = sb("weightedT", [P, PAIRS, S])
        taken = sb("taken", [P, PAIRS, G])
        takenT = sb("takenT", [P, S])
        qk = sb("qk", [P, PAIRS, 2, D])
        v = sb("v", [P, PAIRS, D])
        part = sb("part", [P, 2, PAIRS, 2 * ROT])
        qkT = sb("qkT", [P, 2, S])
        neg_max = sb("neg_max", [P, PAIRS])
        sums = sb("sums", [P, PAIRS])
        inv = sb("inv", [P, PAIRS])
        probs = sb("probs", [P, S])
        probsT = sb("probsT", [P, S])
        avT = sb("avT", [P, S])
        result = sb("result", [P, PAIRS, D])
        psA = ctx.enter_context(nc.psum_tensor("L2f_psA", [P, 2, S], F32))
        psQ = ctx.enter_context(nc.psum_tensor("L2f_psQ", [P, PAIRS, S], F32))
        psT = ctx.enter_context(nc.psum_tensor("L2f_psT2", [P, S], F32))
        psS = ctx.enter_context(nc.psum_tensor("L2f_psS", [P, S], F32))
        (onehot_ready, weighted_ready, taken_done, taken_ready, weights_turned, wt_ready, taken_turned, tt_ready,
         qkv_done, rest_ready, vec, rot_ready, qk_turned, qkt_ready, scores_done, bias_ready, probs_ready,
         probs_turned, pt_ready, av_done, av_ready, result_done, result_ready, out_done, added) = (
            sem(n) for n in (
                "onehot_ready weighted_ready taken_done taken_ready weights_turned wt_ready taken_turned tt_ready "
                "qkv_done rest_ready vec rot_ready qk_turned qkt_ready scores_done bias_ready probs_ready "
                "probs_turned pt_ready av_done av_ready result_done result_ready out_done added").split())
        VEC = 8
        count_up = core.cf[:, C_COUNT:C_COUNT + TOPK].unsqueeze(1).to_broadcast([P, E, TOPK])
        with nc.Block() as block:
            @block.scalar
            def _(act):
                with act.Fori(0, B) as b:
                    for j in range(2):
                        act.wait_ge(taken_done, b * 2 + j + 1)
                        act.activation(taken[:, 2 * j:2 * j + 2, :],
                                       psA[:, j, 0:2 * G].rearrange("p (a g) -> p a g", a=2),
                                       ACT.Copy).then_inc(taken_ready, 1)
                    for t in range(TB):
                        act.wait_ge(weights_turned, b * TB + t + 1)
                        act.activation(weightedT[:, :, t * P:(t + 1) * P],
                                       psQ[:, t, :].rearrange("p (a k) -> p a k", a=PAIRS),
                                       ACT.Copy).then_inc(wt_ready, 1)
                    act.wait_ge(taken_turned, b + 1)
                    act.activation(takenT[:, :], psT[:, :], ACT.Copy).then_inc(tt_ready, 1)
                    act.wait_ge(qkv_done, b + 1)
                    for j in range(2):
                        act.activation(qk[:, :, j, 2 * ROT:D], psQ[:, :, j * D + 2 * ROT:(j + 1) * D], ACT.Copy)
                    act.activation(v[:, :, :], psQ[:, :, 2 * D:3 * D], ACT.Copy).then_inc(rest_ready, 1)
                    for j in range(2):
                        act.wait_ge(qk_turned, b * 2 + j + 1)
                        act.activation(qkT[:, j, :], psA[:, j, :], ACT.Copy).then_inc(qkt_ready, 1)
                    act.wait_ge(bias_ready, b + 1)
                    for a in range(PAIRS):
                        last = act.activation(probs[:, a * P:(a + 1) * P], psS[:, a * P:(a + 1) * P], ACT.Exp,
                                              bias=neg_max[:, a:a + 1], scale=SCALE, accum_out=sums[:, a:a + 1])
                    last.then_inc(probs_ready, 1)
                    act.wait_ge(probs_turned, b + 1)
                    act.activation(probsT[:, :], psT[:, :], ACT.Copy).then_inc(pt_ready, 1)
                    act.wait_ge(av_done, b + 1)
                    act.activation(avT[:, :], psS[:, :], ACT.Copy).then_inc(av_ready, 1)

            @block.tensor
            def _(pe):
                with pe.Fori(0, B) as b:
                    pe.wait_ge(onehot_ready, b + 1)
                    for a in range(PAIRS):
                        for t in range(TB):
                            last = pe.matmul(psA[:, a // 2, (a % 2) * G:(a % 2 + 1) * G],
                                             onehot[:, t, a * P:(a + 1) * P], xg[:, b * TB + t, :],
                                             start=t == 0, stop=t == TB - 1)
                        if a % 2:
                            last.then_inc(taken_done, 1)
                    pe.wait_ge(weighted_ready, b + 1)
                    for t in range(TB):
                        for a in range(PAIRS):
                            last = pe.transpose(psQ[:, t, a * P:(a + 1) * P], weighted[:, t, a * P:(a + 1) * P],
                                                core.ident)
                        last.then_inc(weights_turned, 1)
                    pe.wait_ge(taken_ready, b * 2 + 2)
                    for a in range(PAIRS):
                        last = pe.transpose(psT[:, a * P:(a + 1) * P], taken[:, a, 0:D], core.ident)
                    last.then_inc(taken_turned, 1)
                    pe.wait_ge(tt_ready, b + 1)
                    pe.wait_ge(wt_ready, (b + 1) * TB)
                    for e in range(E):
                        r = TOPK * (e % 2)
                        last = pe.matmul(psQ[r:r + TOPK, e // 2, 0:3 * D], takenT[:, e * TOPK:(e + 1) * TOPK],
                                         w["qkv"][:, e, :], start=True, stop=True)
                    last.then_inc(qkv_done, 1)
                    pe.wait_ge(rest_ready, b + 1)
                    for j in range(2):
                        pe.wait_ge(rot_ready, b * 2 + j + 1)
                        for a in range(PAIRS):
                            last = pe.transpose(psA[:, j, a * P:(a + 1) * P], qk[:, a, j, :], core.ident)
                        last.then_inc(qk_turned, 1)
                    pe.wait_ge(qkt_ready, b * 2 + 2)
                    for a in range(PAIRS):
                        blk = slice(a * P, (a + 1) * P)
                        pe.matmul(psS[:, blk], qkT[:, 0, blk], qkT[:, 1, blk], start=True, stop=False)
                        last = pe.matmul(psS[:, blk], core.identb[:, :], core.pair_mask[:, :], start=False, stop=True)
                    last.then_inc(scores_done, 1)
                    pe.wait_ge(probs_ready, b + 1)
                    for a in range(PAIRS):
                        last = pe.transpose(psT[:, a * P:(a + 1) * P], probs[:, a * P:(a + 1) * P], core.ident)
                    last.then_inc(probs_turned, 1)
                    pe.wait_ge(pt_ready, b + 1)
                    for a in range(PAIRS):
                        blk = slice(a * P, (a + 1) * P)
                        last = pe.matmul(psS[:, blk], v[:, a, :], probsT[:, blk], start=True, stop=True)
                    last.then_inc(av_done, 1)
                    pe.wait_ge(av_ready, b + 1)
                    for e in range(E):
                        r = TOPK * (e % 2)
                        last = pe.matmul(psA[r:r + TOPK, 0, (e // 2) * D:(e // 2 + 1) * D],
                                         avT[:, e * TOPK:(e + 1) * TOPK], w["out"][:, e, :], start=True, stop=True)
                    last.then_inc(result_done, 1)
                    pe.wait_ge(result_ready, b + 1)
                    for t in range(TB):
                        for a in range(PAIRS):
                            last = pe.matmul(psA[:, 1, t * P:(t + 1) * P], weightedT[:, a, t * P:(t + 1) * P],
                                             result[:, a, :], start=a == 0, stop=a == PAIRS - 1)
                    last.then_inc(out_done, 1)

            @block.vector
            def _(dve):
                dve.wait_ge(rank_ready, 2)
                with dve.Fori(0, B) as b:
                    c = Chain(dve, vec, b * VEC)
                    for t in range(TB):
                        last = dve.tensor_tensor(
                            onehot[:, t, :].rearrange("p (e k) -> p e k", e=E), count_up,
                            rankT[:, t, bass.ds(b * BP, E)].unsqueeze(2).to_broadcast([P, E, TOPK]), ALU.is_equal)
                    last.then_inc(onehot_ready, 1)
                    dve.wait_ge(onehot_ready, b + 1)
                    for t in range(TB):
                        last = dve.tensor_tensor(
                            weighted[:, t, :].rearrange("p (e k) -> p e k", e=E),
                            onehot[:, t, :].rearrange("p (e k) -> p e k", e=E),
                            scoreT[:, t, bass.ds(b * BP, E)].unsqueeze(2).to_broadcast([P, E, TOPK]), ALU.mult)
                    last.then_inc(weighted_ready, 1)
                    dve.wait_ge(rest_ready, b + 1)
                    dve.wait_ge(taken_ready, b * 2 + 2)
                    cos = taken[:, :, D:D + ROT].unsqueeze(2).to_broadcast([P, PAIRS, 2, ROT])
                    sin = taken[:, :, D + ROT:G]
                    for j in range(2):
                        src = psQ[:, :, j * D:j * D + 2 * ROT]
                        dst = qk[:, :, j, 0:2 * ROT]
                        c(dve.tensor_tensor(dst.rearrange("p a (h r) -> p a h r", h=2),
                                            src.rearrange("p a (h r) -> p a h r", h=2), cos, ALU.mult))
                        c(dve.scalar_tensor_tensor(out=part[:, j, :, 0:ROT], in0=src[:, :, ROT:2 * ROT], scalar=-1.0,
                                                   in1=sin, op0=ALU.mult, op1=ALU.mult))
                        c(dve.tensor_tensor(part[:, j, :, ROT:2 * ROT], src[:, :, 0:ROT], sin, ALU.mult))
                        c.wait()
                        dve.tensor_tensor(dst, dst, part[:, j, :, :], ALU.add).then_inc(rot_ready, 1)
                    dve.wait_ge(scores_done, b + 1)
                    c(dve.tensor_reduce(neg_max[:, :], psS[:, :].rearrange("p (a k) -> p a k", a=PAIRS), AX,
                                        ALU.max, negate=True))
                    c.wait()
                    dve.tensor_scalar(neg_max[:, :], neg_max[:, :], SCALE, None, ALU.mult).then_inc(bias_ready, 1)
                    dve.wait_ge(probs_ready, b + 1)
                    c(dve.reciprocal(inv[:, :], sums[:, :]))
                    dve.wait_ge(result_done, b + 1)
                    c.wait()
                    dve.tensor_tensor(result[:, :, :], psA[:, 0, :].rearrange("p (a d) -> p a d", a=PAIRS),
                                      inv[:, :].unsqueeze(2).to_broadcast([P, PAIRS, D]),
                                      ALU.mult).then_inc(result_ready, 1)
                    dve.wait_ge(out_done, b + 1)
                    add_to_stream(dve, core, b, psA[:, 1, :], added)
                    dve.wait_ge(added, b + 1)
                    assert c.n == VEC, c.n


def layer3_ffn(nc, core):
    E, INTER, TOPK, CAP = 64, 96, 8, 32
    T = B * S
    PER = P // CAP
    TILES = E // PER
    ROW = D + E
    TB_BANKS = NT // 4
    with ExitStack() as ctx:
        def sb(name, shape, dt=F32):
            return ctx.enter_context(nc.sbuf_tensor("L3f_" + name, shape, dt))

        def sem(name):
            return core.semaphore(ctx, "L3f_" + name)

        ln = LayerNorm(nc, ctx, "L3f_ln", core)
        w = core.w["L3f"]
        rows = nc.dram_tensor("L3f_rows", (T + 1, ROW), F32, kind="Internal").ap()
        xg = sb("xg", [P, NT, ROW])
        empty = sb("empty", [1, ROW])
        xT = sb("xT", [P, S])
        neg_max = sb("neg_max", [P, TB])
        numer = sb("numer", [P, TB, E])
        best = sb("best", [P, TB, TOPK])
        struck = sb("struck", [P, TB, E])
        denom = sb("denom", [P, TB])
        inv = sb("inv", [P, TB])
        key = sb("key", [P, TB, E])
        keyT = sb("keyT", [E, T])
        first = sb("first", [E, CAP])
        firstT = sb("firstT", [CAP, E])
        token_of = sb("token_of", [P, TILES])
        token_idx = sb("token_idx", [P, TILES], U32)
        taken = sb("taken", [P, TILES * (ROW + PER) + D])
        count = sb("count", [P, T])
        onehot = sb("onehot", [P, 2, T])
        takenT = sb("takenT", [P, P])
        th = sb("th", [P, INTER])
        act_up = sb("act_up", [P, 2, INTER])
        hiddenT = sb("hiddenT", [INTER, P])
        gate_pick = sb("gate_pick", [P, PER])
        gate = sb("gate", [P, TILES])
        y = sb("y", [P, TILES, D])

        (turned, xt_ready, logits_done, max_ready, exp_ready, vec, key_ready, key_turned, kt_ready, rows_ready,
         rows_stored, empty_ready, first_turned, ft_ready, places_done, idx_ready, counted, mark) = (
            sem(n) for n in (
                "turned xt_ready logits_done max_ready exp_ready vec key_ready key_turned kt_ready rows_ready "
                "rows_stored empty_ready first_turned ft_ready places_done idx_ready counted mark").split())
        gathered = [sem(f"gathered{j}") for j in range(TILES)]
        VEC = 12
        MARK = 8

        def taken_row(j):
            return taken[:, j * ROW:(j + 1) * ROW]

        with ExitStack() as routing:
            psT = routing.enter_context(nc.psum_tensor("L3f_psT", [P, S], F32))
            psL = routing.enter_context(nc.psum_tensor("L3f_psL", [P, S], F32))
            psK = routing.enter_context(nc.psum_tensor("L3f_psK", [P, S], F32))
            psF = routing.enter_context(nc.psum_tensor("L3f_psF", [P, S], F32))
            psN = routing.enter_context(nc.psum_tensor("L3f_psN", [P, S], F32))
            with nc.Block() as block:
                @block.sync
                def _(sp):
                    sp.wait_ge(empty_ready, 1)
                    sp.dma_start(rows[T:T + 1, :], empty[:, :]).then_inc(rows_stored, 16)
                    for b in range(B):
                        sp.wait_ge(rows_ready, b + 1)
                        sp.dma_start(rows[b * S:(b + 1) * S, :].rearrange("(t p) g -> p t g", p=P),
                                     xg[:, b * TB:(b + 1) * TB, :]).then_inc(rows_stored, 16)

                @block.gpsimd
                def _(pool):
                    pool.memset(empty[:, :], 0.0).then_inc(empty_ready, 1)
                    pool.iota(onehot[:, 0, :].bitcast(mybir.dt.int32), [[1, T]], base=0,
                              channel_multiplier=0).then_inc(counted, 1)
                    pool.wait_ge(counted, 1)
                    pool.tensor_copy(count[:, :], onehot[:, 0, :].bitcast(mybir.dt.int32)).then_inc(counted, 1)
                    pool.wait_ge(rows_stored, 16 * (B + 1))
                    pool.wait_ge(idx_ready, 1)
                    for j in range(TILES):
                        pool.indirect_dma_start(
                            out=taken_row(j), out_offset=None, in_=rows[:, :],
                            in_offset=bass.IndirectOffsetOnAxis(ap=token_idx[:, j:j + 1], axis=0),
                        ).then_inc(gathered[j], 16)

                @block.scalar
                def _(act):
                    core.wait_weights(act, "L3g")
                    for b in range(B):
                        ln.scalar(act, b)
                        act.wait_ge(turned, b + 1)
                        act.activation(xT[:, :], psT[:, :], ACT.Copy).then_inc(xt_ready, 1)
                        act.wait_ge(max_ready, b + 1)
                        for t in range(TB):
                            last = act.activation(numer[:, t, :], psL[:, t * E:(t + 1) * E], ACT.Exp,
                                                  bias=neg_max[:, t:t + 1])
                        last.then_inc(exp_ready, 1)
                        act.wait_ge(key_turned, b + 1)
                        act.activation(keyT[:, b * S:(b + 1) * S], psK[0:E, :], ACT.Copy).then_inc(kt_ready, 1)

                @block.tensor
                def _(pe):
                    core.wait_weights(pe, "L3g")
                    for b in range(B):
                        for t in range(TB):
                            pe.wait_ge(ln.ready, b * TB + t + 1)
                            last = pe.transpose(psT[:, t * P:(t + 1) * P], xg[:, b * TB + t, 0:D], core.ident)
                        last.then_inc(turned, 1)
                        pe.wait_ge(xt_ready, b + 1)
                        if b >= 1:
                            pe.wait_ge(exp_ready, b)
                        for t in range(TB):
                            last = pe.matmul(psL[:, t * E:(t + 1) * E], xT[:, t * P:(t + 1) * P],
                                             core.w["L3g"]["router"], start=True, stop=True)
                        last.then_inc(logits_done, 1)
                        pe.wait_ge(key_ready, b + 1)
                        if b >= 1:
                            pe.wait_ge(kt_ready, b)
                        for t in range(TB):
                            last = pe.transpose(psK[0:E, t * P:(t + 1) * P], key[:, t, :], core.ident)
                        last.then_inc(key_turned, 1)
                    pe.wait_ge(mark, MARK)
                    pe.transpose(psF[0:CAP, 0:E], first[:, :], core.ident[0:E, 0:E]).then_inc(first_turned, 1)
                    pe.wait_ge(ft_ready, 1)
                    for r in range(PER):
                        last = pe.matmul(psN[r * CAP:(r + 1) * CAP, 0:TILES], core.ident[0:CAP, 0:CAP],
                                         firstT[:, r:E:PER], start=True, stop=True)
                    last.then_inc(places_done, 1)

                @block.vector
                def _(dve):
                    core.wait_weights(dve, "L3g")
                    for b in range(B):
                        ln.vector(dve, b, lambda t: core.X[:, b * TB + t, :], lambda t: xg[:, b * TB + t, 0:D])
                        c = Chain(dve, vec, b * VEC)
                        dve.wait_ge(logits_done, b + 1)
                        if b >= 1:
                            dve.wait_ge(exp_ready, b)
                        dve.tensor_reduce(neg_max[:, :], psL[:, 0:TB * E].rearrange("p (t e) -> p t e", t=TB), AX,
                                          ALU.max, negate=True).then_inc(max_ready, 1)
                        dve.wait_ge(exp_ready, b + 1)
                        for t in range(TB):
                            c(dve.max(best[:, t, :], numer[:, t, :]))
                        c.wait()
                        for t in range(TB):
                            c(dve.match_replace(struck[:, t, :], best[:, t, :], numer[:, t, :], -1.0))
                        c(dve.tensor_reduce(denom[:, :], best[:, :, :], AX, ALU.add))
                        c.wait()
                        c(dve.reciprocal(inv[:, :], denom[:, :]))
                        if b >= 1:
                            dve.wait_ge(key_turned, b)
                        ahead = core.cf[:, C_AHEAD + b * TB:C_AHEAD + (b + 1) * TB]
                        dve.scalar_tensor_tensor(out=key[:, :, :], in0=struck[:, :, :], scalar=-1.0,
                                                 in1=ahead.unsqueeze(2).to_broadcast([P, TB, E]),
                                                 op0=ALU.is_equal, op1=ALU.mult).then_inc(key_ready, 1)
                        gates = xg[:, b * TB:(b + 1) * TB, D:ROW]
                        c(dve.scalar_tensor_tensor(out=gates, in0=struck[:, :, :], scalar=-1.0, in1=numer[:, :, :],
                                                   op0=ALU.is_equal, op1=ALU.mult))
                        c.wait()
                        c(dve.tensor_tensor(gates, gates, inv[:, :].unsqueeze(2).to_broadcast([P, TB, E]), ALU.mult))
                        c.wait()
                        dve.wait_ge(ln.ready, (b + 1) * TB)
                        dve.wait_ge(key_ready, b + 1)
                        dve.memset(neg_max[:, 0:1], 0.0).then_inc(rows_ready, 1)
                        dve.wait_ge(rows_ready, b + 1)
                        assert c.n == VEC, c.n
                    dve.wait_ge(kt_ready, B)
                    c = Chain(dve, mark)
                    for k in range(CAP // 8):
                        c(dve.max(first[:, 8 * k:8 * k + 8], keyT[:, :]))
                        c.wait()
                        if k < CAP // 8 - 1:
                            c(dve.match_replace(keyT[:, :], first[:, 8 * k:8 * k + 8], keyT[:, :], 0.0))
                            c.wait()
                    c(dve.tensor_scalar(first[:, :], first[:, :], -1.0, float(T), ALU.mult, ALU.add))
                    assert c.n == MARK, c.n
                    dve.wait_ge(first_turned, 1)
                    dve.tensor_copy(firstT[:, :], psF[0:CAP, 0:E]).then_inc(ft_ready, 1)
                    dve.wait_ge(places_done, 1)
                    c(dve.tensor_copy(token_of[:, :], psN[:, 0:TILES]))
                    c.wait()
                    dve.tensor_copy(token_idx[:, :], token_of[:, :]).then_inc(idx_ready, 1)

        psC = ctx.enter_context(nc.psum_tensor("L3f_psC", [P, TB_BANKS, S], F32))
        psG, psH, psU, psY = (ctx.enter_context(nc.psum_tensor("L3f_ps" + c, [P, S], F32)) for c in "GHUY")
        (taken_turned, tt_ready, h_done, tanh_ready, steps, hidden_ready, hidden_turned, ht_ready, y_done, gate_ready,
         y_ready, onehot_ready, combined, summed) = (sem(n) for n in (
             "taken_turned tt_ready h_done tanh_ready steps hidden_ready hidden_turned ht_ready y_done gate_ready "
             "y_ready onehot_ready combined summed").split())
        with nc.Block() as block:
            @block.scalar
            def _(act):
                for j in range(TILES):
                    act.wait_ge(taken_turned, j + 1)
                    if j >= 1:
                        act.wait_ge(h_done, j)
                    act.activation(takenT[:, :], psG[:, 0:P], ACT.Copy).then_inc(tt_ready, 1)
                    act.wait_ge(h_done, j + 1)
                    if j >= 1:
                        act.wait_ge(hidden_ready, j)
                    act.activation(th[:, :], psH[:, 0:INTER], ACT.Tanh, scale=0.5).then_inc(tanh_ready, 1)
                    act.wait_ge(hidden_turned, j + 1)
                    if j >= 1:
                        act.wait_ge(y_done, j)
                    act.activation(hiddenT[:, :], psU[0:INTER, 0:P], ACT.Copy).then_inc(ht_ready, 1)

            @block.tensor
            def _(pe):
                core.wait_weights(pe, "L3f")

                def turn_taken(j):
                    pe.wait_ge(gathered[j], 16)
                    if j >= 1:
                        pe.wait_ge(tt_ready, j)
                    pe.transpose(psG[:, 0:P], taken_row(j)[:, 0:D], core.ident).then_inc(taken_turned, 1)

                def combine(j, part):
                    if part == 0:
                        pe.wait_ge(onehot_ready, j + 1)
                        pe.wait_ge(y_ready, j + 1)
                    for t in range(part * 4, part * 4 + 4):
                        last = pe.matmul(psC[:, t // 4, (t % 4) * P:(t % 4 + 1) * P],
                                         onehot[:, j % 2, t * P:(t + 1) * P], y[:, j, :],
                                         start=j == 0 and t % 4 == 0, stop=j == TILES - 1, skip_group_check=True)
                    if part == 3:
                        last.then_inc(combined, 1)

                turn_taken(0)
                for j in range(TILES):
                    pe.wait_ge(tt_ready, j + 1)
                    if j >= 1:
                        pe.wait_ge(hidden_ready, j)
                    for r in range(PER):
                        last = pe.matmul(psH[r * CAP:(r + 1) * CAP, 0:2 * INTER], takenT[:, r * CAP:(r + 1) * CAP],
                                         w["gate_up"][:, j * PER + r, :], start=True, stop=True)
                    last.then_inc(h_done, 1)
                    if j + 1 < TILES:
                        turn_taken(j + 1)
                    if j >= 1:
                        combine(j - 1, 0)
                        combine(j - 1, 1)
                    pe.wait_ge(hidden_ready, j + 1)
                    if j >= 1:
                        pe.wait_ge(ht_ready, j)
                    pe.transpose(psU[0:INTER, 0:P], act_up[:, 1, :], core.ident).then_inc(hidden_turned, 1)
                    if j >= 1:
                        combine(j - 1, 2)
                        combine(j - 1, 3)
                    pe.wait_ge(ht_ready, j + 1)
                    if j >= 1:
                        pe.wait_ge(y_ready, j)
                    for r in range(PER):
                        last = pe.matmul(psY[r * CAP:(r + 1) * CAP, 0:D], hiddenT[:, r * CAP:(r + 1) * CAP],
                                         w["down"][:, j * PER + r, :], start=True, stop=True)
                    last.then_inc(y_done, 1)
                for part in range(4):
                    combine(TILES - 1, part)

            @block.vector
            def _(dve):
                dve.wait_ge(counted, 2)
                c = Chain(dve, steps)
                for j in range(TILES):
                    if j >= 2:
                        dve.wait_ge(combined, j - 1)
                    dve.tensor_scalar(onehot[:, j % 2, :], count[:, :], token_of[:, j:j + 1], None,
                                      ALU.is_equal).then_inc(onehot_ready, 1)
                    dve.wait_ge(gathered[j], 16)
                    if j >= 1:
                        dve.wait_ge(gate_ready, j)
                    c(dve.tensor_tensor(gate_pick[:, :], taken_row(j)[:, D + j * PER:D + (j + 1) * PER],
                                        core.cf[:, C_OWN4:C_OWN4 + PER], ALU.mult))
                    c.wait()
                    dve.tensor_reduce(gate[:, j:j + 1], gate_pick[:, :], AX, ALU.add).then_inc(gate_ready, 1)
                    dve.wait_ge(tanh_ready, j + 1)
                    if j >= 1:
                        dve.wait_ge(hidden_turned, j)
                    c(dve.scalar_tensor_tensor(out=act_up[:, 0, :], in0=th[:, :], scalar=1.0, in1=psH[:, 0:INTER],
                                               op0=ALU.add, op1=ALU.mult))
                    c.wait()
                    dve.scalar_tensor_tensor(out=act_up[:, 1, :], in0=act_up[:, 0, :], scalar=0.5,
                                             in1=psH[:, INTER:2 * INTER], op0=ALU.mult,
                                             op1=ALU.mult).then_inc(hidden_ready, 1)
                    dve.wait_ge(y_done, j + 1)
                    dve.wait_ge(gate_ready, j + 1)
                    dve.tensor_scalar(y[:, j, :], psY[:, 0:D], gate[:, j:j + 1], None, ALU.mult).then_inc(y_ready, 1)
                dve.wait_ge(combined, TILES)
                for k in range(TB_BANKS):
                    xk = core.X[:, k * 4:(k + 1) * 4, :]
                    dve.tensor_tensor(xk, xk, psC[:, k, :].rearrange("p (t d) -> p t d", t=4),
                                      ALU.add).then_inc(summed, 1)
                dve.wait_ge(summed, TB_BANKS)


C_IDENT = 0
C_ONES = C_IDENT + P
C_EPS = C_ONES + P
C_ORDER8 = C_EPS + 1
C_CAUSAL = C_ORDER8 + 8
C_AFTER = C_CAUSAL + P
C_SHIFT = C_AFTER + P
C_OVER = C_SHIFT + P
C_BAND = C_OVER + P
C_PAIR = C_BAND + 192
C_COUNT = C_PAIR + P
C_AHEAD = C_COUNT + 64
C_OWN4 = C_AHEAD + NT
CONST_COLS = C_OWN4 + 4
ARENA = 20480

WEIGHTS = {
    "L0a": [("qk", "L0a_qk", [P, 4, D]), ("v", "L0a_v", [P, D]), ("cos", "L0a_cos", [P, 2, S]),
            ("sin", "L0a_sin", [P, 2, S]), ("pick_q", "L0a_pick_q", [P, 16, 32]), ("pick_k", "L0a_pick_k", [P, 16, 112]),
            ("causal_t", "L0a_causal_t", [P, P]), ("o", "L0a_o", [P, D])],
    "L0f": [("wqkv", "L0f_wqkv", [P, 2, 3, 512]), ("wo", "L0f_wo", [P, 2, 4, D]), ("w1", "L0f_w1", [P, 2, 682]),
            ("w2", "L0f_w2", [P, 2, 3, D]), ("ln", "L0f_ln", [P, 4]), ("b1", "L0f_b1", [P, 12]),
            ("b2", "L0f_b2", [1, 2, D]), ("pos", "L0f_pos", [P, 2, 2, 256]), ("scales", "L0f_scales", [P, 8, 64])],
    "L1a": [("qkv", "L1a_qkv", [P, 8, 6, D]), ("out", "L1a_out", [P, 8, D])],
    "L1f": [("router", "L1f_router", [P, 8]), ("router_b", "L1f_router_b", [1, 8]),
            ("W1", "L1f_W1", [P, 8, 512]), ("W2", "L1f_W2", [P, 8, 4, D]), ("b1", "L1f_b1", [P, 32]),
            ("b2", "L1f_b2", [8, D])],
    "L2a": [("cols", "L2a_cols", [P, 2]), ("mix", "L2a_mix", [P, 3]), ("kvr", "L2a_kvr", [P, 3, D]),
            ("out", "L2a_out", [P, D])],
    "L2f": [("router", "L2f_router", [P, 8]), ("angles", "L2f_angles", [P, 4, 64]),
            ("qkv", "L2f_qkv", [P, 8, 384]), ("out", "L2f_out", [P, 8, D])],
    "L3a": [("cols", "L3a_cols", [P, 4]), ("in", "L3a_in", [P, 256]), ("A", "L3a_A", [P, 2, 16]),
            ("B", "L3a_B", [P, 2, 16]), ("C", "L3a_C", [16, 256]), ("out", "L3a_out", [P, 2, D]),
            ("b_out", "L3a_b_out", [1, D])],
    "L3g": [("router", "L3g_router", [P, 64])],
    "L3f": [("gate_up", "L3f_gate_up", [P, 64, 192]), ("down", "L3f_down", [96, 64, D])],
}
PROBS_COLS = 6 * 1280
IN_ARENA = {("L0a", "pick_k"): PROBS_COLS, ("L0a", "pick_q"): PROBS_COLS + 16 * 112,
            ("L0a", "causal_t"): PROBS_COLS + 16 * 144, ("L3f", "gate_up"): 0, ("L3f", "down"): 12288, ("L0f", "wqkv"): 15360, ("L0f", "w1"): 15360 + 3072, ("L1a", "qkv"): 0, ("L1a", "out"): 6144, ("L1f", "W1"): 7168, ("L1f", "W2"): 7168 + 4096}


EARLY = ("L0a", "L0f")


def place_weights(nc, ctx, core, stages):
    for stage in stages:
        parts = WEIGHTS[stage]
        core.w[stage] = {}
        for key, _, shape in parts:
            if (stage, key) in IN_ARENA:
                at, n = IN_ARENA[stage, key], 1
                for k in shape[1:]:
                    n *= k
                flat = core.arena[0:shape[0], at:at + n]
                core.w[stage][key] = flat if len(shape) == 2 else flat.rearrange(
                    "p (a b) -> p a b", a=shape[1]) if len(shape) == 3 else flat.rearrange(
                    "p (a b c) -> p a b c", a=shape[1], b=shape[2])
            else:
                t = ctx.enter_context(nc.sbuf_tensor(f"w_{stage}_{key}", shape, F32))
                core.w[stage][key] = t[:, :] if len(shape) == 2 else t[:, :, :] if len(shape) == 3 else t[:, :, :, :]


def load_weights(core, sp):
    for stage, parts in WEIGHTS.items():
        if stage in ("L1a", "L1f", "L3f"):
            continue
        for key, name, _ in parts:
            core.load(sp, stage, core.w[stage][key], core.dram[name])


def load_layer1_weights(core, sp):
    for stage in ("L1a", "L1f"):
        for key, name, _ in WEIGHTS[stage]:
            core.load(sp, stage, core.w[stage][key], core.dram[name])


def load_late_weights(core, sp):
    for lo in range(0, 64, 16):
        core.load(sp, "L3f", core.w["L3f"]["gate_up"][:, lo:lo + 16, :], core.dram["L3f_gate_up"][:, lo:lo + 16, :])
        core.load(sp, "L3f", core.w["L3f"]["down"][:, lo:lo + 16, :], core.dram["L3f_down"][:, lo:lo + 16, :])


LAYERS = {0: layer0_attn, 1: layer0_ffn, 2: layer1_attn, 3: layer1_ffn, 4: layer2_attn, 5: layer2_ffn,
          6: layer3_attn, 7: layer3_ffn}
STAGES = (0, 1, 2, 3, 4, 5, 6, 7)


def program(nc, dram, out):
    x_dram = dram["x"].rearrange("b (t p) d -> p (b t) d", p=P)
    out_dram = out.rearrange("b (t p) d -> p (b t) d", p=P)
    with ExitStack() as ctx:
        core = Core(nc, ctx, dram)
        ident_ready = ctx.enter_context(nc.semaphore("ident_ready"))
        place_weights(nc, ctx, core, [stage for stage in WEIGHTS if stage not in EARLY])
        with ExitStack() as early:
            place_weights(nc, early, core, ["L0f"])
            earliest = early.enter_context(ExitStack())
            place_weights(nc, earliest, core, ["L0a"])
            with nc.Block() as block:
                @block.sync
                def _(sp):
                    sp.dma_start(core.cf[:, :], dram["consts"]).then_inc(core.const_loaded, 16)
                    sp.dma_start(core.X[:, :, :], x_dram).then_inc(core.x_loaded, 16)
                    load_weights(core, sp)

                @block.vector
                def _(dve):
                    dve.wait_ge(core.const_loaded, 16)
                    dve.wait_ge(core.x_loaded, 16)
                    dve.tensor_copy(core.identb[:, :], core.ident).then_inc(ident_ready, 1)
                    dve.tensor_copy(core.band[:, :], core.cf[:, C_BAND:C_BAND + 64 + P]).then_inc(ident_ready, 1)
                    dve.tensor_copy(core.pair_mask[:, :], core.cf[:, C_PAIR:C_PAIR + P]).then_inc(ident_ready, 1)
                    dve.tensor_copy(core.causal[:, :], core.cf[:, C_CAUSAL:C_CAUSAL + P]).then_inc(ident_ready, 1)

                @block.scalar
                def _(act):
                    act.wait_ge(core.const_loaded, 16)

                @block.tensor
                def _(pe):
                    pe.wait_ge(core.const_loaded, 16)
                    pe.wait_ge(ident_ready, 4)
            if 0 in STAGES:
                layer0_attn(nc, core)
                core.retire()
            elif 1 in STAGES:
                with nc.Block() as block:
                    @block.sync
                    def _(sp):
                        core.wait_weights(sp, "L0a")
            earliest.close()
            if 1 in STAGES:
                layer0_ffn(nc, core)
                core.retire()
            if 1 not in STAGES and set(STAGES) & {2, 3, 7}:
                with nc.Block() as block:
                    @block.sync
                    def _(sp):
                        load_layer1_weights(core, sp)
            if not set(STAGES) >= {0, 1}:
                with nc.Block() as block:
                    @block.sync
                    def _(sp):
                        for stage in EARLY:
                            core.wait_weights(sp, stage)
        if 7 in STAGES and 4 not in STAGES:
            with nc.Block() as block:
                @block.sync
                def _(sp):
                    for stage in ("L1a", "L1f", "L0f"):
                        core.wait_weights(sp, stage)
                    load_late_weights(core, sp)
        for n in STAGES:
            if n >= 2:
                LAYERS[n](nc, core)
                if n != STAGES[-1]:
                    core.retire()
        with nc.Block() as block:
            @block.sync
            def _(sp):
                sp.dma_start(out_dram, core.X[:, :, :]).then_inc(core.stored, 16)
                sp.wait_ge(core.stored, 16)
                for stage in core.loaded:
                    core.wait_weights(sp, stage)


def lay_out(a):
    import numpy as np
    c = np.ascontiguousarray
    w = {"x": a["L0_attn_x"]}
    consts = np.zeros((P, CONST_COLS), np.float32)
    consts[:, C_IDENT:C_IDENT + P] = np.eye(P)
    consts[:, C_ONES:C_ONES + P] = 1.0
    consts[:, C_EPS] = EPS
    consts[:, C_ORDER8:C_ORDER8 + 8] = 8 - np.arange(8)
    q_at, k_at = np.arange(P)[:, None], np.arange(P)[None, :]
    consts[:, C_CAUSAL:C_CAUSAL + P] = np.where(k_at > q_at, np.float32(NEG), 0)
    consts[:, C_AFTER:C_AFTER + P] = np.where(q_at > k_at, 0.5, 0)
    consts[:, C_SHIFT:C_SHIFT + P] = k_at == q_at + 1
    consts[P - 1, C_OVER] = 1.0
    key = np.arange(192)[None, :] - 64
    consts[:, C_BAND:C_BAND + 192] = np.where((key > q_at) | (key < q_at - 64), np.float32(NEG), 0)
    own = (q_at // 64 == k_at // 64) & (k_at <= q_at)
    consts[:, C_PAIR:C_PAIR + P] = np.where(own, 0, np.float32(NEG))
    consts[:, C_COUNT:C_COUNT + 64] = np.arange(1, 65)
    consts[:, C_AHEAD:C_AHEAD + NT] = NT * P - (np.arange(NT)[None, :] * P + q_at)
    consts[:, C_OWN4:C_OWN4 + 4] = q_at // 32 == np.arange(4)[None, :]
    w["consts"] = consts
    swap = np.arange(D) ^ 1
    w["L0a_qk"] = np.stack([a["L0_attn_wq"], a["L0_attn_wq"][:, swap], a["L0_attn_wk"], a["L0_attn_wk"][:, swap]], 1)
    w["L0a_v"] = a["L0_attn_wv"]
    w["L0a_o"] = a["L0_attn_wo"]
    dh = 8
    inv_freq = (1.0 / np.float32(10000.0) ** (np.arange(0, dh, 2, dtype=np.float32) / np.float32(dh))).astype(np.float32)
    angle = (np.arange(S, dtype=np.float32)[None, :] * inv_freq[(np.arange(D) % dh) // 2][:, None]).astype(np.float32)
    sign = np.where(np.arange(D) % 2, 1, -1)[:, None]
    scale = dh ** -0.5
    cos, sin = np.cos(angle.astype(np.float64)), np.sin(angle.astype(np.float64)) * sign
    w["L0a_cos"] = np.stack([cos * scale, cos], 1).astype(np.float32)
    w["L0a_sin"] = np.stack([sin * scale, sin], 1).astype(np.float32)
    row, head = np.arange(P)[:, None, None], np.arange(16)[None, :, None]
    col = np.arange(32)[None, None, :]
    w["L0a_pick_q"] = ((row // dh == head) & (row % dh == col % dh) & (col < 24)).astype(np.float32)
    col = np.arange(112)[None, None, :] - 16
    w["L0a_pick_k"] = ((row // dh == head) & (row % dh == col % 32) & (col >= 0)).astype(np.float32)
    w["L0a_causal_t"] = consts[:, C_CAUSAL:C_CAUSAL + P].T
    w["L0f_wqkv"] = a["L0_ffn_wqkv"].reshape(2, D, 3, 512).transpose(1, 0, 2, 3)
    w["L0f_wo"] = a["L0_ffn_wo"].reshape(2, 4, P, D).transpose(2, 0, 1, 3)
    w["L0f_w1"] = a["L0_ffn_w1"].transpose(1, 0, 2)
    hid, pad = 341, 3 * P - 341
    w["L0f_w2"] = np.pad(a["L0_ffn_w2"], ((0, 0), (0, pad), (0, 0))).reshape(2, 3, P, D).transpose(2, 0, 1, 3)
    w["L0f_ln"] = np.stack([a["L0_ffn_ln_g"][0], a["L0_ffn_ln_b"][0], a["L0_ffn_ln_g"][1], a["L0_ffn_ln_b"][1]], 1)
    w["L0f_b1"] = np.pad(a["L0_ffn_b1"].reshape(2, 2, hid), ((0, 0), (0, 0), (0, pad))).reshape(12, P).T
    w["L0f_b2"] = a["L0_ffn_b2"].reshape(1, 2, D)
    half = np.arange(0, 64, 2, dtype=np.float32)
    inv_freq = (1.0 / np.float32(10000.0) ** (half / np.float32(64))).astype(np.float32)
    t = np.arange(S, dtype=np.float32)
    freqs = (t[:, None] * inv_freq[None, :]).astype(np.float32).astype(np.float64)
    base = (half.astype(np.float64) + 0.4 * 64) / (1.4 * 64)
    xpos = base[None, :] ** ((t[:, None] - S // 2) / 32.0)
    pos = np.zeros((2, 2, S, 64))
    for j, sc in enumerate((xpos, 1.0 / xpos)):
        pos[j, 0] = np.concatenate([np.cos(freqs) * sc] * 2, -1)
        pos[j, 1] = np.concatenate([-np.sin(freqs) * sc, np.sin(freqs) * sc], -1)
    w["L0f_pos"] = pos.reshape(2, 2, TB, P, 64).transpose(3, 0, 1, 2, 4).reshape(P, 2, 2, 256).astype(np.float32)
    other = (np.arange(64) + 32) % 64
    qs, ks = a["L0_ffn_q_scale"], a["L0_ffn_k_scale"]
    scales = np.stack([qs, qs[:, other], ks, ks[:, other]], 1).reshape(1, 8, 64)
    w["L0f_scales"] = np.broadcast_to(scales, (P, 8, 64))
    w["L1a_qkv"] = a["L1_attn_w_qkv"].reshape(D, 6, 8, D).transpose(0, 2, 1, 3)
    w["L1a_out"] = a["L1_attn_w_out"].reshape(8, D, D).transpose(1, 0, 2)
    w["L1f_router"] = a["L1_ffn_router_w"]
    w["L1f_router_b"] = a["L1_ffn_router_b"].reshape(1, 8)
    w["L1f_W1"] = a["L1_ffn_W1"].transpose(1, 0, 2)
    w["L1f_W2"] = a["L1_ffn_W2"].reshape(8, 4, P, D).transpose(2, 0, 1, 3)
    w["L1f_b1"] = a["L1_ffn_b1"].reshape(32, P).T
    w["L1f_b2"] = a["L1_ffn_b2"]
    w["L2a_cols"] = np.stack([a["L2_attn_time_decay"], a["L2_attn_time_first"]], 1)
    w["L2a_mix"] = np.stack([a["L2_attn_time_mix_" + n].reshape(D) for n in "kvr"], 1)
    w["L2a_kvr"] = np.stack([a["L2_attn_W" + n].T for n in "kvr"], 1)
    w["L2a_out"] = a["L2_attn_Wo"].T
    w["L2f_router"] = a["L2_ffn_Wr"].T
    inv_freq = (1.0 / np.float32(10000.0) ** (np.arange(32, dtype=np.float32) * np.float32(2.0) / np.float32(64)))
    ang = (np.arange(S, dtype=np.float32)[:, None] * inv_freq.astype(np.float32)).astype(np.float32).astype(np.float64)
    angles = np.concatenate([np.cos(ang), np.sin(ang)], 1).astype(np.float32)
    w["L2f_angles"] = angles.reshape(TB, P, 64).transpose(1, 0, 2)
    w["L2f_qkv"] = a["L2_ffn_Wqkv"].transpose(1, 0, 2)
    w["L2f_out"] = a["L2_ffn_Wo"].transpose(1, 0, 2)
    w["L3a_cols"] = np.concatenate([np.stack([a["L3_attn_norm_w"], a["L3_attn_norm_b"]], 1),
                                    a["L3_attn_b_in"].reshape(2, P).T], 1)
    w["L3a_in"] = a["L3_attn_W_in"].T
    w["L3a_A"] = a["L3_attn_A"].reshape(2, P, 16).transpose(1, 0, 2)
    w["L3a_B"] = a["L3_attn_B_ssm"].reshape(2, P, 16).transpose(1, 0, 2)
    w["L3a_C"] = a["L3_attn_C_ssm"].T
    w["L3a_out"] = a["L3_attn_W_out"].T.reshape(2, P, D).transpose(1, 0, 2)
    w["L3a_b_out"] = a["L3_attn_b_out"].reshape(1, D)
    w["L3g_router"] = a["L3_ffn_gate_w"].T
    w["L3f_gate_up"] = np.concatenate([a["L3_ffn_w_gate"], a["L3_ffn_w_up"]], 1).transpose(2, 0, 1)
    w["L3f_down"] = a["L3_ffn_w_down"].transpose(2, 0, 1)
    return {k: c(v) for k, v in w.items()}


def kernel(**inputs):
    import numpy as np
    import concourse.bacc as bacc
    from concourse.bass_utils import run_bass_kernel_spmd

    nc = bacc.Bacc("TRN2", target_bir_lowering=False, num_devices=1)
    arrays = lay_out({k: np.asarray(v) for k, v in inputs.items()})
    dram = {k: nc.dram_tensor("in_" + k, v.shape, mybir.dt.from_np(v.dtype), kind="ExternalInput").ap()
            for k, v in arrays.items()}
    out = nc.dram_tensor("out", (B, S, D), F32, kind="ExternalOutput").ap()
    program(nc, dram, out)
    result = run_bass_kernel_spmd(nc, [{"in_" + k: v for k, v in arrays.items()}], core_ids=[0])
    return result.results[0]["out"]
```

```python
from contextlib import ExitStack

import concourse.bass as bass
from concourse import mybir
from concourse.alu_op_type import AluOpType as ALU

ACT = mybir.ActivationFunctionType
AX = mybir.AxisListType.X
F32 = mybir.dt.float32
BF16 = mybir.dt.bfloat16
U32 = mybir.dt.uint32

P = 128
B, S, D = 4, 512, 128
TB = S // P
NT = B * TB
EPS = 1e-5
NEG = -1e30


class Chain:

    def __init__(self, eng, sem, base=0):
        self.eng, self.sem, self.base, self.n = eng, sem, base, 0

    def __call__(self, ins):
        self.n += 1
        return ins.then_inc(self.sem, 1)

    def wait(self, back=0):
        self.eng.wait_ge(self.sem, self.base + self.n - back)


class LayerNorm:
    STEPS = 2 * TB + 5

    def __init__(self, nc, ctx, name, core):
        sb = nc.sbuf_tensor
        self.eps = core.eps
        self.stats = ctx.enter_context(sb(name + "_stats", [P, TB, 6], F32))
        self.mv = ctx.enter_context(sb(name + "_meanvar", [P, TB, 2], F32))
        self.root = ctx.enter_context(sb(name + "_root", [P, TB], F32))
        self.guess = ctx.enter_context(sb(name + "_guess", [P, TB], F32))
        self.corr = ctx.enter_context(sb(name + "_corr", [P, TB], F32))
        self.rstd = ctx.enter_context(sb(name + "_rstd", [P, TB], F32))
        self.step = core.semaphore(ctx, name + "_step")
        self.rooted = core.semaphore(ctx, name + "_rooted")
        self.ready = core.semaphore(ctx, name + "_ready")

    def vector(self, dve, n, src, dst):
        self.statistics(dve, n, src)
        self.finish(dve, n, src, dst)

    def statistics(self, dve, n, src):
        step = Chain(dve, self.step, n * self.STEPS)
        for t in range(TB):
            step(dve.bn_stats(self.stats[:, t, :], src(t)))
        step.wait()
        dve.memset(self.corr[:, 0:1], 0.0)
        for t in range(TB):
            step(dve.bn_aggr(self.mv[:, t, :], self.stats[:, t, :]))

    def finish(self, dve, n, src, dst):
        step = Chain(dve, self.step, n * self.STEPS + 2 * TB)
        dve.wait_ge(self.rooted, n + 1)
        step(dve.reciprocal(self.guess[:, :], self.root[:, :]))
        step.wait()
        step(dve.tensor_tensor(self.corr[:, :], self.guess[:, :], self.guess[:, :], ALU.mult))
        step.wait()
        step(dve.scalar_tensor_tensor(out=self.corr[:, :], in0=self.mv[:, :, 1], scalar=EPS, in1=self.corr[:, :],
                                      op0=ALU.add, op1=ALU.mult))
        step.wait()
        step(dve.tensor_scalar(self.corr[:, :], self.corr[:, :], -0.5, 1.5, ALU.mult, ALU.add))
        step.wait()
        step(dve.tensor_tensor(self.rstd[:, :], self.corr[:, :], self.guess[:, :], ALU.mult))
        step.wait()
        assert step.n == self.STEPS - 2 * TB
        for t in range(TB):
            dve.tensor_scalar(dst(t), src(t), self.mv[:, t, 0:1], self.rstd[:, t:t + 1],
                              ALU.subtract, ALU.mult).then_inc(self.ready, 1)

    def scalar(self, act, n):
        act.wait_ge(self.step, n * self.STEPS + 2 * TB)
        act.activation(self.root[:, :], self.mv[:, :, 1], ACT.Sqrt, bias=self.eps).then_inc(self.rooted, 1)


class Core:

    def __init__(self, nc, ctx, dram):
        self.nc, self.dram, self.w = nc, dram, {}

        def sb(name, shape, dt=F32):
            return ctx.enter_context(nc.sbuf_tensor(name, shape, dt))

        self.sb = sb
        self.X = sb("X", [P, NT + TB, D])
        self.cf = sb("const_f32", [P, CONST_COLS])
        self.ident = self.cf[:, C_IDENT:C_IDENT + P]
        self.eps = self.cf[:, C_EPS:C_EPS + 1]
        self.ones_row = self.cf[0:1, C_ONES:C_ONES + P]
        self.identb = sb("ident_bf16", [P, P], BF16)
        self.causal = sb("causal_bf16", [P, P], BF16)
        self.band = sb("band_bf16", [P, 64 + P], BF16)
        self.pair_mask = sb("pair_mask_bf16", [P, P], BF16)
        self.arena = sb("arena", [P, ARENA])
        self.x_loaded = ctx.enter_context(nc.semaphore("x_loaded"))
        self.const_loaded = ctx.enter_context(nc.semaphore("const_loaded"))
        self.stored = ctx.enter_context(nc.semaphore("stored"))
        self.n_loads = {}
        self.of_layer = []
        self.loaded = {}
        self.ctx = ctx

    def semaphore(self, ctx, name):
        sem = ctx.enter_context(self.nc.semaphore(name))
        self.of_layer.append(sem)
        return sem

    def retire(self):
        sems, self.of_layer = self.of_layer, []
        with self.nc.Block() as block:
            @block.gpsimd
            def _(pool):
                for sem in sems:
                    pool.sem_clear(sem)

    def load(self, eng, stage, dst, src):
        if stage not in self.loaded:
            self.loaded[stage] = self.ctx.enter_context(self.nc.semaphore(f"{stage}_weights"))
            self.n_loads[stage] = 0
        self.n_loads[stage] += 16
        eng.dma_start(dst, src).then_inc(self.loaded[stage], 16)

    def wait_weights(self, eng, stage):
        eng.wait_ge(self.loaded[stage], self.n_loads[stage])


def turn(pe, core, ln, n, xn, ps, turned):
    for t in range(TB):
        pe.wait_ge(ln.ready, n * TB + t + 1)
        last = pe.transpose(ps[:, t * P:(t + 1) * P], xn[:, t, :], core.ident)
    last.then_inc(turned, 1)


def add_to_stream(dve, core, b, ps, done):
    x = core.X[:, bass.ds(b * TB, TB), :]
    dve.tensor_tensor(x, x, ps.rearrange("p (t d) -> p t d", t=TB), ALU.add).then_inc(done, 1)


def layer2_attn(nc, core):
    with ExitStack() as ctx:
        def sb(name, shape, dt=F32):
            return ctx.enter_context(nc.sbuf_tensor("L2a_" + name, shape, dt))

        def sem(name):
            return core.semaphore(ctx, "L2a_" + name)

        ln = LayerNorm(nc, ctx, "L2a_ln", core)
        w = core.w["L2a"]
        xn = sb("xn", [P, TB, D])
        xT = sb("xT", [P, S + 1])
        mixed = sb("mixed", [P, 3, S])
        one_less_mix = sb("one_less_mix", [P, 3])
        neg_decay = sb("neg_decay", [P, 1])
        decay_row = sb("decay_row", [P, S])
        top = sb("top", [P, S + 1])
        num = sb("num", [P, S + 1])
        den = sb("den", [P, S + 1])
        ww = sb("ww", [P, S])
        peak = sb("peak", [P, S])
        diff = sb("diff", [P, 4, S])
        gate = sb("gate", [P, S])
        tmp = sb("tmp", [P, S])
        out_num = sb("out_num", [P, S])
        out_den = sb("out_den", [P, S])
        res = sb("res", [P, S])
        psT = ctx.enter_context(nc.psum_tensor("L2a_psT", [P, S], F32))
        psY = ctx.enter_context(nc.psum_tensor("L2a_psY", [P, S], F32))
        psK, psV, psR = (ctx.enter_context(nc.psum_tensor("L2a_ps" + c, [P, S], F32)) for c in "KVR")
        setup, exp_decay, mixing, banks_used = sem("setup"), sem("exp_decay"), sem("mixing"), sem("banks_used")
        turned, xt_ready, mixed_ready, projected = sem("turned"), sem("xt_ready"), sem("mixed_ready"), sem("projected")
        vec, diffs_ready, exps_ready, res_ready, y_ready, added = (
            sem("vec"), sem("diffs_ready"), sem("exps_ready"), sem("res_ready"), sem("y_ready"), sem("added"))
        VEC = 13
        SETUP = 7
        mix_of, first = w["mix"], w["cols"][:, 1:2]
        with nc.Block() as block:
            @block.sync
            def _(sp):
                load_late_weights(core, sp)

            @block.scalar
            def _(act):
                core.wait_weights(act, "L2a")
                act.activation(neg_decay[:, :], w["cols"][:, 0:1], ACT.Exp).then_inc(exp_decay, 1)

                def copy_tokens(b):
                    act.wait_ge(turned, b + 1)
                    act.activation(xT[:, 1:S + 1], psT[:, :], ACT.Copy).then_inc(xt_ready, 1)

                ln.scalar(act, 0)
                copy_tokens(0)
                with act.Fori(0, B) as b:
                    act.wait_ge(projected, b + 1)
                    act.activation(gate[:, :], psR[:, :], ACT.Exp, scale=-1.0).then_inc(exps_ready, 1)
                    for j in range(4):
                        act.wait_ge(diffs_ready, b * 4 + j + 1)
                        act.activation(diff[:, j, :], diff[:, j, :], ACT.Exp).then_inc(exps_ready, 1)
                    ln.scalar(act, b + 1)
                    copy_tokens(b + 1)

            @block.tensor
            def _(pe):
                core.wait_weights(pe, "L2a")

                def project(b):
                    pe.wait_ge(mixed_ready, b + 1)
                    for j, ps in enumerate((psK, psV, psR)):
                        last = pe.matmul(ps[:, :], w["kvr"][:, j, :], mixed[:, j, :], start=True, stop=True)
                    last.then_inc(projected, 1)

                turn(pe, core, ln, 0, xn, psT, turned)
                project(0)
                with pe.Fori(0, B) as b:
                    turn(pe, core, ln, b + 1, xn, psT, turned)
                    pe.wait_ge(banks_used, b + 1)
                    pe.wait_ge(exps_ready, b * 5 + 1)
                    project(b + 1)
                    pe.wait_ge(res_ready, b + 1)
                    for t in range(TB):
                        last = pe.matmul(psY[:, t * P:(t + 1) * P], res[:, t * P:(t + 1) * P], w["out"][:, :],
                                         start=True, stop=True)
                    last.then_inc(y_ready, 1)

            @block.vector
            def _(dve):
                core.wait_weights(dve, "L2a")
                c = Chain(dve, setup)
                c(dve.memset(xT[:, 0:1], 0.0))
                c(dve.memset(top[:, 0:1], -1e30))
                c(dve.memset(num[:, 0:1], 0.0))
                c(dve.memset(den[:, 0:1], 0.0))
                c(dve.memset(decay_row[:, :], 0.0))
                c(dve.tensor_scalar(one_less_mix[:, :], mix_of, -1.0, 1.0, ALU.mult, ALU.add))
                dve.wait_ge(exp_decay, 1)
                c.wait()
                c(dve.tensor_scalar(decay_row[:, :], decay_row[:, :], neg_decay[:, 0:1], None, ALU.subtract))
                c.wait()
                assert c.n == SETUP

                def mix(b):
                    c = Chain(dve, mixing, b * 5)
                    dve.wait_ge(xt_ready, b + 1)
                    for j in range(3):
                        c(dve.tensor_scalar(mixed[:, j, :], xT[:, 0:S], one_less_mix[:, j:j + 1], None, ALU.mult))
                    for j in range(3):
                        c.wait(2)
                        last = dve.scalar_tensor_tensor(out=mixed[:, j, :], in0=xT[:, 1:S + 1], scalar=mix_of[:, j:j + 1],
                                                        in1=mixed[:, j, :], op0=ALU.mult, op1=ALU.add)
                        c(last) if j < 2 else last.then_inc(mixed_ready, 1)
                    assert c.n == 5

                ln.vector(dve, 0, lambda t: core.X[:, t, :], lambda t: xn[:, t, :])
                mix(0)
                with dve.Fori(0, B) as b:
                    def next_tokens(t):
                        return core.X[:, b * TB + TB + t, :]

                    c = Chain(dve, vec, b * VEC)
                    dve.wait_ge(projected, b + 1)
                    c(dve.tensor_tensor_scan(top[:, 1:S + 1], decay_row[:, :], psK[:, :], -1e30, ALU.add, ALU.max))
                    c.wait()
                    dve.tensor_tensor(diff[:, 0, :], psK[:, :], top[:, 1:S + 1], ALU.subtract).then_inc(diffs_ready, 1)
                    c(dve.tensor_tensor(tmp[:, :], top[:, 0:S], decay_row[:, :], ALU.add))
                    c.wait()
                    dve.tensor_tensor(diff[:, 1, :], tmp[:, :], top[:, 1:S + 1], ALU.subtract).then_inc(diffs_ready, 1)
                    c(dve.tensor_scalar(ww[:, :], psK[:, :], first, None, ALU.add))
                    c.wait()
                    c(dve.tensor_tensor(peak[:, :], ww[:, :], top[:, 0:S], ALU.max))
                    c.wait()
                    dve.tensor_tensor(diff[:, 2, :], top[:, 0:S], peak[:, :], ALU.subtract).then_inc(diffs_ready, 1)
                    dve.tensor_tensor(diff[:, 3, :], ww[:, :], peak[:, :], ALU.subtract).then_inc(diffs_ready, 1)
                    ln.statistics(dve, b + 1, next_tokens)
                    dve.wait_ge(exps_ready, b * 5 + 2)
                    c(dve.tensor_tensor(tmp[:, :], diff[:, 0, :], psV[:, :], ALU.mult))
                    dve.wait_ge(exps_ready, b * 5 + 3)
                    c.wait()
                    c(dve.tensor_tensor_scan(num[:, 1:S + 1], diff[:, 1, :], tmp[:, :], 0.0, ALU.mult, ALU.add))
                    c(dve.tensor_tensor_scan(den[:, 1:S + 1], diff[:, 1, :], diff[:, 0, :], 0.0, ALU.mult, ALU.add))
                    dve.wait_ge(exps_ready, b * 5 + 5)
                    ln.finish(dve, b + 1, next_tokens, lambda t: xn[:, t, :])
                    dve.tensor_tensor(out_num[:, :], diff[:, 3, :], psV[:, :], ALU.mult).then_inc(banks_used, 1)
                    c.wait()
                    c(dve.tensor_tensor(tmp[:, :], diff[:, 2, :], num[:, 0:S], ALU.mult))
                    c(dve.tensor_tensor(out_den[:, :], diff[:, 2, :], den[:, 0:S], ALU.mult))
                    c.wait()
                    dve.wait_ge(banks_used, b + 1)
                    c(dve.tensor_tensor(out_num[:, :], out_num[:, :], tmp[:, :], ALU.add))
                    c(dve.tensor_tensor(out_den[:, :], out_den[:, :], diff[:, 3, :], ALU.add))
                    c.wait()
                    c(dve.scalar_tensor_tensor(out=out_den[:, :], in0=gate[:, :], scalar=1.0, in1=out_den[:, :],
                                               op0=ALU.add, op1=ALU.mult))
                    c.wait()
                    mix(b + 1)
                    c(dve.reciprocal(out_den[:, :], out_den[:, :]))
                    c.wait()
                    dve.tensor_tensor(res[:, :], out_num[:, :], out_den[:, :], ALU.mult).then_inc(res_ready, 1)
                    dve.wait_ge(y_ready, b + 1)
                    add_to_stream(dve, core, b, psY[:, :], added)
                    dve.wait_ge(added, b + 1)
                    assert c.n == VEC, c.n


def layer3_attn(nc, core):
    NS, CH = 16, 2
    with ExitStack() as ctx:
        def sb(name, shape, dt=F32):
            return ctx.enter_context(nc.sbuf_tensor("L3a_" + name, shape, dt))

        def sem(name):
            return core.semaphore(ctx, "L3a_" + name)

        ln = LayerNorm(nc, ctx, "L3a_ln", core)
        w = core.w["L3a"]
        xo = sb("xo", [P, TB, D])
        xn = sb("xn", [P, TB, D])
        xT = sb("xT", [P, S])
        hT = sb("hT", [P, CH, S])
        decay = sb("decay", [NS, S])
        drive = sb("drive", [NS, S])
        states = sb("states", [NS, S])
        yT = sb("yT", [P, CH, S])
        psT, psA, psU, psY = (ctx.enter_context(nc.psum_tensor("L3a_ps" + c, [P, S], F32)) for c in "TAUY")
        psH = ctx.enter_context(nc.psum_tensor("L3a_psH", [P, CH, S], F32))
        turned, xt_ready, h_done, h_ready, au_done, exp_ready = (
            sem(n) for n in ("turned", "xt_ready", "h_done", "h_ready", "au_done", "exp_ready"))
        vec, states_ready, yt_done, yt_ready, out_done, added = (
            sem(n) for n in ("vec", "states_ready", "yt_done", "yt_ready", "out_done", "added"))
        VEC = 3
        nw, nb = w["cols"][:, 0:1], w["cols"][:, 1:2]
        with nc.Block() as block:
            @block.scalar
            def _(act):
                core.wait_weights(act, "L3a")
                with act.Fori(0, B) as b:
                    ln.scalar(act, b * 2)
                    ln.scalar(act, b * 2 + 1)
                    act.wait_ge(turned, b + 1)
                    act.activation(xT[:, :], psT[:, :], ACT.Identity, bias=nb, scale=nw).then_inc(xt_ready, 1)
                    for c in range(CH):
                        act.wait_ge(h_done, b * CH + c + 1)
                        act.activation(hT[:, c, :], psH[:, c, :], ACT.Identity,
                                       bias=w["cols"][:, 2 + c:3 + c]).then_inc(h_ready, 1)
                    act.wait_ge(au_done, b + 1)
                    act.activation(decay[:, :], psA[0:NS, :], ACT.Exp, scale=-1.0).then_inc(exp_ready, 1)
                    act.activation(drive[:, :], psU[0:NS, :], ACT.Copy).then_inc(exp_ready, 1)
                    for c in range(CH):
                        act.wait_ge(yt_done, b * CH + c + 1)
                        act.activation(yT[:, c, :], psH[:, c, :], ACT.Copy).then_inc(yt_ready, 1)

            @block.tensor
            def _(pe):
                core.wait_weights(pe, "L3a")
                with pe.Fori(0, B) as b:
                    for t in range(TB):
                        pe.wait_ge(ln.ready, b * 2 * TB + TB + t + 1)
                        last = pe.transpose(psT[:, t * P:(t + 1) * P], xn[:, t, :], core.ident)
                    last.then_inc(turned, 1)
                    pe.wait_ge(xt_ready, b + 1)
                    for c in range(CH):
                        pe.matmul(psH[:, c, :], w["in"][:, c * P:(c + 1) * P], xT[:, :],
                                  start=True, stop=True).then_inc(h_done, 1)
                    for c in range(CH):
                        pe.wait_ge(h_ready, b * CH + c + 1)
                        pe.matmul(psA[0:NS, :], w["A"][:, c, :], hT[:, c, :], start=c == 0, stop=c == CH - 1)
                        last = pe.matmul(psU[0:NS, :], w["B"][:, c, :], hT[:, c, :], start=c == 0, stop=c == CH - 1)
                    last.then_inc(au_done, 1)
                    pe.wait_ge(states_ready, b + 1)
                    for c in range(CH):
                        pe.matmul(psH[:, c, :], w["C"][:, c * P:(c + 1) * P], states[:, :],
                                  start=True, stop=True).then_inc(yt_done, 1)
                    pe.wait_ge(yt_ready, (b + 1) * CH)
                    for t in range(TB):
                        o = psY[:, t * P:(t + 1) * P]
                        for c in range(CH):
                            pe.matmul(o, yT[:, c, t * P:(t + 1) * P], w["out"][:, c, :], start=c == 0, stop=False)
                        last = pe.matmul(o, core.ones_row, w["b_out"][0:1, :], start=False, stop=True)
                    last.then_inc(out_done, 1)

            @block.vector
            def _(dve):
                with dve.Fori(0, B) as b:
                    ln.vector(dve, b * 2, lambda t: core.X[:, b * TB + t, :], lambda t: xo[:, t, :])
                    dve.wait_ge(ln.ready, b * 2 * TB + TB)
                    ln.vector(dve, b * 2 + 1, lambda t: xo[:, t, :], lambda t: xn[:, t, :])
                    c = Chain(dve, vec, b * VEC)
                    x = core.X[:, bass.ds(b * TB, TB), :]
                    c(dve.tensor_tensor(x, x, xo[:, :, :], ALU.add))
                    dve.wait_ge(exp_ready, b * 2 + 2)
                    c(dve.tensor_scalar(decay[:, :], decay[:, :], 1.0, None, ALU.add))
                    c.wait()
                    c(dve.reciprocal(decay[:, :], decay[:, :]))
                    c.wait()
                    dve.tensor_tensor_scan(states[:, :], decay[:, :], drive[:, :], 0.0,
                                           ALU.mult, ALU.add).then_inc(states_ready, 1)
                    dve.wait_ge(out_done, b + 1)
                    add_to_stream(dve, core, b, psY[:, :], added)
                    dve.wait_ge(added, b + 1)
                    assert c.n == VEC


def layer1_ffn(nc, core):
    E, FC = 8, 4
    STATS_AT, NORM_AT, TURN_AT, ROUTE_AT, CHOOSE_AT, GATES_AT = 1, 2, 3, 4, 5, 6
    with ExitStack() as ctx:
        def sb(name, shape, dt=F32):
            return ctx.enter_context(nc.sbuf_tensor("L1f_" + name, shape, dt))

        def sem(name):
            return core.semaphore(ctx, "L1f_" + name)

        ln = LayerNorm(nc, ctx, "L1f_ln", core)
        w = core.w["L1f"]
        xn = sb("xn", [P, TB, D])
        xT = sb("xT", [P, S])
        xT_next = sb("xT_next", [P, S])
        hT = sb("hT", [P, 2, FC, S])
        logits = sb("logits", [P, TB, E])
        hit = sb("hit", [P, TB, E])
        first = sb("first", [P, TB, E])
        second = sb("second", [P, TB, E])
        gates = sb("gates", [P, TB, E])
        gates_next = sb("gates_next", [P, TB, E])
        best = sb("best", [P, 3, TB])
        place = sb("place", [P, TB])
        e21 = sb("e21", [P, TB])
        g1 = sb("g1", [P, TB])
        g2 = sb("g2", [P, TB])
        gatesT = sb("gatesT", [E, S])
        psT, psL = (ctx.enter_context(nc.psum_tensor("L1f_ps" + c, [P, S], F32)) for c in "TL")
        psH = ctx.enter_context(nc.psum_tensor("L1f_psH", [P, FC, S], F32))
        psY = ctx.enter_context(nc.psum_tensor("L1f_psY", [P, 2, S], F32))
        names = ("turned xt_ready xt_moved logits_done vec margin_ready exp_ready gates_ready gates_moved gates_turned "
                 "gatesT_ready bias_done bias_added h_done h_ready y_done y_used").split()
        (turned, xt_ready, xt_moved, logits_done, vec, margin_ready, exp_ready, gates_ready, gates_moved, gates_turned,
         gatesT_ready, bias_done, bias_added, h_done, h_ready, y_done, y_used) = (sem(n) for n in names)
        VEC = 17
        order = core.cf[:, C_ORDER8:C_ORDER8 + E].unsqueeze(1).to_broadcast([P, TB, E])
        with nc.Block() as block:
            @block.scalar
            def _(act):
                core.wait_weights(act, "L1f")

                def copy_tokens(b):
                    act.wait_ge(turned, b + 1)
                    act.activation(xT_next[:, :], psT[:, :], ACT.Copy).then_inc(xt_ready, 1)

                def rectify(b, e, f):
                    act.wait_ge(h_done, (b * E + e) * FC + f + 1)
                    if e >= 2:
                        act.wait_ge(y_done, b * E + e - 1)
                    act.activation(hT[:, e % 2, f, :], psH[:, f, :], ACT.Relu,
                                   bias=w["b1"][:, e % E * FC + f:e % E * FC + f + 1]).then_inc(h_ready, 1)

                def exp_of_margin(b):
                    act.wait_ge(margin_ready, b + 1)
                    act.activation(e21[:, :], e21[:, :], ACT.Exp).then_inc(exp_ready, 1)

                ln.scalar(act, 0)
                copy_tokens(0)
                for f in range(FC):
                    rectify(0, 0, f)
                exp_of_margin(0)
                with act.Fori(0, B) as b:
                    for e in range(E):
                        for f in range(FC):
                            rectify(b, e + 1, f)
                        if e == STATS_AT:
                            ln.scalar(act, b + 1)
                        if e == TURN_AT:
                            copy_tokens(b + 1)
                        if e == CHOOSE_AT:
                            exp_of_margin(b + 1)

            @block.tensor
            def _(pe):
                core.wait_weights(pe, "L1f")

                def route(b):
                    pe.wait_ge(xt_ready, b + 1)
                    for t in range(TB):
                        o = psL[:, t * E:(t + 1) * E]
                        pe.matmul(o, xT_next[:, t * P:(t + 1) * P], w["router"][:, :], start=True, stop=False)
                        last = pe.matmul(o, core.ones_row, w["router_b"][0:1, :], start=False, stop=True)
                    last.then_inc(logits_done, 1)

                def expand(b, e, tokens, first=False):
                    for f in range(FC):
                        if not first:
                            pe.wait_ge(h_ready, (b * E + e - 1) * FC + f + 1)
                        pe.matmul(psH[:, f, :], w["W1"][:, e % E, f * P:(f + 1) * P], tokens[:, :],
                                  start=True, stop=True).then_inc(h_done, 1)

                def contract(b, e):
                    if e >= 2:
                        pe.wait_ge(y_used, b * E + e - 1)
                    pe.wait_ge(h_ready, b * (E * FC) + e * FC + FC)
                    for t in range(TB):
                        for f in range(FC):
                            last = pe.matmul(psY[:, e % 2, t * P:(t + 1) * P], hT[:, e % 2, f, t * P:(t + 1) * P],
                                             w["W2"][:, e, f, :], start=f == 0, stop=f == FC - 1)
                    last.then_inc(y_done, 1)

                turn(pe, core, ln, 0, xn, psT, turned)
                route(0)
                expand(0, 0, xT_next, first=True)
                with pe.Fori(0, B) as b:
                    for e in range(E):
                        if e == 0:
                            pe.wait_ge(xt_moved, b + 1)
                        expand(b, e + 1, xT if e + 1 < E else xT_next)
                        if e == 0:
                            pe.wait_ge(gates_moved, b + 1)
                            for t in range(TB):
                                last = pe.transpose(psT[0:E, t * P:(t + 1) * P], gates[:, t, :], core.ident)
                            last.then_inc(gates_turned, 1)
                        contract(b, e)
                        if e == 0:
                            pe.wait_ge(gatesT_ready, b + 1)
                            for t in range(TB):
                                last = pe.matmul(psL[:, t * P:(t + 1) * P], gatesT[:, t * P:(t + 1) * P],
                                                 w["b2"][0:E, :], start=True, stop=True)
                            last.then_inc(bias_done, 1)
                        if e == TURN_AT:
                            turn(pe, core, ln, b + 1, xn, psT, turned)
                        if e == ROUTE_AT:
                            pe.wait_ge(bias_added, b + 1)
                            route(b + 1)

            @block.vector
            def _(dve):
                def choose(b):
                    c = Chain(dve, vec, b * VEC)
                    dve.wait_ge(logits_done, b + 1)
                    c(dve.tensor_copy(logits[:, :, :], psL[:, 0:TB * E].rearrange("p (t e) -> p t e", t=TB)))
                    for k, chosen in enumerate((first, second)):
                        c.wait()
                        c(dve.tensor_reduce(best[:, k, :], logits[:, :, :], AX, ALU.max))
                        c.wait()
                        c(dve.tensor_tensor(hit[:, :, :], logits[:, :, :],
                                            best[:, k, :].unsqueeze(2).to_broadcast([P, TB, E]), ALU.is_equal))
                        c.wait()
                        c(dve.tensor_tensor(hit[:, :, :], hit[:, :, :], order, ALU.mult))
                        c.wait()
                        c(dve.tensor_reduce(place[:, :], hit[:, :, :], AX, ALU.max))
                        c.wait()
                        c(dve.tensor_tensor(chosen[:, :, :], order,
                                            place[:, :].unsqueeze(2).to_broadcast([P, TB, E]), ALU.is_equal))
                        c.wait()
                        if k == 0:
                            c(dve.scalar_tensor_tensor(out=logits[:, :, :], in0=chosen[:, :, :], scalar=-3e38,
                                                       in1=logits[:, :, :], op0=ALU.mult, op1=ALU.add))
                    dve.tensor_tensor(e21[:, :], best[:, 1, :], best[:, 0, :], ALU.subtract).then_inc(margin_ready, 1)
                    return c.n

                def weigh(b, n):
                    c = Chain(dve, vec, b * VEC + n)
                    dve.wait_ge(exp_ready, b + 1)
                    c(dve.tensor_scalar(g2[:, :], e21[:, :], 1.0, None, ALU.add))
                    c.wait()
                    c(dve.reciprocal(g1[:, :], g2[:, :]))
                    c.wait()
                    c(dve.tensor_tensor(g2[:, :], g1[:, :], e21[:, :], ALU.mult))
                    c(dve.tensor_tensor(first[:, :, :], first[:, :, :],
                                        g1[:, :].unsqueeze(2).to_broadcast([P, TB, E]), ALU.mult))
                    c.wait(1)
                    c(dve.tensor_tensor(second[:, :, :], second[:, :, :],
                                        g2[:, :].unsqueeze(2).to_broadcast([P, TB, E]), ALU.mult))
                    c.wait()
                    dve.tensor_tensor(gates_next[:, :, :], first[:, :, :], second[:, :, :],
                                      ALU.add).then_inc(gates_ready, 1)
                    assert n + c.n == VEC, n + c.n

                def move_gates(b):
                    dve.wait_ge(gates_ready, b + 1)
                    dve.tensor_copy(gates[:, :, :], gates_next[:, :, :]).then_inc(gates_moved, 1)

                ln.vector(dve, 0, lambda t: core.X[:, t, :], lambda t: xn[:, t, :])
                chain = choose(0)
                weigh(0, chain)
                dve.wait_ge(xt_ready, 1)
                dve.tensor_copy(xT[:, :], xT_next[:, :]).then_inc(xt_moved, 1)
                move_gates(0)
                with dve.Fori(0, B) as b:
                    def next_tokens(t):
                        return core.X[:, b * TB + TB + t, :]

                    dve.wait_ge(gates_turned, b + 1)
                    dve.tensor_copy(gatesT[:, :], psT[0:E, :]).then_inc(gatesT_ready, 1)
                    dve.wait_ge(gates_moved, b + 1)
                    for e in range(E):
                        dve.wait_ge(y_done, b * E + e + 1)
                        if e >= 1:
                            dve.wait_ge(y_used, b * E + e)
                        for t in range(TB):
                            x = core.X[:, b * TB + t, :]
                            last = dve.scalar_tensor_tensor(out=x, in0=psY[:, e % 2, t * P:(t + 1) * P],
                                                            scalar=gates[:, t, e:e + 1], in1=x,
                                                            op0=ALU.mult, op1=ALU.add)
                        last.then_inc(y_used, 1)
                        if e == 0:
                            dve.wait_ge(y_used, b * E + 1)
                            dve.wait_ge(bias_done, b + 1)
                            add_to_stream(dve, core, b, psL[:, :], bias_added)
                            dve.wait_ge(bias_added, b + 1)
                        if e == STATS_AT:
                            ln.statistics(dve, b + 1, next_tokens)
                        if e == NORM_AT:
                            ln.finish(dve, b + 1, next_tokens, lambda t: xn[:, t, :])
                        if e == CHOOSE_AT:
                            choose(b + 1)
                        if e == GATES_AT:
                            weigh(b + 1, chain)
                            dve.wait_ge(h_done, (b * E + E) * FC)
                            dve.tensor_copy(xT[:, :], xT_next[:, :]).then_inc(xt_moved, 1)
                    dve.wait_ge(y_used, (b + 1) * E)
                    move_gates(b + 1)


UNITS = (((3, 0),), ((2, 0), (0, 384)), ((1, 0),))


def unit_width(u):
    return sum((i + 1) * P for i, _ in UNITS[u])


UNITS_T = (((0, 0),), ((1, 0), (3, 384)), ((2, 0),))


def unit_width_t(u):
    return sum((TB - k) * P for k, _ in UNITS_T[u])


def layer0_attn(nc, core):
    H, DH, PER = 16, 8, 4
    NU = len(UNITS)
    PARTS = 3
    ROWS = 32 * PARTS
    KEEP = 4
    PSLOTS = 6
    LAG = 3
    assert PSLOTS * sum(unit_width_t(u) for u in range(NU)) == PROBS_COLS
    G = H // PER
    with ExitStack() as ctx:
        def sb(name, shape, dt=F32):
            return ctx.enter_context(nc.sbuf_tensor("L0a_" + name, shape, dt))

        def sem(name):
            return core.semaphore(ctx, "L0a_" + name)

        ln = LayerNorm(nc, ctx, "L0a_ln", core)
        w = core.w["L0a"]
        xn = sb("xn", [P, TB, D])
        xT = sb("xT", [P, S])
        scratch = sb("scratch", [P, G, S])
        rot, part, o_heads = scratch[:, 0:2, :], scratch[:, 2:4, :], scratch
        parts = sb("parts", [P, 2, PARTS, S], BF16)
        q_stack = sb("q_stack", [P, KEEP, S], BF16)
        k_stack = sb("k_stack", [P, KEEP, S], BF16)
        pick_q = sb("pick_q", [P, H, 32], BF16)
        pick_k = sb("pick_k", [P, H, 112], BF16)
        causal_t = sb("causal_t", [P, P], BF16)
        v = sb("v", [P, TB, H, 32])
        neg_max = sb("neg_max", [P, 2, TB])
        rest = sb("rest", [P, TB])
        zero = sb("zero", [P, TB])
        max_parts = sb("max_parts", [P, 3, TB, PARTS], BF16)
        probs = core.arena[:, 0:PROBS_COLS].rearrange("p (n c) -> p n c", n=PSLOTS)
        inv = sb("inv", [P, TB, H])
        o = sb("o", [P, TB, D])
        oT = sb("oT", [P, S])
        psM = ctx.enter_context(nc.psum_tensor("L0a_psM", [P, S], F32))
        psO = ctx.enter_context(nc.psum_tensor("L0a_psO", [P, S], F32))
        psR = ctx.enter_context(nc.psum_tensor("L0a_psR", [P, 2, S], F32))
        psA = ctx.enter_context(nc.psum_tensor("L0a_psA", [P, 2, S], F32))
        psB = ctx.enter_context(nc.psum_tensor("L0a_psB", [P, 2, S], F32))
        (setup, turned, xt_ready, qk_done, v_done, v_ready, vec, rot_ready, first_parts, second_parts, parts_ready,
         q_picked, k_picked, q_ready, k_ready, scores_done, max_ready, max_split, max_turned, max_rows, keyed_done,
         probs_ready, av_done, heads_ready, heads_turned, inv_ready, o_ready, o_turned, ot_ready, y_done, added) = (
            sem(n) for n in (
                "setup turned xt_ready qk_done v_done v_ready vec rot_ready first_parts second_parts parts_ready "
                "q_picked k_picked q_ready k_ready scores_done max_ready max_split max_turned max_rows keyed_done "
                "probs_ready av_done heads_ready heads_turned inv_ready o_ready o_turned ot_ready y_done added"
            ).split())
        VEC = 4
        SETUP = 6
        SPLIT = 4
        unit_at = [sum(unit_width_t(j) for j in range(u)) for u in range(NU)]
        key_at = {k: (unit_at[u] + at, (TB - k) * P) for u in range(NU) for k, at in UNITS_T[u]}

        def bank(m):
            return psB[:, m % 2, :]

        def tile_bank(t):
            return (psA if t < 2 else psB)[:, t % 2, :]

        with nc.Block() as block:
            @block.scalar
            def _(act):
                core.wait_weights(act, "L0a")
                act.activation(pick_k[:, :, :], w["pick_k"], ACT.Copy).then_inc(setup, 1)
                with act.Fori(0, B) as b:
                    ln.scalar(act, b)
                    act.wait_ge(turned, b + 1)
                    act.activation(xT[:, :], psM[:, :], ACT.Copy).then_inc(xt_ready, 1)
                    act.wait_ge(v_done, b + 1)
                    act.activation(v[:, :, :, 0:DH], psM[:, :].rearrange("p (t h d) -> p t h d", t=TB, h=H),
                                   ACT.Copy).then_inc(v_ready, 1)
                    for j in range(2):
                        act.wait_ge(rot_ready, b * 2 + j + 1)
                        act.activation(parts[:, j, 0, :], rot[:, j, :], ACT.Copy).then_inc(first_parts, 1)
                        act.wait_ge(second_parts, b * 2 + j + 1)
                        act.activation(parts[:, j, 1, :], part[:, j, :], ACT.Copy).then_inc(first_parts, 1)
                    for n in range(H + LAG):
                        m = n - LAG
                        if m >= 0:
                            act.wait_ge(max_turned, b * H + m + 1)
                            act.activation(q_stack[ROWS:ROWS + PARTS, m % KEEP, :], psM[ROWS:ROWS + PARTS, :],
                                           ACT.Copy).then_inc(max_rows, 1)
                        if n < H:
                            act.wait_ge(q_picked, b * H + n + 1)
                            act.activation(q_stack[0:ROWS, n % KEEP, :], psR[0:ROWS, 0, :],
                                           ACT.Copy).then_inc(q_ready, 1)
                        if m >= 0:
                            if m >= PSLOTS:
                                act.wait_ge(av_done, b * G + (m - PSLOTS) // PER + 1)
                            for u in range(NU):
                                act.wait_ge(keyed_done, b * (H * NU) + m * NU + u + 1)
                                act.activation(probs[:, m % PSLOTS, unit_at[u]:unit_at[u] + unit_width_t(u)],
                                               bank(m * NU + u)[:, 0:unit_width_t(u)],
                                               ACT.Exp).then_inc(probs_ready, 1)
                        if n >= 2 * PER and n % PER == 0:
                            g = n // PER - 2
                            act.wait_ge(av_done, b * G + g + 1)
                            act.activation(o_heads[:, g, :], psO[:, :], ACT.Copy).then_inc(heads_ready, 1)
                    act.wait_ge(av_done, b * G + G)
                    act.activation(o_heads[:, G - 1, :], psO[:, :], ACT.Copy).then_inc(heads_ready, 1)
                    act.wait_ge(o_turned, b + 1)
                    act.activation(oT[:, :], psM[:, :], ACT.Copy).then_inc(ot_ready, 1)

            @block.tensor
            def _(pe):
                core.wait_weights(pe, "L0a")
                pe.wait_ge(setup, SETUP + 1)

                def pick_queries(b, n):
                    if n >= 1:
                        pe.wait_ge(q_ready, b * H + n)
                    for i in range(PARTS):
                        last = pe.matmul(psR[32 * i:32 * (i + 1), 0, :], pick_q[:, n, :], parts[:, 0, i, :],
                                         start=True, stop=True)
                    last.then_inc(q_picked, 1)

                def pick_keys(b, n):
                    if n >= 1:
                        pe.wait_ge(k_ready, b * H + n)
                    for j in range(PARTS):
                        at = DH * (PARTS - 1 - j)
                        last = pe.matmul(psR[0:ROWS, 1, :], pick_k[:, n, at:at + ROWS], parts[:, 1, j, :],
                                         start=j == 0, stop=j == PARTS - 1)
                    last.then_inc(k_picked, 1)

                def scores(b, n, u):
                    m = n * NU + u
                    if u == 0:
                        pe.wait_ge(q_ready, b * H + n + 1)
                        pe.wait_ge(k_ready, b * H + n + 1)
                    if m >= 2:
                        pe.wait_ge(max_ready, b * (H * NU) + m - 1)
                    for i, at in UNITS[u]:
                        pe.matmul(psA[:, m % 2, at:at + (i + 1) * P], q_stack[0:ROWS, n % KEEP, i * P:(i + 1) * P],
                                  k_stack[0:ROWS, n % KEEP, 0:(i + 1) * P], start=True, stop=False)
                        last = pe.matmul(psA[:, m % 2, at + i * P:at + (i + 1) * P], core.identb[:, :],
                                         core.causal[:, :], start=False, stop=True)
                    last.then_inc(scores_done, 1)

                def turn_maxima(b, n):
                    pe.wait_ge(max_split, (b * H + n) * SPLIT + SPLIT)
                    if n >= 1:
                        pe.wait_ge(max_rows, b * H + n)
                    for t in range(TB):
                        last = pe.matmul(psM[ROWS:ROWS + PARTS, t * P:(t + 1) * P], max_parts[:, n % 3, t, :],
                                         core.identb[:, :], start=True, stop=True)
                    last.then_inc(max_turned, 1)

                def keyed_scores(b, n, u):
                    m = n * NU + u
                    if u == 0:
                        pe.wait_ge(max_rows, b * H + n + 1)
                    if m >= 2:
                        pe.wait_ge(probs_ready, b * (H * NU) + m - 1)
                    for k, at in UNITS_T[u]:
                        pe.matmul(bank(m)[:, at:at + (TB - k) * P],
                                  k_stack[0:ROWS + PARTS, n % KEEP, k * P:(k + 1) * P],
                                  q_stack[0:ROWS + PARTS, n % KEEP, k * P:S], start=True, stop=False)
                        last = pe.matmul(bank(m)[:, at:at + P], core.identb[:, :], causal_t[:, :],
                                         start=False, stop=True)
                    last.then_inc(keyed_done, 1)

                def weigh_values(b, g):
                    pe.wait_ge(probs_ready, b * (H * NU) + (g + 1) * PER * NU)
                    if g >= 1:
                        pe.wait_ge(heads_ready, b * G + g)
                    for k in range(TB):
                        at, width = key_at[k]
                        for j in range(PER):
                            n = g * PER + j
                            last = pe.matmul(psO[32 * j:32 * (j + 1), k * P:S], v[:, k, n, :],
                                             probs[:, n % PSLOTS, at:at + width], start=k == 0, stop=k == TB - 1)
                    last.then_inc(av_done, 1)

                with pe.Fori(0, B) as b:
                    turn(pe, core, ln, b, xn, psM, turned)
                    pe.wait_ge(xt_ready, b + 1)
                    for j in range(4):
                        last = pe.matmul((psR if j < 2 else psA)[:, j % 2, :], w["qk"][:, j, :], xT[:, :],
                                         start=True, stop=True)
                        if j % 2:
                            last.then_inc(qk_done, 1)
                    for t in range(TB):
                        last = pe.matmul(psM[:, t * P:(t + 1) * P], xT[:, t * P:(t + 1) * P], w["v"][:, :],
                                         start=True, stop=True)
                    last.then_inc(v_done, 1)
                    pe.wait_ge(parts_ready, b * 2 + 2)
                    pe.wait_ge(v_ready, b + 1)
                    for n in range(H + LAG):
                        if n >= LAG:
                            turn_maxima(b, n - LAG)
                        if n < H:
                            pick_queries(b, n)
                        if 1 <= n <= H:
                            scores(b, n - 1, 0)
                            scores(b, n - 1, 1)
                        if n >= LAG:
                            keyed_scores(b, n - LAG, 0)
                        if n < H:
                            pick_keys(b, n)
                        if 1 <= n <= H:
                            scores(b, n - 1, 2)
                        if n >= LAG:
                            keyed_scores(b, n - LAG, 1)
                            keyed_scores(b, n - LAG, 2)
                        if n >= PER + LAG and (n - LAG) % PER == 0:
                            weigh_values(b, (n - LAG) // PER - 1)
                    weigh_values(b, G - 1)
                    pe.wait_ge(heads_ready, b * G + G)
                    for t in range(TB):
                        for g in range(G):
                            last = pe.transpose(tile_bank(t)[:, g * P:(g + 1) * P],
                                                o_heads[:, g, t * P:(t + 1) * P], core.ident)
                        last.then_inc(heads_turned, 1)
                    for t in range(TB):
                        pe.wait_ge(o_ready, b * TB + t + 1)
                        last = pe.transpose(psM[:, t * P:(t + 1) * P], o[:, t, :], core.ident)
                    last.then_inc(o_turned, 1)
                    pe.wait_ge(ot_ready, b + 1)
                    for t in range(TB):
                        last = pe.matmul(psO[:, t * P:(t + 1) * P], oT[:, t * P:(t + 1) * P], w["o"][:, :],
                                         start=True, stop=True)
                    last.then_inc(y_done, 1)

            @block.gpsimd
            def _(pool):
                pool.wait_ge(setup, SETUP + 1)
                with pool.Fori(0, B) as b:
                    for n in range(H):
                        c = Chain(pool, max_split, (b * H + n) * SPLIT)
                        pool.wait_ge(max_ready, b * (H * NU) + (n + 1) * NU)
                        if n >= 3:
                            pool.wait_ge(max_turned, b * H + n - 2)
                        c(pool.tensor_tensor(max_parts[:, n % 3, :, 0], neg_max[:, n % 2, :], zero[:, :], ALU.add))
                        c.wait()
                        c(pool.tensor_tensor(rest[:, :], neg_max[:, n % 2, :], max_parts[:, n % 3, :, 0],
                                             ALU.subtract))
                        c.wait()
                        c(pool.tensor_tensor(max_parts[:, n % 3, :, 1], rest[:, :], zero[:, :], ALU.add))
                        c.wait()
                        c(pool.tensor_tensor(max_parts[:, n % 3, :, 2], rest[:, :], max_parts[:, n % 3, :, 1],
                                             ALU.subtract))
                        c.wait()

            @block.vector
            def _(dve):
                core.wait_weights(dve, "L0a")
                c = Chain(dve, setup)
                c(dve.tensor_copy(pick_q[:, :, :], w["pick_q"]))
                c(dve.tensor_copy(causal_t[:, :], w["causal_t"]))
                c(dve.memset(v[:, :, :, :], 0.0))
                c(dve.memset(k_stack[ROWS:P, :, :], 1.0))
                c(dve.memset(zero[:, :], 0.0))
                dve.wait_ge(setup, SETUP)
                c(dve.memset(v[:, :, :, DH], 1.0))
                dve.wait_ge(setup, SETUP + 1)
                with dve.Fori(0, B) as b:
                    ln.vector(dve, b, lambda t: core.X[:, b * TB + t, :], lambda t: xn[:, t, :])
                    c = Chain(dve, vec, b * VEC)
                    for j in range(2):
                        ps = psA if j else psR
                        dve.wait_ge(qk_done, b * 2 + j + 1)
                        c(dve.tensor_tensor(rot[:, j, :], ps[:, 0, :], w["cos"][:, j, :], ALU.mult))
                        c(dve.tensor_tensor(part[:, j, :], ps[:, 1, :], w["sin"][:, j, :], ALU.mult))
                        c.wait()
                        dve.tensor_tensor(rot[:, j, :], rot[:, j, :], part[:, j, :], ALU.add).then_inc(rot_ready, 1)
                    for j in range(2):
                        dve.wait_ge(first_parts, b * 4 + 2 * j + 1)
                        dve.tensor_tensor(part[:, j, :], rot[:, j, :], parts[:, j, 0, :],
                                          ALU.subtract).then_inc(second_parts, 1)
                        dve.wait_ge(first_parts, b * 4 + 2 * j + 2)
                        dve.tensor_tensor(parts[:, j, 2, :], part[:, j, :], parts[:, j, 1, :],
                                          ALU.subtract).then_inc(parts_ready, 1)
                    for n in range(H + 1):
                        if n >= 3:
                            dve.wait_ge(max_split, (b * H + n - 2) * SPLIT)
                        for u in range(NU):
                            if u == NU - 1 and n < H:
                                dve.wait_ge(k_picked, b * H + n + 1)
                                dve.tensor_copy(k_stack[0:ROWS, n % KEEP, :], psR[0:ROWS, 1, :]).then_inc(k_ready, 1)
                            if 1 <= n <= H:
                                m = (n - 1) * NU + u
                                dve.wait_ge(scores_done, b * (H * NU) + m + 1)
                                for i, at in UNITS[u]:
                                    last = dve.tensor_reduce(neg_max[:, (n - 1) % 2, i:i + 1],
                                                             psA[:, m % 2, at:at + (i + 1) * P],
                                                             AX, ALU.max, negate=True)
                                last.then_inc(max_ready, 1)
                    for t in range(TB):
                        heads = tile_bank(t).rearrange("p (h c) -> p h c", c=32)
                        dve.wait_ge(heads_turned, b * TB + t + 1)
                        dve.reciprocal(inv[:, t, :], heads[:, :, DH]).then_inc(inv_ready, 1)
                        dve.wait_ge(inv_ready, b * TB + t + 1)
                        dve.tensor_tensor(o[:, t, :].rearrange("p (h d) -> p h d", h=H), heads[:, :, 0:DH],
                                          inv[:, t, :].unsqueeze(2).to_broadcast([P, H, DH]),
                                          ALU.mult).then_inc(o_ready, 1)
                    dve.wait_ge(y_done, b + 1)
                    add_to_stream(dve, core, b, psO[:, :], added)
                    dve.wait_ge(added, b + 1)
                    assert c.n == VEC, c.n


def layer1_attn(nc, core):
    H = 8
    SCALE = float(D) ** -0.5
    KINDS = 4
    AU, VU, AC, VO = range(KINDS)
    W_QU, W_KU, W_VU, W_QC, W_KC, W_VC = range(6)
    NU = len(UNITS)
    LN_AT, TURN_AT = 3, 5
    RING = 4
    with ExitStack() as ctx:
        def sb(name, shape, dt=F32):
            return ctx.enter_context(nc.sbuf_tensor("L1a_" + name, shape, dt))

        def sem(name):
            return core.semaphore(ctx, "L1a_" + name)

        ln = LayerNorm(nc, ctx, "L1a_ln", core)
        w = core.w["L1a"]
        xn = sb("xn", [P, TB, D])
        xT = sb("xT", [P, S])
        xT_next = sb("xT_next", [P, S])
        folded = sb("folded", [P, 3, H, D])
        proj = sb("proj", [P, RING, KINDS, S])
        th_look = sb("th_look", [P, S])
        look = sb("look", [P, S])
        th_sum = sb("th_sum", [P, S])
        lower = sb("lower", [P, 2, S])
        neg_max = sb("neg_max", [P, TB])
        sums = sb("sums", [P, TB])
        inv = sb("inv", [P, TB])
        probs = sb("probs", [P, NU, S])
        probsT = sb("probsT", [P, TB, S])
        yT = sb("yT", [P, S])
        psJ = ctx.enter_context(nc.psum_tensor("L1a_psJ", [P, 2, S], F32))
        psD = ctx.enter_context(nc.psum_tensor("L1a_psD", [P, S], F32))
        psS = ctx.enter_context(nc.psum_tensor("L1a_psS", [P, NU, S], F32))
        psP = ctx.enter_context(nc.psum_tensor("L1a_psP", [P, S], F32))
        psO = ctx.enter_context(nc.psum_tensor("L1a_psO", [P, S], F32))
        (fold_done, fold_ready, turned, xt_ready, xt_moved, proj_done, proj_ready, look_done, look_tanh, look_ready, sum_done,
         sum_tanh, lower_ready, scores_done, vec, max_ready, probs_ready, normed, probs_turned, pt_ready, y_done,
         y_ready, y_turned,
         added) = (
            sem(n) for n in (
                "fold_done fold_ready turned xt_ready xt_moved proj_done proj_ready look_done look_tanh look_ready sum_done "
                "sum_tanh lower_ready scores_done vec max_ready probs_ready normed probs_turned pt_ready y_done "
                "y_ready y_turned "
                "added").split())
        VEC = 8
        FOLDS = 3 * H // TB
        after = core.cf[:, C_AFTER:C_AFTER + P].unsqueeze(1).to_broadcast([P, TB, P])

        with nc.Block() as block:
            @block.scalar
            def _(act):
                def evacuate(b, h, kind):
                    act.wait_ge(proj_done, (b * H + h) * KINDS + kind + 1)
                    act.activation(proj[:, h % RING, kind, :], psJ[:, kind % 2, :], ACT.Copy,
                                   scale=SCALE if kind == AC else 1.0).then_inc(proj_ready, 1)

                def look_tanhs(b, h):
                    act.wait_ge(look_done, b * H + h + 1)
                    act.activation(th_look[:, :], psD[:, :], ACT.Tanh, scale=0.5 * SCALE).then_inc(look_tanh, 1)

                def sum_tanhs(b, h):
                    act.wait_ge(sum_done, b * H + h + 1)
                    act.activation(th_sum[:, :], psD[:, :], ACT.Tanh, scale=0.5).then_inc(sum_tanh, 1)

                def exponential(b, h, u):
                    act.wait_ge(max_ready, (b * H + h) * NU + u + 1)
                    for i, at in UNITS[u]:
                        last = act.activation(probs[:, u, at:at + (i + 1) * P], psS[:, u, at:at + (i + 1) * P],
                                              ACT.Exp, bias=neg_max[:, i:i + 1], accum_out=sums[:, i:i + 1])
                    last.then_inc(probs_ready, 1)

                def copy_turned(b, h, u):
                    act.wait_ge(probs_turned, (b * H + h) * NU + u + 1)
                    for i, at in UNITS[u]:
                        last = act.activation(probsT[:, 0:i + 1, i * P:(i + 1) * P],
                                              psP[:, at:at + (i + 1) * P].rearrange("p (k q) -> p k q", q=P), ACT.Copy)
                    last.then_inc(pt_ready, 1)

                def copy_tokens(b):
                    act.wait_ge(turned, b + 1)
                    act.activation(xT_next[:, :], psP[:, :], ACT.Copy).then_inc(xt_ready, 1)

                flat = folded[:, :, :, :].rearrange("p a h d -> p (a h d)")
                for n in range(FOLDS):
                    act.wait_ge(fold_done, n + 1)
                    act.activation(flat[:, n * S:(n + 1) * S], psJ[:, n % 2, :], ACT.Copy).then_inc(fold_ready, 1)
                ln.scalar(act, 0)
                copy_tokens(0)
                for kind in range(KINDS):
                    evacuate(0, 0, kind)
                look_tanhs(0, 0)
                for kind in range(KINDS):
                    evacuate(0, 1, kind)
                sum_tanhs(0, 0)
                look_tanhs(0, 1)
                with act.Fori(0, B) as b:
                    for h in range(H):
                        if h == LN_AT:
                            ln.scalar(act, b + 1)
                        sum_tanhs(b, h + 1)
                        exponential(b, h, 0)
                        exponential(b, h, 1)
                        evacuate(b, h + 2, 0)
                        exponential(b, h, 2)
                        for u in range(NU):
                            copy_turned(b, h, u)
                            evacuate(b, h + 2, u + 1)
                        look_tanhs(b, h + 2)
                        if h == TURN_AT:
                            copy_tokens(b + 1)
                    act.wait_ge(y_done, b + 1)
                    act.activation(yT[:, :], psO[:, :], ACT.Copy).then_inc(y_ready, 1)

            @block.tensor
            def _(pe):
                core.wait_weights(pe, "L1a")

                def project(b, h, kind, first=False):
                    if not (first and kind < 2):
                        pe.wait_ge(proj_ready, (b * H + h) * KINDS + kind - 1)
                    weights = w["qkv"][:, h % H, W_VU, :] if kind == VU else folded[:, (AU, AC, VO).index(kind), h % H, :]
                    ps = psJ[:, kind % 2, :]
                    if kind in (VU, VO):
                        for t in range(TB):
                            last = pe.matmul(ps[:, t * P:(t + 1) * P], tokens_of(h)[:, t * P:(t + 1) * P], weights,
                                             start=True, stop=True)
                    else:
                        last = pe.matmul(ps, weights, tokens_of(h)[:, :], start=True, stop=True)
                    last.then_inc(proj_done, 1)

                def look_scores(b, h, first=False):
                    pe.wait_ge(proj_ready, (b * H + h) * KINDS + AU + 1)
                    if not first:
                        pe.wait_ge(lower_ready, b * H + h)
                    for t in range(TB):
                        blk = slice(t * P, (t + 1) * P)
                        last = pe.matmul(psD[:, blk], tokens_of(h)[:, blk], proj[:, h % RING, AU, blk],
                                         start=True, stop=True)
                    last.then_inc(look_done, 1)

                def look_sums(b, h):
                    pe.wait_ge(proj_ready, (b * H + h) * KINDS + VU + 1)
                    pe.wait_ge(look_ready, b * H + h + 1)
                    for t in range(TB):
                        blk = slice(t * P, (t + 1) * P)
                        last = pe.matmul(psD[:, blk], look[:, blk], proj[:, h % RING, VU, blk], start=True, stop=True)
                    last.then_inc(sum_done, 1)

                def scores(b, h):
                    pe.wait_ge(proj_ready, (b * H + h + 1) * KINDS)
                    if h == 0:
                        pe.wait_ge(xt_moved, b + 1)
                    for u in range(NU):
                        for i, at in UNITS[u]:
                            pe.matmul(psS[:, u, at:at + (i + 1) * P], proj[:, h % RING, AC, i * P:(i + 1) * P],
                                      xT[:, 0:(i + 1) * P], start=True, stop=False)
                            last = pe.matmul(psS[:, u, at + i * P:at + (i + 1) * P], core.identb[:, :],
                                             core.causal[:, :], start=False, stop=True)
                        last.then_inc(scores_done, 1)

                def turn_probs(b, h, u):
                    pe.wait_ge(normed, (b * H + h) * NU + u + 1)
                    if h or u:
                        pe.wait_ge(pt_ready, (b * H + h) * NU + u)
                    for c in range(unit_width(u) // P):
                        last = pe.transpose(psP[:, c * P:(c + 1) * P], probs[:, u, c * P:(c + 1) * P], core.ident)
                    last.then_inc(probs_turned, 1)

                def weigh_values(b, h):
                    pe.wait_ge(pt_ready, (b * H + h + 1) * NU)
                    for k in range(TB):
                        last = pe.matmul(psO[:, k * P:S], proj[:, h % RING, VO, k * P:(k + 1) * P],
                                         probsT[:, k, k * P:S], start=h == 0 and k == 0,
                                         stop=h == H - 1 and k == TB - 1)
                    if h == H - 1:
                        last.then_inc(y_done, 1)

                for n in range(FOLDS):
                    if n >= 2:
                        pe.wait_ge(fold_ready, n - 1)
                    for j in range(TB):
                        kind, h = (n * TB + j) // H, (n * TB + j) % H
                        left = w["qkv"][:, h, (W_QU, W_QC, W_VC)[kind], :]
                        right = w["out"][:, h, :] if kind == 2 else w["qkv"][:, h, (W_KU, W_KC)[kind], :]
                        last = pe.matmul(psJ[:, n % 2, j * P:(j + 1) * P], left, right, start=True, stop=True)
                    last.then_inc(fold_done, 1)
                pe.wait_ge(fold_ready, FOLDS)
                turn(pe, core, ln, 0, xn, psP, turned)
                tokens_of = lambda h: xT_next
                pe.wait_ge(xt_ready, 1)
                for kind in range(KINDS):
                    project(0, 0, kind, first=True)
                look_scores(0, 0, first=True)
                for kind in range(KINDS):
                    project(0, 1, kind)
                look_sums(0, 0)
                look_scores(0, 1)
                tokens_of = lambda h: xT if h < H else xT_next
                with pe.Fori(0, B) as b:
                    for h in range(H):
                        look_sums(b, h + 1)
                        scores(b, h)
                        if h + 2 == H:
                            pe.wait_ge(xt_ready, b + 2)
                        project(b, h + 2, 0)
                        for u in range(NU):
                            project(b, h + 2, u + 1)
                            turn_probs(b, h, u)
                        look_scores(b, h + 2)
                        if h == 0:
                            pe.wait_ge(added, b + 1)
                        weigh_values(b, h)
                        if h == TURN_AT:
                            turn(pe, core, ln, b + 1, xn, psP, turned)
                    pe.wait_ge(y_ready, b + 1)
                    for t in range(TB):
                        last = pe.transpose(psO[:, t * P:(t + 1) * P], yT[:, t * P:(t + 1) * P], core.ident)
                    last.then_inc(y_turned, 1)

            @block.vector
            def _(dve):
                def mask_look(b, h):
                    dve.wait_ge(look_tanh, b * H + h + 1)
                    dve.scalar_tensor_tensor(out=look[:, :].rearrange("p (t i) -> p t i", t=TB),
                                             in0=th_look[:, :].rearrange("p (t i) -> p t i", t=TB), scalar=1.0,
                                             in1=after, op0=ALU.add, op1=ALU.mult).then_inc(look_ready, 1)

                def lowering(b, h):
                    dve.wait_ge(sum_tanh, b * H + h + 1)
                    dve.scalar_tensor_tensor(out=lower[:, h % 2, :], in0=th_sum[:, :], scalar=1.0, in1=psD[:, :],
                                             op0=ALU.add, op1=ALU.mult).then_inc(lower_ready, 1)

                ln.vector(dve, 0, lambda t: core.X[:, t, :], lambda t: xn[:, t, :])
                mask_look(0, 0)
                lowering(0, 0)
                mask_look(0, 1)
                dve.wait_ge(xt_ready, 1)
                dve.tensor_copy(xT[:, :], xT_next[:, :]).then_inc(xt_moved, 1)
                dve.memset(inv[:, :], 0.0).then_inc(added, 1)
                dve.wait_ge(added, 1)
                with dve.Fori(0, B) as b:
                    def next_tokens(t):
                        return core.X[:, b * TB + TB + t, :]

                    for h in range(H):
                        c = Chain(dve, vec, b * (H * VEC) + h * VEC)
                        if h == LN_AT:
                            ln.statistics(dve, b + 1, next_tokens)
                        if h == LN_AT + 1:
                            ln.finish(dve, b + 1, next_tokens, lambda t: xn[:, t, :])
                        lowering(b, h + 1)
                        dve.wait_ge(lower_ready, b * H + h + 1)
                        for u in range(NU + 1):
                            if u < NU:
                                dve.wait_ge(scores_done, (b * H + h) * NU + u + 1)
                                for i, at in UNITS[u]:
                                    diag = psS[:, u, at + i * P:at + (i + 1) * P]
                                    c(dve.scalar_tensor_tensor(out=diag, in0=lower[:, h % 2, i * P:(i + 1) * P],
                                                               scalar=-0.5, in1=diag, op0=ALU.mult, op1=ALU.add))
                                c.wait()
                                for i, at in UNITS[u]:
                                    last = dve.tensor_reduce(neg_max[:, i:i + 1], psS[:, u, at:at + (i + 1) * P],
                                                             AX, ALU.max, negate=True)
                                last.then_inc(max_ready, 1)
                            if u >= 1:
                                dve.wait_ge(probs_ready, (b * H + h) * NU + u)
                                for i, at in UNITS[u - 1]:
                                    c(dve.reciprocal(inv[:, i:i + 1], sums[:, i:i + 1]))
                                c.wait()
                                for i, at in UNITS[u - 1]:
                                    row = probs[:, u - 1, at:at + (i + 1) * P]
                                    last = dve.tensor_scalar(row, row, inv[:, i:i + 1], None, ALU.mult)
                                last.then_inc(normed, 1)
                        assert c.n == VEC, c.n
                        mask_look(b, h + 2)
                    dve.tensor_copy(xT[:, :], xT_next[:, :]).then_inc(xt_moved, 1)
                    dve.wait_ge(y_turned, b + 1)
                    add_to_stream(dve, core, b, psO[:, :], added)
                    dve.wait_ge(added, b + 2)


def layer0_ffn(nc, core):
    DEPTH, H, DH, WIN = 2, 8, 64, 64
    HALF = D // 2
    HID = 341
    CH = (HID + P - 1) // P
    last_rows = HID - (CH - 1) * P
    K = WIN + P
    QK_SCALE = 8.0
    NU = TB * 2
    HU = H // 2
    NB = NU - 2
    KINDS = [(1, t) for t in range(TB)] + [(0, t) for t in range(TB)]
    NQK = len(KINDS)
    NPOOL = NQK - 2
    with ExitStack() as ctx:
        def sb(name, shape, dt=F32):
            return ctx.enter_context(nc.sbuf_tensor("L0f_" + name, shape, dt))

        def sem(name):
            return core.semaphore(ctx, "L0f_" + name)

        ln = LayerNorm(nc, ctx, "L0f_ln", core)
        w = core.w["L0f"]
        x = sb("x", [P, TB, D])
        h = sb("h", [P, TB, D])
        hT = sb("hT", [P, S])
        table = sb("table", [P, DEPTH, 2, 2, TB * DH])
        scratch = sb("scratch", [P, 2 * HU * K])
        squares = scratch[:, 0:2 * S].rearrange("p (j n) -> p j n", j=2)
        norms = sb("norms", [P, 2, TB, H])
        root = sb("root", [P, 2, TB, H])
        guess = sb("guess", [P, 2, TB, H])
        corr = sb("corr", [P, 2, TB, H])
        inv_norm = sb("inv_norm", [P, 2, TB, H])
        qk = sb("qk", [P, 2, TB, S])
        part = sb("part", [P, 2, S])
        qkT = sb("qkT", [P, 2, HU, S])
        v = sb("v", [P, TB, S])
        v_before = sb("v_before", [WIN, TB, S])
        neg_max = sb("neg_max", [P, TB, H])
        bias = sb("bias", [P, TB, H])
        sums = sb("sums", [P, TB, H])
        inv = sb("inv", [P, TB, H])
        probs = scratch[:, :].rearrange("p (j g k) -> p j g k", j=2, g=HU)
        own_T = qk[:, 1, 0:2, :]
        before_T = qk[0:WIN, 1, 2:4, :]
        o = part[:, 0, :]
        oT = part[:, 1, :]
        gelu = qk[:, 0, 0:CH, :]
        gated = qk[:, 1, 0:CH, :]
        psS = ctx.enter_context(nc.psum_tensor("L0f_psS", [P, 4, S], F32))
        psP = ctx.enter_context(nc.psum_tensor("L0f_psP", [P, 2, S], F32))
        psO = ctx.enter_context(nc.psum_tensor("L0f_psO", [P, S], F32))
        psX = ctx.enter_context(nc.psum_tensor("L0f_psX", [P, S], F32))
        (tables, shifted, half_ready, h_ready, turned, ht_ready, qk_done, squared, vec, v_done, v_ready, squares_used,
         rotated, before_loaded, norms_ready, rooted, inv_ready, k_scaled, q_late, qk_ready, qk_turned, qkt_ready, scores_done, bias_ready, probs_ready, own_turned, before_turned,
         own_ready, before_ready, av_done, o_ready, o_turned, ot_ready, y_done, x_ready, a_done, g_done, gelu_ready,
         gated_ready, out_done, added) = (sem(n) for n in (
             "tables shifted half_ready h_ready turned ht_ready qk_done squared vec v_done v_ready squares_used "
             "rotated before_loaded norms_ready rooted inv_ready k_scaled q_late qk_ready qk_turned qkt_ready scores_done bias_ready probs_ready own_turned before_turned "
             "own_ready before_ready av_done o_ready o_turned ot_ready y_done x_ready a_done g_done gelu_ready "
             "gated_ready out_done added").split())
        VEC = 2 * 20
        shift_in = core.cf[:, C_SHIFT:C_SHIFT + P]
        shift_over = core.cf[:, C_OVER:C_OVER + P]

        def rows(c):
            return P if c < CH - 1 else last_rows

        def halves(ap):
            return ap.rearrange("p (h a d) -> p h a d", h=H, a=2)

        def first_key(t):
            return WIN if t == 0 else 0

        def scores_of(n):
            return psS[:, 2 * (n % 2):2 * (n % 2) + 2, 0:2 * K].rearrange("p b (g k) -> p b g k", g=2)

        with nc.Block() as block:
            @block.sync
            def _(sp):
                load_layer1_weights(core, sp)
                for bl in range(B * DEPTH):
                    sp.wait_ge(v_ready, bl * TB + TB)
                    sp.dma_start(v_before[:, 1:TB, :], v[WIN:P, 0:TB - 1, :]).then_inc(before_loaded, 16)
                    sp.wait_ge(before_loaded, bl * 16 + 16)

            @block.gpsimd
            def _(pool):
                with pool.Fori(0, B * DEPTH) as bl:
                    def add_swapped(n):
                        j, t = KINDS[n]
                        pool.wait_ge(rotated, bl * NQK + n + 1)
                        pool.tensor_tensor(qk[:, j, t, :], qk[:, j, t, :], part[:, n % 2, :],
                                           ALU.add).then_inc(qk_ready, 1)

                    for n in range(TB):
                        add_swapped(n)
                    for t in range(TB):
                        k = qk[:, 1, t, :].rearrange("p (h d) -> p h d", h=H)
                        pool.wait_ge(qk_ready, bl * NPOOL + t + 1)
                        pool.wait_ge(inv_ready, bl * 2 + 1)
                        pool.tensor_tensor(k, k, inv_norm[:, 1, t, :].unsqueeze(2).to_broadcast([P, H, DH]),
                                           ALU.mult).then_inc(k_scaled, 1)
                        if TB + t < NPOOL:
                            add_swapped(TB + t)

            @block.scalar
            def _(act):
                core.wait_weights(act, "L0f")

                def shift_and_turn(b, s):
                    act.wait_ge(shifted, b * 4 + s + 1)
                    act.activation(h[:, :, HALF:D], psX[:, 0:TB * HALF].rearrange("p (t d) -> p t d", t=TB),
                                   ACT.Copy).then_inc(half_ready, 1)

                def roots(bl, j):
                    act.wait_ge(norms_ready, bl * 2 + (1 - j) + 1)
                    act.activation(root[:, j, :, :], norms[:, j, :, :], ACT.Sqrt).then_inc(rooted, 1)

                with act.Fori(0, B) as b:
                    ln.scalar(act, b * 3)
                    for l in range(DEPTH):
                        bl = b * DEPTH + l
                        shift_and_turn(b, 2 * l)
                        act.wait_ge(turned, bl * 2 + 1)
                        act.activation(hT[:, :], psX[:, :], ACT.Copy).then_inc(ht_ready, 1)
                        for n in range(NQK):
                            act.wait_ge(qk_done, bl * NQK + n + 1)
                            if n >= 2:
                                act.wait_ge(squares_used, bl * NQK + n - 1)
                            act.activation(squares[:, n % 2, :], psS[:, n % 4, :], ACT.Square).then_inc(squared, 1)
                            if n < TB:
                                act.wait_ge(v_done, bl * TB + n + 1)
                                act.activation(v[:, n, :], psP[:, n % 2, :], ACT.Copy).then_inc(v_ready, 1)
                            if n == TB:
                                roots(bl, 1)
                        for m in range(NQK):
                            if m == NQK // 2:
                                roots(bl, 0)
                            t = m // 2
                            act.wait_ge(qk_turned, bl * NQK + m + 1)
                            act.activation(qkT[:, 1 - m % 2, :, t * P:(t + 1) * P],
                                           (psX[:, :] if m % 2 else psP[:, t % 2, :]).rearrange("p (g k) -> p g k", g=HU),
                                           ACT.Copy).then_inc(qkt_ready, 1)
                        for n in range(NU + 3):
                            if n < NU:
                                t, half = n // 2, n % 2
                                act.wait_ge(bias_ready, bl * NU + n + 1)
                                if n >= 2:
                                    act.wait_ge(own_turned, bl * NU + n - 1)
                                if n >= 4:
                                    act.wait_ge(before_turned, bl * NB + n - 3)
                                for g in range(HU):
                                    hd, k0 = half * HU + g, first_key(t)
                                    last = act.activation(probs[:, n % 2, g, k0:K], scores_of(n)[:, g % 2, g // 2, k0:K],
                                                          ACT.Exp, bias=bias[:, t, hd:hd + 1],
                                                          scale=inv_norm[:, 0, t, hd:hd + 1],
                                                          accum_out=sums[:, t, hd:hd + 1])
                                last.then_inc(probs_ready, 1)
                            m = n - 1
                            if 2 <= m < NU:
                                act.wait_ge(before_turned, bl * NB + m - 1)
                                act.wait_ge(av_done, bl * NU + m - 1)
                                act.activation(before_T[:, m % 2, :], psP[0:WIN, 1, :],
                                               ACT.Copy).then_inc(before_ready, 1)
                            m = n - 3
                            if m >= 0 and m % 2:
                                act.wait_ge(o_turned, bl * TB + m // 2 + 1)
                                act.activation(oT, psX[:, :], ACT.Copy).then_inc(ot_ready, 1)
                        shift_and_turn(b, 2 * l + 1)
                        ln.scalar(act, b * 3 + 1 + l)
                        act.wait_ge(turned, bl * 2 + 2)
                        act.activation(hT[:, :], psX[:, :], ACT.Identity, bias=w["ln"][:, 2 * l + 1:2 * l + 2],
                                       scale=w["ln"][:, 2 * l:2 * l + 1]).then_inc(ht_ready, 1)
                        for c in range(CH):
                            act.wait_ge(g_done, bl * CH + c + 1)
                            col = w["b1"][0:rows(c), (l * 2 + 1) * CH + c:(l * 2 + 1) * CH + c + 1]
                            ps = psS[:, 3, :] if c == 0 else psP[:, c - 1, :]
                            act.activation(gelu[0:rows(c), c, :], ps[0:rows(c), :], ACT.Gelu,
                                           bias=col).then_inc(gelu_ready, 1)

            @block.tensor
            def _(pe):
                core.wait_weights(pe, "L0f")

                def shift(n_x, b):
                    pe.matmul(psX[:, 0:TB * HALF], shift_in, x[:, :, HALF:D], start=True, stop=False)
                    pe.matmul(psX[:, HALF:TB * HALF], shift_over, x[:, 0:TB - 1, HALF:D],
                              start=False, stop=True).then_inc(shifted, 1)

                def scores(bl, n):
                    t, half = n // 2, n % 2
                    k0 = first_key(t)
                    if n >= 2:
                        pe.wait_ge(probs_ready, bl * NU + n - 1)
                    for g in range(HU):
                        hd = half * HU + g
                        r = slice(DH * (hd % 2), DH * (hd % 2) + DH)
                        out = scores_of(n)[:, g % 2, g // 2, k0:K]
                        pe.matmul(out, qkT[r, 0, hd // 2, t * P:(t + 1) * P],
                                  qkT[r, 1, hd // 2, t * P - WIN + k0:(t + 1) * P], start=True, stop=False)
                        last = pe.matmul(out, core.identb[:, :], core.band[:, k0:K], start=False, stop=True)
                    last.then_inc(scores_done, 1)

                def turn_probs(bl, n):
                    t = n // 2
                    pe.wait_ge(probs_ready, bl * NU + n + 1)
                    if n >= 1:
                        pe.wait_ge(own_ready, bl * NU + n)
                    if n >= 3:
                        pe.wait_ge(before_ready, bl * NB + n - 2)
                    for g in range(HU):
                        last = pe.transpose(psP[:, 0, g * P:(g + 1) * P], probs[:, n % 2, g, WIN:K], core.ident)
                    last.then_inc(own_turned, 1)
                    if t >= 1:
                        for g in range(HU):
                            last = pe.transpose(psP[0:WIN, 1, g * P:(g + 1) * P], probs[:, n % 2, g, 0:WIN],
                                                core.ident)
                        last.then_inc(before_turned, 1)

                def weigh_values(bl, n):
                    t, half = n // 2, n % 2
                    pe.wait_ge(own_ready, bl * NU + n + 1)
                    if t >= 1:
                        pe.wait_ge(before_ready, bl * NB + n - 1)
                        pe.wait_ge(before_loaded, bl * 16 + 16)
                    if half == 0 and t >= 1:
                        pe.wait_ge(o_ready, bl * TB + t)
                    for g in range(HU):
                        hd = half * HU + g
                        out = psO[:, hd * DH:(hd + 1) * DH]
                        if t >= 1:
                            pe.matmul(out, before_T[:, n % 2, g * P:(g + 1) * P],
                                      v_before[:, t, hd * DH:(hd + 1) * DH], start=True, stop=False)
                        last = pe.matmul(out, own_T[:, n % 2, g * P:(g + 1) * P], v[:, t, hd * DH:(hd + 1) * DH],
                                         start=t == 0, stop=True)
                    last.then_inc(av_done, 1)

                def turn_out(bl, t):
                    pe.wait_ge(o_ready, bl * TB + t + 1)
                    if t >= 1:
                        pe.wait_ge(x_ready, bl * (TB + 1) + t)
                    for g in range(HU):
                        last = pe.transpose(psX[:, g * P:(g + 1) * P], o[:, g * P:(g + 1) * P], core.ident)
                    last.then_inc(o_turned, 1)

                def project_out(bl, l, t):
                    pe.wait_ge(ot_ready, bl * TB + t + 1)
                    for g in range(HU):
                        last = pe.matmul(psX[:, 0:D], oT[:, g * P:(g + 1) * P], w["wo"][:, l, g, :],
                                         start=g == 0, stop=g == HU - 1)
                    last.then_inc(y_done, 1)

                with pe.Fori(0, B) as b:
                    for l in range(DEPTH):
                        bl = b * DEPTH + l
                        if l == 0:
                            pe.wait_ge(ln.ready, b * (3 * TB) + TB)
                        else:
                            pe.wait_ge(x_ready, b * (2 * TB + 2) + TB + 1)
                        shift(0, b)
                        pe.wait_ge(h_ready, bl * 2 + 1)
                        pe.wait_ge(half_ready, bl * 2 + 1)
                        for t in range(TB):
                            last = pe.transpose(psX[:, t * P:(t + 1) * P], h[:, t, :], core.ident)
                        last.then_inc(turned, 1)
                        pe.wait_ge(ht_ready, bl * 2 + 1)
                        for n in range(NQK):
                            j, t = KINDS[n]
                            if n >= 4:
                                pe.wait_ge(rotated, bl * NQK + n - 3)
                                pe.wait_ge(squared, bl * NQK + n - 3)
                            pe.matmul(psS[:, n % 4, :], hT[:, t * P:(t + 1) * P], w["wqkv"][:, l, j, :],
                                      start=True, stop=True).then_inc(qk_done, 1)
                            if n < TB:
                                if n >= 2:
                                    pe.wait_ge(v_ready, bl * TB + n - 1)
                                pe.matmul(psP[:, n % 2, :], hT[:, n * P:(n + 1) * P], w["wqkv"][:, l, 2, :],
                                          start=True, stop=True).then_inc(v_done, 1)
                        pe.wait_ge(v_ready, bl * TB + TB)
                        for m in range(NQK):
                            t = m // 2
                            if m % 2:
                                if TB + t < NPOOL:
                                    pe.wait_ge(qk_ready, bl * NPOOL + TB + t + 1)
                                else:
                                    pe.wait_ge(q_late, bl * (NQK - NPOOL) + TB + t - NPOOL + 1)
                                if t >= 1:
                                    pe.wait_ge(qkt_ready, bl * NQK + m - 1)
                            else:
                                pe.wait_ge(k_scaled, bl * TB + t + 1)
                                if t >= 2:
                                    pe.wait_ge(qkt_ready, bl * NQK + m - 3)
                            for g in range(HU):
                                ps = psX[:, g * P:(g + 1) * P] if m % 2 else psP[:, t % 2, g * P:(g + 1) * P]
                                last = pe.transpose(ps, qk[:, 1 - m % 2, t, g * P:(g + 1) * P], core.ident)
                            last.then_inc(qk_turned, 1)
                        pe.wait_ge(qkt_ready, bl * 8 + 8)
                        for n in range(NU + 4):
                            if n < NU:
                                scores(bl, n)
                            if 0 <= n - 1 < NU:
                                turn_probs(bl, n - 1)
                            if 0 <= n - 2 < NU:
                                weigh_values(bl, n - 2)
                            if n - 3 >= 0 and (n - 3) % 2 and n - 3 < NU:
                                turn_out(bl, (n - 3) // 2)
                            if n - 4 >= 0 and (n - 4) % 2:
                                project_out(bl, l, (n - 4) // 2)
                        pe.wait_ge(x_ready, bl * (TB + 1) + TB)
                        shift(0, b)
                        for t in range(TB):
                            pe.wait_ge(ln.ready, b * (3 * TB) + (l + 1) * TB + t + 1)
                            last = pe.transpose(psX[:, t * P:(t + 1) * P], h[:, t, :], core.ident)
                        last.then_inc(turned, 1)
                        pe.wait_ge(ht_ready, bl * 2 + 2)
                        for c in range(CH):
                            ps = psS[:, 3, :] if c == 0 else psP[:, c - 1, :]
                            pe.matmul(ps[0:rows(c), :], w["w1"][:, l, HID + c * P:HID + c * P + rows(c)], hT[:, :],
                                      start=True, stop=True).then_inc(g_done, 1)
                            pe.matmul(psS[0:rows(c), c, :], w["w1"][:, l, c * P:c * P + rows(c)], hT[:, :],
                                      start=True, stop=True).then_inc(a_done, 1)
                        pe.wait_ge(gated_ready, bl * CH + CH)
                        for t in range(TB):
                            out = psO[:, t * P:(t + 1) * P]
                            for c in range(CH):
                                pe.matmul(out, gated[0:rows(c), c, t * P:(t + 1) * P], w["w2"][0:rows(c), l, c, :],
                                          start=c == 0, stop=False)
                            last = pe.matmul(out, core.ones_row, w["b2"][0:1, l, :], start=False, stop=True)
                        last.then_inc(out_done, 1)

            @block.vector
            def _(dve):
                core.wait_weights(dve, "L0f")
                for l in range(DEPTH):
                    for j in range(2):
                        for f in range(2):
                            last = dve.tensor_tensor(
                                table[:, l, j, f, :].rearrange("p (t d) -> p t d", t=TB),
                                w["pos"][:, j, f, :].rearrange("p (t d) -> p t d", t=TB),
                                w["scales"][:, l * 4 + j * 2 + f, :].unsqueeze(1).to_broadcast([P, TB, DH]), ALU.mult)
                last.then_inc(tables, 1)
                dve.wait_ge(tables, 1)

                def inverse(c, bl, j):
                    scale = 1.0 if j else QK_SCALE
                    dve.wait_ge(rooted, bl * 2 + (1 - j) + 1)
                    c(dve.reciprocal(guess[:, j, :, :], root[:, j, :, :]))
                    c.wait()
                    c(dve.tensor_tensor(corr[:, j, :, :], guess[:, j, :, :], guess[:, j, :, :], ALU.mult))
                    c.wait()
                    c(dve.tensor_tensor(corr[:, j, :, :], corr[:, j, :, :], norms[:, j, :, :], ALU.mult))
                    c.wait()
                    c(dve.tensor_scalar(corr[:, j, :, :], corr[:, j, :, :], -0.5 * scale, 1.5 * scale,
                                        ALU.mult, ALU.add))
                    c.wait()
                    dve.tensor_tensor(inv_norm[:, j, :, :], corr[:, j, :, :], guess[:, j, :, :],
                                      ALU.mult).then_inc(inv_ready, 1)

                with dve.Fori(0, B) as b:
                    ln.vector(dve, b * 3, lambda t: core.X[:, b * TB + t, :], lambda t: x[:, t, :])
                    c = Chain(dve, vec, b * VEC)
                    for l in range(DEPTH):
                        bl = b * DEPTH + l
                        if l == 0:
                            dve.wait_ge(ln.ready, b * (3 * TB) + TB)
                        dve.tensor_copy(h[:, :, 0:HALF], x[:, :, 0:HALF]).then_inc(h_ready, 1)
                        for n in range(NQK):
                            j, t = KINDS[n]
                            ps = psS[:, n % 4, :]
                            cos = table[:, l, j, 0, t * DH:(t + 1) * DH].unsqueeze(1).to_broadcast([P, H, DH])
                            sin = table[:, l, j, 1, t * DH:(t + 1) * DH].rearrange("p (a d) -> p a d", a=2)
                            dve.wait_ge(squared, bl * NQK + n + 1)
                            dve.tensor_reduce(norms[:, j, t, :], squares[:, n % 2, :].rearrange("p (h d) -> p h d", h=H),
                                              AX, ALU.add).then_inc(squares_used, 1)
                            dve.tensor_tensor(qk[:, j, t, :].rearrange("p (h d) -> p h d", h=H),
                                              ps.rearrange("p (h d) -> p h d", h=H), cos, ALU.mult)
                            if n >= 2:
                                dve.wait_ge(qk_ready, bl * NPOOL + n - 1)
                            for a in range(2):
                                last = dve.tensor_tensor(halves(part[:, n % 2, :])[:, :, a, :],
                                                         halves(ps)[:, :, 1 - a, :],
                                                         sin[:, a, :].unsqueeze(1).to_broadcast([P, H, DH // 2]),
                                                         ALU.mult)
                            last.then_inc(rotated, 1)
                            if n >= NPOOL:
                                dve.wait_ge(rotated, bl * NQK + n + 1)
                                dve.tensor_tensor(qk[:, j, t, :], qk[:, j, t, :], part[:, n % 2, :],
                                                  ALU.add).then_inc(q_late, 1)
                            if t == TB - 1:
                                dve.wait_ge(squares_used, bl * NQK + n + 1)
                                dve.tensor_scalar(norms[:, j, :, :], norms[:, j, :, :], 1e-24, None,
                                                  ALU.max).then_inc(norms_ready, 1)
                            if n == TB:
                                inverse(c, bl, 1)
                        inverse(c, bl, 0)
                        dve.wait_ge(inv_ready, bl * 2 + 2)
                        for n in range(NU + 4):
                            if n < NU:
                                t, half = n // 2, n % 2
                                hs = slice(half * HU, half * HU + HU)
                                dve.wait_ge(scores_done, bl * NU + n + 1)
                                c(dve.tensor_reduce(neg_max[:, t, hs].rearrange("p (g b) -> p b g", b=2),
                                                    scores_of(n)[:, :, :, first_key(t):K], AX, ALU.max, negate=True))
                                c.wait()
                                dve.tensor_tensor(bias[:, t, hs], neg_max[:, t, hs], inv_norm[:, 0, t, hs],
                                                  ALU.mult).then_inc(bias_ready, 1)
                            m = n - 1
                            if 0 <= m < NU:
                                dve.wait_ge(own_turned, bl * NU + m + 1)
                                if m >= 2:
                                    dve.wait_ge(av_done, bl * NU + m - 1)
                                dve.tensor_copy(own_T[:, m % 2, :], psP[:, 0, :]).then_inc(own_ready, 1)
                            m = n - 2
                            if m >= 0 and m % 2 and m < NU:
                                t = m // 2
                                dve.wait_ge(av_done, bl * NU + m + 1)
                                dve.wait_ge(probs_ready, bl * NU + m + 1)
                                if t >= 1:
                                    dve.wait_ge(o_turned, bl * TB + t)
                                c(dve.reciprocal(inv[:, t, :], sums[:, t, :]))
                                c.wait()
                                dve.tensor_tensor(o.rearrange("p (h d) -> p h d", h=H),
                                                  psO[:, :].rearrange("p (h d) -> p h d", h=H),
                                                  inv[:, t, :].unsqueeze(2).to_broadcast([P, H, DH]),
                                                  ALU.mult).then_inc(o_ready, 1)
                            m = n - 4
                            if m >= 0 and m % 2:
                                t = m // 2
                                dve.wait_ge(y_done, bl * TB + t + 1)
                                dve.tensor_tensor(x[:, t, :], x[:, t, :], psX[:, 0:D], ALU.add).then_inc(x_ready, 1)
                        dve.wait_ge(x_ready, bl * (TB + 1) + TB)
                        dve.tensor_copy(h[:, :, 0:HALF], x[:, :, 0:HALF]).then_inc(h_ready, 1)
                        dve.wait_ge(h_ready, bl * 2 + 2)
                        dve.wait_ge(half_ready, bl * 2 + 2)
                        ln.vector(dve, b * 3 + 1 + l, lambda t: h[:, t, :], lambda t: h[:, t, :])
                        for k in range(CH):
                            r = rows(k)
                            dve.wait_ge(gelu_ready, bl * CH + k + 1)
                            dve.wait_ge(a_done, bl * CH + k + 1)
                            dve.scalar_tensor_tensor(out=gated[0:r, k, :], in0=psS[0:r, k, :],
                                                     scalar=w["b1"][0:r, l * 2 * CH + k:l * 2 * CH + k + 1],
                                                     in1=gelu[0:r, k, :], op0=ALU.add,
                                                     op1=ALU.mult).then_inc(gated_ready, 1)
                        dve.wait_ge(out_done, bl + 1)
                        dve.tensor_tensor(x[:, :, :], x[:, :, :], psO[:, :].rearrange("p (t d) -> p t d", t=TB),
                                          ALU.add).then_inc(x_ready, 1)
                        dve.wait_ge(x_ready, bl * (TB + 1) + TB + 1)
                    xb = core.X[:, bass.ds(b * TB, TB), :]
                    dve.tensor_tensor(xb, xb, x[:, :, :], ALU.add).then_inc(added, 1)
                    dve.wait_ge(added, b + 1)
                    assert c.n == VEC, c.n


def layer2_ffn(nc, core):
    E, TOPK = 8, 64
    PAIRS = E // 2
    ROT = 32
    SCALE = float(D) ** -0.5
    G = D + 2 * ROT
    BP = P // B
    TOP = 23
    with ExitStack() as ctx:
        def sb(name, shape, dt=F32):
            return ctx.enter_context(nc.sbuf_tensor("L2f_" + name, shape, dt))

        def sem(name):
            return core.semaphore(ctx, "L2f_" + name)

        ln = LayerNorm(nc, ctx, "L2f_ln", core)
        w = core.w["L2f"]
        xg = sb("xg", [P, NT, G])
        xT = sb("xT", [P, S])
        score = sb("score", [P, S])
        work = sb("work", [P, S])
        top8 = sb("top8", [P, 8])
        chosen = sb("chosen", [P, S])
        rank = sb("rank", [P, S])
        rankT = sb("rankT", [P, TB, P + BP])
        scoreT = sb("scoreT", [P, TB, P + BP])
        (turned, xt_ready, logits_done, exp_ready, top, angles, rank_turned, rank_ready) = (
            sem(n) for n in "turned xt_ready logits_done exp_ready top angles rank_turned rank_ready".split())
        with ExitStack() as first:
            psT = first.enter_context(nc.psum_tensor("L2f_psT", [P, S], F32))
            psL = first.enter_context(nc.psum_tensor("L2f_psL", [P, S], F32))
            psK = first.enter_context(nc.psum_tensor("L2f_psK", [P, 2, S], F32))
            with nc.Block() as block:
                @block.gpsimd
                def _(pool):
                    core.wait_weights(pool, "L2f")
                    pool.memset(rankT[:, :, P:P + BP], 0.0)
                    pool.memset(scoreT[:, :, P:P + BP], 0.0)
                    for b in range(B):
                        last = pool.tensor_copy(xg[:, b * TB:(b + 1) * TB, D:G], w["angles"])
                    last.then_inc(angles, 1)

                @block.scalar
                def _(act):
                    core.wait_weights(act, "L2f")
                    for b in range(B):
                        ln.scalar(act, b)
                        act.wait_ge(turned, b + 1)
                        act.activation(xT[:, :], psT[:, :], ACT.Copy).then_inc(xt_ready, 1)
                        act.wait_ge(logits_done, b + 1)
                        if b == 0:
                            act.wait_ge(top, 1)
                        act.activation(score[b * BP:b * BP + E, :], psL[b * BP:b * BP + E, :], ACT.Exp,
                                       scale=-1.0).then_inc(exp_ready, 1)
                    for j, dst in enumerate((rankT, scoreT)):
                        act.wait_ge(rank_turned, j + 1)
                        act.activation(dst[:, :, 0:P], psK[:, j, :].rearrange("p (t r) -> p t r", t=TB),
                                       ACT.Copy).then_inc(rank_ready, 1)

                @block.tensor
                def _(pe):
                    core.wait_weights(pe, "L2f")
                    for b in range(B):
                        for t in range(TB):
                            pe.wait_ge(ln.ready, b * TB + t + 1)
                            last = pe.transpose(psT[:, t * P:(t + 1) * P], xg[:, b * TB + t, 0:D], core.ident)
                        last.then_inc(turned, 1)
                        pe.wait_ge(xt_ready, b + 1)
                        pe.matmul(psL[b * BP:b * BP + E, :], w["router"], xT[:, :],
                                  start=True, stop=True).then_inc(logits_done, 1)
                    for j, src in enumerate((rank, score)):
                        if j == 0:
                            pe.wait_ge(top, TOP)
                        for t in range(TB):
                            last = pe.transpose(psK[:, j, t * P:(t + 1) * P], src[:, t * P:(t + 1) * P], core.ident)
                        last.then_inc(rank_turned, 1)

                @block.vector
                def _(dve):
                    c = Chain(dve, top)
                    c(dve.memset(score[:, :], 0.0))
                    for b in range(B):
                        ln.vector(dve, b, lambda t: core.X[:, b * TB + t, :], lambda t: xg[:, b * TB + t, 0:D])
                    dve.wait_ge(exp_ready, B)
                    c(dve.tensor_scalar(score[:, :], score[:, :], 1.0, None, ALU.add))
                    c.wait()
                    c(dve.reciprocal(score[:, :], score[:, :]))
                    c.wait()
                    c(dve.tensor_copy(work[:, :], score[:, :]))
                    for _ in range(TOPK // 8):
                        c.wait()
                        c(dve.max(top8[:, :], work[:, :]))
                        c.wait()
                        c(dve.match_replace(work[:, :], top8[:, :], work[:, :], -1.0))
                    c.wait()
                    c(dve.tensor_scalar(chosen[:, :], work[:, :], -1.0, None, ALU.is_equal))
                    c.wait()
                    c(dve.tensor_tensor_scan(rank[:, :], chosen[:, :], chosen[:, :], 0.0, ALU.add, ALU.max))
                    c.wait()
                    c(dve.tensor_tensor(rank[:, :], rank[:, :], chosen[:, :], ALU.mult))
                    assert c.n == TOP, c.n
        onehot = sb("onehot", [P, TB, E * TOPK])
        weighted = sb("weighted", [P, TB, E * TOPK])
        weightedT = sb("weightedT", [P, PAIRS, S])
        taken = sb("taken", [P, PAIRS, G])
        takenT = sb("takenT", [P, S])
        qk = sb("qk", [P, PAIRS, 2, D])
        v = sb("v", [P, PAIRS, D])
        part = sb("part", [P, 2, PAIRS, 2 * ROT])
        qkT = sb("qkT", [P, 2, S])
        neg_max = sb("neg_max", [P, PAIRS])
        sums = sb("sums", [P, PAIRS])
        inv = sb("inv", [P, PAIRS])
        probs = sb("probs", [P, S])
        probsT = sb("probsT", [P, S])
        avT = sb("avT", [P, S])
        result = sb("result", [P, PAIRS, D])
        psA = ctx.enter_context(nc.psum_tensor("L2f_psA", [P, 2, S], F32))
        psQ = ctx.enter_context(nc.psum_tensor("L2f_psQ", [P, PAIRS, S], F32))
        psT = ctx.enter_context(nc.psum_tensor("L2f_psT2", [P, S], F32))
        psS = ctx.enter_context(nc.psum_tensor("L2f_psS", [P, S], F32))
        (onehot_ready, weighted_ready, taken_done, taken_ready, weights_turned, wt_ready, taken_turned, tt_ready,
         qkv_done, rest_ready, vec, rot_ready, qk_turned, qkt_ready, scores_done, bias_ready, probs_ready,
         probs_turned, pt_ready, av_done, av_ready, result_done, result_ready, out_done, added) = (
            sem(n) for n in (
                "onehot_ready weighted_ready taken_done taken_ready weights_turned wt_ready taken_turned tt_ready "
                "qkv_done rest_ready vec rot_ready qk_turned qkt_ready scores_done bias_ready probs_ready "
                "probs_turned pt_ready av_done av_ready result_done result_ready out_done added").split())
        VEC = 8
        count_up = core.cf[:, C_COUNT:C_COUNT + TOPK].unsqueeze(1).to_broadcast([P, E, TOPK])
        with nc.Block() as block:
            @block.scalar
            def _(act):
                with act.Fori(0, B) as b:
                    for j in range(2):
                        act.wait_ge(taken_done, b * 2 + j + 1)
                        act.activation(taken[:, 2 * j:2 * j + 2, :],
                                       psA[:, j, 0:2 * G].rearrange("p (a g) -> p a g", a=2),
                                       ACT.Copy).then_inc(taken_ready, 1)
                    for t in range(TB):
                        act.wait_ge(weights_turned, b * TB + t + 1)
                        act.activation(weightedT[:, :, t * P:(t + 1) * P],
                                       psQ[:, t, :].rearrange("p (a k) -> p a k", a=PAIRS),
                                       ACT.Copy).then_inc(wt_ready, 1)
                    act.wait_ge(taken_turned, b + 1)
                    act.activation(takenT[:, :], psT[:, :], ACT.Copy).then_inc(tt_ready, 1)
                    act.wait_ge(qkv_done, b + 1)
                    for j in range(2):
                        act.activation(qk[:, :, j, 2 * ROT:D], psQ[:, :, j * D + 2 * ROT:(j + 1) * D], ACT.Copy)
                    act.activation(v[:, :, :], psQ[:, :, 2 * D:3 * D], ACT.Copy).then_inc(rest_ready, 1)
                    for j in range(2):
                        act.wait_ge(qk_turned, b * 2 + j + 1)
                        act.activation(qkT[:, j, :], psA[:, j, :], ACT.Copy).then_inc(qkt_ready, 1)
                    act.wait_ge(bias_ready, b + 1)
                    for a in range(PAIRS):
                        last = act.activation(probs[:, a * P:(a + 1) * P], psS[:, a * P:(a + 1) * P], ACT.Exp,
                                              bias=neg_max[:, a:a + 1], scale=SCALE, accum_out=sums[:, a:a + 1])
                    last.then_inc(probs_ready, 1)
                    act.wait_ge(probs_turned, b + 1)
                    act.activation(probsT[:, :], psT[:, :], ACT.Copy).then_inc(pt_ready, 1)
                    act.wait_ge(av_done, b + 1)
                    act.activation(avT[:, :], psS[:, :], ACT.Copy).then_inc(av_ready, 1)

            @block.tensor
            def _(pe):
                with pe.Fori(0, B) as b:
                    pe.wait_ge(onehot_ready, b + 1)
                    pe.wait_ge(added, b + 1)
                    for a in range(PAIRS):
                        for t in range(TB):
                            last = pe.matmul(psA[:, a // 2, (a % 2) * G:(a % 2 + 1) * G],
                                             onehot[:, t, a * P:(a + 1) * P], xg[:, b * TB + t, :],
                                             start=t == 0, stop=t == TB - 1)
                        if a % 2:
                            last.then_inc(taken_done, 1)
                    pe.wait_ge(weighted_ready, b + 1)
                    for t in range(TB):
                        for a in range(PAIRS):
                            last = pe.transpose(psQ[:, t, a * P:(a + 1) * P], weighted[:, t, a * P:(a + 1) * P],
                                                core.ident)
                        last.then_inc(weights_turned, 1)
                    pe.wait_ge(taken_ready, b * 2 + 2)
                    for a in range(PAIRS):
                        last = pe.transpose(psT[:, a * P:(a + 1) * P], taken[:, a, 0:D], core.ident)
                    last.then_inc(taken_turned, 1)
                    pe.wait_ge(tt_ready, b + 1)
                    pe.wait_ge(wt_ready, (b + 1) * TB)
                    for e in range(E):
                        r = TOPK * (e % 2)
                        last = pe.matmul(psQ[r:r + TOPK, e // 2, 0:3 * D], takenT[:, e * TOPK:(e + 1) * TOPK],
                                         w["qkv"][:, e, :], start=True, stop=True)
                    last.then_inc(qkv_done, 1)
                    pe.wait_ge(rest_ready, b + 1)
                    for j in range(2):
                        pe.wait_ge(rot_ready, b * 2 + j + 1)
                        for a in range(PAIRS):
                            last = pe.transpose(psA[:, j, a * P:(a + 1) * P], qk[:, a, j, :], core.ident)
                        last.then_inc(qk_turned, 1)
                    pe.wait_ge(qkt_ready, b * 2 + 2)
                    for a in range(PAIRS):
                        blk = slice(a * P, (a + 1) * P)
                        pe.matmul(psS[:, blk], qkT[:, 0, blk], qkT[:, 1, blk], start=True, stop=False)
                        last = pe.matmul(psS[:, blk], core.identb[:, :], core.pair_mask[:, :], start=False, stop=True)
                    last.then_inc(scores_done, 1)
                    pe.wait_ge(probs_ready, b + 1)
                    for a in range(PAIRS):
                        last = pe.transpose(psT[:, a * P:(a + 1) * P], probs[:, a * P:(a + 1) * P], core.ident)
                    last.then_inc(probs_turned, 1)
                    pe.wait_ge(pt_ready, b + 1)
                    for a in range(PAIRS):
                        blk = slice(a * P, (a + 1) * P)
                        last = pe.matmul(psS[:, blk], v[:, a, :], probsT[:, blk], start=True, stop=True)
                    last.then_inc(av_done, 1)
                    pe.wait_ge(av_ready, b + 1)
                    for e in range(E):
                        r = TOPK * (e % 2)
                        last = pe.matmul(psA[r:r + TOPK, 0, (e // 2) * D:(e // 2 + 1) * D],
                                         avT[:, e * TOPK:(e + 1) * TOPK], w["out"][:, e, :], start=True, stop=True)
                    last.then_inc(result_done, 1)
                    pe.wait_ge(result_ready, b + 1)
                    for t in range(TB):
                        for a in range(PAIRS):
                            last = pe.matmul(psA[:, 1, t * P:(t + 1) * P], weightedT[:, a, t * P:(t + 1) * P],
                                             result[:, a, :], start=a == 0, stop=a == PAIRS - 1)
                    last.then_inc(out_done, 1)

            @block.vector
            def _(dve):
                def make_onehots(b):
                    for t in range(TB):
                        last = dve.tensor_tensor(
                            onehot[:, t, :].rearrange("p (e k) -> p e k", e=E), count_up,
                            rankT[:, t, bass.ds(b * BP, E)].unsqueeze(2).to_broadcast([P, E, TOPK]), ALU.is_equal)
                    last.then_inc(onehot_ready, 1)
                    dve.wait_ge(onehot_ready, b + 1)
                    for t in range(TB):
                        last = dve.tensor_tensor(
                            weighted[:, t, :].rearrange("p (e k) -> p e k", e=E),
                            onehot[:, t, :].rearrange("p (e k) -> p e k", e=E),
                            scoreT[:, t, bass.ds(b * BP, E)].unsqueeze(2).to_broadcast([P, E, TOPK]), ALU.mult)
                    last.then_inc(weighted_ready, 1)

                dve.wait_ge(rank_ready, 2)
                make_onehots(0)
                dve.memset(inv[:, :], 0.0).then_inc(added, 1)
                dve.wait_ge(added, 1)
                with dve.Fori(0, B) as b:
                    c = Chain(dve, vec, b * VEC)
                    dve.wait_ge(rest_ready, b + 1)
                    dve.wait_ge(taken_ready, b * 2 + 2)
                    cos = taken[:, :, D:D + ROT].unsqueeze(2).to_broadcast([P, PAIRS, 2, ROT])
                    sin = taken[:, :, D + ROT:G]
                    for j in range(2):
                        src = psQ[:, :, j * D:j * D + 2 * ROT]
                        dst = qk[:, :, j, 0:2 * ROT]
                        c(dve.tensor_tensor(dst.rearrange("p a (h r) -> p a h r", h=2),
                                            src.rearrange("p a (h r) -> p a h r", h=2), cos, ALU.mult))
                        c(dve.scalar_tensor_tensor(out=part[:, j, :, 0:ROT], in0=src[:, :, ROT:2 * ROT], scalar=-1.0,
                                                   in1=sin, op0=ALU.mult, op1=ALU.mult))
                        c(dve.tensor_tensor(part[:, j, :, ROT:2 * ROT], src[:, :, 0:ROT], sin, ALU.mult))
                        c.wait()
                        dve.tensor_tensor(dst, dst, part[:, j, :, :], ALU.add).then_inc(rot_ready, 1)
                    dve.wait_ge(scores_done, b + 1)
                    c(dve.tensor_reduce(neg_max[:, :], psS[:, :].rearrange("p (a k) -> p a k", a=PAIRS), AX,
                                        ALU.max, negate=True))
                    c.wait()
                    dve.tensor_scalar(neg_max[:, :], neg_max[:, :], SCALE, None, ALU.mult).then_inc(bias_ready, 1)
                    dve.wait_ge(weights_turned, (b + 1) * TB)
                    make_onehots(b + 1)
                    dve.wait_ge(probs_ready, b + 1)
                    c(dve.reciprocal(inv[:, :], sums[:, :]))
                    dve.wait_ge(result_done, b + 1)
                    c.wait()
                    dve.tensor_tensor(result[:, :, :], psA[:, 0, :].rearrange("p (a d) -> p a d", a=PAIRS),
                                      inv[:, :].unsqueeze(2).to_broadcast([P, PAIRS, D]),
                                      ALU.mult).then_inc(result_ready, 1)
                    dve.wait_ge(out_done, b + 1)
                    add_to_stream(dve, core, b, psA[:, 1, :], added)
                    dve.wait_ge(added, b + 2)
                    assert c.n == VEC, c.n


def layer3_ffn(nc, core):
    E, INTER, TOPK, CAP = 64, 96, 8, 32
    T = B * S
    PER = P // CAP
    TILES = E // PER
    ROW = D + E
    TB_BANKS = NT // 4
    with ExitStack() as ctx:
        def sb(name, shape, dt=F32):
            return ctx.enter_context(nc.sbuf_tensor("L3f_" + name, shape, dt))

        def sem(name):
            return core.semaphore(ctx, "L3f_" + name)

        ln = LayerNorm(nc, ctx, "L3f_ln", core)
        w = core.w["L3f"]
        rows = nc.dram_tensor("L3f_rows", (T + 1, ROW), F32, kind="Internal").ap()
        xg = sb("xg", [P, NT, ROW])
        empty = sb("empty", [1, ROW])
        xT = sb("xT", [P, S])
        neg_max = sb("neg_max", [P, TB])
        numer = sb("numer", [P, TB, E])
        best = sb("best", [P, TB, TOPK])
        struck = sb("struck", [P, TB, E])
        denom = sb("denom", [P, TB])
        inv = sb("inv", [P, TB])
        key = sb("key", [P, TB, E])
        keyT = sb("keyT", [E, T])
        first = sb("first", [E, CAP])
        firstT = sb("firstT", [CAP, E])
        token_of = sb("token_of", [P, TILES])
        token_idx = sb("token_idx", [P, TILES], U32)
        taken = sb("taken", [P, TILES * (ROW + PER) + D])
        count = sb("count", [P, T])
        onehot = sb("onehot", [P, 2, T])
        takenT = sb("takenT", [P, P])
        th = sb("th", [P, INTER])
        act_up = sb("act_up", [P, 2, INTER])
        hiddenT = sb("hiddenT", [INTER, P])
        gate_pick = sb("gate_pick", [P, PER])
        gate = sb("gate", [P, TILES])
        y = sb("y", [P, TILES, D])

        (turned, xt_ready, logits_done, max_ready, exp_ready, vec, key_ready, key_turned, kt_ready, rows_ready,
         rows_stored, empty_ready, first_turned, ft_ready, places_done, idx_ready, counted, mark) = (
            sem(n) for n in (
                "turned xt_ready logits_done max_ready exp_ready vec key_ready key_turned kt_ready rows_ready "
                "rows_stored empty_ready first_turned ft_ready places_done idx_ready counted mark").split())
        gathered = [sem(f"gathered{j}") for j in range(TILES)]
        VEC = 12
        MARK = 8

        def taken_row(j):
            return taken[:, j * ROW:(j + 1) * ROW]

        with ExitStack() as routing:
            psT = routing.enter_context(nc.psum_tensor("L3f_psT", [P, S], F32))
            psL = routing.enter_context(nc.psum_tensor("L3f_psL", [P, S], F32))
            psK = routing.enter_context(nc.psum_tensor("L3f_psK", [P, S], F32))
            psF = routing.enter_context(nc.psum_tensor("L3f_psF", [P, S], F32))
            psN = routing.enter_context(nc.psum_tensor("L3f_psN", [P, S], F32))
            with nc.Block() as block:
                @block.sync
                def _(sp):
                    sp.wait_ge(empty_ready, 1)
                    sp.dma_start(rows[T:T + 1, :], empty[:, :]).then_inc(rows_stored, 16)
                    for b in range(B):
                        sp.wait_ge(rows_ready, b + 1)
                        sp.dma_start(rows[b * S:(b + 1) * S, :].rearrange("(t p) g -> p t g", p=P),
                                     xg[:, b * TB:(b + 1) * TB, :]).then_inc(rows_stored, 16)

                @block.gpsimd
                def _(pool):
                    pool.memset(empty[:, :], 0.0).then_inc(empty_ready, 1)
                    pool.iota(onehot[:, 0, :].bitcast(mybir.dt.int32), [[1, T]], base=0,
                              channel_multiplier=0).then_inc(counted, 1)
                    pool.wait_ge(counted, 1)
                    pool.tensor_copy(count[:, :], onehot[:, 0, :].bitcast(mybir.dt.int32)).then_inc(counted, 1)
                    pool.wait_ge(rows_stored, 16 * (B + 1))
                    pool.wait_ge(idx_ready, 1)
                    for j in range(TILES):
                        pool.indirect_dma_start(
                            out=taken_row(j), out_offset=None, in_=rows[:, :],
                            in_offset=bass.IndirectOffsetOnAxis(ap=token_idx[:, j:j + 1], axis=0),
                        ).then_inc(gathered[j], 16)

                @block.scalar
                def _(act):
                    core.wait_weights(act, "L3g")
                    for b in range(B):
                        ln.scalar(act, b)
                        act.wait_ge(turned, b + 1)
                        act.activation(xT[:, :], psT[:, :], ACT.Copy).then_inc(xt_ready, 1)
                        act.wait_ge(max_ready, b + 1)
                        for t in range(TB):
                            last = act.activation(numer[:, t, :], psL[:, t * E:(t + 1) * E], ACT.Exp,
                                                  bias=neg_max[:, t:t + 1])
                        last.then_inc(exp_ready, 1)
                        act.wait_ge(key_turned, b + 1)
                        act.activation(keyT[:, b * S:(b + 1) * S], psK[0:E, :], ACT.Copy).then_inc(kt_ready, 1)

                @block.tensor
                def _(pe):
                    core.wait_weights(pe, "L3g")
                    for b in range(B):
                        for t in range(TB):
                            pe.wait_ge(ln.ready, b * TB + t + 1)
                            last = pe.transpose(psT[:, t * P:(t + 1) * P], xg[:, b * TB + t, 0:D], core.ident)
                        last.then_inc(turned, 1)
                        pe.wait_ge(xt_ready, b + 1)
                        if b >= 1:
                            pe.wait_ge(exp_ready, b)
                        for t in range(TB):
                            last = pe.matmul(psL[:, t * E:(t + 1) * E], xT[:, t * P:(t + 1) * P],
                                             core.w["L3g"]["router"], start=True, stop=True)
                        last.then_inc(logits_done, 1)
                        pe.wait_ge(key_ready, b + 1)
                        if b >= 1:
                            pe.wait_ge(kt_ready, b)
                        for t in range(TB):
                            last = pe.transpose(psK[0:E, t * P:(t + 1) * P], key[:, t, :], core.ident)
                        last.then_inc(key_turned, 1)
                    pe.wait_ge(mark, MARK)
                    pe.transpose(psF[0:CAP, 0:E], first[:, :], core.ident[0:E, 0:E]).then_inc(first_turned, 1)
                    pe.wait_ge(ft_ready, 1)
                    for r in range(PER):
                        last = pe.matmul(psN[r * CAP:(r + 1) * CAP, 0:TILES], core.ident[0:CAP, 0:CAP],
                                         firstT[:, r:E:PER], start=True, stop=True)
                    last.then_inc(places_done, 1)

                @block.vector
                def _(dve):
                    core.wait_weights(dve, "L3g")
                    for b in range(B):
                        ln.vector(dve, b, lambda t: core.X[:, b * TB + t, :], lambda t: xg[:, b * TB + t, 0:D])
                        c = Chain(dve, vec, b * VEC)
                        dve.wait_ge(logits_done, b + 1)
                        if b >= 1:
                            dve.wait_ge(exp_ready, b)
                        dve.tensor_reduce(neg_max[:, :], psL[:, 0:TB * E].rearrange("p (t e) -> p t e", t=TB), AX,
                                          ALU.max, negate=True).then_inc(max_ready, 1)
                        dve.wait_ge(exp_ready, b + 1)
                        for t in range(TB):
                            c(dve.max(best[:, t, :], numer[:, t, :]))
                        c.wait()
                        for t in range(TB):
                            c(dve.match_replace(struck[:, t, :], best[:, t, :], numer[:, t, :], -1.0))
                        c(dve.tensor_reduce(denom[:, :], best[:, :, :], AX, ALU.add))
                        c.wait()
                        c(dve.reciprocal(inv[:, :], denom[:, :]))
                        if b >= 1:
                            dve.wait_ge(key_turned, b)
                        ahead = core.cf[:, C_AHEAD + b * TB:C_AHEAD + (b + 1) * TB]
                        dve.scalar_tensor_tensor(out=key[:, :, :], in0=struck[:, :, :], scalar=-1.0,
                                                 in1=ahead.unsqueeze(2).to_broadcast([P, TB, E]),
                                                 op0=ALU.is_equal, op1=ALU.mult).then_inc(key_ready, 1)
                        gates = xg[:, b * TB:(b + 1) * TB, D:ROW]
                        c(dve.scalar_tensor_tensor(out=gates, in0=struck[:, :, :], scalar=-1.0, in1=numer[:, :, :],
                                                   op0=ALU.is_equal, op1=ALU.mult))
                        c.wait()
                        c(dve.tensor_tensor(gates, gates, inv[:, :].unsqueeze(2).to_broadcast([P, TB, E]), ALU.mult))
                        c.wait()
                        dve.wait_ge(ln.ready, (b + 1) * TB)
                        dve.wait_ge(key_ready, b + 1)
                        dve.memset(neg_max[:, 0:1], 0.0).then_inc(rows_ready, 1)
                        dve.wait_ge(rows_ready, b + 1)
                        assert c.n == VEC, c.n
                    dve.wait_ge(kt_ready, B)
                    c = Chain(dve, mark)
                    for k in range(CAP // 8):
                        c(dve.max(first[:, 8 * k:8 * k + 8], keyT[:, :]))
                        c.wait()
                        if k < CAP // 8 - 1:
                            c(dve.match_replace(keyT[:, :], first[:, 8 * k:8 * k + 8], keyT[:, :], 0.0))
                            c.wait()
                    c(dve.tensor_scalar(first[:, :], first[:, :], -1.0, float(T), ALU.mult, ALU.add))
                    assert c.n == MARK, c.n
                    dve.wait_ge(first_turned, 1)
                    dve.tensor_copy(firstT[:, :], psF[0:CAP, 0:E]).then_inc(ft_ready, 1)
                    dve.wait_ge(places_done, 1)
                    c(dve.tensor_copy(token_of[:, :], psN[:, 0:TILES]))
                    c.wait()
                    dve.tensor_copy(token_idx[:, :], token_of[:, :]).then_inc(idx_ready, 1)

        psC = ctx.enter_context(nc.psum_tensor("L3f_psC", [P, TB_BANKS, S], F32))
        psG, psH, psU, psY = (ctx.enter_context(nc.psum_tensor("L3f_ps" + c, [P, S], F32)) for c in "GHUY")
        (taken_turned, tt_ready, h_done, tanh_ready, steps, hidden_ready, hidden_turned, ht_ready, y_done, gate_ready,
         y_ready, onehot_ready, combined, summed) = (sem(n) for n in (
             "taken_turned tt_ready h_done tanh_ready steps hidden_ready hidden_turned ht_ready y_done gate_ready "
             "y_ready onehot_ready combined summed").split())
        with nc.Block() as block:
            @block.scalar
            def _(act):
                for j in range(TILES):
                    act.wait_ge(taken_turned, j + 1)
                    if j >= 1:
                        act.wait_ge(h_done, j)
                    act.activation(takenT[:, :], psG[:, 0:P], ACT.Copy).then_inc(tt_ready, 1)
                    act.wait_ge(h_done, j + 1)
                    if j >= 1:
                        act.wait_ge(hidden_ready, j)
                    act.activation(th[:, :], psH[:, 0:INTER], ACT.Tanh, scale=0.5).then_inc(tanh_ready, 1)
                    act.wait_ge(hidden_turned, j + 1)
                    if j >= 1:
                        act.wait_ge(y_done, j)
                    act.activation(hiddenT[:, :], psU[0:INTER, 0:P], ACT.Copy).then_inc(ht_ready, 1)

            @block.tensor
            def _(pe):
                core.wait_weights(pe, "L3f")

                def turn_taken(j):
                    pe.wait_ge(gathered[j], 16)
                    if j >= 1:
                        pe.wait_ge(tt_ready, j)
                    pe.transpose(psG[:, 0:P], taken_row(j)[:, 0:D], core.ident).then_inc(taken_turned, 1)

                def combine(j, part):
                    if part == 0:
                        pe.wait_ge(onehot_ready, j + 1)
                        pe.wait_ge(y_ready, j + 1)
                    for t in range(part * 4, part * 4 + 4):
                        last = pe.matmul(psC[:, t // 4, (t % 4) * P:(t % 4 + 1) * P],
                                         onehot[:, j % 2, t * P:(t + 1) * P], y[:, j, :],
                                         start=j == 0 and t % 4 == 0, stop=j == TILES - 1, skip_group_check=True)
                    if part == 3:
                        last.then_inc(combined, 1)

                turn_taken(0)
                for j in range(TILES):
                    pe.wait_ge(tt_ready, j + 1)
                    if j >= 1:
                        pe.wait_ge(hidden_ready, j)
                    for r in range(PER):
                        last = pe.matmul(psH[r * CAP:(r + 1) * CAP, 0:2 * INTER], takenT[:, r * CAP:(r + 1) * CAP],
                                         w["gate_up"][:, j * PER + r, :], start=True, stop=True)
                    last.then_inc(h_done, 1)
                    if j + 1 < TILES:
                        turn_taken(j + 1)
                    if j >= 1:
                        combine(j - 1, 0)
                        combine(j - 1, 1)
                    pe.wait_ge(hidden_ready, j + 1)
                    if j >= 1:
                        pe.wait_ge(ht_ready, j)
                    pe.transpose(psU[0:INTER, 0:P], act_up[:, 1, :], core.ident).then_inc(hidden_turned, 1)
                    if j >= 1:
                        combine(j - 1, 2)
                        combine(j - 1, 3)
                    pe.wait_ge(ht_ready, j + 1)
                    if j >= 1:
                        pe.wait_ge(y_ready, j)
                    for r in range(PER):
                        last = pe.matmul(psY[r * CAP:(r + 1) * CAP, 0:D], hiddenT[:, r * CAP:(r + 1) * CAP],
                                         w["down"][:, j * PER + r, :], start=True, stop=True)
                    last.then_inc(y_done, 1)
                for part in range(4):
                    combine(TILES - 1, part)

            @block.vector
            def _(dve):
                dve.wait_ge(counted, 2)
                c = Chain(dve, steps)
                for j in range(TILES):
                    if j >= 2:
                        dve.wait_ge(combined, j - 1)
                    dve.tensor_scalar(onehot[:, j % 2, :], count[:, :], token_of[:, j:j + 1], None,
                                      ALU.is_equal).then_inc(onehot_ready, 1)
                    dve.wait_ge(gathered[j], 16)
                    if j >= 1:
                        dve.wait_ge(gate_ready, j)
                    c(dve.tensor_tensor(gate_pick[:, :], taken_row(j)[:, D + j * PER:D + (j + 1) * PER],
                                        core.cf[:, C_OWN4:C_OWN4 + PER], ALU.mult))
                    c.wait()
                    dve.tensor_reduce(gate[:, j:j + 1], gate_pick[:, :], AX, ALU.add).then_inc(gate_ready, 1)
                    dve.wait_ge(tanh_ready, j + 1)
                    if j >= 1:
                        dve.wait_ge(hidden_turned, j)
                    c(dve.scalar_tensor_tensor(out=act_up[:, 0, :], in0=th[:, :], scalar=1.0, in1=psH[:, 0:INTER],
                                               op0=ALU.add, op1=ALU.mult))
                    c.wait()
                    dve.scalar_tensor_tensor(out=act_up[:, 1, :], in0=act_up[:, 0, :], scalar=0.5,
                                             in1=psH[:, INTER:2 * INTER], op0=ALU.mult,
                                             op1=ALU.mult).then_inc(hidden_ready, 1)
                    dve.wait_ge(y_done, j + 1)
                    dve.wait_ge(gate_ready, j + 1)
                    dve.tensor_scalar(y[:, j, :], psY[:, 0:D], gate[:, j:j + 1], None, ALU.mult).then_inc(y_ready, 1)
                dve.wait_ge(combined, TILES)
                for k in range(TB_BANKS):
                    xk = core.X[:, k * 4:(k + 1) * 4, :]
                    dve.tensor_tensor(xk, xk, psC[:, k, :].rearrange("p (t d) -> p t d", t=4),
                                      ALU.add).then_inc(summed, 1)
                dve.wait_ge(summed, TB_BANKS)


C_IDENT = 0
C_ONES = C_IDENT + P
C_EPS = C_ONES + P
C_ORDER8 = C_EPS + 1
C_CAUSAL = C_ORDER8 + 8
C_AFTER = C_CAUSAL + P
C_SHIFT = C_AFTER + P
C_OVER = C_SHIFT + P
C_BAND = C_OVER + P
C_PAIR = C_BAND + 192
C_COUNT = C_PAIR + P
C_AHEAD = C_COUNT + 64
C_OWN4 = C_AHEAD + NT
CONST_COLS = C_OWN4 + 4
ARENA = 20480

WEIGHTS = {
    "L0a": [("qk", "L0a_qk", [P, 4, D]), ("v", "L0a_v", [P, D]), ("cos", "L0a_cos", [P, 2, S]),
            ("sin", "L0a_sin", [P, 2, S]), ("pick_q", "L0a_pick_q", [P, 16, 32]), ("pick_k", "L0a_pick_k", [P, 16, 112]),
            ("causal_t", "L0a_causal_t", [P, P]), ("o", "L0a_o", [P, D])],
    "L0f": [("wqkv", "L0f_wqkv", [P, 2, 3, 512]), ("wo", "L0f_wo", [P, 2, 4, D]), ("w1", "L0f_w1", [P, 2, 682]),
            ("w2", "L0f_w2", [P, 2, 3, D]), ("ln", "L0f_ln", [P, 4]), ("b1", "L0f_b1", [P, 12]),
            ("b2", "L0f_b2", [1, 2, D]), ("pos", "L0f_pos", [P, 2, 2, 256]), ("scales", "L0f_scales", [P, 8, 64])],
    "L1a": [("qkv", "L1a_qkv", [P, 8, 6, D]), ("out", "L1a_out", [P, 8, D])],
    "L1f": [("router", "L1f_router", [P, 8]), ("router_b", "L1f_router_b", [1, 8]),
            ("W1", "L1f_W1", [P, 8, 512]), ("W2", "L1f_W2", [P, 8, 4, D]), ("b1", "L1f_b1", [P, 32]),
            ("b2", "L1f_b2", [8, D])],
    "L2a": [("cols", "L2a_cols", [P, 2]), ("mix", "L2a_mix", [P, 3]), ("kvr", "L2a_kvr", [P, 3, D]),
            ("out", "L2a_out", [P, D])],
    "L2f": [("router", "L2f_router", [P, 8]), ("angles", "L2f_angles", [P, 4, 64]),
            ("qkv", "L2f_qkv", [P, 8, 384]), ("out", "L2f_out", [P, 8, D])],
    "L3a": [("cols", "L3a_cols", [P, 4]), ("in", "L3a_in", [P, 256]), ("A", "L3a_A", [P, 2, 16]),
            ("B", "L3a_B", [P, 2, 16]), ("C", "L3a_C", [16, 256]), ("out", "L3a_out", [P, 2, D]),
            ("b_out", "L3a_b_out", [1, D])],
    "L3g": [("router", "L3g_router", [P, 64])],
    "L3f": [("gate_up", "L3f_gate_up", [P, 64, 192]), ("down", "L3f_down", [96, 64, D])],
}
PROBS_COLS = 6 * 1280
IN_ARENA = {("L0a", "pick_k"): PROBS_COLS, ("L0a", "pick_q"): PROBS_COLS + 16 * 112,
            ("L0a", "causal_t"): PROBS_COLS + 16 * 144, ("L3f", "gate_up"): 0, ("L3f", "down"): 12288, ("L0f", "wqkv"): 15360, ("L0f", "w1"): 15360 + 3072, ("L1a", "qkv"): 0, ("L1a", "out"): 6144, ("L1f", "W1"): 7168, ("L1f", "W2"): 7168 + 4096}


EARLY = ("L0a", "L0f")


def place_weights(nc, ctx, core, stages):
    for stage in stages:
        parts = WEIGHTS[stage]
        core.w[stage] = {}
        for key, _, shape in parts:
            if (stage, key) in IN_ARENA:
                at, n = IN_ARENA[stage, key], 1
                for k in shape[1:]:
                    n *= k
                flat = core.arena[0:shape[0], at:at + n]
                core.w[stage][key] = flat if len(shape) == 2 else flat.rearrange(
                    "p (a b) -> p a b", a=shape[1]) if len(shape) == 3 else flat.rearrange(
                    "p (a b c) -> p a b c", a=shape[1], b=shape[2])
            else:
                t = ctx.enter_context(nc.sbuf_tensor(f"w_{stage}_{key}", shape, F32))
                core.w[stage][key] = t[:, :] if len(shape) == 2 else t[:, :, :] if len(shape) == 3 else t[:, :, :, :]


def load_weights(core, sp):
    for stage, parts in WEIGHTS.items():
        if stage in ("L1a", "L1f", "L3f"):
            continue
        for key, name, _ in parts:
            core.load(sp, stage, core.w[stage][key], core.dram[name])


def load_layer1_weights(core, sp):
    core.wait_weights(sp, "L0a")
    for stage in ("L1a", "L1f"):
        for key, name, _ in WEIGHTS[stage]:
            core.load(sp, stage, core.w[stage][key], core.dram[name])


def load_late_weights(core, sp):
    for lo in range(0, 64, 16):
        core.load(sp, "L3f", core.w["L3f"]["gate_up"][:, lo:lo + 16, :], core.dram["L3f_gate_up"][:, lo:lo + 16, :])
        core.load(sp, "L3f", core.w["L3f"]["down"][:, lo:lo + 16, :], core.dram["L3f_down"][:, lo:lo + 16, :])


LAYERS = {0: layer0_attn, 1: layer0_ffn, 2: layer1_attn, 3: layer1_ffn, 4: layer2_attn, 5: layer2_ffn,
          6: layer3_attn, 7: layer3_ffn}
STAGES = (0, 1, 2, 3, 4, 5, 6, 7)


def program(nc, dram, out):
    x_dram = dram["x"].rearrange("b (t p) d -> p (b t) d", p=P)
    out_dram = out.rearrange("b (t p) d -> p (b t) d", p=P)
    with ExitStack() as ctx:
        core = Core(nc, ctx, dram)
        ident_ready = ctx.enter_context(nc.semaphore("ident_ready"))
        place_weights(nc, ctx, core, [stage for stage in WEIGHTS if stage not in EARLY])
        with ExitStack() as early:
            place_weights(nc, early, core, ["L0f"])
            earliest = early.enter_context(ExitStack())
            place_weights(nc, earliest, core, ["L0a"])
            with nc.Block() as block:
                @block.sync
                def _(sp):
                    sp.dma_start(core.cf[:, :], dram["consts"]).then_inc(core.const_loaded, 16)
                    sp.dma_start(core.X[:, 0:NT, :], x_dram).then_inc(core.x_loaded, 16)
                    load_weights(core, sp)

                @block.vector
                def _(dve):
                    dve.wait_ge(core.const_loaded, 16)
                    dve.wait_ge(core.x_loaded, 16)
                    dve.memset(core.X[:, NT:NT + TB, :], 0.0).then_inc(ident_ready, 1)
                    dve.tensor_copy(core.identb[:, :], core.ident).then_inc(ident_ready, 1)
                    dve.tensor_copy(core.band[:, :], core.cf[:, C_BAND:C_BAND + 64 + P]).then_inc(ident_ready, 1)
                    dve.tensor_copy(core.pair_mask[:, :], core.cf[:, C_PAIR:C_PAIR + P]).then_inc(ident_ready, 1)
                    dve.tensor_copy(core.causal[:, :], core.cf[:, C_CAUSAL:C_CAUSAL + P]).then_inc(ident_ready, 1)

                @block.scalar
                def _(act):
                    act.wait_ge(core.const_loaded, 16)

                @block.tensor
                def _(pe):
                    pe.wait_ge(core.const_loaded, 16)
                    pe.wait_ge(ident_ready, 5)
            if 0 in STAGES:
                layer0_attn(nc, core)
                core.retire()
            elif 1 in STAGES:
                with nc.Block() as block:
                    @block.sync
                    def _(sp):
                        core.wait_weights(sp, "L0a")
            earliest.close()
            if 1 in STAGES:
                layer0_ffn(nc, core)
                core.retire()
            if 1 not in STAGES and set(STAGES) & {2, 3, 7}:
                with nc.Block() as block:
                    @block.sync
                    def _(sp):
                        load_layer1_weights(core, sp)
            if not set(STAGES) >= {0, 1}:
                with nc.Block() as block:
                    @block.sync
                    def _(sp):
                        for stage in EARLY:
                            core.wait_weights(sp, stage)
        if 7 in STAGES and 4 not in STAGES:
            with nc.Block() as block:
                @block.sync
                def _(sp):
                    for stage in ("L1a", "L1f", "L0f"):
                        core.wait_weights(sp, stage)
                    load_late_weights(core, sp)
        for n in STAGES:
            if n >= 2:
                LAYERS[n](nc, core)
                if n != STAGES[-1]:
                    core.retire()
        with nc.Block() as block:
            @block.sync
            def _(sp):
                sp.dma_start(out_dram, core.X[:, 0:NT, :]).then_inc(core.stored, 16)
                sp.wait_ge(core.stored, 16)
                for stage in core.loaded:
                    core.wait_weights(sp, stage)


def lay_out(a):
    import numpy as np
    c = np.ascontiguousarray
    w = {"x": a["L0_attn_x"]}
    consts = np.zeros((P, CONST_COLS), np.float32)
    consts[:, C_IDENT:C_IDENT + P] = np.eye(P)
    consts[:, C_ONES:C_ONES + P] = 1.0
    consts[:, C_EPS] = EPS
    consts[:, C_ORDER8:C_ORDER8 + 8] = 8 - np.arange(8)
    q_at, k_at = np.arange(P)[:, None], np.arange(P)[None, :]
    consts[:, C_CAUSAL:C_CAUSAL + P] = np.where(k_at > q_at, np.float32(NEG), 0)
    consts[:, C_AFTER:C_AFTER + P] = np.where(q_at > k_at, 0.5, 0)
    consts[:, C_SHIFT:C_SHIFT + P] = k_at == q_at + 1
    consts[P - 1, C_OVER] = 1.0
    key = np.arange(192)[None, :] - 64
    consts[:, C_BAND:C_BAND + 192] = np.where((key > q_at) | (key < q_at - 64), np.float32(NEG), 0)
    own = (q_at // 64 == k_at // 64) & (k_at <= q_at)
    consts[:, C_PAIR:C_PAIR + P] = np.where(own, 0, np.float32(NEG))
    consts[:, C_COUNT:C_COUNT + 64] = np.arange(1, 65)
    consts[:, C_AHEAD:C_AHEAD + NT] = NT * P - (np.arange(NT)[None, :] * P + q_at)
    consts[:, C_OWN4:C_OWN4 + 4] = q_at // 32 == np.arange(4)[None, :]
    w["consts"] = consts
    swap = np.arange(D) ^ 1
    w["L0a_qk"] = np.stack([a["L0_attn_wq"], a["L0_attn_wq"][:, swap], a["L0_attn_wk"], a["L0_attn_wk"][:, swap]], 1)
    w["L0a_v"] = a["L0_attn_wv"]
    w["L0a_o"] = a["L0_attn_wo"]
    dh = 8
    inv_freq = (1.0 / np.float32(10000.0) ** (np.arange(0, dh, 2, dtype=np.float32) / np.float32(dh))).astype(np.float32)
    angle = (np.arange(S, dtype=np.float32)[None, :] * inv_freq[(np.arange(D) % dh) // 2][:, None]).astype(np.float32)
    sign = np.where(np.arange(D) % 2, 1, -1)[:, None]
    scale = dh ** -0.5
    cos, sin = np.cos(angle.astype(np.float64)), np.sin(angle.astype(np.float64)) * sign
    w["L0a_cos"] = np.stack([cos * scale, cos], 1).astype(np.float32)
    w["L0a_sin"] = np.stack([sin * scale, sin], 1).astype(np.float32)
    row, head = np.arange(P)[:, None, None], np.arange(16)[None, :, None]
    col = np.arange(32)[None, None, :]
    w["L0a_pick_q"] = ((row // dh == head) & (row % dh == col % dh) & (col < 24)).astype(np.float32)
    col = np.arange(112)[None, None, :] - 16
    w["L0a_pick_k"] = ((row // dh == head) & (row % dh == col % 32) & (col >= 0)).astype(np.float32)
    w["L0a_causal_t"] = consts[:, C_CAUSAL:C_CAUSAL + P].T
    w["L0f_wqkv"] = a["L0_ffn_wqkv"].reshape(2, D, 3, 512).transpose(1, 0, 2, 3)
    w["L0f_wo"] = a["L0_ffn_wo"].reshape(2, 4, P, D).transpose(2, 0, 1, 3)
    w["L0f_w1"] = a["L0_ffn_w1"].transpose(1, 0, 2)
    hid, pad = 341, 3 * P - 341
    w["L0f_w2"] = np.pad(a["L0_ffn_w2"], ((0, 0), (0, pad), (0, 0))).reshape(2, 3, P, D).transpose(2, 0, 1, 3)
    w["L0f_ln"] = np.stack([a["L0_ffn_ln_g"][0], a["L0_ffn_ln_b"][0], a["L0_ffn_ln_g"][1], a["L0_ffn_ln_b"][1]], 1)
    w["L0f_b1"] = np.pad(a["L0_ffn_b1"].reshape(2, 2, hid), ((0, 0), (0, 0), (0, pad))).reshape(12, P).T
    w["L0f_b2"] = a["L0_ffn_b2"].reshape(1, 2, D)
    half = np.arange(0, 64, 2, dtype=np.float32)
    inv_freq = (1.0 / np.float32(10000.0) ** (half / np.float32(64))).astype(np.float32)
    t = np.arange(S, dtype=np.float32)
    freqs = (t[:, None] * inv_freq[None, :]).astype(np.float32).astype(np.float64)
    base = (half.astype(np.float64) + 0.4 * 64) / (1.4 * 64)
    xpos = base[None, :] ** ((t[:, None] - S // 2) / 32.0)
    pos = np.zeros((2, 2, S, 64))
    for j, sc in enumerate((xpos, 1.0 / xpos)):
        pos[j, 0] = np.concatenate([np.cos(freqs) * sc] * 2, -1)
        pos[j, 1] = np.concatenate([-np.sin(freqs) * sc, np.sin(freqs) * sc], -1)
    w["L0f_pos"] = pos.reshape(2, 2, TB, P, 64).transpose(3, 0, 1, 2, 4).reshape(P, 2, 2, 256).astype(np.float32)
    other = (np.arange(64) + 32) % 64
    qs, ks = a["L0_ffn_q_scale"], a["L0_ffn_k_scale"]
    scales = np.stack([qs, qs[:, other], ks, ks[:, other]], 1).reshape(1, 8, 64)
    w["L0f_scales"] = np.broadcast_to(scales, (P, 8, 64))
    qkv = a["L1_attn_w_qkv"].reshape(D, 6, 8, D)
    w["L1a_qkv"] = np.stack([qkv[:, n].transpose(0, 1, 2) if n == 2 else qkv[:, n].transpose(2, 1, 0)
                             for n in range(6)], 2)
    w["L1a_out"] = a["L1_attn_w_out"].reshape(8, D, D).transpose(1, 0, 2)
    w["L1f_router"] = a["L1_ffn_router_w"]
    w["L1f_router_b"] = a["L1_ffn_router_b"].reshape(1, 8)
    w["L1f_W1"] = a["L1_ffn_W1"].transpose(1, 0, 2)
    w["L1f_W2"] = a["L1_ffn_W2"].reshape(8, 4, P, D).transpose(2, 0, 1, 3)
    w["L1f_b1"] = a["L1_ffn_b1"].reshape(32, P).T
    w["L1f_b2"] = a["L1_ffn_b2"]
    w["L2a_cols"] = np.stack([a["L2_attn_time_decay"], a["L2_attn_time_first"]], 1)
    w["L2a_mix"] = np.stack([a["L2_attn_time_mix_" + n].reshape(D) for n in "kvr"], 1)
    w["L2a_kvr"] = np.stack([a["L2_attn_W" + n].T for n in "kvr"], 1)
    w["L2a_out"] = a["L2_attn_Wo"].T
    w["L2f_router"] = a["L2_ffn_Wr"].T
    inv_freq = (1.0 / np.float32(10000.0) ** (np.arange(32, dtype=np.float32) * np.float32(2.0) / np.float32(64)))
    ang = (np.arange(S, dtype=np.float32)[:, None] * inv_freq.astype(np.float32)).astype(np.float32).astype(np.float64)
    angles = np.concatenate([np.cos(ang), np.sin(ang)], 1).astype(np.float32)
    w["L2f_angles"] = angles.reshape(TB, P, 64).transpose(1, 0, 2)
    w["L2f_qkv"] = a["L2_ffn_Wqkv"].transpose(1, 0, 2)
    w["L2f_out"] = a["L2_ffn_Wo"].transpose(1, 0, 2)
    w["L3a_cols"] = np.concatenate([np.stack([a["L3_attn_norm_w"], a["L3_attn_norm_b"]], 1),
                                    a["L3_attn_b_in"].reshape(2, P).T], 1)
    w["L3a_in"] = a["L3_attn_W_in"].T
    w["L3a_A"] = a["L3_attn_A"].reshape(2, P, 16).transpose(1, 0, 2)
    w["L3a_B"] = a["L3_attn_B_ssm"].reshape(2, P, 16).transpose(1, 0, 2)
    w["L3a_C"] = a["L3_attn_C_ssm"].T
    w["L3a_out"] = a["L3_attn_W_out"].T.reshape(2, P, D).transpose(1, 0, 2)
    w["L3a_b_out"] = a["L3_attn_b_out"].reshape(1, D)
    w["L3g_router"] = a["L3_ffn_gate_w"].T
    w["L3f_gate_up"] = np.concatenate([a["L3_ffn_w_gate"], a["L3_ffn_w_up"]], 1).transpose(2, 0, 1)
    w["L3f_down"] = a["L3_ffn_w_down"].transpose(2, 0, 1)
    return {k: c(v) for k, v in w.items()}


def kernel(**inputs):
    import numpy as np
    import concourse.bacc as bacc
    from concourse.bass_utils import run_bass_kernel_spmd

    nc = bacc.Bacc("TRN2", target_bir_lowering=False, num_devices=1)
    arrays = lay_out({k: np.asarray(v) for k, v in inputs.items()})
    dram = {k: nc.dram_tensor("in_" + k, v.shape, mybir.dt.from_np(v.dtype), kind="ExternalInput").ap()
            for k, v in arrays.items()}
    out = nc.dram_tensor("out", (B, S, D), F32, kind="ExternalOutput").ap()
    program(nc, dram, out)
    result = run_bass_kernel_spmd(nc, [{"in_" + k: v for k, v in arrays.items()}], core_ids=[0])
    return result.results[0]["out"]
```

```python
from contextlib import ExitStack

import concourse.bass as bass
from concourse import mybir
from concourse.alu_op_type import AluOpType as ALU

ACT = mybir.ActivationFunctionType
AX = mybir.AxisListType.X
F32 = mybir.dt.float32
BF16 = mybir.dt.bfloat16
U32 = mybir.dt.uint32

P = 128
B, S, D = 4, 512, 128
TB = S // P
NT = B * TB
EPS = 1e-5
NEG = -1e30


class Chain:

    def __init__(self, eng, sem, base=0):
        self.eng, self.sem, self.base, self.n = eng, sem, base, 0

    def __call__(self, ins):
        self.n += 1
        return ins.then_inc(self.sem, 1)

    def wait(self, back=0):
        self.eng.wait_ge(self.sem, self.base + self.n - back)


class LayerNorm:
    STEPS = 2 * TB + 5

    def __init__(self, nc, ctx, name, core):
        sb = nc.sbuf_tensor
        self.eps = core.eps
        self.stats = ctx.enter_context(sb(name + "_stats", [P, TB, 6], F32))
        self.mv = ctx.enter_context(sb(name + "_meanvar", [P, TB, 2], F32))
        self.root = ctx.enter_context(sb(name + "_root", [P, TB], F32))
        self.guess = ctx.enter_context(sb(name + "_guess", [P, TB], F32))
        self.corr = ctx.enter_context(sb(name + "_corr", [P, TB], F32))
        self.rstd = ctx.enter_context(sb(name + "_rstd", [P, TB], F32))
        self.step = core.semaphore(ctx, name + "_step")
        self.rooted = core.semaphore(ctx, name + "_rooted")
        self.ready = core.semaphore(ctx, name + "_ready")

    def vector(self, dve, n, src, dst):
        self.statistics(dve, n, src)
        self.finish(dve, n, src, dst)

    def statistics(self, dve, n, src):
        step = Chain(dve, self.step, n * self.STEPS)
        for t in range(TB):
            step(dve.bn_stats(self.stats[:, t, :], src(t)))
        step.wait()
        dve.memset(self.corr[:, 0:1], 0.0)
        for t in range(TB):
            step(dve.bn_aggr(self.mv[:, t, :], self.stats[:, t, :]))

    def finish(self, dve, n, src, dst):
        step = Chain(dve, self.step, n * self.STEPS + 2 * TB)
        dve.wait_ge(self.rooted, n + 1)
        step(dve.reciprocal(self.guess[:, :], self.root[:, :]))
        step.wait()
        step(dve.tensor_tensor(self.corr[:, :], self.guess[:, :], self.guess[:, :], ALU.mult))
        step.wait()
        step(dve.scalar_tensor_tensor(out=self.corr[:, :], in0=self.mv[:, :, 1], scalar=EPS, in1=self.corr[:, :],
                                      op0=ALU.add, op1=ALU.mult))
        step.wait()
        step(dve.tensor_scalar(self.corr[:, :], self.corr[:, :], -0.5, 1.5, ALU.mult, ALU.add))
        step.wait()
        step(dve.tensor_tensor(self.rstd[:, :], self.corr[:, :], self.guess[:, :], ALU.mult))
        step.wait()
        assert step.n == self.STEPS - 2 * TB
        for t in range(TB):
            dve.tensor_scalar(dst(t), src(t), self.mv[:, t, 0:1], self.rstd[:, t:t + 1],
                              ALU.subtract, ALU.mult).then_inc(self.ready, 1)

    def scalar(self, act, n):
        act.wait_ge(self.step, n * self.STEPS + 2 * TB)
        act.activation(self.root[:, :], self.mv[:, :, 1], ACT.Sqrt, bias=self.eps).then_inc(self.rooted, 1)


class Core:

    def __init__(self, nc, ctx, dram):
        self.nc, self.dram, self.w = nc, dram, {}

        def sb(name, shape, dt=F32):
            return ctx.enter_context(nc.sbuf_tensor(name, shape, dt))

        self.sb = sb
        self.X = sb("X", [P, NT + TB, D])
        self.cf = sb("const_f32", [P, CONST_COLS])
        self.ident = self.cf[:, C_IDENT:C_IDENT + P]
        self.eps = self.cf[:, C_EPS:C_EPS + 1]
        self.ones_row = self.cf[0:1, C_ONES:C_ONES + P]
        self.identb = sb("ident_bf16", [P, P], BF16)
        self.causal = sb("causal_bf16", [P, P], BF16)
        self.band = sb("band_bf16", [P, 64 + P], BF16)
        self.pair_mask = sb("pair_mask_bf16", [P, P], BF16)
        self.arena = sb("arena", [P, ARENA])
        self.x_loaded = ctx.enter_context(nc.semaphore("x_loaded"))
        self.const_loaded = ctx.enter_context(nc.semaphore("const_loaded"))
        self.stored = ctx.enter_context(nc.semaphore("stored"))
        self.n_loads = {}
        self.of_layer = []
        self.loaded = {}
        self.ctx = ctx

    def semaphore(self, ctx, name):
        sem = ctx.enter_context(self.nc.semaphore(name))
        self.of_layer.append(sem)
        return sem

    def retire(self):
        sems, self.of_layer = self.of_layer, []
        with self.nc.Block() as block:
            @block.gpsimd
            def _(pool):
                for sem in sems:
                    pool.sem_clear(sem)

    def load(self, eng, stage, dst, src):
        if stage not in self.loaded:
            self.loaded[stage] = self.ctx.enter_context(self.nc.semaphore(f"{stage}_weights"))
            self.n_loads[stage] = 0
        self.n_loads[stage] += 16
        eng.dma_start(dst, src).then_inc(self.loaded[stage], 16)

    def wait_weights(self, eng, stage):
        eng.wait_ge(self.loaded[stage], self.n_loads[stage])


def turn(pe, core, ln, n, xn, ps, turned):
    for t in range(TB):
        pe.wait_ge(ln.ready, n * TB + t + 1)
        last = pe.transpose(ps[:, t * P:(t + 1) * P], xn[:, t, :], core.ident)
    last.then_inc(turned, 1)


def add_to_stream(dve, core, b, ps, done):
    x = core.X[:, bass.ds(b * TB, TB), :]
    dve.tensor_tensor(x, x, ps.rearrange("p (t d) -> p t d", t=TB), ALU.add).then_inc(done, 1)


def layer2_attn(nc, core):
    with ExitStack() as ctx:
        def sb(name, shape, dt=F32):
            return ctx.enter_context(nc.sbuf_tensor("L2a_" + name, shape, dt))

        def sem(name):
            return core.semaphore(ctx, "L2a_" + name)

        ln = LayerNorm(nc, ctx, "L2a_ln", core)
        w = core.w["L2a"]
        xn = sb("xn", [P, TB, D])
        xT = sb("xT", [P, S + 1])
        mixed = sb("mixed", [P, 3, S])
        one_less_mix = sb("one_less_mix", [P, 3])
        neg_decay = sb("neg_decay", [P, 1])
        decay_row = sb("decay_row", [P, S])
        top = sb("top", [P, S + 1])
        num = sb("num", [P, S + 1])
        den = sb("den", [P, S + 1])
        ww = sb("ww", [P, S])
        peak = sb("peak", [P, S])
        diff = sb("diff", [P, 4, S])
        gate = sb("gate", [P, S])
        tmp = sb("tmp", [P, S])
        out_num = sb("out_num", [P, S])
        out_den = sb("out_den", [P, S])
        res = sb("res", [P, S])
        psT = ctx.enter_context(nc.psum_tensor("L2a_psT", [P, S], F32))
        psY = ctx.enter_context(nc.psum_tensor("L2a_psY", [P, S], F32))
        psK, psV, psR = (ctx.enter_context(nc.psum_tensor("L2a_ps" + c, [P, S], F32)) for c in "KVR")
        setup, exp_decay, mixing, banks_used = sem("setup"), sem("exp_decay"), sem("mixing"), sem("banks_used")
        turned, xt_ready, mixed_ready, projected = sem("turned"), sem("xt_ready"), sem("mixed_ready"), sem("projected")
        vec, diffs_ready, exps_ready, res_ready, y_ready, added = (
            sem("vec"), sem("diffs_ready"), sem("exps_ready"), sem("res_ready"), sem("y_ready"), sem("added"))
        VEC = 13
        SETUP = 7
        mix_of, first = w["mix"], w["cols"][:, 1:2]
        with nc.Block() as block:
            @block.sync
            def _(sp):
                load_late_weights(core, sp)

            @block.scalar
            def _(act):
                core.wait_weights(act, "L2a")
                act.activation(neg_decay[:, :], w["cols"][:, 0:1], ACT.Exp).then_inc(exp_decay, 1)

                def copy_tokens(b):
                    act.wait_ge(turned, b + 1)
                    act.activation(xT[:, 1:S + 1], psT[:, :], ACT.Copy).then_inc(xt_ready, 1)

                ln.scalar(act, 0)
                copy_tokens(0)
                with act.Fori(0, B) as b:
                    act.wait_ge(projected, b + 1)
                    act.activation(gate[:, :], psR[:, :], ACT.Exp, scale=-1.0).then_inc(exps_ready, 1)
                    for j in range(4):
                        act.wait_ge(diffs_ready, b * 4 + j + 1)
                        act.activation(diff[:, j, :], diff[:, j, :], ACT.Exp).then_inc(exps_ready, 1)
                    ln.scalar(act, b + 1)
                    copy_tokens(b + 1)

            @block.tensor
            def _(pe):
                core.wait_weights(pe, "L2a")

                def project(b):
                    pe.wait_ge(mixed_ready, b + 1)
                    for j, ps in enumerate((psK, psV, psR)):
                        last = pe.matmul(ps[:, :], w["kvr"][:, j, :], mixed[:, j, :], start=True, stop=True)
                    last.then_inc(projected, 1)

                turn(pe, core, ln, 0, xn, psT, turned)
                project(0)
                with pe.Fori(0, B) as b:
                    turn(pe, core, ln, b + 1, xn, psT, turned)
                    pe.wait_ge(banks_used, b + 1)
                    pe.wait_ge(exps_ready, b * 5 + 1)
                    project(b + 1)
                    pe.wait_ge(res_ready, b + 1)
                    for t in range(TB):
                        last = pe.matmul(psY[:, t * P:(t + 1) * P], res[:, t * P:(t + 1) * P], w["out"][:, :],
                                         start=True, stop=True)
                    last.then_inc(y_ready, 1)

            @block.vector
            def _(dve):
                core.wait_weights(dve, "L2a")
                c = Chain(dve, setup)
                c(dve.memset(xT[:, 0:1], 0.0))
                c(dve.memset(top[:, 0:1], -1e30))
                c(dve.memset(num[:, 0:1], 0.0))
                c(dve.memset(den[:, 0:1], 0.0))
                c(dve.memset(decay_row[:, :], 0.0))
                c(dve.tensor_scalar(one_less_mix[:, :], mix_of, -1.0, 1.0, ALU.mult, ALU.add))
                dve.wait_ge(exp_decay, 1)
                c.wait()
                c(dve.tensor_scalar(decay_row[:, :], decay_row[:, :], neg_decay[:, 0:1], None, ALU.subtract))
                c.wait()
                assert c.n == SETUP

                def mix(b):
                    c = Chain(dve, mixing, b * 5)
                    dve.wait_ge(xt_ready, b + 1)
                    for j in range(3):
                        c(dve.tensor_scalar(mixed[:, j, :], xT[:, 0:S], one_less_mix[:, j:j + 1], None, ALU.mult))
                    for j in range(3):
                        c.wait(2)
                        last = dve.scalar_tensor_tensor(out=mixed[:, j, :], in0=xT[:, 1:S + 1],
                                                        scalar=mix_of[:, j:j + 1], in1=mixed[:, j, :],
                                                        op0=ALU.mult, op1=ALU.add)
                        c(last) if j < 2 else last.then_inc(mixed_ready, 1)
                    assert c.n == 5

                ln.vector(dve, 0, lambda t: core.X[:, t, :], lambda t: xn[:, t, :])
                mix(0)
                with dve.Fori(0, B) as b:
                    def next_tokens(t):
                        return core.X[:, b * TB + TB + t, :]

                    c = Chain(dve, vec, b * VEC)
                    dve.wait_ge(projected, b + 1)
                    c(dve.tensor_tensor_scan(top[:, 1:S + 1], decay_row[:, :], psK[:, :], -1e30, ALU.add, ALU.max))
                    c.wait()
                    dve.tensor_tensor(diff[:, 0, :], psK[:, :], top[:, 1:S + 1], ALU.subtract).then_inc(diffs_ready, 1)
                    c(dve.tensor_tensor(tmp[:, :], top[:, 0:S], decay_row[:, :], ALU.add))
                    c.wait()
                    dve.tensor_tensor(diff[:, 1, :], tmp[:, :], top[:, 1:S + 1], ALU.subtract).then_inc(diffs_ready, 1)
                    c(dve.tensor_scalar(ww[:, :], psK[:, :], first, None, ALU.add))
                    c.wait()
                    c(dve.tensor_tensor(peak[:, :], ww[:, :], top[:, 0:S], ALU.max))
                    c.wait()
                    dve.tensor_tensor(diff[:, 2, :], top[:, 0:S], peak[:, :], ALU.subtract).then_inc(diffs_ready, 1)
                    dve.tensor_tensor(diff[:, 3, :], ww[:, :], peak[:, :], ALU.subtract).then_inc(diffs_ready, 1)
                    ln.statistics(dve, b + 1, next_tokens)
                    dve.wait_ge(exps_ready, b * 5 + 2)
                    c(dve.tensor_tensor(tmp[:, :], diff[:, 0, :], psV[:, :], ALU.mult))
                    dve.wait_ge(exps_ready, b * 5 + 3)
                    c.wait()
                    c(dve.tensor_tensor_scan(num[:, 1:S + 1], diff[:, 1, :], tmp[:, :], 0.0, ALU.mult, ALU.add))
                    c(dve.tensor_tensor_scan(den[:, 1:S + 1], diff[:, 1, :], diff[:, 0, :], 0.0, ALU.mult, ALU.add))
                    dve.wait_ge(exps_ready, b * 5 + 5)
                    ln.finish(dve, b + 1, next_tokens, lambda t: xn[:, t, :])
                    dve.tensor_tensor(out_num[:, :], diff[:, 3, :], psV[:, :], ALU.mult).then_inc(banks_used, 1)
                    c.wait()
                    c(dve.tensor_tensor(tmp[:, :], diff[:, 2, :], num[:, 0:S], ALU.mult))
                    c(dve.tensor_tensor(out_den[:, :], diff[:, 2, :], den[:, 0:S], ALU.mult))
                    c.wait()
                    dve.wait_ge(banks_used, b + 1)
                    c(dve.tensor_tensor(out_num[:, :], out_num[:, :], tmp[:, :], ALU.add))
                    c(dve.tensor_tensor(out_den[:, :], out_den[:, :], diff[:, 3, :], ALU.add))
                    c.wait()
                    c(dve.scalar_tensor_tensor(out=out_den[:, :], in0=gate[:, :], scalar=1.0, in1=out_den[:, :],
                                               op0=ALU.add, op1=ALU.mult))
                    c.wait()
                    mix(b + 1)
                    c(dve.reciprocal(out_den[:, :], out_den[:, :]))
                    c.wait()
                    dve.tensor_tensor(res[:, :], out_num[:, :], out_den[:, :], ALU.mult).then_inc(res_ready, 1)
                    dve.wait_ge(y_ready, b + 1)
                    add_to_stream(dve, core, b, psY[:, :], added)
                    dve.wait_ge(added, b + 1)
                    assert c.n == VEC, c.n


def layer3_attn(nc, core):
    NS, CH = 16, 2
    with ExitStack() as ctx:
        def sb(name, shape, dt=F32):
            return ctx.enter_context(nc.sbuf_tensor("L3a_" + name, shape, dt))

        def sem(name):
            return core.semaphore(ctx, "L3a_" + name)

        ln = LayerNorm(nc, ctx, "L3a_ln", core)
        w = core.w["L3a"]
        xo = sb("xo", [P, TB, D])
        xn = sb("xn", [P, TB, D])
        xT = sb("xT", [P, S])
        hT = sb("hT", [P, CH, S])
        decay = sb("decay", [NS, S])
        drive = sb("drive", [NS, S])
        states = sb("states", [NS, S])
        yT = sb("yT", [P, CH, S])
        psT, psA, psU, psY = (ctx.enter_context(nc.psum_tensor("L3a_ps" + c, [P, S], F32)) for c in "TAUY")
        psH = ctx.enter_context(nc.psum_tensor("L3a_psH", [P, CH, S], F32))
        turned, xt_ready, h_done, h_ready, au_done, rates_ready = (
            sem(n) for n in ("turned", "xt_ready", "h_done", "h_ready", "au_done", "rates_ready"))
        vec, states_ready, yt_done, yt_ready, out_done, added = (
            sem(n) for n in ("vec", "states_ready", "yt_done", "yt_ready", "out_done", "added"))
        VEC = 2
        nw, nb = w["cols"][:, 0:1], w["cols"][:, 1:2]
        with nc.Block() as block:
            @block.scalar
            def _(act):
                core.wait_weights(act, "L3a")
                ln.scalar(act, 0)
                ln.scalar(act, 1)
                with act.Fori(0, B) as b:
                    act.wait_ge(turned, b + 1)
                    act.activation(xT[:, :], psT[:, :], ACT.Identity, bias=nb, scale=nw).then_inc(xt_ready, 1)
                    ln.scalar(act, b * 2 + 2)
                    for c in range(CH):
                        act.wait_ge(h_done, b * CH + c + 1)
                        act.activation(hT[:, c, :], psH[:, c, :], ACT.Identity,
                                       bias=w["cols"][:, 2 + c:3 + c]).then_inc(h_ready, 1)
                    ln.scalar(act, b * 2 + 3)
                    act.wait_ge(au_done, b + 1)
                    act.activation(decay[:, :], psA[0:NS, :], ACT.Tanh, scale=0.5).then_inc(rates_ready, 1)
                    act.activation(drive[:, :], psU[0:NS, :], ACT.Copy).then_inc(rates_ready, 1)
                    for c in range(CH):
                        act.wait_ge(yt_done, b * CH + c + 1)
                        act.activation(yT[:, c, :], psH[:, c, :], ACT.Copy).then_inc(yt_ready, 1)

            @block.tensor
            def _(pe):
                core.wait_weights(pe, "L3a")
                with pe.Fori(0, B) as b:
                    for t in range(TB):
                        pe.wait_ge(ln.ready, b * 2 * TB + TB + t + 1)
                        last = pe.transpose(psT[:, t * P:(t + 1) * P], xn[:, t, :], core.ident)
                    last.then_inc(turned, 1)
                    pe.wait_ge(xt_ready, b + 1)
                    for c in range(CH):
                        pe.matmul(psH[:, c, :], w["in"][:, c * P:(c + 1) * P], xT[:, :],
                                  start=True, stop=True).then_inc(h_done, 1)
                    for c in range(CH):
                        pe.wait_ge(h_ready, b * CH + c + 1)
                        pe.matmul(psA[0:NS, :], w["A"][:, c, :], hT[:, c, :], start=c == 0, stop=c == CH - 1)
                        last = pe.matmul(psU[0:NS, :], w["B"][:, c, :], hT[:, c, :], start=c == 0, stop=c == CH - 1)
                    last.then_inc(au_done, 1)
                    pe.wait_ge(states_ready, b + 1)
                    for c in range(CH):
                        pe.matmul(psH[:, c, :], w["C"][:, c * P:(c + 1) * P], states[:, :],
                                  start=True, stop=True).then_inc(yt_done, 1)
                    pe.wait_ge(yt_ready, (b + 1) * CH)
                    for t in range(TB):
                        o = psY[:, t * P:(t + 1) * P]
                        for c in range(CH):
                            pe.matmul(o, yT[:, c, t * P:(t + 1) * P], w["out"][:, c, :], start=c == 0, stop=False)
                        last = pe.matmul(o, core.ones_row, w["b_out"][0:1, :], start=False, stop=True)
                    last.then_inc(out_done, 1)

            @block.vector
            def _(dve):
                def normalise_twice(b, tokens):
                    ln.vector(dve, b * 2, tokens, lambda t: xo[:, t, :])
                    dve.wait_ge(ln.ready, b * 2 * TB + TB)
                    ln.vector(dve, b * 2 + 1, lambda t: xo[:, t, :], lambda t: xn[:, t, :])

                normalise_twice(0, lambda t: core.X[:, t, :])
                with dve.Fori(0, B) as b:
                    c = Chain(dve, vec, b * VEC)
                    x = core.X[:, bass.ds(b * TB, TB), :]
                    c(dve.tensor_tensor(x, x, xo[:, :, :], ALU.add))
                    c.wait()
                    dve.wait_ge(turned, b + 1)
                    normalise_twice(b + 1, lambda t: core.X[:, b * TB + TB + t, :])
                    dve.wait_ge(rates_ready, b * 2 + 2)
                    c(dve.tensor_scalar(decay[:, :], decay[:, :], 0.5, 0.5, ALU.mult, ALU.add))
                    c.wait()
                    dve.tensor_tensor_scan(states[:, :], decay[:, :], drive[:, :], 0.0,
                                           ALU.mult, ALU.add).then_inc(states_ready, 1)
                    dve.wait_ge(out_done, b + 1)
                    add_to_stream(dve, core, b, psY[:, :], added)
                    dve.wait_ge(added, b + 1)
                    assert c.n == VEC


def layer1_ffn(nc, core):
    E, FC = 8, 4
    STATS_AT, NORM_AT, TURN_AT, ROUTE_AT, CHOOSE_AT, GATES_AT = 1, 2, 3, 4, 5, 6
    with ExitStack() as ctx:
        def sb(name, shape, dt=F32):
            return ctx.enter_context(nc.sbuf_tensor("L1f_" + name, shape, dt))

        def sem(name):
            return core.semaphore(ctx, "L1f_" + name)

        ln = LayerNorm(nc, ctx, "L1f_ln", core)
        w = core.w["L1f"]
        xn = sb("xn", [P, TB, D])
        xT = sb("xT", [P, S])
        xT_next = sb("xT_next", [P, S])
        hT = sb("hT", [P, 2, FC, S])
        logits = sb("logits", [P, TB, E])
        hit = sb("hit", [P, TB, E])
        first = sb("first", [P, TB, E])
        second = sb("second", [P, TB, E])
        gates = sb("gates", [P, TB, E])
        gates_next = sb("gates_next", [P, TB, E])
        best = sb("best", [P, 3, TB])
        place = sb("place", [P, TB])
        e21 = sb("e21", [P, TB])
        g1 = sb("g1", [P, TB])
        g2 = sb("g2", [P, TB])
        gatesT = sb("gatesT", [E, S])
        psT, psL = (ctx.enter_context(nc.psum_tensor("L1f_ps" + c, [P, S], F32)) for c in "TL")
        psH = ctx.enter_context(nc.psum_tensor("L1f_psH", [P, FC, S], F32))
        psY = ctx.enter_context(nc.psum_tensor("L1f_psY", [P, 2, S], F32))
        names = ("turned xt_ready xt_moved logits_done vec margin_ready exp_ready gates_ready gates_moved gates_turned "
                 "gatesT_ready bias_done bias_added h_done h_ready y_done y_used").split()
        (turned, xt_ready, xt_moved, logits_done, vec, margin_ready, exp_ready, gates_ready, gates_moved, gates_turned,
         gatesT_ready, bias_done, bias_added, h_done, h_ready, y_done, y_used) = (sem(n) for n in names)
        VEC = 17
        order = core.cf[:, C_ORDER8:C_ORDER8 + E].unsqueeze(1).to_broadcast([P, TB, E])
        with nc.Block() as block:
            @block.scalar
            def _(act):
                core.wait_weights(act, "L1f")

                def copy_tokens(b):
                    act.wait_ge(turned, b + 1)
                    act.activation(xT_next[:, :], psT[:, :], ACT.Copy).then_inc(xt_ready, 1)

                def rectify(b, e, f):
                    act.wait_ge(h_done, (b * E + e) * FC + f + 1)
                    if e >= 2:
                        act.wait_ge(y_done, b * E + e - 1)
                    act.activation(hT[:, e % 2, f, :], psH[:, f, :], ACT.Relu,
                                   bias=w["b1"][:, e % E * FC + f:e % E * FC + f + 1]).then_inc(h_ready, 1)

                def exp_of_margin(b):
                    act.wait_ge(margin_ready, b + 1)
                    act.activation(e21[:, :], e21[:, :], ACT.Exp).then_inc(exp_ready, 1)

                ln.scalar(act, 0)
                copy_tokens(0)
                for f in range(FC):
                    rectify(0, 0, f)
                exp_of_margin(0)
                with act.Fori(0, B) as b:
                    for e in range(E):
                        for f in range(FC):
                            rectify(b, e + 1, f)
                        if e == STATS_AT:
                            ln.scalar(act, b + 1)
                        if e == TURN_AT:
                            copy_tokens(b + 1)
                        if e == CHOOSE_AT:
                            exp_of_margin(b + 1)

            @block.tensor
            def _(pe):
                core.wait_weights(pe, "L1f")

                def route(b):
                    pe.wait_ge(xt_ready, b + 1)
                    for t in range(TB):
                        o = psL[:, t * E:(t + 1) * E]
                        pe.matmul(o, xT_next[:, t * P:(t + 1) * P], w["router"][:, :], start=True, stop=False)
                        last = pe.matmul(o, core.ones_row, w["router_b"][0:1, :], start=False, stop=True)
                    last.then_inc(logits_done, 1)

                def expand(b, e, tokens, first=False):
                    for f in range(FC):
                        if not first:
                            pe.wait_ge(h_ready, (b * E + e - 1) * FC + f + 1)
                        pe.matmul(psH[:, f, :], w["W1"][:, e % E, f * P:(f + 1) * P], tokens[:, :],
                                  start=True, stop=True).then_inc(h_done, 1)

                def contract(b, e):
                    if e >= 2:
                        pe.wait_ge(y_used, b * E + e - 1)
                    pe.wait_ge(h_ready, b * (E * FC) + e * FC + FC)
                    for t in range(TB):
                        for f in range(FC):
                            last = pe.matmul(psY[:, e % 2, t * P:(t + 1) * P], hT[:, e % 2, f, t * P:(t + 1) * P],
                                             w["W2"][:, e, f, :], start=f == 0, stop=f == FC - 1)
                    last.then_inc(y_done, 1)

                turn(pe, core, ln, 0, xn, psT, turned)
                route(0)
                expand(0, 0, xT_next, first=True)
                with pe.Fori(0, B) as b:
                    for e in range(E):
                        if e == 0:
                            pe.wait_ge(xt_moved, b + 1)
                        expand(b, e + 1, xT if e + 1 < E else xT_next)
                        if e == 0:
                            pe.wait_ge(gates_moved, b + 1)
                            for t in range(TB):
                                last = pe.transpose(psT[0:E, t * P:(t + 1) * P], gates[:, t, :], core.ident)
                            last.then_inc(gates_turned, 1)
                        contract(b, e)
                        if e == 0:
                            pe.wait_ge(gatesT_ready, b + 1)
                            for t in range(TB):
                                last = pe.matmul(psL[:, t * P:(t + 1) * P], gatesT[:, t * P:(t + 1) * P],
                                                 w["b2"][0:E, :], start=True, stop=True)
                            last.then_inc(bias_done, 1)
                        if e == TURN_AT:
                            turn(pe, core, ln, b + 1, xn, psT, turned)
                        if e == ROUTE_AT:
                            pe.wait_ge(bias_added, b + 1)
                            route(b + 1)

            @block.vector
            def _(dve):
                def choose(b):
                    c = Chain(dve, vec, b * VEC)
                    dve.wait_ge(logits_done, b + 1)
                    c(dve.tensor_copy(logits[:, :, :], psL[:, 0:TB * E].rearrange("p (t e) -> p t e", t=TB)))
                    for k, chosen in enumerate((first, second)):
                        c.wait()
                        c(dve.tensor_reduce(best[:, k, :], logits[:, :, :], AX, ALU.max))
                        c.wait()
                        c(dve.tensor_tensor(hit[:, :, :], logits[:, :, :],
                                            best[:, k, :].unsqueeze(2).to_broadcast([P, TB, E]), ALU.is_equal))
                        c.wait()
                        c(dve.tensor_tensor(hit[:, :, :], hit[:, :, :], order, ALU.mult))
                        c.wait()
                        c(dve.tensor_reduce(place[:, :], hit[:, :, :], AX, ALU.max))
                        c.wait()
                        c(dve.tensor_tensor(chosen[:, :, :], order,
                                            place[:, :].unsqueeze(2).to_broadcast([P, TB, E]), ALU.is_equal))
                        c.wait()
                        if k == 0:
                            c(dve.scalar_tensor_tensor(out=logits[:, :, :], in0=chosen[:, :, :], scalar=-3e38,
                                                       in1=logits[:, :, :], op0=ALU.mult, op1=ALU.add))
                    dve.tensor_tensor(e21[:, :], best[:, 1, :], best[:, 0, :], ALU.subtract).then_inc(margin_ready, 1)
                    return c.n

                def weigh(b, n):
                    c = Chain(dve, vec, b * VEC + n)
                    dve.wait_ge(exp_ready, b + 1)
                    c(dve.tensor_scalar(g2[:, :], e21[:, :], 1.0, None, ALU.add))
                    c.wait()
                    c(dve.reciprocal(g1[:, :], g2[:, :]))
                    c.wait()
                    c(dve.tensor_tensor(g2[:, :], g1[:, :], e21[:, :], ALU.mult))
                    c(dve.tensor_tensor(first[:, :, :], first[:, :, :],
                                        g1[:, :].unsqueeze(2).to_broadcast([P, TB, E]), ALU.mult))
                    c.wait(1)
                    c(dve.tensor_tensor(second[:, :, :], second[:, :, :],
                                        g2[:, :].unsqueeze(2).to_broadcast([P, TB, E]), ALU.mult))
                    c.wait()
                    dve.tensor_tensor(gates_next[:, :, :], first[:, :, :], second[:, :, :],
                                      ALU.add).then_inc(gates_ready, 1)
                    assert n + c.n == VEC, n + c.n

                def move_gates(b):
                    dve.wait_ge(gates_ready, b + 1)
                    dve.tensor_copy(gates[:, :, :], gates_next[:, :, :]).then_inc(gates_moved, 1)

                ln.vector(dve, 0, lambda t: core.X[:, t, :], lambda t: xn[:, t, :])
                chain = choose(0)
                weigh(0, chain)
                dve.wait_ge(xt_ready, 1)
                dve.tensor_copy(xT[:, :], xT_next[:, :]).then_inc(xt_moved, 1)
                move_gates(0)
                with dve.Fori(0, B) as b:
                    def next_tokens(t):
                        return core.X[:, b * TB + TB + t, :]

                    dve.wait_ge(gates_turned, b + 1)
                    dve.tensor_copy(gatesT[:, :], psT[0:E, :]).then_inc(gatesT_ready, 1)
                    dve.wait_ge(gates_moved, b + 1)
                    for e in range(E):
                        dve.wait_ge(y_done, b * E + e + 1)
                        if e >= 1:
                            dve.wait_ge(y_used, b * E + e)
                        for t in range(TB):
                            x = core.X[:, b * TB + t, :]
                            last = dve.scalar_tensor_tensor(out=x, in0=psY[:, e % 2, t * P:(t + 1) * P],
                                                            scalar=gates[:, t, e:e + 1], in1=x,
                                                            op0=ALU.mult, op1=ALU.add)
                        last.then_inc(y_used, 1)
                        if e == 0:
                            dve.wait_ge(y_used, b * E + 1)
                            dve.wait_ge(bias_done, b + 1)
                            add_to_stream(dve, core, b, psL[:, :], bias_added)
                            dve.wait_ge(bias_added, b + 1)
                        if e == STATS_AT:
                            ln.statistics(dve, b + 1, next_tokens)
                        if e == NORM_AT:
                            ln.finish(dve, b + 1, next_tokens, lambda t: xn[:, t, :])
                        if e == CHOOSE_AT:
                            choose(b + 1)
                        if e == GATES_AT:
                            weigh(b + 1, chain)
                            dve.wait_ge(h_done, (b * E + E) * FC)
                            dve.tensor_copy(xT[:, :], xT_next[:, :]).then_inc(xt_moved, 1)
                    dve.wait_ge(y_used, (b + 1) * E)
                    move_gates(b + 1)


UNITS = (((3, 0),), ((2, 0), (0, 384)), ((1, 0),))


def unit_width(u):
    return sum((i + 1) * P for i, _ in UNITS[u])


UNITS_T = (((0, 0),), ((1, 0), (3, 384)), ((2, 0),))


def unit_width_t(u):
    return sum((TB - k) * P for k, _ in UNITS_T[u])


def layer0_attn(nc, core):
    H, DH, PER = 16, 8, 4
    NU = len(UNITS)
    PARTS = 3
    ROWS = 32 * PARTS
    KEEP = 4
    PSLOTS = 8
    MSLOTS = 4
    assert PSLOTS * sum(unit_width_t(u) for u in range(NU)) == PROBS_COLS
    SCORES, STACK = 2, 3
    G = H // PER
    FIRST = ["tokens", "q", "q swapped", "k", "k swapped", "v"]
    USES = [("tokens", 3), ("sums 0", 4), ("turn 0", 5), ("q", 6), ("q swapped", 7), ("sums 1", 8), ("turn 1", 9),
            ("k", 10), ("k swapped", 11), ("sums 2", 12), ("turn 2", 13), ("v", 14), ("sums 3", H), ("turn 3", H),
            ("out turned", H), ("out", H)]
    AFTER = {step: use for use, step in USES if step < H}
    ORDER = [use for use, _ in USES]
    with ExitStack() as ctx:
        def sb(name, shape, dt=F32):
            return ctx.enter_context(nc.sbuf_tensor("L0a_" + name, shape, dt))

        def sem(name):
            return core.semaphore(ctx, "L0a_" + name)

        ln = LayerNorm(nc, ctx, "L0a_ln", core)
        w = core.w["L0a"]
        xn = sb("xn", [P, TB, D])
        xT = sb("xT", [P, S])
        rot = sb("rot", [P, 2, S])
        part = sb("part", [P, 2, S])
        o_heads = sb("o_heads", [P, S])
        parts = sb("parts", [P, 2, 2, PARTS, S], BF16)
        q_stack = sb("q_stack", [P, KEEP, S], BF16)
        k_stack = sb("k_stack", [P, KEEP, S], BF16)
        pick_q = sb("pick_q", [P, H, 32], BF16)
        pick_k = sb("pick_k", [P, H, 112], BF16)
        causal_t = sb("causal_t", [P, P], BF16)
        v = [sb("v_even", [P, TB, H, 32]), sb("v_odd", [P, TB, H, 32])]
        neg_max = sb("neg_max", [P, 2, TB])
        rest = sb("rest", [P, TB])
        zero = sb("zero", [P, TB])
        max_parts = sb("max_parts", [P, MSLOTS, TB, PARTS], BF16)
        probs = core.arena[:, 0:PROBS_COLS].rearrange("p (n c) -> p n c", n=PSLOTS)
        inv = sb("inv", [P, TB, PER])
        o = sb("o", [P, TB, D])
        oT = sb("oT", [P, S])
        psM = ctx.enter_context(nc.psum_tensor("L0a_psM", [P, S], F32))
        psO = ctx.enter_context(nc.psum_tensor("L0a_psO", [P, S], F32))
        psR = ctx.enter_context(nc.psum_tensor("L0a_psR", [P, 2, S], F32))
        psA = ctx.enter_context(nc.psum_tensor("L0a_psA", [P, 2, S], F32))
        psB = ctx.enter_context(nc.psum_tensor("L0a_psB", [P, 2, S], F32))
        (setup, values_laid, filled, emptied, rot_ready, leading, left, parts_ready, q_picked, k_picked, q_ready,
         k_ready, scores_done, max_ready, max_split, max_turned, max_rows, keyed_done, probs_ready, inv_ready) = (
            sem(n) for n in (
                "setup values_laid filled emptied rot_ready leading left parts_ready q_picked k_picked q_ready "
                "k_ready scores_done max_ready max_split max_turned max_rows keyed_done probs_ready inv_ready").split())
        SETUP = 4
        SPLIT = 4
        unit_at = [sum(unit_width_t(j) for j in range(u)) for u in range(NU)]
        key_at = {k: (unit_at[u] + at, (TB - k) * P) for u in range(NU) for k, at in UNITS_T[u]}

        def fills(b, use):
            return len(FIRST) + b * len(USES) + ORDER.index(use)

        def first_fills(use):
            return FIRST.index(use)

        with nc.Block() as block:
            @block.sync
            def _(sp):
                load_weights(core, sp, ("L0f", "L2a", "L2f", "L3a", "L3g"))

            @block.scalar
            def _(act):
                def copy_tokens(count):
                    act.wait_ge(filled, count + 1)
                    act.activation(xT[:, :], psO[:, :], ACT.Copy).then_inc(emptied, 1)

                def copy_values(count, half):
                    act.wait_ge(filled, count + 1)
                    act.activation(v[half][:, :, :, 0:DH], psO[:, :].rearrange("p (t h d) -> p t h d", t=TB, h=H),
                                   ACT.Copy).then_inc(emptied, 1)

                def copy_sums(count):
                    act.wait_ge(filled, count + 1)
                    act.activation(o_heads[:, :], psO[:, :], ACT.Copy).then_inc(emptied, 1)

                def leading_part(b, half, j, i):
                    if i == 0:
                        act.wait_ge(rot_ready, b * 2 + j + 1)
                    else:
                        act.wait_ge(left, b * 2 + j + 1)
                    act.activation(parts[:, half, j, i, :], (part if i else rot)[:, j, :],
                                   ACT.Copy).then_inc(leading, 1)

                def stack_queries(b, n):
                    act.wait_ge(q_picked, b * H + n + 1)
                    act.activation(q_stack[0:ROWS, n % KEEP, :], psR[0:ROWS, 0, :], ACT.Copy).then_inc(q_ready, 1)

                def step(b, half, n):
                    if n == 4:
                        copy_tokens(fills(b, "tokens"))
                    if n in (5, 9, 13):
                        copy_sums(fills(b, f"sums {n // PER - 1}"))
                    if n == 15:
                        copy_values(fills(b, "v"), 1 - half)
                    if n == 9:
                        leading_part(b + 1, 1 - half, 0, 0)
                    if n == 11:
                        leading_part(b + 1, 1 - half, 0, 1)
                    if n == 13:
                        leading_part(b + 1, 1 - half, 1, 1)
                    act.wait_ge(max_turned, b * H + n + 1)
                    act.activation(q_stack[ROWS:ROWS + PARTS, n % KEEP, :], psM[ROWS:ROWS + PARTS, :],
                                   ACT.Copy).then_inc(max_rows, 1)
                    stack_queries(b, n + STACK)
                    if n == 0:
                        act.wait_ge(emptied, fills(b, "tokens"))
                    if n >= PSLOTS and (n - PSLOTS) % PER == 0:
                        act.wait_ge(filled, fills(b, f"sums {(n - PSLOTS) // PER}") + 1)
                    for u in range(NU):
                        act.wait_ge(keyed_done, (b * H + n) * NU + u + 1)
                        act.activation(probs[:, n % PSLOTS, unit_at[u]:unit_at[u] + unit_width_t(u)],
                                       psB[:, (n * NU + u) % 2, 0:unit_width_t(u)], ACT.Exp).then_inc(probs_ready, 1)
                    if n == 1:
                        ln.scalar(act, b + 1)
                    if n == 12:
                        leading_part(b + 1, 1 - half, 1, 0)

                ln.scalar(act, 0)
                copy_tokens(first_fills("tokens"))
                for j in range(2):
                    for i in range(2):
                        leading_part(0, 0, j, i)
                act.wait_ge(values_laid, 3)
                copy_values(first_fills("v"), 0)
                for n in range(STACK):
                    stack_queries(0, n)
                with act.Fori(0, B // 2) as pair:
                    for half in range(2):
                        b = pair * 2 + half
                        for n in range(H):
                            step(b, half, n)
                        copy_sums(fills(b, "sums 3"))
                        act.wait_ge(filled, fills(b, "out turned") + 1)
                        act.activation(oT[:, :], psO[:, :], ACT.Copy).then_inc(emptied, 1)

            @block.tensor
            def _(pe):
                def pick_queries(b, half, n):
                    if n >= 1:
                        pe.wait_ge(q_ready, b * H + n)
                    if n % H == 0:
                        pe.wait_ge(parts_ready, (b + n // H) * 2 + 1)
                    for i in range(PARTS):
                        last = pe.matmul(psR[32 * i:32 * (i + 1), 0, :], pick_q[:, n % H, :],
                                         parts[:, (half + n // H) % 2, 0, i, :], start=True, stop=True)
                    last.then_inc(q_picked, 1)

                def pick_keys(b, half, n):
                    if n >= 1:
                        pe.wait_ge(k_ready, b * H + n)
                    if n % H == 0:
                        pe.wait_ge(parts_ready, (b + n // H) * 2 + 2)
                    for j in range(PARTS):
                        at = DH * (PARTS - 1 - j)
                        last = pe.matmul(psR[0:ROWS, 1, :], pick_k[:, n % H, at:at + ROWS],
                                         parts[:, (half + n // H) % 2, 1, j, :], start=j == 0, stop=j == PARTS - 1)
                    last.then_inc(k_picked, 1)

                def scores(b, n, u):
                    m = n * NU + u
                    if u == 0:
                        pe.wait_ge(q_ready, b * H + n + 1)
                        pe.wait_ge(k_ready, b * H + n + 1)
                    if m >= 2:
                        pe.wait_ge(max_ready, b * (H * NU) + m - 1)
                    for i, at in UNITS[u]:
                        pe.matmul(psA[:, m % 2, at:at + (i + 1) * P], q_stack[0:ROWS, n % KEEP, i * P:(i + 1) * P],
                                  k_stack[0:ROWS, n % KEEP, 0:(i + 1) * P], start=True, stop=False)
                        last = pe.matmul(psA[:, m % 2, at + i * P:at + (i + 1) * P], core.identb[:, :],
                                         core.causal[:, :], start=False, stop=True)
                    last.then_inc(scores_done, 1)

                def turn_maxima(b, n):
                    pe.wait_ge(max_split, (b * H + n) * SPLIT + SPLIT)
                    if n >= 1:
                        pe.wait_ge(max_rows, b * H + n)
                    for t in range(TB):
                        last = pe.matmul(psM[ROWS:ROWS + PARTS, t * P:(t + 1) * P], max_parts[:, n % MSLOTS, t, :],
                                         core.identb[:, :], start=True, stop=True)
                    last.then_inc(max_turned, 1)

                def keyed_scores(b, n, u):
                    m = n * NU + u
                    if u == 0:
                        pe.wait_ge(max_rows, b * H + n + 1)
                    if m >= 2:
                        pe.wait_ge(probs_ready, b * (H * NU) + m - 1)
                    for k, at in UNITS_T[u]:
                        pe.matmul(psB[:, m % 2, at:at + (TB - k) * P],
                                  k_stack[0:ROWS + PARTS, n % KEEP, k * P:(k + 1) * P],
                                  q_stack[0:ROWS + PARTS, n % KEEP, k * P:S], start=True, stop=False)
                        last = pe.matmul(psB[:, m % 2, at:at + P], core.identb[:, :], causal_t[:, :],
                                         start=False, stop=True)
                    last.then_inc(keyed_done, 1)

                def fill(b, half, use):
                    if b is None:
                        count, ln_n = first_fills(use), 0
                    else:
                        count, ln_n = fills(b, use), b + 1
                    if b is not None or count >= 1:
                        pe.wait_ge(emptied, count)
                    kind, g = use.split()[0], use.split()[-1]
                    if kind == "tokens":
                        turn(pe, core, ln, ln_n, xn, psO, filled)
                        return
                    if kind in ("q", "k"):
                        j = 2 * (kind == "k") + (g == "swapped")
                        last = pe.matmul(psO[:, :], w["qk"][:, j, :], xT[:, :], start=True, stop=True)
                    elif kind == "v":
                        for t in range(TB):
                            last = pe.matmul(psO[:, t * P:(t + 1) * P], xT[:, t * P:(t + 1) * P], w["v"][:, :],
                                             start=True, stop=True)
                    elif kind == "sums":
                        g = int(g)
                        pe.wait_ge(probs_ready, (b * H + (g + 1) * PER) * NU)
                        for k in range(TB):
                            at, width = key_at[k]
                            for j in range(PER):
                                n = g * PER + j
                                last = pe.matmul(psO[32 * j:32 * (j + 1), k * P:S], v[half][:, k, n, :],
                                                 probs[:, n % PSLOTS, at:at + width], start=k == 0, stop=k == TB - 1)
                    elif kind == "turn":
                        for t in range(TB):
                            last = pe.transpose(psO[:, t * P:(t + 1) * P], o_heads[:, t * P:(t + 1) * P], core.ident)
                    elif g == "turned":
                        for t in range(TB):
                            last = pe.transpose(psO[:, t * P:(t + 1) * P], o[:, t, :], core.ident)
                    else:
                        for t in range(TB):
                            last = pe.matmul(psO[:, t * P:(t + 1) * P], oT[:, t * P:(t + 1) * P], w["o"][:, :],
                                             start=True, stop=True)
                    last.then_inc(filled, 1)

                for use in FIRST:
                    fill(None, 0, use)
                    if use == "tokens":
                        core.wait_weights(pe, "L0a")
                pe.wait_ge(setup, SETUP)
                for n in range(STACK):
                    pick_queries(0, 0, n)
                    pick_keys(0, 0, n)
                    if n < SCORES:
                        for u in range(NU):
                            scores(0, n, u)
                pe.wait_ge(emptied, len(FIRST))
                pe.wait_ge(values_laid, 3)
                with pe.Fori(0, B // 2) as pair:
                    for half in range(2):
                        b = pair * 2 + half
                        for n in range(H):
                            turn_maxima(b, n)
                            pick_queries(b, half, n + STACK)
                            scores(b, n + SCORES, 0)
                            scores(b, n + SCORES, 1)
                            keyed_scores(b, n, 0)
                            pick_keys(b, half, n + STACK)
                            scores(b, n + SCORES, 2)
                            keyed_scores(b, n, 1)
                            keyed_scores(b, n, 2)
                            if n in AFTER:
                                fill(b, half, AFTER[n])
                        for use in ("sums 3", "turn 3", "out turned", "out"):
                            fill(b, half, use)
                        pe.wait_ge(emptied, fills(b, "out") + 1)

            @block.gpsimd
            def _(pool):
                for half in range(2):
                    pool.memset(v[half][:, :, :, :], 0.0).then_inc(values_laid, 1)
                pool.wait_ge(values_laid, 2)
                pool.memset(v[0][:, :, :, DH], 1.0)
                pool.memset(v[1][:, :, :, DH], 1.0).then_inc(values_laid, 1)
                pool.wait_ge(setup, SETUP)

                def split_maxima(b, n):
                    c = Chain(pool, max_split, (b * H + n) * SPLIT)
                    pool.wait_ge(max_ready, (b * H + n + 1) * NU)
                    if n >= MSLOTS:
                        pool.wait_ge(max_turned, b * H + n - MSLOTS + 1)
                    parts_of = max_parts[:, n % MSLOTS, :, :]
                    c(pool.tensor_tensor(parts_of[:, :, 0], neg_max[:, n % 2, :], zero[:, :], ALU.add))
                    c.wait()
                    c(pool.tensor_tensor(rest[:, :], neg_max[:, n % 2, :], parts_of[:, :, 0], ALU.subtract))
                    c.wait()
                    c(pool.tensor_tensor(parts_of[:, :, 1], rest[:, :], zero[:, :], ALU.add))
                    c.wait()
                    c(pool.tensor_tensor(parts_of[:, :, 2], rest[:, :], parts_of[:, :, 1], ALU.subtract))
                    c.wait()

                for n in range(SCORES):
                    split_maxima(0, n)
                with pool.Fori(0, B) as b:
                    for n in range(SCORES, H + SCORES):
                        split_maxima(b, n)

            @block.vector
            def _(dve):
                def rotate(b, count, j, swapped):
                    dve.wait_ge(filled, count + 1)
                    if not swapped:
                        dve.tensor_tensor(rot[:, j, :], psO[:, :], w["cos"][:, j, :], ALU.mult).then_inc(emptied, 1)
                        return
                    dve.tensor_tensor(part[:, j, :], psO[:, :], w["sin"][:, j, :], ALU.mult).then_inc(emptied, 1)
                    dve.wait_ge(emptied, count + 1)
                    dve.tensor_tensor(rot[:, j, :], rot[:, j, :], part[:, j, :], ALU.add).then_inc(rot_ready, 1)

                def leave(b, half, j, i):
                    dve.wait_ge(leading, b * 4 + 2 * j + i + 1)
                    if i == 0:
                        dve.wait_ge(rot_ready, b * 2 + j + 1)
                        dve.tensor_tensor(part[:, j, :], rot[:, j, :], parts[:, half, j, 0, :],
                                          ALU.subtract).then_inc(left, 1)
                    else:
                        dve.tensor_tensor(parts[:, half, j, 2, :], part[:, j, :], parts[:, half, j, 1, :],
                                          ALU.subtract).then_inc(parts_ready, 1)

                def stack_keys(b, n):
                    dve.wait_ge(k_picked, b * H + n + 1)
                    dve.tensor_copy(k_stack[0:ROWS, n % KEEP, :], psR[0:ROWS, 1, :]).then_inc(k_ready, 1)

                def maxima(b, n, u):
                    m = n * NU + u
                    dve.wait_ge(scores_done, b * (H * NU) + m + 1)
                    for i, at in UNITS[u]:
                        last = dve.tensor_reduce(neg_max[:, n % 2, i:i + 1], psA[:, m % 2, at:at + (i + 1) * P],
                                                 AX, ALU.max, negate=True)
                    last.then_inc(max_ready, 1)

                def divide(b, g):
                    count = fills(b, f"turn {g}")
                    heads = psO[:, :].rearrange("p (t h c) -> p t h c", t=TB, h=PER)
                    dve.wait_ge(filled, count + 1)
                    dve.reciprocal(inv[:, :, :], heads[:, :, :, DH]).then_inc(inv_ready, 1)
                    dve.wait_ge(inv_ready, b * G + g + 1)
                    for t in range(TB):
                        last = dve.tensor_tensor(
                            o[:, t, g * PER * DH:(g + 1) * PER * DH].rearrange("p (h d) -> p h d", h=PER),
                            heads[:, t, :, 0:DH], inv[:, t, :].unsqueeze(2).to_broadcast([P, PER, DH]), ALU.mult)
                    last.then_inc(emptied, 1)

                ln.vector(dve, 0, lambda t: core.X[:, t, :], lambda t: xn[:, t, :])
                c = Chain(dve, setup)
                c(dve.memset(pick_q[:, :, :], 0.0))
                c(dve.memset(pick_k[:, :, :], 0.0))
                dve.memset(k_stack[ROWS:P, :, :], 1.0)
                c(dve.memset(zero[:, :], 0.0))
                c.wait()
                rows_of_head = core.ident.rearrange("p (h d) -> p h d", h=H)
                for j in range(PARTS):
                    dve.tensor_copy(pick_q[:, :, j * DH:(j + 1) * DH], rows_of_head)
                    dve.tensor_copy(pick_k[:, :, 2 * DH + 32 * j:3 * DH + 32 * j], rows_of_head)
                core.wait_weights(dve, "L0a")
                c(dve.tensor_copy(causal_t[:, :], w["causal_t"]))
                assert c.n == SETUP
                for j, kind in enumerate("qk"):
                    rotate(0, first_fills(kind), j, False)
                    rotate(0, first_fills(kind + " swapped"), j, True)
                for j in range(2):
                    for i in range(2):
                        leave(0, 0, j, i)
                for n in range(STACK):
                    stack_keys(0, n)
                    if n < SCORES:
                        for u in range(NU):
                            maxima(0, n, u)
                with dve.Fori(0, B // 2) as pair:
                    for half in range(2):
                        b = pair * 2 + half

                        def next_tokens(t):
                            return core.X[:, (pair * 2 + half + 1) * TB + t, :]

                        for n in range(H):
                            if n == 1:
                                ln.statistics(dve, b + 1, next_tokens)
                            if n == 2:
                                ln.finish(dve, b + 1, next_tokens, lambda t: xn[:, t, :])
                            if n in (6, 10, 14):
                                divide(b, n // PER - 1)
                            if n in (7, 8):
                                rotate(b + 1, fills(b, AFTER[n - 1]), 0, n == 8)
                            if n in (11, 12):
                                rotate(b + 1, fills(b, AFTER[n - 1]), 1, n == 12)
                            if n == 10:
                                leave(b + 1, 1 - half, 0, 0)
                            if n == 12:
                                leave(b + 1, 1 - half, 0, 1)
                            if n == 13:
                                leave(b + 1, 1 - half, 1, 1)
                            dve.wait_ge(max_split, (b * H + n + 1) * SPLIT)
                            maxima(b, n + SCORES, 0)
                            maxima(b, n + SCORES, 1)
                            stack_keys(b, n + STACK)
                            maxima(b, n + SCORES, 2)
                            if n == 12:
                                leave(b + 1, 1 - half, 1, 0)
                        divide(b, G - 1)
                        dve.wait_ge(filled, fills(b, "out") + 1)
                        add_to_stream(dve, core, b, psO[:, :], emptied)
                        dve.wait_ge(emptied, fills(b, "out") + 1)


def layer1_attn(nc, core):
    H = 8
    SCALE = float(D) ** -0.5
    KINDS = 4
    AU, VU, AC, VO = range(KINDS)
    W_QU, W_KU, W_VU, W_QC, W_KC, W_VC = range(6)
    NU = len(UNITS)
    LN_AT, TURN_AT = 3, 5
    RING = 4
    with ExitStack() as ctx:
        def sb(name, shape, dt=F32):
            return ctx.enter_context(nc.sbuf_tensor("L1a_" + name, shape, dt))

        def sem(name):
            return core.semaphore(ctx, "L1a_" + name)

        ln = LayerNorm(nc, ctx, "L1a_ln", core)
        w = core.w["L1a"]
        xn = sb("xn", [P, TB, D])
        xT = sb("xT", [P, S])
        xT_next = sb("xT_next", [P, S])
        folded = sb("folded", [P, 3, H, D])
        proj = sb("proj", [P, RING, KINDS, S])
        th_look = sb("th_look", [P, S])
        look = sb("look", [P, S])
        th_sum = sb("th_sum", [P, S])
        lower = sb("lower", [P, 2, S])
        neg_max = sb("neg_max", [P, TB])
        sums = sb("sums", [P, TB])
        inv = sb("inv", [P, TB])
        probs = sb("probs", [P, NU, S])
        probsT = sb("probsT", [P, TB, S])
        yT = sb("yT", [P, S])
        psJ = ctx.enter_context(nc.psum_tensor("L1a_psJ", [P, 2, S], F32))
        psD = ctx.enter_context(nc.psum_tensor("L1a_psD", [P, S], F32))
        psS = ctx.enter_context(nc.psum_tensor("L1a_psS", [P, NU, S], F32))
        psP = ctx.enter_context(nc.psum_tensor("L1a_psP", [P, S], F32))
        psO = ctx.enter_context(nc.psum_tensor("L1a_psO", [P, S], F32))
        (fold_done, fold_ready, turned, xt_ready, xt_moved, proj_done, proj_ready, look_done, look_tanh,
         look_ready, sum_done,
         sum_tanh, lower_ready, scores_done, vec, max_ready, probs_ready, normed, probs_turned, pt_ready, y_done,
         y_ready, y_turned,
         added) = (
            sem(n) for n in (
                "fold_done fold_ready turned xt_ready xt_moved proj_done proj_ready look_done look_tanh "
                "look_ready sum_done "
                "sum_tanh lower_ready scores_done vec max_ready probs_ready normed probs_turned pt_ready y_done "
                "y_ready y_turned "
                "added").split())
        VEC = 8
        FOLDS = 3 * H // TB
        after = core.cf[:, C_AFTER:C_AFTER + P].unsqueeze(1).to_broadcast([P, TB, P])

        with nc.Block() as block:
            @block.scalar
            def _(act):
                def evacuate(b, h, kind):
                    act.wait_ge(proj_done, (b * H + h) * KINDS + kind + 1)
                    act.activation(proj[:, h % RING, kind, :], psJ[:, kind % 2, :], ACT.Copy,
                                   scale=SCALE if kind == AC else 1.0).then_inc(proj_ready, 1)

                def look_tanhs(b, h):
                    act.wait_ge(look_done, b * H + h + 1)
                    act.activation(th_look[:, :], psD[:, :], ACT.Tanh, scale=0.5 * SCALE).then_inc(look_tanh, 1)

                def sum_tanhs(b, h):
                    act.wait_ge(sum_done, b * H + h + 1)
                    act.activation(th_sum[:, :], psD[:, :], ACT.Tanh, scale=0.5).then_inc(sum_tanh, 1)

                def exponential(b, h, u):
                    act.wait_ge(max_ready, (b * H + h) * NU + u + 1)
                    for i, at in UNITS[u]:
                        last = act.activation(probs[:, u, at:at + (i + 1) * P], psS[:, u, at:at + (i + 1) * P],
                                              ACT.Exp, bias=neg_max[:, i:i + 1], accum_out=sums[:, i:i + 1])
                    last.then_inc(probs_ready, 1)

                def copy_turned(b, h, u):
                    act.wait_ge(probs_turned, (b * H + h) * NU + u + 1)
                    for i, at in UNITS[u]:
                        last = act.activation(probsT[:, 0:i + 1, i * P:(i + 1) * P],
                                              psP[:, at:at + (i + 1) * P].rearrange("p (k q) -> p k q", q=P), ACT.Copy)
                    last.then_inc(pt_ready, 1)

                def copy_tokens(b):
                    act.wait_ge(turned, b + 1)
                    act.activation(xT_next[:, :], psP[:, :], ACT.Copy).then_inc(xt_ready, 1)

                flat = folded[:, :, :, :].rearrange("p a h d -> p (a h d)")
                for n in range(FOLDS):
                    act.wait_ge(fold_done, n + 1)
                    act.activation(flat[:, n * S:(n + 1) * S], psJ[:, n % 2, :], ACT.Copy).then_inc(fold_ready, 1)
                ln.scalar(act, 0)
                copy_tokens(0)
                for kind in range(KINDS):
                    evacuate(0, 0, kind)
                look_tanhs(0, 0)
                for kind in range(KINDS):
                    evacuate(0, 1, kind)
                sum_tanhs(0, 0)
                look_tanhs(0, 1)
                with act.Fori(0, B) as b:
                    for h in range(H):
                        if h == LN_AT:
                            ln.scalar(act, b + 1)
                        sum_tanhs(b, h + 1)
                        exponential(b, h, 0)
                        exponential(b, h, 1)
                        evacuate(b, h + 2, 0)
                        exponential(b, h, 2)
                        for u in range(NU):
                            copy_turned(b, h, u)
                            evacuate(b, h + 2, u + 1)
                        look_tanhs(b, h + 2)
                        if h == TURN_AT:
                            copy_tokens(b + 1)
                    act.wait_ge(y_done, b + 1)
                    act.activation(yT[:, :], psO[:, :], ACT.Copy).then_inc(y_ready, 1)

            @block.tensor
            def _(pe):
                core.wait_weights(pe, "L1a")

                def project(b, h, kind, first=False):
                    if not (first and kind < 2):
                        pe.wait_ge(proj_ready, (b * H + h) * KINDS + kind - 1)
                    weights = (w["qkv"][:, h % H, W_VU, :] if kind == VU else
                               folded[:, (AU, AC, VO).index(kind), h % H, :])
                    ps = psJ[:, kind % 2, :]
                    if kind in (VU, VO):
                        for t in range(TB):
                            last = pe.matmul(ps[:, t * P:(t + 1) * P], tokens_of(h)[:, t * P:(t + 1) * P], weights,
                                             start=True, stop=True)
                    else:
                        last = pe.matmul(ps, weights, tokens_of(h)[:, :], start=True, stop=True)
                    last.then_inc(proj_done, 1)

                def look_scores(b, h, first=False):
                    pe.wait_ge(proj_ready, (b * H + h) * KINDS + AU + 1)
                    if not first:
                        pe.wait_ge(lower_ready, b * H + h)
                    for t in range(TB):
                        blk = slice(t * P, (t + 1) * P)
                        last = pe.matmul(psD[:, blk], tokens_of(h)[:, blk], proj[:, h % RING, AU, blk],
                                         start=True, stop=True)
                    last.then_inc(look_done, 1)

                def look_sums(b, h):
                    pe.wait_ge(proj_ready, (b * H + h) * KINDS + VU + 1)
                    pe.wait_ge(look_ready, b * H + h + 1)
                    for t in range(TB):
                        blk = slice(t * P, (t + 1) * P)
                        last = pe.matmul(psD[:, blk], look[:, blk], proj[:, h % RING, VU, blk], start=True, stop=True)
                    last.then_inc(sum_done, 1)

                def scores(b, h):
                    pe.wait_ge(proj_ready, (b * H + h + 1) * KINDS)
                    if h == 0:
                        pe.wait_ge(xt_moved, b + 1)
                    for u in range(NU):
                        for i, at in UNITS[u]:
                            pe.matmul(psS[:, u, at:at + (i + 1) * P], proj[:, h % RING, AC, i * P:(i + 1) * P],
                                      xT[:, 0:(i + 1) * P], start=True, stop=False)
                            last = pe.matmul(psS[:, u, at + i * P:at + (i + 1) * P], core.identb[:, :],
                                             core.causal[:, :], start=False, stop=True)
                        last.then_inc(scores_done, 1)

                def turn_probs(b, h, u):
                    pe.wait_ge(normed, (b * H + h) * NU + u + 1)
                    if h or u:
                        pe.wait_ge(pt_ready, (b * H + h) * NU + u)
                    for c in range(unit_width(u) // P):
                        last = pe.transpose(psP[:, c * P:(c + 1) * P], probs[:, u, c * P:(c + 1) * P], core.ident)
                    last.then_inc(probs_turned, 1)

                def weigh_values(b, h):
                    pe.wait_ge(pt_ready, (b * H + h + 1) * NU)
                    for k in range(TB):
                        last = pe.matmul(psO[:, k * P:S], proj[:, h % RING, VO, k * P:(k + 1) * P],
                                         probsT[:, k, k * P:S], start=h == 0 and k == 0,
                                         stop=h == H - 1 and k == TB - 1)
                    if h == H - 1:
                        last.then_inc(y_done, 1)

                for n in range(FOLDS):
                    if n >= 2:
                        pe.wait_ge(fold_ready, n - 1)
                    for j in range(TB):
                        kind, h = (n * TB + j) // H, (n * TB + j) % H
                        left = w["qkv"][:, h, (W_QU, W_QC, W_VC)[kind], :]
                        right = w["out"][:, h, :] if kind == 2 else w["qkv"][:, h, (W_KU, W_KC)[kind], :]
                        last = pe.matmul(psJ[:, n % 2, j * P:(j + 1) * P], left, right, start=True, stop=True)
                    last.then_inc(fold_done, 1)
                pe.wait_ge(fold_ready, FOLDS)
                turn(pe, core, ln, 0, xn, psP, turned)
                tokens_of = lambda h: xT_next
                pe.wait_ge(xt_ready, 1)
                for kind in range(KINDS):
                    project(0, 0, kind, first=True)
                look_scores(0, 0, first=True)
                for kind in range(KINDS):
                    project(0, 1, kind)
                look_sums(0, 0)
                look_scores(0, 1)
                tokens_of = lambda h: xT if h < H else xT_next
                with pe.Fori(0, B) as b:
                    for h in range(H):
                        look_sums(b, h + 1)
                        scores(b, h)
                        if h + 2 == H:
                            pe.wait_ge(xt_ready, b + 2)
                        project(b, h + 2, 0)
                        for u in range(NU):
                            project(b, h + 2, u + 1)
                            turn_probs(b, h, u)
                        look_scores(b, h + 2)
                        if h == 0:
                            pe.wait_ge(added, b + 1)
                        weigh_values(b, h)
                        if h == TURN_AT:
                            turn(pe, core, ln, b + 1, xn, psP, turned)
                    pe.wait_ge(y_ready, b + 1)
                    for t in range(TB):
                        last = pe.transpose(psO[:, t * P:(t + 1) * P], yT[:, t * P:(t + 1) * P], core.ident)
                    last.then_inc(y_turned, 1)

            @block.vector
            def _(dve):
                def mask_look(b, h):
                    dve.wait_ge(look_tanh, b * H + h + 1)
                    dve.scalar_tensor_tensor(out=look[:, :].rearrange("p (t i) -> p t i", t=TB),
                                             in0=th_look[:, :].rearrange("p (t i) -> p t i", t=TB), scalar=1.0,
                                             in1=after, op0=ALU.add, op1=ALU.mult).then_inc(look_ready, 1)

                def lowering(b, h):
                    dve.wait_ge(sum_tanh, b * H + h + 1)
                    dve.scalar_tensor_tensor(out=lower[:, h % 2, :], in0=th_sum[:, :], scalar=1.0, in1=psD[:, :],
                                             op0=ALU.add, op1=ALU.mult).then_inc(lower_ready, 1)

                ln.vector(dve, 0, lambda t: core.X[:, t, :], lambda t: xn[:, t, :])
                mask_look(0, 0)
                lowering(0, 0)
                mask_look(0, 1)
                dve.wait_ge(xt_ready, 1)
                dve.tensor_copy(xT[:, :], xT_next[:, :]).then_inc(xt_moved, 1)
                dve.memset(inv[:, :], 0.0).then_inc(added, 1)
                dve.wait_ge(added, 1)
                with dve.Fori(0, B) as b:
                    def next_tokens(t):
                        return core.X[:, b * TB + TB + t, :]

                    for h in range(H):
                        c = Chain(dve, vec, b * (H * VEC) + h * VEC)
                        if h == LN_AT:
                            ln.statistics(dve, b + 1, next_tokens)
                        if h == LN_AT + 1:
                            ln.finish(dve, b + 1, next_tokens, lambda t: xn[:, t, :])
                        lowering(b, h + 1)
                        dve.wait_ge(lower_ready, b * H + h + 1)
                        for u in range(NU + 1):
                            if u < NU:
                                dve.wait_ge(scores_done, (b * H + h) * NU + u + 1)
                                for i, at in UNITS[u]:
                                    diag = psS[:, u, at + i * P:at + (i + 1) * P]
                                    c(dve.scalar_tensor_tensor(out=diag, in0=lower[:, h % 2, i * P:(i + 1) * P],
                                                               scalar=-0.5, in1=diag, op0=ALU.mult, op1=ALU.add))
                                c.wait()
                                for i, at in UNITS[u]:
                                    last = dve.tensor_reduce(neg_max[:, i:i + 1], psS[:, u, at:at + (i + 1) * P],
                                                             AX, ALU.max, negate=True)
                                last.then_inc(max_ready, 1)
                            if u >= 1:
                                dve.wait_ge(probs_ready, (b * H + h) * NU + u)
                                for i, at in UNITS[u - 1]:
                                    c(dve.reciprocal(inv[:, i:i + 1], sums[:, i:i + 1]))
                                c.wait()
                                for i, at in UNITS[u - 1]:
                                    row = probs[:, u - 1, at:at + (i + 1) * P]
                                    last = dve.tensor_scalar(row, row, inv[:, i:i + 1], None, ALU.mult)
                                last.then_inc(normed, 1)
                        assert c.n == VEC, c.n
                        mask_look(b, h + 2)
                    dve.tensor_copy(xT[:, :], xT_next[:, :]).then_inc(xt_moved, 1)
                    dve.wait_ge(y_turned, b + 1)
                    add_to_stream(dve, core, b, psO[:, :], added)
                    dve.wait_ge(added, b + 2)


def layer0_ffn(nc, core):
    DEPTH, H, DH, WIN = 2, 8, 64, 64
    HALF = D // 2
    HID = 341
    CH = (HID + P - 1) // P
    last_rows = HID - (CH - 1) * P
    K = WIN + P
    QK_SCALE = 8.0
    NU = TB * 2
    HU = H // 2
    NB = NU - 2
    KINDS = [(1, t) for t in range(TB)] + [(0, t) for t in range(TB)]
    NQK = len(KINDS)
    NPOOL = NQK - 2
    with ExitStack() as ctx:
        def sb(name, shape, dt=F32):
            return ctx.enter_context(nc.sbuf_tensor("L0f_" + name, shape, dt))

        def sem(name):
            return core.semaphore(ctx, "L0f_" + name)

        ln = LayerNorm(nc, ctx, "L0f_ln", core)
        w = core.w["L0f"]
        x = sb("x", [P, TB, D])
        h = sb("h", [P, TB, D])
        hT = sb("hT", [P, S])
        table = sb("table", [P, DEPTH, 2, 2, TB * DH])
        scratch = sb("scratch", [P, 2 * HU * K])
        squares = scratch[:, 0:2 * S].rearrange("p (j n) -> p j n", j=2)
        norms = sb("norms", [P, 2, TB, H])
        root = sb("root", [P, 2, TB, H])
        guess = sb("guess", [P, 2, TB, H])
        corr = sb("corr", [P, 2, TB, H])
        inv_norm = sb("inv_norm", [P, 2, TB, H])
        qk = sb("qk", [P, 2, TB, S])
        part = sb("part", [P, 2, S])
        qkT = sb("qkT", [P, 2, HU, S])
        v = sb("v", [P, TB, S])
        v_before = sb("v_before", [WIN, TB, S])
        neg_max = sb("neg_max", [P, TB, H])
        bias = sb("bias", [P, TB, H])
        sums = sb("sums", [P, TB, H])
        inv = sb("inv", [P, TB, H])
        probs = scratch[:, :].rearrange("p (j g k) -> p j g k", j=2, g=HU)
        own_T = qk[:, 1, 0:2, :]
        before_T = qk[0:WIN, 1, 2:4, :]
        o = part[:, 0, :]
        oT = part[:, 1, :]
        gelu = qk[:, 0, 0:CH, :]
        gated = qk[:, 1, 0:CH, :]
        psS = ctx.enter_context(nc.psum_tensor("L0f_psS", [P, 4, S], F32))
        psP = ctx.enter_context(nc.psum_tensor("L0f_psP", [P, 2, S], F32))
        psO = ctx.enter_context(nc.psum_tensor("L0f_psO", [P, S], F32))
        psX = ctx.enter_context(nc.psum_tensor("L0f_psX", [P, S], F32))
        (tables, shifted, half_ready, h_ready, turned, ht_ready, qk_done, squared, vec, v_done, v_ready, squares_used,
         rotated, before_loaded, norms_ready, rooted, inv_ready, k_scaled, q_late, qk_ready,
         qk_turned, qkt_ready, scores_done, bias_ready, probs_ready, own_turned, before_turned,
         own_ready, before_ready, av_done, o_ready, o_turned, ot_ready, y_done, x_ready, a_done, g_done, gelu_ready,
         gated_ready, out_done, added) = (sem(n) for n in (
             "tables shifted half_ready h_ready turned ht_ready qk_done squared vec v_done v_ready squares_used "
             "rotated before_loaded norms_ready rooted inv_ready k_scaled q_late qk_ready "
             "qk_turned qkt_ready scores_done bias_ready probs_ready own_turned before_turned "
             "own_ready before_ready av_done o_ready o_turned ot_ready y_done x_ready a_done g_done gelu_ready "
             "gated_ready out_done added").split())
        VEC = 2 * 20
        shift_in = core.cf[:, C_SHIFT:C_SHIFT + P]
        shift_over = core.cf[:, C_OVER:C_OVER + P]

        def rows(c):
            return P if c < CH - 1 else last_rows

        def halves(ap):
            return ap.rearrange("p (h a d) -> p h a d", h=H, a=2)

        def first_key(t):
            return WIN if t == 0 else 0

        def scores_of(n):
            return psS[:, 2 * (n % 2):2 * (n % 2) + 2, 0:2 * K].rearrange("p b (g k) -> p b g k", g=2)

        with nc.Block() as block:
            @block.sync
            def _(sp):
                load_layer1_weights(core, sp)
                for bl in range(B * DEPTH):
                    sp.wait_ge(v_ready, bl * TB + TB)
                    sp.dma_start(v_before[:, 1:TB, :], v[WIN:P, 0:TB - 1, :]).then_inc(before_loaded, 16)
                    sp.wait_ge(before_loaded, bl * 16 + 16)

            @block.gpsimd
            def _(pool):
                with pool.Fori(0, B * DEPTH) as bl:
                    def add_swapped(n):
                        j, t = KINDS[n]
                        pool.wait_ge(rotated, bl * NQK + n + 1)
                        pool.tensor_tensor(qk[:, j, t, :], qk[:, j, t, :], part[:, n % 2, :],
                                           ALU.add).then_inc(qk_ready, 1)

                    for n in range(TB):
                        add_swapped(n)
                    for t in range(TB):
                        k = qk[:, 1, t, :].rearrange("p (h d) -> p h d", h=H)
                        pool.wait_ge(qk_ready, bl * NPOOL + t + 1)
                        pool.wait_ge(inv_ready, bl * 2 + 1)
                        pool.tensor_tensor(k, k, inv_norm[:, 1, t, :].unsqueeze(2).to_broadcast([P, H, DH]),
                                           ALU.mult).then_inc(k_scaled, 1)
                        if TB + t < NPOOL:
                            add_swapped(TB + t)

            @block.scalar
            def _(act):
                core.wait_weights(act, "L0f")

                def copy_shifted(b, s):
                    act.wait_ge(shifted, b * 4 + s + 1)
                    act.activation(h[:, :, HALF:D], psX[:, 0:TB * HALF].rearrange("p (t d) -> p t d", t=TB),
                                   ACT.Copy).then_inc(half_ready, 1)

                def roots(bl, j):
                    act.wait_ge(norms_ready, bl * 2 + (1 - j) + 1)
                    act.activation(root[:, j, :, :], norms[:, j, :, :], ACT.Sqrt).then_inc(rooted, 1)

                with act.Fori(0, B) as b:
                    ln.scalar(act, b * 3)
                    for l in range(DEPTH):
                        bl = b * DEPTH + l
                        copy_shifted(b, 2 * l)
                        act.wait_ge(turned, bl * 2 + 1)
                        act.activation(hT[:, :], psX[:, :], ACT.Copy).then_inc(ht_ready, 1)
                        for n in range(NQK):
                            act.wait_ge(qk_done, bl * NQK + n + 1)
                            if n >= 2:
                                act.wait_ge(squares_used, bl * NQK + n - 1)
                            act.activation(squares[:, n % 2, :], psS[:, n % 4, :], ACT.Square).then_inc(squared, 1)
                            if n < TB:
                                act.wait_ge(v_done, bl * TB + n + 1)
                                act.activation(v[:, n, :], psP[:, n % 2, :], ACT.Copy).then_inc(v_ready, 1)
                            if n == TB:
                                roots(bl, 1)
                        for m in range(NQK):
                            if m == NQK // 2:
                                roots(bl, 0)
                            t = m // 2
                            act.wait_ge(qk_turned, bl * NQK + m + 1)
                            ps = psX[:, :] if m % 2 else psP[:, t % 2, :]
                            act.activation(qkT[:, 1 - m % 2, :, t * P:(t + 1) * P],
                                           ps.rearrange("p (g k) -> p g k", g=HU), ACT.Copy).then_inc(qkt_ready, 1)
                        for n in range(NU + 3):
                            if n < NU:
                                t, half = n // 2, n % 2
                                act.wait_ge(bias_ready, bl * NU + n + 1)
                                if n >= 2:
                                    act.wait_ge(own_turned, bl * NU + n - 1)
                                if n >= 4:
                                    act.wait_ge(before_turned, bl * NB + n - 3)
                                for g in range(HU):
                                    hd, k0 = half * HU + g, first_key(t)
                                    last = act.activation(probs[:, n % 2, g, k0:K],
                                                          scores_of(n)[:, g % 2, g // 2, k0:K], ACT.Exp, bias=bias[:, t, hd:hd + 1],
                                                          scale=inv_norm[:, 0, t, hd:hd + 1],
                                                          accum_out=sums[:, t, hd:hd + 1])
                                last.then_inc(probs_ready, 1)
                            m = n - 1
                            if 2 <= m < NU:
                                act.wait_ge(before_turned, bl * NB + m - 1)
                                act.wait_ge(av_done, bl * NU + m - 1)
                                act.activation(before_T[:, m % 2, :], psP[0:WIN, 1, :],
                                               ACT.Copy).then_inc(before_ready, 1)
                            m = n - 3
                            if m >= 0 and m % 2:
                                act.wait_ge(o_turned, bl * TB + m // 2 + 1)
                                act.activation(oT, psX[:, :], ACT.Copy).then_inc(ot_ready, 1)
                        copy_shifted(b, 2 * l + 1)
                        ln.scalar(act, b * 3 + 1 + l)
                        act.wait_ge(turned, bl * 2 + 2)
                        act.activation(hT[:, :], psX[:, :], ACT.Identity, bias=w["ln"][:, 2 * l + 1:2 * l + 2],
                                       scale=w["ln"][:, 2 * l:2 * l + 1]).then_inc(ht_ready, 1)
                        for c in range(CH):
                            act.wait_ge(g_done, bl * CH + c + 1)
                            col = w["b1"][0:rows(c), (l * 2 + 1) * CH + c:(l * 2 + 1) * CH + c + 1]
                            ps = psS[:, 3, :] if c == 0 else psP[:, c - 1, :]
                            act.activation(gelu[0:rows(c), c, :], ps[0:rows(c), :], ACT.Gelu,
                                           bias=col).then_inc(gelu_ready, 1)

            @block.tensor
            def _(pe):
                core.wait_weights(pe, "L0f")

                def shift():
                    pe.matmul(psX[:, 0:TB * HALF], shift_in, x[:, :, HALF:D], start=True, stop=False)
                    pe.matmul(psX[:, HALF:TB * HALF], shift_over, x[:, 0:TB - 1, HALF:D],
                              start=False, stop=True).then_inc(shifted, 1)

                def scores(bl, n):
                    t, half = n // 2, n % 2
                    k0 = first_key(t)
                    if n >= 2:
                        pe.wait_ge(probs_ready, bl * NU + n - 1)
                    for g in range(HU):
                        hd = half * HU + g
                        r = slice(DH * (hd % 2), DH * (hd % 2) + DH)
                        out = scores_of(n)[:, g % 2, g // 2, k0:K]
                        pe.matmul(out, qkT[r, 0, hd // 2, t * P:(t + 1) * P],
                                  qkT[r, 1, hd // 2, t * P - WIN + k0:(t + 1) * P], start=True, stop=False)
                        last = pe.matmul(out, core.identb[:, :], core.band[:, k0:K], start=False, stop=True)
                    last.then_inc(scores_done, 1)

                def turn_probs(bl, n):
                    t = n // 2
                    pe.wait_ge(probs_ready, bl * NU + n + 1)
                    if n >= 1:
                        pe.wait_ge(own_ready, bl * NU + n)
                    if n >= 3:
                        pe.wait_ge(before_ready, bl * NB + n - 2)
                    for g in range(HU):
                        last = pe.transpose(psP[:, 0, g * P:(g + 1) * P], probs[:, n % 2, g, WIN:K], core.ident)
                    last.then_inc(own_turned, 1)
                    if t >= 1:
                        for g in range(HU):
                            last = pe.transpose(psP[0:WIN, 1, g * P:(g + 1) * P], probs[:, n % 2, g, 0:WIN],
                                                core.ident)
                        last.then_inc(before_turned, 1)

                def weigh_values(bl, n):
                    t, half = n // 2, n % 2
                    pe.wait_ge(own_ready, bl * NU + n + 1)
                    if t >= 1:
                        pe.wait_ge(before_ready, bl * NB + n - 1)
                        pe.wait_ge(before_loaded, bl * 16 + 16)
                    if half == 0 and t >= 1:
                        pe.wait_ge(o_ready, bl * TB + t)
                    for g in range(HU):
                        hd = half * HU + g
                        out = psO[:, hd * DH:(hd + 1) * DH]
                        if t >= 1:
                            pe.matmul(out, before_T[:, n % 2, g * P:(g + 1) * P],
                                      v_before[:, t, hd * DH:(hd + 1) * DH], start=True, stop=False)
                        last = pe.matmul(out, own_T[:, n % 2, g * P:(g + 1) * P], v[:, t, hd * DH:(hd + 1) * DH],
                                         start=t == 0, stop=True)
                    last.then_inc(av_done, 1)

                def turn_out(bl, t):
                    pe.wait_ge(o_ready, bl * TB + t + 1)
                    if t >= 1:
                        pe.wait_ge(x_ready, bl * (TB + 1) + t)
                    for g in range(HU):
                        last = pe.transpose(psX[:, g * P:(g + 1) * P], o[:, g * P:(g + 1) * P], core.ident)
                    last.then_inc(o_turned, 1)

                def project_out(bl, l, t):
                    pe.wait_ge(ot_ready, bl * TB + t + 1)
                    for g in range(HU):
                        last = pe.matmul(psX[:, 0:D], oT[:, g * P:(g + 1) * P], w["wo"][:, l, g, :],
                                         start=g == 0, stop=g == HU - 1)
                    last.then_inc(y_done, 1)

                with pe.Fori(0, B) as b:
                    for l in range(DEPTH):
                        bl = b * DEPTH + l
                        if l == 0:
                            pe.wait_ge(ln.ready, b * (3 * TB) + TB)
                        else:
                            pe.wait_ge(x_ready, b * (2 * TB + 2) + TB + 1)
                        shift()
                        pe.wait_ge(h_ready, bl * 2 + 1)
                        pe.wait_ge(half_ready, bl * 2 + 1)
                        for t in range(TB):
                            last = pe.transpose(psX[:, t * P:(t + 1) * P], h[:, t, :], core.ident)
                        last.then_inc(turned, 1)
                        pe.wait_ge(ht_ready, bl * 2 + 1)
                        for n in range(NQK):
                            j, t = KINDS[n]
                            if n >= 4:
                                pe.wait_ge(rotated, bl * NQK + n - 3)
                                pe.wait_ge(squared, bl * NQK + n - 3)
                            pe.matmul(psS[:, n % 4, :], hT[:, t * P:(t + 1) * P], w["wqkv"][:, l, j, :],
                                      start=True, stop=True).then_inc(qk_done, 1)
                            if n < TB:
                                if n >= 2:
                                    pe.wait_ge(v_ready, bl * TB + n - 1)
                                pe.matmul(psP[:, n % 2, :], hT[:, n * P:(n + 1) * P], w["wqkv"][:, l, 2, :],
                                          start=True, stop=True).then_inc(v_done, 1)
                        pe.wait_ge(v_ready, bl * TB + TB)
                        for m in range(NQK):
                            t = m // 2
                            if m % 2:
                                if TB + t < NPOOL:
                                    pe.wait_ge(qk_ready, bl * NPOOL + TB + t + 1)
                                else:
                                    pe.wait_ge(q_late, bl * (NQK - NPOOL) + TB + t - NPOOL + 1)
                                if t >= 1:
                                    pe.wait_ge(qkt_ready, bl * NQK + m - 1)
                            else:
                                pe.wait_ge(k_scaled, bl * TB + t + 1)
                                if t >= 2:
                                    pe.wait_ge(qkt_ready, bl * NQK + m - 3)
                            for g in range(HU):
                                ps = psX[:, g * P:(g + 1) * P] if m % 2 else psP[:, t % 2, g * P:(g + 1) * P]
                                last = pe.transpose(ps, qk[:, 1 - m % 2, t, g * P:(g + 1) * P], core.ident)
                            last.then_inc(qk_turned, 1)
                        pe.wait_ge(qkt_ready, bl * 8 + 8)
                        for n in range(NU + 4):
                            if n < NU:
                                scores(bl, n)
                            if 0 <= n - 1 < NU:
                                turn_probs(bl, n - 1)
                            if 0 <= n - 2 < NU:
                                weigh_values(bl, n - 2)
                            if n - 3 >= 0 and (n - 3) % 2 and n - 3 < NU:
                                turn_out(bl, (n - 3) // 2)
                            if n - 4 >= 0 and (n - 4) % 2:
                                project_out(bl, l, (n - 4) // 2)
                        pe.wait_ge(x_ready, bl * (TB + 1) + TB)
                        shift()
                        for t in range(TB):
                            pe.wait_ge(ln.ready, b * (3 * TB) + (l + 1) * TB + t + 1)
                            last = pe.transpose(psX[:, t * P:(t + 1) * P], h[:, t, :], core.ident)
                        last.then_inc(turned, 1)
                        pe.wait_ge(ht_ready, bl * 2 + 2)
                        for c in range(CH):
                            ps = psS[:, 3, :] if c == 0 else psP[:, c - 1, :]
                            pe.matmul(ps[0:rows(c), :], w["w1"][:, l, HID + c * P:HID + c * P + rows(c)], hT[:, :],
                                      start=True, stop=True).then_inc(g_done, 1)
                            pe.matmul(psS[0:rows(c), c, :], w["w1"][:, l, c * P:c * P + rows(c)], hT[:, :],
                                      start=True, stop=True).then_inc(a_done, 1)
                        pe.wait_ge(gated_ready, bl * CH + CH)
                        for t in range(TB):
                            out = psO[:, t * P:(t + 1) * P]
                            for c in range(CH):
                                pe.matmul(out, gated[0:rows(c), c, t * P:(t + 1) * P], w["w2"][0:rows(c), l, c, :],
                                          start=c == 0, stop=False)
                            last = pe.matmul(out, core.ones_row, w["b2"][0:1, l, :], start=False, stop=True)
                        last.then_inc(out_done, 1)

            @block.vector
            def _(dve):
                core.wait_weights(dve, "L0f")
                for l in range(DEPTH):
                    for j in range(2):
                        for f in range(2):
                            last = dve.tensor_tensor(
                                table[:, l, j, f, :].rearrange("p (t d) -> p t d", t=TB),
                                w["pos"][:, j, f, :].rearrange("p (t d) -> p t d", t=TB),
                                w["scales"][:, l * 4 + j * 2 + f, :].unsqueeze(1).to_broadcast([P, TB, DH]), ALU.mult)
                last.then_inc(tables, 1)
                dve.wait_ge(tables, 1)

                def inverse(c, bl, j):
                    scale = 1.0 if j else QK_SCALE
                    dve.wait_ge(rooted, bl * 2 + (1 - j) + 1)
                    c(dve.reciprocal(guess[:, j, :, :], root[:, j, :, :]))
                    c.wait()
                    c(dve.tensor_tensor(corr[:, j, :, :], guess[:, j, :, :], guess[:, j, :, :], ALU.mult))
                    c.wait()
                    c(dve.tensor_tensor(corr[:, j, :, :], corr[:, j, :, :], norms[:, j, :, :], ALU.mult))
                    c.wait()
                    c(dve.tensor_scalar(corr[:, j, :, :], corr[:, j, :, :], -0.5 * scale, 1.5 * scale,
                                        ALU.mult, ALU.add))
                    c.wait()
                    dve.tensor_tensor(inv_norm[:, j, :, :], corr[:, j, :, :], guess[:, j, :, :],
                                      ALU.mult).then_inc(inv_ready, 1)

                with dve.Fori(0, B) as b:
                    ln.vector(dve, b * 3, lambda t: core.X[:, b * TB + t, :], lambda t: x[:, t, :])
                    c = Chain(dve, vec, b * VEC)
                    for l in range(DEPTH):
                        bl = b * DEPTH + l
                        if l == 0:
                            dve.wait_ge(ln.ready, b * (3 * TB) + TB)
                        dve.tensor_copy(h[:, :, 0:HALF], x[:, :, 0:HALF]).then_inc(h_ready, 1)
                        for n in range(NQK):
                            j, t = KINDS[n]
                            ps = psS[:, n % 4, :]
                            cos = table[:, l, j, 0, t * DH:(t + 1) * DH].unsqueeze(1).to_broadcast([P, H, DH])
                            sin = table[:, l, j, 1, t * DH:(t + 1) * DH].rearrange("p (a d) -> p a d", a=2)
                            dve.wait_ge(squared, bl * NQK + n + 1)
                            dve.tensor_reduce(norms[:, j, t, :],
                                              squares[:, n % 2, :].rearrange("p (h d) -> p h d", h=H), AX, ALU.add).then_inc(squares_used, 1)
                            dve.tensor_tensor(qk[:, j, t, :].rearrange("p (h d) -> p h d", h=H),
                                              ps.rearrange("p (h d) -> p h d", h=H), cos, ALU.mult)
                            if n >= 2:
                                dve.wait_ge(qk_ready, bl * NPOOL + n - 1)
                            for a in range(2):
                                last = dve.tensor_tensor(halves(part[:, n % 2, :])[:, :, a, :],
                                                         halves(ps)[:, :, 1 - a, :],
                                                         sin[:, a, :].unsqueeze(1).to_broadcast([P, H, DH // 2]),
                                                         ALU.mult)
                            last.then_inc(rotated, 1)
                            if n >= NPOOL:
                                dve.wait_ge(rotated, bl * NQK + n + 1)
                                dve.tensor_tensor(qk[:, j, t, :], qk[:, j, t, :], part[:, n % 2, :],
                                                  ALU.add).then_inc(q_late, 1)
                            if t == TB - 1:
                                dve.wait_ge(squares_used, bl * NQK + n + 1)
                                dve.tensor_scalar(norms[:, j, :, :], norms[:, j, :, :], 1e-24, None,
                                                  ALU.max).then_inc(norms_ready, 1)
                            if n == TB:
                                inverse(c, bl, 1)
                        inverse(c, bl, 0)
                        dve.wait_ge(inv_ready, bl * 2 + 2)
                        for n in range(NU + 4):
                            if n < NU:
                                t, half = n // 2, n % 2
                                hs = slice(half * HU, half * HU + HU)
                                dve.wait_ge(scores_done, bl * NU + n + 1)
                                c(dve.tensor_reduce(neg_max[:, t, hs].rearrange("p (g b) -> p b g", b=2),
                                                    scores_of(n)[:, :, :, first_key(t):K], AX, ALU.max, negate=True))
                                c.wait()
                                dve.tensor_tensor(bias[:, t, hs], neg_max[:, t, hs], inv_norm[:, 0, t, hs],
                                                  ALU.mult).then_inc(bias_ready, 1)
                            m = n - 1
                            if 0 <= m < NU:
                                dve.wait_ge(own_turned, bl * NU + m + 1)
                                if m >= 2:
                                    dve.wait_ge(av_done, bl * NU + m - 1)
                                dve.tensor_copy(own_T[:, m % 2, :], psP[:, 0, :]).then_inc(own_ready, 1)
                            m = n - 2
                            if m >= 0 and m % 2 and m < NU:
                                t = m // 2
                                dve.wait_ge(av_done, bl * NU + m + 1)
                                dve.wait_ge(probs_ready, bl * NU + m + 1)
                                if t >= 1:
                                    dve.wait_ge(o_turned, bl * TB + t)
                                c(dve.reciprocal(inv[:, t, :], sums[:, t, :]))
                                c.wait()
                                dve.tensor_tensor(o.rearrange("p (h d) -> p h d", h=H),
                                                  psO[:, :].rearrange("p (h d) -> p h d", h=H),
                                                  inv[:, t, :].unsqueeze(2).to_broadcast([P, H, DH]),
                                                  ALU.mult).then_inc(o_ready, 1)
                            m = n - 4
                            if m >= 0 and m % 2:
                                t = m // 2
                                dve.wait_ge(y_done, bl * TB + t + 1)
                                dve.tensor_tensor(x[:, t, :], x[:, t, :], psX[:, 0:D], ALU.add).then_inc(x_ready, 1)
                        dve.wait_ge(x_ready, bl * (TB + 1) + TB)
                        dve.tensor_copy(h[:, :, 0:HALF], x[:, :, 0:HALF]).then_inc(h_ready, 1)
                        dve.wait_ge(h_ready, bl * 2 + 2)
                        dve.wait_ge(half_ready, bl * 2 + 2)
                        ln.vector(dve, b * 3 + 1 + l, lambda t: h[:, t, :], lambda t: h[:, t, :])
                        for k in range(CH):
                            r = rows(k)
                            dve.wait_ge(gelu_ready, bl * CH + k + 1)
                            dve.wait_ge(a_done, bl * CH + k + 1)
                            dve.scalar_tensor_tensor(out=gated[0:r, k, :], in0=psS[0:r, k, :],
                                                     scalar=w["b1"][0:r, l * 2 * CH + k:l * 2 * CH + k + 1],
                                                     in1=gelu[0:r, k, :], op0=ALU.add,
                                                     op1=ALU.mult).then_inc(gated_ready, 1)
                        dve.wait_ge(out_done, bl + 1)
                        dve.tensor_tensor(x[:, :, :], x[:, :, :], psO[:, :].rearrange("p (t d) -> p t d", t=TB),
                                          ALU.add).then_inc(x_ready, 1)
                        dve.wait_ge(x_ready, bl * (TB + 1) + TB + 1)
                    xb = core.X[:, bass.ds(b * TB, TB), :]
                    dve.tensor_tensor(xb, xb, x[:, :, :], ALU.add).then_inc(added, 1)
                    dve.wait_ge(added, b + 1)
                    assert c.n == VEC, c.n


def layer2_ffn(nc, core):
    E, TOPK = 8, 64
    PAIRS = E // 2
    ROT = 32
    SCALE = float(D) ** -0.5
    G = D + 2 * ROT
    BP = P // B
    TOP = 23
    with ExitStack() as ctx:
        def sb(name, shape, dt=F32):
            return ctx.enter_context(nc.sbuf_tensor("L2f_" + name, shape, dt))

        def sem(name):
            return core.semaphore(ctx, "L2f_" + name)

        ln = LayerNorm(nc, ctx, "L2f_ln", core)
        w = core.w["L2f"]
        xg = sb("xg", [P, NT + TB, G])
        xT = sb("xT", [P, S])
        score = sb("score", [P, S])
        work = sb("work", [P, S])
        top8 = sb("top8", [P, 8])
        chosen = sb("chosen", [P, S])
        rank = sb("rank", [P, S])
        rankT = sb("rankT", [P, TB, P + BP])
        scoreT = sb("scoreT", [P, TB, P + BP])
        (turned, xt_ready, logits_done, exp_ready, top, angles, rank_turned, rank_ready) = (
            sem(n) for n in "turned xt_ready logits_done exp_ready top angles rank_turned rank_ready".split())
        with ExitStack() as first:
            psT = first.enter_context(nc.psum_tensor("L2f_psT", [P, S], F32))
            psL = first.enter_context(nc.psum_tensor("L2f_psL", [P, S], F32))
            psK = first.enter_context(nc.psum_tensor("L2f_psK", [P, 2, S], F32))
            with nc.Block() as block:
                @block.gpsimd
                def _(pool):
                    core.wait_weights(pool, "L2f")
                    pool.memset(xg[:, NT:NT + TB, :], 0.0)
                    pool.memset(rankT[:, :, P:P + BP], 0.0)
                    pool.memset(scoreT[:, :, P:P + BP], 0.0)
                    for b in range(B):
                        last = pool.tensor_copy(xg[:, b * TB:(b + 1) * TB, D:G], w["angles"])
                    last.then_inc(angles, 1)

                @block.scalar
                def _(act):
                    core.wait_weights(act, "L2f")
                    for b in range(B):
                        ln.scalar(act, b)
                        act.wait_ge(turned, b + 1)
                        act.activation(xT[:, :], psT[:, :], ACT.Copy).then_inc(xt_ready, 1)
                        act.wait_ge(logits_done, b + 1)
                        if b == 0:
                            act.wait_ge(top, 1)
                        act.activation(score[b * BP:b * BP + E, :], psL[b * BP:b * BP + E, :], ACT.Exp,
                                       scale=-1.0).then_inc(exp_ready, 1)
                    for j, dst in enumerate((rankT, scoreT)):
                        act.wait_ge(rank_turned, j + 1)
                        act.activation(dst[:, :, 0:P], psK[:, j, :].rearrange("p (t r) -> p t r", t=TB),
                                       ACT.Copy).then_inc(rank_ready, 1)

                @block.tensor
                def _(pe):
                    core.wait_weights(pe, "L2f")
                    for b in range(B):
                        for t in range(TB):
                            pe.wait_ge(ln.ready, b * TB + t + 1)
                            last = pe.transpose(psT[:, t * P:(t + 1) * P], xg[:, b * TB + t, 0:D], core.ident)
                        last.then_inc(turned, 1)
                        pe.wait_ge(xt_ready, b + 1)
                        pe.matmul(psL[b * BP:b * BP + E, :], w["router"], xT[:, :],
                                  start=True, stop=True).then_inc(logits_done, 1)
                    for j, src in enumerate((rank, score)):
                        if j == 0:
                            pe.wait_ge(top, TOP)
                        for t in range(TB):
                            last = pe.transpose(psK[:, j, t * P:(t + 1) * P], src[:, t * P:(t + 1) * P], core.ident)
                        last.then_inc(rank_turned, 1)

                @block.vector
                def _(dve):
                    c = Chain(dve, top)
                    c(dve.memset(score[:, :], 0.0))
                    for b in range(B):
                        ln.vector(dve, b, lambda t: core.X[:, b * TB + t, :], lambda t: xg[:, b * TB + t, 0:D])
                    dve.wait_ge(exp_ready, B)
                    c(dve.tensor_scalar(score[:, :], score[:, :], 1.0, None, ALU.add))
                    c.wait()
                    c(dve.reciprocal(score[:, :], score[:, :]))
                    c.wait()
                    c(dve.tensor_copy(work[:, :], score[:, :]))
                    for _ in range(TOPK // 8):
                        c.wait()
                        c(dve.max(top8[:, :], work[:, :]))
                        c.wait()
                        c(dve.match_replace(work[:, :], top8[:, :], work[:, :], -1.0))
                    c.wait()
                    c(dve.tensor_scalar(chosen[:, :], work[:, :], -1.0, None, ALU.is_equal))
                    c.wait()
                    c(dve.tensor_tensor_scan(rank[:, :], chosen[:, :], chosen[:, :], 0.0, ALU.add, ALU.max))
                    c.wait()
                    c(dve.tensor_tensor(rank[:, :], rank[:, :], chosen[:, :], ALU.mult))
                    assert c.n == TOP, c.n
        onehot = sb("onehot", [P, TB, E * TOPK])
        weighted = sb("weighted", [P, TB, E * TOPK])
        weightedT = sb("weightedT", [P, 2, PAIRS, S])
        taken = sb("taken", [P, PAIRS, G])
        takenT = sb("takenT", [P, S])
        qk = sb("qk", [P, PAIRS, 2, D])
        v = sb("v", [P, PAIRS, D])
        part = sb("part", [P, 2, PAIRS, 2 * ROT])
        qkT = sb("qkT", [P, 2, S])
        neg_max = sb("neg_max", [P, PAIRS])
        sums = sb("sums", [P, PAIRS])
        inv = sb("inv", [P, PAIRS])
        probs = sb("probs", [P, S])
        probsT = sb("probsT", [P, S])
        avT = sb("avT", [P, S])
        result = sb("result", [P, PAIRS, D])
        psA = ctx.enter_context(nc.psum_tensor("L2f_psA", [P, 2, S], F32))
        psQ = ctx.enter_context(nc.psum_tensor("L2f_psQ", [P, PAIRS, S], F32))
        psT = ctx.enter_context(nc.psum_tensor("L2f_psT2", [P, S], F32))
        psS = ctx.enter_context(nc.psum_tensor("L2f_psS", [P, S], F32))
        (onehot_ready, weighted_ready, taken_done, taken_ready, weights_turned, wt_ready, taken_turned, tt_ready,
         qkv_done, rest_ready, vec, rot_ready, qk_turned, qkt_ready, scores_done, bias_ready, probs_ready,
         probs_turned, pt_ready, av_done, av_ready, result_done, result_ready, out_done, added) = (
            sem(n) for n in (
                "onehot_ready weighted_ready taken_done taken_ready weights_turned wt_ready taken_turned tt_ready "
                "qkv_done rest_ready vec rot_ready qk_turned qkt_ready scores_done bias_ready probs_ready "
                "probs_turned pt_ready av_done av_ready result_done result_ready out_done added").split())
        VEC = 8
        count_up = core.cf[:, C_COUNT:C_COUNT + TOPK].unsqueeze(1).to_broadcast([P, E, TOPK])
        with nc.Block() as block:
            @block.scalar
            def _(act):
                def copy_taken(b):
                    for j in range(2):
                        act.wait_ge(taken_done, b * 2 + j + 1)
                        act.activation(taken[:, 2 * j:2 * j + 2, :],
                                       psA[:, j, 0:2 * G].rearrange("p (a g) -> p a g", a=2),
                                       ACT.Copy).then_inc(taken_ready, 1)

                def copy_weights(b, half):
                    for t in range(TB):
                        act.wait_ge(weights_turned, b * TB + t + 1)
                        act.activation(weightedT[:, half, :, t * P:(t + 1) * P],
                                       psQ[:, t, :].rearrange("p (a k) -> p a k", a=PAIRS),
                                       ACT.Copy).then_inc(wt_ready, 1)

                def copy_taken_turned(b):
                    act.wait_ge(taken_turned, b + 1)
                    act.activation(takenT[:, :], psT[:, :], ACT.Copy).then_inc(tt_ready, 1)

                copy_taken(0)
                copy_weights(0, 0)
                copy_taken_turned(0)
                with act.Fori(0, B // 2) as pair:
                    for half in range(2):
                        b = pair * 2 + half
                        act.wait_ge(qkv_done, b + 1)
                        for j in range(2):
                            act.activation(qk[:, :, j, 2 * ROT:D], psQ[:, :, j * D + 2 * ROT:(j + 1) * D], ACT.Copy)
                        act.activation(v[:, :, :], psQ[:, :, 2 * D:3 * D], ACT.Copy).then_inc(rest_ready, 1)
                        for j in range(2):
                            act.wait_ge(qk_turned, b * 2 + j + 1)
                            act.activation(qkT[:, j, :], psA[:, j, :], ACT.Copy).then_inc(qkt_ready, 1)
                        act.wait_ge(bias_ready, b + 1)
                        for a in range(PAIRS):
                            last = act.activation(probs[:, a * P:(a + 1) * P], psS[:, a * P:(a + 1) * P], ACT.Exp,
                                                  bias=neg_max[:, a:a + 1], scale=SCALE, accum_out=sums[:, a:a + 1])
                        last.then_inc(probs_ready, 1)
                        copy_taken(b + 1)
                        act.wait_ge(probs_turned, b + 1)
                        act.activation(probsT[:, :], psT[:, :], ACT.Copy).then_inc(pt_ready, 1)
                        copy_weights(b + 1, 1 - half)
                        act.wait_ge(av_done, b + 1)
                        act.activation(avT[:, :], psS[:, :], ACT.Copy).then_inc(av_ready, 1)
                        copy_taken_turned(b + 1)

            @block.tensor
            def _(pe):
                def gather(b):
                    pe.wait_ge(onehot_ready, b + 1)
                    for a in range(PAIRS):
                        for t in range(TB):
                            last = pe.matmul(psA[:, a // 2, (a % 2) * G:(a % 2 + 1) * G],
                                             onehot[:, t, a * P:(a + 1) * P], xg[:, b * TB + t, :],
                                             start=t == 0, stop=t == TB - 1)
                        if a % 2:
                            last.then_inc(taken_done, 1)

                def turn_weights(b):
                    pe.wait_ge(weighted_ready, b + 1)
                    for t in range(TB):
                        for a in range(PAIRS):
                            last = pe.transpose(psQ[:, t, a * P:(a + 1) * P], weighted[:, t, a * P:(a + 1) * P],
                                                core.ident)
                        last.then_inc(weights_turned, 1)

                def turn_taken(b):
                    pe.wait_ge(taken_ready, b * 2 + 2)
                    for a in range(PAIRS):
                        last = pe.transpose(psT[:, a * P:(a + 1) * P], taken[:, a, 0:D], core.ident)
                    last.then_inc(taken_turned, 1)

                gather(0)
                turn_weights(0)
                turn_taken(0)
                with pe.Fori(0, B // 2) as pair:
                    for half in range(2):
                        b = pair * 2 + half
                        pe.wait_ge(tt_ready, b + 1)
                        pe.wait_ge(wt_ready, (b + 1) * TB)
                        for e in range(E):
                            r = TOPK * (e % 2)
                            last = pe.matmul(psQ[r:r + TOPK, e // 2, 0:3 * D], takenT[:, e * TOPK:(e + 1) * TOPK],
                                             w["qkv"][:, e, :], start=True, stop=True)
                        last.then_inc(qkv_done, 1)
                        pe.wait_ge(rest_ready, b + 1)
                        pe.wait_ge(added, b + 1)
                        for j in range(2):
                            pe.wait_ge(rot_ready, b * 2 + j + 1)
                            for a in range(PAIRS):
                                last = pe.transpose(psA[:, j, a * P:(a + 1) * P], qk[:, a, j, :], core.ident)
                            last.then_inc(qk_turned, 1)
                        pe.wait_ge(qkt_ready, b * 2 + 2)
                        for a in range(PAIRS):
                            blk = slice(a * P, (a + 1) * P)
                            pe.matmul(psS[:, blk], qkT[:, 0, blk], qkT[:, 1, blk], start=True, stop=False)
                            last = pe.matmul(psS[:, blk], core.identb[:, :], core.pair_mask[:, :],
                                             start=False, stop=True)
                        last.then_inc(scores_done, 1)
                        gather(b + 1)
                        pe.wait_ge(probs_ready, b + 1)
                        for a in range(PAIRS):
                            last = pe.transpose(psT[:, a * P:(a + 1) * P], probs[:, a * P:(a + 1) * P], core.ident)
                        last.then_inc(probs_turned, 1)
                        turn_weights(b + 1)
                        pe.wait_ge(pt_ready, b + 1)
                        for a in range(PAIRS):
                            blk = slice(a * P, (a + 1) * P)
                            last = pe.matmul(psS[:, blk], v[:, a, :], probsT[:, blk], start=True, stop=True)
                        last.then_inc(av_done, 1)
                        pe.wait_ge(av_ready, b + 1)
                        pe.wait_ge(taken_ready, (b + 1) * 2 + 2)
                        for e in range(E):
                            r = TOPK * (e % 2)
                            last = pe.matmul(psA[r:r + TOPK, 0, (e // 2) * D:(e // 2 + 1) * D],
                                             avT[:, e * TOPK:(e + 1) * TOPK], w["out"][:, e, :], start=True, stop=True)
                        last.then_inc(result_done, 1)
                        turn_taken(b + 1)
                        pe.wait_ge(result_ready, b + 1)
                        for t in range(TB):
                            for a in range(PAIRS):
                                last = pe.matmul(psA[:, 1, t * P:(t + 1) * P],
                                                 weightedT[:, half, a, t * P:(t + 1) * P], result[:, a, :],
                                                 start=a == 0, stop=a == PAIRS - 1)
                        last.then_inc(out_done, 1)

            @block.vector
            def _(dve):
                def make_onehots(b):
                    for t in range(TB):
                        last = dve.tensor_tensor(
                            onehot[:, t, :].rearrange("p (e k) -> p e k", e=E), count_up,
                            rankT[:, t, bass.ds(b * BP, E)].unsqueeze(2).to_broadcast([P, E, TOPK]), ALU.is_equal)
                    last.then_inc(onehot_ready, 1)

                def weigh_onehots(b):
                    dve.wait_ge(onehot_ready, b + 1)
                    for t in range(TB):
                        last = dve.tensor_tensor(
                            weighted[:, t, :].rearrange("p (e k) -> p e k", e=E),
                            onehot[:, t, :].rearrange("p (e k) -> p e k", e=E),
                            scoreT[:, t, bass.ds(b * BP, E)].unsqueeze(2).to_broadcast([P, E, TOPK]), ALU.mult)
                    last.then_inc(weighted_ready, 1)

                dve.wait_ge(rank_ready, 2)
                make_onehots(0)
                weigh_onehots(0)
                dve.memset(inv[:, :], 0.0).then_inc(added, 1)
                dve.wait_ge(added, 1)
                with dve.Fori(0, B // 2) as pair:
                    for half in range(2):
                        b = pair * 2 + half
                        c = Chain(dve, vec, b * VEC)
                        dve.wait_ge(taken_done, b * 2 + 2)
                        make_onehots(b + 1)
                        dve.wait_ge(rest_ready, b + 1)
                        dve.wait_ge(taken_ready, b * 2 + 2)
                        cos = taken[:, :, D:D + ROT].unsqueeze(2).to_broadcast([P, PAIRS, 2, ROT])
                        sin = taken[:, :, D + ROT:G]
                        for j in range(2):
                            src = psQ[:, :, j * D:j * D + 2 * ROT]
                            dst = qk[:, :, j, 0:2 * ROT]
                            c(dve.tensor_tensor(dst.rearrange("p a (h r) -> p a h r", h=2),
                                                src.rearrange("p a (h r) -> p a h r", h=2), cos, ALU.mult))
                            c(dve.scalar_tensor_tensor(out=part[:, j, :, 0:ROT], in0=src[:, :, ROT:2 * ROT],
                                                       scalar=-1.0, in1=sin, op0=ALU.mult, op1=ALU.mult))
                            c(dve.tensor_tensor(part[:, j, :, ROT:2 * ROT], src[:, :, 0:ROT], sin, ALU.mult))
                            c.wait()
                            dve.tensor_tensor(dst, dst, part[:, j, :, :], ALU.add).then_inc(rot_ready, 1)
                        dve.wait_ge(weights_turned, (b + 1) * TB)
                        weigh_onehots(b + 1)
                        dve.wait_ge(scores_done, b + 1)
                        c(dve.tensor_reduce(neg_max[:, :], psS[:, :].rearrange("p (a k) -> p a k", a=PAIRS), AX,
                                            ALU.max, negate=True))
                        c.wait()
                        dve.tensor_scalar(neg_max[:, :], neg_max[:, :], SCALE, None, ALU.mult).then_inc(bias_ready, 1)
                        dve.wait_ge(probs_ready, b + 1)
                        c(dve.reciprocal(inv[:, :], sums[:, :]))
                        dve.wait_ge(result_done, b + 1)
                        c.wait()
                        dve.tensor_tensor(result[:, :, :], psA[:, 0, :].rearrange("p (a d) -> p a d", a=PAIRS),
                                          inv[:, :].unsqueeze(2).to_broadcast([P, PAIRS, D]),
                                          ALU.mult).then_inc(result_ready, 1)
                        dve.wait_ge(out_done, b + 1)
                        add_to_stream(dve, core, b, psA[:, 1, :], added)
                        dve.wait_ge(added, b + 2)
                        assert c.n == VEC, c.n


def layer3_ffn(nc, core):
    E, INTER, TOPK, CAP = 64, 96, 8, 32
    T = B * S
    PER = P // CAP
    TILES = E // PER
    ROW = D + E
    TB_BANKS = NT // 4
    with ExitStack() as ctx:
        def sb(name, shape, dt=F32):
            return ctx.enter_context(nc.sbuf_tensor("L3f_" + name, shape, dt))

        def sem(name):
            return core.semaphore(ctx, "L3f_" + name)

        ln = LayerNorm(nc, ctx, "L3f_ln", core)
        w = core.w["L3f"]
        rows = nc.dram_tensor("L3f_rows", (T + 1, ROW), F32, kind="Internal").ap()
        xg = sb("xg", [P, NT, ROW])
        empty = sb("empty", [1, ROW])
        xT = sb("xT", [P, S])
        neg_max = sb("neg_max", [P, TB])
        numer = sb("numer", [P, TB, E])
        best = sb("best", [P, TB, TOPK])
        struck = sb("struck", [P, TB, E])
        denom = sb("denom", [P, TB])
        inv = sb("inv", [P, TB])
        key = sb("key", [P, TB, E])
        keyT = sb("keyT", [E, T])
        first = sb("first", [E, CAP])
        firstT = sb("firstT", [CAP, E])
        token_of = sb("token_of", [P, TILES])
        token_idx = sb("token_idx", [P, TILES], U32)
        taken = sb("taken", [P, TILES * (ROW + PER) + D])
        count = sb("count", [P, T])
        onehot = sb("onehot", [P, 2, T])
        takenT = sb("takenT", [P, P])
        th = sb("th", [P, INTER])
        act_up = sb("act_up", [P, 2, INTER])
        hiddenT = sb("hiddenT", [INTER, P])
        gate_pick = sb("gate_pick", [P, PER])
        gate = sb("gate", [P, TILES])
        y = sb("y", [P, TILES, D])

        (turned, xt_ready, logits_done, max_ready, exp_ready, vec, key_ready, key_turned, kt_ready, rows_ready,
         rows_stored, empty_ready, first_turned, ft_ready, places_done, idx_ready, counted, mark) = (
            sem(n) for n in (
                "turned xt_ready logits_done max_ready exp_ready vec key_ready key_turned kt_ready rows_ready "
                "rows_stored empty_ready first_turned ft_ready places_done idx_ready counted mark").split())
        gathered = [sem(f"gathered{j}") for j in range(TILES)]
        VEC = 12
        MARK = 8

        def taken_row(j):
            return taken[:, j * ROW:(j + 1) * ROW]

        with ExitStack() as routing:
            psT = routing.enter_context(nc.psum_tensor("L3f_psT", [P, S], F32))
            psL = routing.enter_context(nc.psum_tensor("L3f_psL", [P, S], F32))
            psK = routing.enter_context(nc.psum_tensor("L3f_psK", [P, S], F32))
            psF = routing.enter_context(nc.psum_tensor("L3f_psF", [P, S], F32))
            psN = routing.enter_context(nc.psum_tensor("L3f_psN", [P, S], F32))
            with nc.Block() as block:
                @block.sync
                def _(sp):
                    sp.wait_ge(empty_ready, 1)
                    sp.dma_start(rows[T:T + 1, :], empty[:, :]).then_inc(rows_stored, 16)
                    for b in range(B):
                        sp.wait_ge(rows_ready, b + 1)
                        sp.dma_start(rows[b * S:(b + 1) * S, :].rearrange("(t p) g -> p t g", p=P),
                                     xg[:, b * TB:(b + 1) * TB, :]).then_inc(rows_stored, 16)

                @block.gpsimd
                def _(pool):
                    pool.memset(empty[:, :], 0.0).then_inc(empty_ready, 1)
                    pool.iota(onehot[:, 0, :].bitcast(mybir.dt.int32), [[1, T]], base=0,
                              channel_multiplier=0).then_inc(counted, 1)
                    pool.wait_ge(counted, 1)
                    pool.tensor_copy(count[:, :], onehot[:, 0, :].bitcast(mybir.dt.int32)).then_inc(counted, 1)

                @block.scalar
                def _(act):
                    core.wait_weights(act, "L3g")
                    ln.scalar(act, 0)
                    for b in range(B):
                        act.wait_ge(turned, b + 1)
                        act.activation(xT[:, :], psT[:, :], ACT.Copy).then_inc(xt_ready, 1)
                        if b + 1 < B:
                            ln.scalar(act, b + 1)
                        act.wait_ge(max_ready, b + 1)
                        for t in range(TB):
                            last = act.activation(numer[:, t, :], psL[:, t * E:(t + 1) * E], ACT.Exp,
                                                  bias=neg_max[:, t:t + 1])
                        last.then_inc(exp_ready, 1)
                        act.wait_ge(key_turned, b + 1)
                        act.activation(keyT[:, b * S:(b + 1) * S], psK[0:E, :], ACT.Copy).then_inc(kt_ready, 1)

                @block.tensor
                def _(pe):
                    core.wait_weights(pe, "L3g")
                    for b in range(B):
                        for t in range(TB):
                            pe.wait_ge(ln.ready, b * TB + t + 1)
                            last = pe.transpose(psT[:, t * P:(t + 1) * P], xg[:, b * TB + t, 0:D], core.ident)
                        last.then_inc(turned, 1)
                        pe.wait_ge(xt_ready, b + 1)
                        if b >= 1:
                            pe.wait_ge(exp_ready, b)
                        for t in range(TB):
                            last = pe.matmul(psL[:, t * E:(t + 1) * E], xT[:, t * P:(t + 1) * P],
                                             core.w["L3g"]["router"], start=True, stop=True)
                        last.then_inc(logits_done, 1)
                        pe.wait_ge(key_ready, b + 1)
                        if b >= 1:
                            pe.wait_ge(kt_ready, b)
                        for t in range(TB):
                            last = pe.transpose(psK[0:E, t * P:(t + 1) * P], key[:, t, :], core.ident)
                        last.then_inc(key_turned, 1)
                    pe.wait_ge(mark, MARK)
                    pe.transpose(psF[0:CAP, 0:E], first[:, :], core.ident[0:E, 0:E]).then_inc(first_turned, 1)
                    pe.wait_ge(ft_ready, 1)
                    for r in range(PER):
                        last = pe.matmul(psN[r * CAP:(r + 1) * CAP, 0:TILES], core.ident[0:CAP, 0:CAP],
                                         firstT[:, r:E:PER], start=True, stop=True)
                    last.then_inc(places_done, 1)

                @block.vector
                def _(dve):
                    core.wait_weights(dve, "L3g")

                    def normalise(b):
                        ln.vector(dve, b, lambda t: core.X[:, b * TB + t, :], lambda t: xg[:, b * TB + t, 0:D])

                    normalise(0)
                    for b in range(B):
                        if b + 1 < B:
                            normalise(b + 1)
                        c = Chain(dve, vec, b * VEC)
                        dve.wait_ge(logits_done, b + 1)
                        if b >= 1:
                            dve.wait_ge(exp_ready, b)
                        dve.tensor_reduce(neg_max[:, :], psL[:, 0:TB * E].rearrange("p (t e) -> p t e", t=TB), AX,
                                          ALU.max, negate=True).then_inc(max_ready, 1)
                        dve.wait_ge(exp_ready, b + 1)
                        for t in range(TB):
                            c(dve.max(best[:, t, :], numer[:, t, :]))
                        c.wait()
                        for t in range(TB):
                            c(dve.match_replace(struck[:, t, :], best[:, t, :], numer[:, t, :], -1.0))
                        c(dve.tensor_reduce(denom[:, :], best[:, :, :], AX, ALU.add))
                        c.wait()
                        c(dve.reciprocal(inv[:, :], denom[:, :]))
                        if b >= 1:
                            dve.wait_ge(key_turned, b)
                        ahead = core.cf[:, C_AHEAD + b * TB:C_AHEAD + (b + 1) * TB]
                        dve.scalar_tensor_tensor(out=key[:, :, :], in0=struck[:, :, :], scalar=-1.0,
                                                 in1=ahead.unsqueeze(2).to_broadcast([P, TB, E]),
                                                 op0=ALU.is_equal, op1=ALU.mult).then_inc(key_ready, 1)
                        gates = xg[:, b * TB:(b + 1) * TB, D:ROW]
                        c(dve.scalar_tensor_tensor(out=gates, in0=struck[:, :, :], scalar=-1.0, in1=numer[:, :, :],
                                                   op0=ALU.is_equal, op1=ALU.mult))
                        c.wait()
                        c(dve.tensor_tensor(gates, gates, inv[:, :].unsqueeze(2).to_broadcast([P, TB, E]), ALU.mult))
                        c.wait()
                        dve.wait_ge(ln.ready, (b + 1) * TB)
                        dve.wait_ge(key_ready, b + 1)
                        dve.memset(neg_max[:, 0:1], 0.0).then_inc(rows_ready, 1)
                        dve.wait_ge(rows_ready, b + 1)
                        assert c.n == VEC, c.n
                    dve.wait_ge(kt_ready, B)
                    c = Chain(dve, mark)
                    for k in range(CAP // 8):
                        c(dve.max(first[:, 8 * k:8 * k + 8], keyT[:, :]))
                        c.wait()
                        if k < CAP // 8 - 1:
                            c(dve.match_replace(keyT[:, :], first[:, 8 * k:8 * k + 8], keyT[:, :], 0.0))
                            c.wait()
                    c(dve.tensor_scalar(first[:, :], first[:, :], -1.0, float(T), ALU.mult, ALU.add))
                    assert c.n == MARK, c.n
                    dve.wait_ge(first_turned, 1)
                    dve.tensor_copy(firstT[:, :], psF[0:CAP, 0:E]).then_inc(ft_ready, 1)
                    dve.wait_ge(places_done, 1)
                    c(dve.tensor_copy(token_of[:, :], psN[:, 0:TILES]))
                    c.wait()
                    dve.tensor_copy(token_idx[:, :], token_of[:, :]).then_inc(idx_ready, 1)

        psC = ctx.enter_context(nc.psum_tensor("L3f_psC", [P, TB_BANKS, S], F32))
        psG, psH, psU, psY = (ctx.enter_context(nc.psum_tensor("L3f_ps" + c, [P, S], F32)) for c in "GHUY")
        (taken_turned, tt_ready, h_done, tanh_ready, steps, hidden_ready, hidden_turned, ht_ready, y_done, gate_ready,
         y_ready, onehot_ready, combined, summed) = (sem(n) for n in (
             "taken_turned tt_ready h_done tanh_ready steps hidden_ready hidden_turned ht_ready y_done gate_ready "
             "y_ready onehot_ready combined summed").split())
        with nc.Block() as block:
            @block.gpsimd
            def _(pool):
                pool.wait_ge(rows_stored, 16 * (B + 1))
                pool.wait_ge(idx_ready, 1)
                for j in range(TILES):
                    pool.indirect_dma_start(
                        out=taken_row(j), out_offset=None, in_=rows[:, :],
                        in_offset=bass.IndirectOffsetOnAxis(ap=token_idx[:, j:j + 1], axis=0),
                    ).then_inc(gathered[j], 16)

            @block.scalar
            def _(act):
                for j in range(TILES):
                    act.wait_ge(taken_turned, j + 1)
                    if j >= 1:
                        act.wait_ge(h_done, j)
                    act.activation(takenT[:, :], psG[:, 0:P], ACT.Copy).then_inc(tt_ready, 1)
                    act.wait_ge(h_done, j + 1)
                    if j >= 1:
                        act.wait_ge(hidden_ready, j)
                    act.activation(th[:, :], psH[:, 0:INTER], ACT.Tanh, scale=0.5).then_inc(tanh_ready, 1)
                    act.wait_ge(hidden_turned, j + 1)
                    if j >= 1:
                        act.wait_ge(y_done, j)
                    act.activation(hiddenT[:, :], psU[0:INTER, 0:P], ACT.Copy).then_inc(ht_ready, 1)

            @block.tensor
            def _(pe):
                core.wait_weights(pe, "L3f")

                def turn_taken(j):
                    pe.wait_ge(gathered[j], 16)
                    if j >= 1:
                        pe.wait_ge(tt_ready, j)
                    pe.transpose(psG[:, 0:P], taken_row(j)[:, 0:D], core.ident).then_inc(taken_turned, 1)

                def combine(j, part):
                    if part == 0:
                        pe.wait_ge(onehot_ready, j + 1)
                        pe.wait_ge(y_ready, j + 1)
                    for t in range(part * 4, part * 4 + 4):
                        last = pe.matmul(psC[:, t // 4, (t % 4) * P:(t % 4 + 1) * P],
                                         onehot[:, j % 2, t * P:(t + 1) * P], y[:, j, :],
                                         start=j == 0 and t % 4 == 0, stop=j == TILES - 1, skip_group_check=True)
                    if part == 3:
                        last.then_inc(combined, 1)

                turn_taken(0)
                for j in range(TILES):
                    pe.wait_ge(tt_ready, j + 1)
                    if j >= 1:
                        pe.wait_ge(hidden_ready, j)
                    for r in range(PER):
                        last = pe.matmul(psH[r * CAP:(r + 1) * CAP, 0:2 * INTER], takenT[:, r * CAP:(r + 1) * CAP],
                                         w["gate_up"][:, j * PER + r, :], start=True, stop=True)
                    last.then_inc(h_done, 1)
                    if j + 1 < TILES:
                        turn_taken(j + 1)
                    if j >= 1:
                        combine(j - 1, 0)
                        combine(j - 1, 1)
                    pe.wait_ge(hidden_ready, j + 1)
                    if j >= 1:
                        pe.wait_ge(ht_ready, j)
                    pe.transpose(psU[0:INTER, 0:P], act_up[:, 1, :], core.ident).then_inc(hidden_turned, 1)
                    if j >= 1:
                        combine(j - 1, 2)
                        combine(j - 1, 3)
                    pe.wait_ge(ht_ready, j + 1)
                    if j >= 1:
                        pe.wait_ge(y_ready, j)
                    for r in range(PER):
                        last = pe.matmul(psY[r * CAP:(r + 1) * CAP, 0:D], hiddenT[:, r * CAP:(r + 1) * CAP],
                                         w["down"][:, j * PER + r, :], start=True, stop=True)
                    last.then_inc(y_done, 1)
                for part in range(4):
                    combine(TILES - 1, part)

            @block.vector
            def _(dve):
                dve.wait_ge(counted, 2)
                c = Chain(dve, steps)
                for j in range(TILES):
                    if j >= 2:
                        dve.wait_ge(combined, j - 1)
                    dve.tensor_scalar(onehot[:, j % 2, :], count[:, :], token_of[:, j:j + 1], None,
                                      ALU.is_equal).then_inc(onehot_ready, 1)
                    dve.wait_ge(gathered[j], 16)
                    if j >= 1:
                        dve.wait_ge(gate_ready, j)
                    c(dve.tensor_tensor(gate_pick[:, :], taken_row(j)[:, D + j * PER:D + (j + 1) * PER],
                                        core.cf[:, C_OWN4:C_OWN4 + PER], ALU.mult))
                    c.wait()
                    dve.tensor_reduce(gate[:, j:j + 1], gate_pick[:, :], AX, ALU.add).then_inc(gate_ready, 1)
                    dve.wait_ge(tanh_ready, j + 1)
                    if j >= 1:
                        dve.wait_ge(hidden_turned, j)
                    c(dve.scalar_tensor_tensor(out=act_up[:, 0, :], in0=th[:, :], scalar=1.0, in1=psH[:, 0:INTER],
                                               op0=ALU.add, op1=ALU.mult))
                    c.wait()
                    dve.scalar_tensor_tensor(out=act_up[:, 1, :], in0=act_up[:, 0, :], scalar=0.5,
                                             in1=psH[:, INTER:2 * INTER], op0=ALU.mult,
                                             op1=ALU.mult).then_inc(hidden_ready, 1)
                    dve.wait_ge(y_done, j + 1)
                    dve.wait_ge(gate_ready, j + 1)
                    dve.tensor_scalar(y[:, j, :], psY[:, 0:D], gate[:, j:j + 1], None, ALU.mult).then_inc(y_ready, 1)
                dve.wait_ge(combined, TILES)
                for k in range(TB_BANKS):
                    xk = core.X[:, k * 4:(k + 1) * 4, :]
                    dve.tensor_tensor(xk, xk, psC[:, k, :].rearrange("p (t d) -> p t d", t=4),
                                      ALU.add).then_inc(summed, 1)
                dve.wait_ge(summed, TB_BANKS)


C_IDENT = 0
C_ONES = C_IDENT + P
C_EPS = C_ONES + P
C_ORDER8 = C_EPS + 1
C_CAUSAL = C_ORDER8 + 8
C_AFTER = C_CAUSAL + P
C_SHIFT = C_AFTER + P
C_OVER = C_SHIFT + P
C_BAND = C_OVER + P
C_PAIR = C_BAND + 192
C_COUNT = C_PAIR + P
C_AHEAD = C_COUNT + 64
C_OWN4 = C_AHEAD + NT
CONST_COLS = C_OWN4 + 4
ARENA = 20480

WEIGHTS = {
    "L0a": [("qk", "L0a_qk", [P, 4, D]), ("v", "L0a_v", [P, D]), ("cos", "L0a_cos", [P, 2, S]),
            ("sin", "L0a_sin", [P, 2, S]), ("causal_t", "L0a_causal_t", [P, P]), ("o", "L0a_o", [P, D])],
    "L0f": [("wqkv", "L0f_wqkv", [P, 2, 3, 512]), ("wo", "L0f_wo", [P, 2, 4, D]), ("w1", "L0f_w1", [P, 2, 682]),
            ("w2", "L0f_w2", [P, 2, 3, D]), ("ln", "L0f_ln", [P, 4]), ("b1", "L0f_b1", [P, 12]),
            ("b2", "L0f_b2", [1, 2, D]), ("pos", "L0f_pos", [P, 2, 2, 256]), ("scales", "L0f_scales", [P, 8, 64])],
    "L1a": [("qkv", "L1a_qkv", [P, 8, 6, D]), ("out", "L1a_out", [P, 8, D])],
    "L1f": [("router", "L1f_router", [P, 8]), ("router_b", "L1f_router_b", [1, 8]),
            ("W1", "L1f_W1", [P, 8, 512]), ("W2", "L1f_W2", [P, 8, 4, D]), ("b1", "L1f_b1", [P, 32]),
            ("b2", "L1f_b2", [8, D])],
    "L2a": [("cols", "L2a_cols", [P, 2]), ("mix", "L2a_mix", [P, 3]), ("kvr", "L2a_kvr", [P, 3, D]),
            ("out", "L2a_out", [P, D])],
    "L2f": [("router", "L2f_router", [P, 8]), ("angles", "L2f_angles", [P, 4, 64]),
            ("qkv", "L2f_qkv", [P, 8, 384]), ("out", "L2f_out", [P, 8, D])],
    "L3a": [("cols", "L3a_cols", [P, 4]), ("in", "L3a_in", [P, 256]), ("A", "L3a_A", [P, 2, 16]),
            ("B", "L3a_B", [P, 2, 16]), ("C", "L3a_C", [16, 256]), ("out", "L3a_out", [P, 2, D]),
            ("b_out", "L3a_b_out", [1, D])],
    "L3g": [("router", "L3g_router", [P, 64])],
    "L3f": [("gate_up", "L3f_gate_up", [P, 64, 192]), ("down", "L3f_down", [96, 64, D])],
}
PROBS_COLS = 8 * 1280
IN_ARENA = {("L0a", "causal_t"): PROBS_COLS,
            ("L1a", "qkv"): 0, ("L1a", "out"): 6144, ("L1f", "W1"): 7168, ("L1f", "W2"): 7168 + 4096,
            ("L0f", "wqkv"): 15360, ("L0f", "w1"): 15360 + 3072,
            ("L3f", "gate_up"): 0, ("L3f", "down"): 12288}


EARLY = ("L0a", "L0f")


def place_weights(nc, ctx, core, stages):
    for stage in stages:
        parts = WEIGHTS[stage]
        core.w[stage] = {}
        for key, _, shape in parts:
            if (stage, key) in IN_ARENA:
                at, n = IN_ARENA[stage, key], 1
                for k in shape[1:]:
                    n *= k
                flat = core.arena[0:shape[0], at:at + n]
                core.w[stage][key] = flat if len(shape) == 2 else flat.rearrange(
                    "p (a b) -> p a b", a=shape[1]) if len(shape) == 3 else flat.rearrange(
                    "p (a b c) -> p a b c", a=shape[1], b=shape[2])
            else:
                t = ctx.enter_context(nc.sbuf_tensor(f"w_{stage}_{key}", shape, F32))
                core.w[stage][key] = t[:, :] if len(shape) == 2 else t[:, :, :] if len(shape) == 3 else t[:, :, :, :]


def load_weights(core, sp, stages):
    for stage in stages:
        for key, name, _ in WEIGHTS[stage]:
            core.load(sp, stage, core.w[stage][key], core.dram[name])


def load_layer1_weights(core, sp):
    core.wait_weights(sp, "L0a")
    load_weights(core, sp, ("L1a", "L1f"))


def load_late_weights(core, sp):
    for lo in range(0, 64, 16):
        core.load(sp, "L3f", core.w["L3f"]["gate_up"][:, lo:lo + 16, :], core.dram["L3f_gate_up"][:, lo:lo + 16, :])
        core.load(sp, "L3f", core.w["L3f"]["down"][:, lo:lo + 16, :], core.dram["L3f_down"][:, lo:lo + 16, :])


def program(nc, dram, out):
    x_dram = dram["x"].rearrange("b (t p) d -> p (b t) d", p=P)
    out_dram = out.rearrange("b (t p) d -> p (b t) d", p=P)
    with ExitStack() as ctx:
        core = Core(nc, ctx, dram)
        constants_ready = ctx.enter_context(nc.semaphore("constants_ready"))
        place_weights(nc, ctx, core, [stage for stage in WEIGHTS if stage not in EARLY])
        with ExitStack() as early:
            place_weights(nc, early, core, ["L0f"])
            earliest = early.enter_context(ExitStack())
            place_weights(nc, earliest, core, ["L0a"])
            with nc.Block() as block:
                @block.sync
                def _(sp):
                    sp.dma_start(core.cf[:, :], dram["consts"]).then_inc(core.const_loaded, 16)
                    sp.dma_start(core.X[:, 0:NT, :], x_dram).then_inc(core.x_loaded, 16)
                    load_weights(core, sp, ["L0a"])

                @block.vector
                def _(dve):
                    dve.wait_ge(core.const_loaded, 16)
                    dve.wait_ge(core.x_loaded, 16)
                    dve.memset(core.X[:, NT:NT + TB, :], 0.0).then_inc(constants_ready, 1)
                    dve.tensor_copy(core.identb[:, :], core.ident).then_inc(constants_ready, 1)
                    dve.tensor_copy(core.band[:, :], core.cf[:, C_BAND:C_BAND + 64 + P]).then_inc(constants_ready, 1)
                    dve.tensor_copy(core.pair_mask[:, :], core.cf[:, C_PAIR:C_PAIR + P]).then_inc(constants_ready, 1)
                    dve.tensor_copy(core.causal[:, :], core.cf[:, C_CAUSAL:C_CAUSAL + P]).then_inc(constants_ready, 1)

                @block.scalar
                def _(act):
                    act.wait_ge(core.const_loaded, 16)

                @block.tensor
                def _(pe):
                    pe.wait_ge(core.const_loaded, 16)
                    pe.wait_ge(constants_ready, 5)
            layer0_attn(nc, core)
            core.retire()
            earliest.close()
            layer0_ffn(nc, core)
            core.retire()
        for layer in (layer1_attn, layer1_ffn, layer2_attn, layer2_ffn, layer3_attn):
            layer(nc, core)
            core.retire()
        layer3_ffn(nc, core)
        with nc.Block() as block:
            @block.sync
            def _(sp):
                sp.dma_start(out_dram, core.X[:, 0:NT, :]).then_inc(core.stored, 16)
                sp.wait_ge(core.stored, 16)
                for stage in core.loaded:
                    core.wait_weights(sp, stage)


def lay_out(a):
    import numpy as np
    c = np.ascontiguousarray
    w = {"x": a["L0_attn_x"]}
    consts = np.zeros((P, CONST_COLS), np.float32)
    consts[:, C_IDENT:C_IDENT + P] = np.eye(P)
    consts[:, C_ONES:C_ONES + P] = 1.0
    consts[:, C_EPS] = EPS
    consts[:, C_ORDER8:C_ORDER8 + 8] = 8 - np.arange(8)
    q_at, k_at = np.arange(P)[:, None], np.arange(P)[None, :]
    consts[:, C_CAUSAL:C_CAUSAL + P] = np.where(k_at > q_at, np.float32(NEG), 0)
    consts[:, C_AFTER:C_AFTER + P] = np.where(q_at > k_at, 0.5, 0)
    consts[:, C_SHIFT:C_SHIFT + P] = k_at == q_at + 1
    consts[P - 1, C_OVER] = 1.0
    key = np.arange(192)[None, :] - 64
    consts[:, C_BAND:C_BAND + 192] = np.where((key > q_at) | (key < q_at - 64), np.float32(NEG), 0)
    own = (q_at // 64 == k_at // 64) & (k_at <= q_at)
    consts[:, C_PAIR:C_PAIR + P] = np.where(own, 0, np.float32(NEG))
    consts[:, C_COUNT:C_COUNT + 64] = np.arange(1, 65)
    consts[:, C_AHEAD:C_AHEAD + NT] = NT * P - (np.arange(NT)[None, :] * P + q_at)
    consts[:, C_OWN4:C_OWN4 + 4] = q_at // 32 == np.arange(4)[None, :]
    w["consts"] = consts
    swap = np.arange(D) ^ 1
    w["L0a_qk"] = np.stack([a["L0_attn_wq"], a["L0_attn_wq"][:, swap], a["L0_attn_wk"], a["L0_attn_wk"][:, swap]], 1)
    w["L0a_v"] = a["L0_attn_wv"]
    w["L0a_o"] = a["L0_attn_wo"]
    dh = 8
    inv_freq = (1.0 / np.float32(10000.0) ** (np.arange(0, dh, 2, dtype=np.float32) / np.float32(dh))).astype(np.float32)
    angle = (np.arange(S, dtype=np.float32)[None, :] * inv_freq[(np.arange(D) % dh) // 2][:, None]).astype(np.float32)
    sign = np.where(np.arange(D) % 2, 1, -1)[:, None]
    scale = dh ** -0.5
    cos, sin = np.cos(angle.astype(np.float64)), np.sin(angle.astype(np.float64)) * sign
    w["L0a_cos"] = np.stack([cos * scale, cos], 1).astype(np.float32)
    w["L0a_sin"] = np.stack([sin * scale, sin], 1).astype(np.float32)
    w["L0a_causal_t"] = consts[:, C_CAUSAL:C_CAUSAL + P].T
    w["L0f_wqkv"] = a["L0_ffn_wqkv"].reshape(2, D, 3, 512).transpose(1, 0, 2, 3)
    w["L0f_wo"] = a["L0_ffn_wo"].reshape(2, 4, P, D).transpose(2, 0, 1, 3)
    w["L0f_w1"] = a["L0_ffn_w1"].transpose(1, 0, 2)
    hid, pad = 341, 3 * P - 341
    w["L0f_w2"] = np.pad(a["L0_ffn_w2"], ((0, 0), (0, pad), (0, 0))).reshape(2, 3, P, D).transpose(2, 0, 1, 3)
    w["L0f_ln"] = np.stack([a["L0_ffn_ln_g"][0], a["L0_ffn_ln_b"][0], a["L0_ffn_ln_g"][1], a["L0_ffn_ln_b"][1]], 1)
    w["L0f_b1"] = np.pad(a["L0_ffn_b1"].reshape(2, 2, hid), ((0, 0), (0, 0), (0, pad))).reshape(12, P).T
    w["L0f_b2"] = a["L0_ffn_b2"].reshape(1, 2, D)
    half = np.arange(0, 64, 2, dtype=np.float32)
    inv_freq = (1.0 / np.float32(10000.0) ** (half / np.float32(64))).astype(np.float32)
    t = np.arange(S, dtype=np.float32)
    freqs = (t[:, None] * inv_freq[None, :]).astype(np.float32).astype(np.float64)
    base = (half.astype(np.float64) + 0.4 * 64) / (1.4 * 64)
    xpos = base[None, :] ** ((t[:, None] - S // 2) / 32.0)
    pos = np.zeros((2, 2, S, 64))
    for j, sc in enumerate((xpos, 1.0 / xpos)):
        pos[j, 0] = np.concatenate([np.cos(freqs) * sc] * 2, -1)
        pos[j, 1] = np.concatenate([-np.sin(freqs) * sc, np.sin(freqs) * sc], -1)
    w["L0f_pos"] = pos.reshape(2, 2, TB, P, 64).transpose(3, 0, 1, 2, 4).reshape(P, 2, 2, 256).astype(np.float32)
    other = (np.arange(64) + 32) % 64
    qs, ks = a["L0_ffn_q_scale"], a["L0_ffn_k_scale"]
    scales = np.stack([qs, qs[:, other], ks, ks[:, other]], 1).reshape(1, 8, 64)
    w["L0f_scales"] = np.broadcast_to(scales, (P, 8, 64))
    qkv = a["L1_attn_w_qkv"].reshape(D, 6, 8, D)
    w["L1a_qkv"] = np.stack([qkv[:, n].transpose(0, 1, 2) if n == 2 else qkv[:, n].transpose(2, 1, 0)
                             for n in range(6)], 2)
    w["L1a_out"] = a["L1_attn_w_out"].reshape(8, D, D).transpose(1, 0, 2)
    w["L1f_router"] = a["L1_ffn_router_w"]
    w["L1f_router_b"] = a["L1_ffn_router_b"].reshape(1, 8)
    w["L1f_W1"] = a["L1_ffn_W1"].transpose(1, 0, 2)
    w["L1f_W2"] = a["L1_ffn_W2"].reshape(8, 4, P, D).transpose(2, 0, 1, 3)
    w["L1f_b1"] = a["L1_ffn_b1"].reshape(32, P).T
    w["L1f_b2"] = a["L1_ffn_b2"]
    w["L2a_cols"] = np.stack([a["L2_attn_time_decay"], a["L2_attn_time_first"]], 1)
    w["L2a_mix"] = np.stack([a["L2_attn_time_mix_" + n].reshape(D) for n in "kvr"], 1)
    w["L2a_kvr"] = np.stack([a["L2_attn_W" + n].T for n in "kvr"], 1)
    w["L2a_out"] = a["L2_attn_Wo"].T
    w["L2f_router"] = a["L2_ffn_Wr"].T
    inv_freq = (1.0 / np.float32(10000.0) ** (np.arange(32, dtype=np.float32) * np.float32(2.0) / np.float32(64)))
    ang = (np.arange(S, dtype=np.float32)[:, None] * inv_freq.astype(np.float32)).astype(np.float32).astype(np.float64)
    angles = np.concatenate([np.cos(ang), np.sin(ang)], 1).astype(np.float32)
    w["L2f_angles"] = angles.reshape(TB, P, 64).transpose(1, 0, 2)
    w["L2f_qkv"] = a["L2_ffn_Wqkv"].transpose(1, 0, 2)
    w["L2f_out"] = a["L2_ffn_Wo"].transpose(1, 0, 2)
    w["L3a_cols"] = np.concatenate([np.stack([a["L3_attn_norm_w"], a["L3_attn_norm_b"]], 1),
                                    a["L3_attn_b_in"].reshape(2, P).T], 1)
    w["L3a_in"] = a["L3_attn_W_in"].T
    w["L3a_A"] = a["L3_attn_A"].reshape(2, P, 16).transpose(1, 0, 2)
    w["L3a_B"] = a["L3_attn_B_ssm"].reshape(2, P, 16).transpose(1, 0, 2)
    w["L3a_C"] = a["L3_attn_C_ssm"].T
    w["L3a_out"] = a["L3_attn_W_out"].T.reshape(2, P, D).transpose(1, 0, 2)
    w["L3a_b_out"] = a["L3_attn_b_out"].reshape(1, D)
    w["L3g_router"] = a["L3_ffn_gate_w"].T
    w["L3f_gate_up"] = np.concatenate([a["L3_ffn_w_gate"], a["L3_ffn_w_up"]], 1).transpose(2, 0, 1)
    w["L3f_down"] = a["L3_ffn_w_down"].transpose(2, 0, 1)
    return {k: c(v) for k, v in w.items()}


def kernel(**inputs):
    import numpy as np
    import concourse.bacc as bacc
    from concourse.bass_utils import run_bass_kernel_spmd

    nc = bacc.Bacc("TRN2", target_bir_lowering=False, num_devices=1)
    arrays = lay_out({k: np.asarray(v) for k, v in inputs.items()})
    dram = {k: nc.dram_tensor("in_" + k, v.shape, mybir.dt.from_np(v.dtype), kind="ExternalInput").ap()
            for k, v in arrays.items()}
    out = nc.dram_tensor("out", (B, S, D), F32, kind="ExternalOutput").ap()
    program(nc, dram, out)
    result = run_bass_kernel_spmd(nc, [{"in_" + k: v for k, v in arrays.items()}], core_ids=[0])
    return result.results[0]["out"]
```
